# Optimizing a Trainium2 kernel written in Bass

```python
import numpy as np
import jax
import jax.numpy as jnp

def _softmax(x, axis=-1):
    return jax.nn.softmax(x, axis=axis)

def _gelu(x):
    return jax.nn.gelu(x, approximate=True)

def _silu(x):
    return jax.nn.silu(x)

def _sigmoid(x):
    return jax.nn.sigmoid(x)

def _layernorm(x, axis=-1, eps=1e-05):
    m = jnp.mean(x, axis=axis, keepdims=True)
    v = jnp.var(x, axis=axis, keepdims=True)
    return (x - m) / jnp.sqrt(v + eps)

def _scatter_add(tgt, idx, src, axis=0):
    return tgt.at[idx].add(src)

def _segment_sum(src, seg, n):
    return jax.ops.segment_sum(src, seg, n)
kernel_name = 'mk_decoder_postln_d2_seqx_r8_8328ba'

def setup_inputs(seed: int=0):
    np.random.seed(seed)
    _w = jnp.asarray

    def _rec_inputs():
        import jax
        import jax.numpy as jnp
        _rk = jax.random.key(seed)
        x = -0.0002928 + 1 * jax.random.normal(jax.random.fold_in(_rk, 1), (16, 256, 128), jnp.float32)
        _lenS = 256 - jax.random.randint(jax.random.fold_in(_rk, 7), (16,), 0, max(1, 256 // 4) + 1, jnp.int32)
        _lenS2 = 64 - jax.random.randint(jax.random.fold_in(_rk, 8), (16,), 0, max(1, 64 // 4) + 1, jnp.int32)
        _ctx_1024P = jax.random.normal(jax.random.fold_in(_rk, 11), (16, 16, 128), jnp.float32)
        _ctx_1024c = jax.random.dirichlet(jax.random.fold_in(_rk, 511), 0.3 * jnp.ones((16,), jnp.float32), (16, 64))
        _ctx_1024t = jnp.einsum('bsk,bkd->bsd', _ctx_1024c, _ctx_1024P)
        _ctx_1024t = _ctx_1024t * jax.lax.rsqrt(jnp.mean(jnp.square(_ctx_1024t)) + 1e-12) * 0.953939
        ctx_1024 = 4.13588e-05 + 0.999923 * (_ctx_1024t + 0.3 * jax.random.normal(jax.random.fold_in(_rk, 611), (16, 64, 128), jnp.float32))
        return (x, ctx_1024)
    x, ctx_1024 = _rec_inputs()

    def _L0_attn_setup():
        import jax, jax.numpy as jnp
        import numpy as np
        H = 16
        SPLAT_RATIO = 0.4
        STD_RATIO = 1.0 - SPLAT_RATIO
        key = jax.random.key(seed)
        ks = jax.random.split(key, 12)
        B, N, D, S = (2, 128, 128, 64)
        Db = D // 2
        f32 = jnp.float32
        n = lambda k, shape, s: jax.random.normal(k, shape, dtype=f32) * s
        return {'x': n(ks[0], (B, N, D), 1.0), 'Wq': n(ks[1], (D, D), 0.02), 'Wk': n(ks[2], (D, D), 0.02), 'Wv': n(ks[3], (D, D), 0.02), 'Wo': n(ks[4], (D, D), 0.02), 'splat_positions': n(ks[5], (S, D), 0.02), 'splat_scales': jnp.ones((S,), f32), 'splat_importance': jnp.ones((S,), f32), 'We': n(ks[6], (D, Db), 0.02), 'be': jnp.zeros((Db,), f32), 'Wt': n(ks[7], (S, Db, Db), 0.02), 'bt': jnp.zeros((S, Db), f32), 'Wd': n(ks[8], (Db, D), 0.02), 'bd': jnp.zeros((D,), f32), 'Wg': n(ks[9], (D, D), 0.02), 'bg': jnp.zeros((D,), f32)}
    _L0_attn_all = _L0_attn_setup()
    _L0_attn_in = {k: v for k, v in _L0_attn_all.items() if k in ('Wq', 'Wk', 'Wv', 'Wo', 'splat_positions', 'splat_scales', 'splat_importance', 'We', 'be', 'Wt', 'bt', 'Wd', 'bd', 'Wg', 'bg')}
    del _L0_attn_all

    def _L0_xattn_setup():
        import jax, jax.numpy as jnp
        import numpy as np
        B, SQ, SK, D, H = (2, 256, 512, 128, 16)
        HD = D // H

        def _local_allowed_mask(num_q, num_k):
            kpq, extra = (num_k // num_q, num_k % num_q)
            i = jnp.arange(num_q)
            start = i * kpq + jnp.minimum(i, extra)
            end = start + kpq + (i < extra)
            j = jnp.arange(num_k)
            return (j[None, :] >= start[:, None]) & (j[None, :] < end[:, None])
        key = jax.random.key(seed)
        ks = jax.random.split(key, 6)
        s = 0.02
        return {'x': jax.random.normal(ks[0], (B, SQ, D), jnp.float32), 'c': jax.random.normal(ks[1], (B, SK, D), jnp.float32), 'Wq': jax.random.normal(ks[2], (D, D), jnp.float32) * s, 'bq': jnp.zeros((D,), jnp.float32), 'Wk': jax.random.normal(ks[3], (D, D), jnp.float32) * s, 'bk': jnp.zeros((D,), jnp.float32), 'Wv': jax.random.normal(ks[4], (D, D), jnp.float32) * s, 'bv': jnp.zeros((D,), jnp.float32), 'Wo': jax.random.normal(ks[5], (D, D), jnp.float32) * s, 'bo': jnp.zeros((D,), jnp.float32)}
    _L0_xattn_all = _L0_xattn_setup()
    _L0_xattn_in = {k: v for k, v in _L0_xattn_all.items() if k in ('Wq', 'bq', 'Wk', 'bk', 'Wv', 'bv', 'Wo', 'bo')}
    del _L0_xattn_all

    def _L0_ffn_setup():
        import jax, jax.numpy as jnp
        import numpy as np
        NUM_EXPERTS = 8
        HIDDEN = 128
        D_FF = 512
        SCALE = 0.8
        SPARSITY = 0.1

        def _perturb_attractive(w, scale=SCALE, sparsity=SPARSITY):
            a = jnp.abs(w)
            flat = a.ravel()
            n = flat.shape[0]
            k = max(1, int(n * sparsity / 2))
            s = jnp.sort(flat)
            thr_bot = s[k - 1]
            thr_top = s[n - k]
            tier = jnp.where(a >= thr_top, -1.0, jnp.where(a <= thr_bot, 1.0, 0.0))
            return w + scale * w * tier

        def _stack_expert_params(w):
            pw = _perturb_attractive(w)
            return jnp.concatenate([w[None], jnp.broadcast_to(pw, (NUM_EXPERTS - 1,) + w.shape)], axis=0)
        key = jax.random.key(seed)
        ks = jax.random.split(key, 6)
        B, S, H, F, E = (2, 256, HIDDEN, D_FF, NUM_EXPERTS)
        return {'x': jax.random.normal(ks[0], (B, S, H), dtype=jnp.float32), 'W1': jax.random.normal(ks[1], (H, F), dtype=jnp.float32) * (1.0 / np.sqrt(H)), 'b1': jax.random.normal(ks[2], (F,), dtype=jnp.float32) * 0.02, 'W2': jax.random.normal(ks[3], (F, H), dtype=jnp.float32) * (1.0 / np.sqrt(F)), 'b2': jax.random.normal(ks[4], (H,), dtype=jnp.float32) * 0.02, 'ln_gamma': jnp.ones((H,), dtype=jnp.float32), 'ln_beta': jnp.zeros((H,), dtype=jnp.float32), 'Wr': jax.random.normal(ks[5], (H, E), dtype=jnp.float32) * (1.0 / np.sqrt(H)), 'br': jnp.zeros((E,), dtype=jnp.float32)}
    _L0_ffn_all = _L0_ffn_setup()
    _L0_ffn_in = {k: v for k, v in _L0_ffn_all.items() if k in ('W1', 'b1', 'W2', 'b2', 'ln_gamma', 'ln_beta', 'Wr', 'br')}
    del _L0_ffn_all

    def _L1_attn_setup():
        import jax, jax.numpy as jnp
        import numpy as np
        import math
        B, N, DIM, H, DH, NNULL = (2, 256, 128, 16, 64, 2)
        SCALE = 8.0
        LN_EPS = 1e-05

        def _alibi_slopes(heads):
            start = 2.0 ** (-2.0 ** (-(math.log2(heads) - 3)))
            return np.array([start * start ** i for i in range(heads)], dtype=np.float32)

        def _l2norm(t):
            n = jnp.sqrt(jnp.sum(t * t, axis=-1, keepdims=True))
            return t / jnp.maximum(n, 1e-12)
        key = jax.random.key(seed)
        ks = jax.random.split(key, 6)
        inner = H * DH
        return {'x': jax.random.normal(ks[0], (B, N, DIM), dtype=jnp.float32), 'norm_g': jnp.ones((DIM,), jnp.float32), 'norm_b': jnp.zeros((DIM,), jnp.float32), 'Wq': jax.random.normal(ks[1], (DIM, inner), jnp.float32) * 0.02, 'Wkv': jax.random.normal(ks[2], (DIM, 2 * inner), jnp.float32) * 0.02, 'q_scale': jnp.ones((DH,), jnp.float32), 'k_scale': jnp.ones((DH,), jnp.float32), 'null_kv': jax.random.normal(ks[3], (H, 2 * NNULL, DH), jnp.float32), 'Wout': jax.random.normal(ks[4], (inner, DIM), jnp.float32) * 0.02}
    _L1_attn_all = _L1_attn_setup()
    _L1_attn_in = {k: v for k, v in _L1_attn_all.items() if k in ('norm_g', 'norm_b', 'Wq', 'Wkv', 'q_scale', 'k_scale', 'null_kv', 'Wout')}
    del _L1_attn_all

    def _L1_xattn_setup():
        import jax, jax.numpy as jnp
        import numpy as np
        DIM = 128
        CTX_DIM = 128
        HEADS = 8
        DIM_HEAD = 64
        INNER = HEADS * DIM_HEAD
        EPS = 1e-05

        def _layer_norm(x, gamma, beta):
            mu = jnp.mean(x, axis=-1, keepdims=True)
            var = jnp.mean(jnp.square(x - mu), axis=-1, keepdims=True)
            return (x - mu) * jax.lax.rsqrt(var + EPS) * gamma + beta
        key = jax.random.key(seed)
        ks = jax.random.split(key, 8)
        b, n, m = (4, 256, 256)
        x = jax.random.normal(ks[0], (b, n, DIM), dtype=jnp.float32)
        context = jax.random.normal(ks[1], (b, m, CTX_DIM), dtype=jnp.float32)
        Wq = jax.random.normal(ks[2], (DIM, INNER), dtype=jnp.float32) / np.sqrt(DIM)
        Wkv = jax.random.normal(ks[3], (CTX_DIM, 2 * INNER), dtype=jnp.float32) / np.sqrt(CTX_DIM)
        Wout = jax.random.normal(ks[4], (INNER, DIM), dtype=jnp.float32) / np.sqrt(INNER)
        bout = jnp.zeros((DIM,), dtype=jnp.float32)
        g1 = jnp.ones((DIM,), dtype=jnp.float32)
        b1 = jnp.zeros((DIM,), dtype=jnp.float32)
        g2 = jnp.ones((CTX_DIM,), dtype=jnp.float32)
        b2 = jnp.zeros((CTX_DIM,), dtype=jnp.float32)
        return {'x': x, 'context': context, 'g1': g1, 'b1': b1, 'g2': g2, 'b2': b2, 'Wq': Wq, 'Wkv': Wkv, 'Wout': Wout, 'bout': bout}
    _L1_xattn_all = _L1_xattn_setup()
    _L1_xattn_in = {k: v for k, v in _L1_xattn_all.items() if k in ('g1', 'b1', 'g2', 'b2', 'Wq', 'Wkv', 'Wout', 'bout')}
    del _L1_xattn_all

    def _L1_ffn_setup():
        import jax, jax.numpy as jnp
        import numpy as np
        S_LEN, BATCH, HIDDEN = (256, 2, 128)
        N_HEADS, N_KV = (16, 8)
        N_EXP, TOP_K, CAP_F = (8, 2, 1.25)
        FFN = 512
        HEAD_DIM = HIDDEN // N_HEADS
        Q_PER_KV = N_HEADS // N_KV
        EPS = 1e-05
        NEG = -1000000000.0

        def _ln(x, w, b):
            mu = jnp.mean(x, -1, keepdims=True)
            var = jnp.var(x, -1, keepdims=True)
            return (x - mu) * jax.lax.rsqrt(var + EPS) * w + b

        def _forward(hidden_states, ln1_weight, ln1_bias, ln2_weight, ln2_bias, qkv_weight, proj_weight, router_weight, moe_w1, moe_w2):
            S, B, H = hidden_states.shape
            ln1 = _ln(hidden_states, ln1_weight, ln1_bias)
            qkv = (ln1 @ qkv_weight.T).reshape(S, B, N_KV, (Q_PER_KV + 2) * HEAD_DIM)
            q_dim = Q_PER_KV * HEAD_DIM
            q = qkv[..., :q_dim].reshape(S, B, N_HEADS, HEAD_DIM)
            k = jnp.repeat(qkv[..., q_dim:q_dim + HEAD_DIM], Q_PER_KV, axis=2)
            v = jnp.repeat(qkv[..., q_dim + HEAD_DIM:], Q_PER_KV, axis=2)
            scores = jnp.einsum('sbhd,tbhd->bhst', q, k) / jnp.sqrt(jnp.float32(HEAD_DIM))
            causal = jnp.tril(jnp.ones((S, S), bool))
            attn = jax.nn.softmax(jnp.where(causal[None, None], scores, NEG), axis=-1)
            attn_out = jnp.einsum('bhst,tbhd->sbhd', attn, v).reshape(S, B, H)
            hidden_after_attn = hidden_states + attn_out @ proj_weight.T
            x = _ln(hidden_after_attn, ln2_weight, ln2_bias).reshape(-1, H)
            N = S * B
            probs = jax.nn.softmax(x.astype(jnp.float32) @ router_weight, axis=-1)
            top_p, top_i = jax.lax.top_k(probs, TOP_K)
            top_p = top_p / jnp.sum(top_p, -1, keepdims=True)
            flat_exp = top_i.reshape(-1)
            order = jnp.argsort(flat_exp)
            sorted_exp = flat_exp[order]
            counts = jnp.bincount(sorted_exp, length=N_EXP)
            offsets = jnp.concatenate([jnp.zeros((1,), counts.dtype), jnp.cumsum(counts)])
            within = jnp.arange(N * TOP_K) - offsets[sorted_exp]
            cap = int(np.ceil(N * TOP_K / N_EXP * CAP_F))
            keep = within < cap
            slot = jnp.where(keep, sorted_exp * cap + within, N_EXP * cap)
            tok_id = order // TOP_K
            padded_tokens = jnp.zeros((N_EXP * cap + 1, H), x.dtype).at[slot].set(x[tok_id])[:-1]
            padded_probs = jnp.zeros((N_EXP * cap + 1,), jnp.float32).at[slot].set(top_p.reshape(-1)[order])[:-1]
            padded_ids = jnp.zeros((N_EXP * cap + 1,), jnp.int32).at[slot].set(tok_id.astype(jnp.int32))[:-1]
            exp_in = padded_tokens.reshape(N_EXP, cap, H)
            act = jax.nn.gelu(jnp.einsum('ech,ehf->ecf', exp_in, moe_w1), approximate=False)
            exp_out = jnp.einsum('ecf,efh->ech', act, moe_w2).reshape(N_EXP * cap, H)
            weighted = exp_out * padded_probs[:, None].astype(exp_out.dtype)
            moe = jnp.zeros((N, H), exp_out.dtype).at[padded_ids].add(weighted)
            return hidden_after_attn + moe.reshape(S, B, H)
        ks = jax.random.split(jax.random.key(seed), 6)
        qkv_out = N_KV * (Q_PER_KV + 2) * HEAD_DIM
        sc = 0.02
        return {'hidden_states': jax.random.normal(ks[0], (S_LEN, BATCH, HIDDEN), jnp.float32), 'ln1_weight': jnp.ones((HIDDEN,), jnp.float32), 'ln1_bias': jnp.zeros((HIDDEN,), jnp.float32), 'ln2_weight': jnp.ones((HIDDEN,), jnp.float32), 'ln2_bias': jnp.zeros((HIDDEN,), jnp.float32), 'qkv_weight': jax.random.normal(ks[1], (qkv_out, HIDDEN), jnp.float32) * sc, 'proj_weight': jax.random.normal(ks[2], (HIDDEN, HIDDEN), jnp.float32) * sc, 'router_weight': jax.random.normal(ks[3], (HIDDEN, N_EXP), jnp.float32) * sc, 'moe_w1': jax.random.normal(ks[4], (N_EXP, HIDDEN, FFN), jnp.float32) * sc, 'moe_w2': jax.random.normal(ks[5], (N_EXP, FFN, HIDDEN), jnp.float32) * sc}
    _L1_ffn_all = _L1_ffn_setup()
    _L1_ffn_in = {k: v for k, v in _L1_ffn_all.items() if k in ('ln1_weight', 'ln1_bias', 'ln2_weight', 'ln2_bias', 'qkv_weight', 'proj_weight', 'router_weight', 'moe_w1', 'moe_w2')}
    del _L1_ffn_all
    return {'x': x, 'ctx_1024': ctx_1024, 'L0_attn_Wq': _L0_attn_in['Wq'], 'L0_attn_Wk': _L0_attn_in['Wk'], 'L0_attn_Wv': _L0_attn_in['Wv'], 'L0_attn_Wo': _L0_attn_in['Wo'], 'L0_attn_splat_positions': _L0_attn_in['splat_positions'], 'L0_attn_splat_scales': _L0_attn_in['splat_scales'], 'L0_attn_splat_importance': _L0_attn_in['splat_importance'], 'L0_attn_We': _L0_attn_in['We'], 'L0_attn_be': _L0_attn_in['be'], 'L0_attn_Wt': _L0_attn_in['Wt'], 'L0_attn_bt': _L0_attn_in['bt'], 'L0_attn_Wd': _L0_attn_in['Wd'], 'L0_attn_bd': _L0_attn_in['bd'], 'L0_attn_Wg': _L0_attn_in['Wg'], 'L0_attn_bg': _L0_attn_in['bg'], 'L0_xattn_Wq': _L0_xattn_in['Wq'], 'L0_xattn_bq': _L0_xattn_in['bq'], 'L0_xattn_Wk': _L0_xattn_in['Wk'], 'L0_xattn_bk': _L0_xattn_in['bk'], 'L0_xattn_Wv': _L0_xattn_in['Wv'], 'L0_xattn_bv': _L0_xattn_in['bv'], 'L0_xattn_Wo': _L0_xattn_in['Wo'], 'L0_xattn_bo': _L0_xattn_in['bo'], 'L0_ffn_W1': _L0_ffn_in['W1'], 'L0_ffn_b1': _L0_ffn_in['b1'], 'L0_ffn_W2': _L0_ffn_in['W2'], 'L0_ffn_b2': _L0_ffn_in['b2'], 'L0_ffn_ln_gamma': _L0_ffn_in['ln_gamma'], 'L0_ffn_ln_beta': _L0_ffn_in['ln_beta'], 'L0_ffn_Wr': _L0_ffn_in['Wr'], 'L0_ffn_br': _L0_ffn_in['br'], 'L1_attn_norm_g': _L1_attn_in['norm_g'], 'L1_attn_norm_b': _L1_attn_in['norm_b'], 'L1_attn_Wq': _L1_attn_in['Wq'], 'L1_attn_Wkv': _L1_attn_in['Wkv'], 'L1_attn_q_scale': _L1_attn_in['q_scale'], 'L1_attn_k_scale': _L1_attn_in['k_scale'], 'L1_attn_null_kv': _L1_attn_in['null_kv'], 'L1_attn_Wout': _L1_attn_in['Wout'], 'L1_xattn_g1': _L1_xattn_in['g1'], 'L1_xattn_b1': _L1_xattn_in['b1'], 'L1_xattn_g2': _L1_xattn_in['g2'], 'L1_xattn_b2': _L1_xattn_in['b2'], 'L1_xattn_Wq': _L1_xattn_in['Wq'], 'L1_xattn_Wkv': _L1_xattn_in['Wkv'], 'L1_xattn_Wout': _L1_xattn_in['Wout'], 'L1_xattn_bout': _L1_xattn_in['bout'], 'L1_ffn_ln1_weight': _L1_ffn_in['ln1_weight'], 'L1_ffn_ln1_bias': _L1_ffn_in['ln1_bias'], 'L1_ffn_ln2_weight': _L1_ffn_in['ln2_weight'], 'L1_ffn_ln2_bias': _L1_ffn_in['ln2_bias'], 'L1_ffn_qkv_weight': _L1_ffn_in['qkv_weight'], 'L1_ffn_proj_weight': _L1_ffn_in['proj_weight'], 'L1_ffn_router_weight': _L1_ffn_in['router_weight'], 'L1_ffn_moe_w1': _L1_ffn_in['moe_w1'], 'L1_ffn_moe_w2': _L1_ffn_in['moe_w2']}

def reference(x, ctx_1024, L0_attn_Wq, L0_attn_Wk, L0_attn_Wv, L0_attn_Wo, L0_attn_splat_positions, L0_attn_splat_scales, L0_attn_splat_importance, L0_attn_We, L0_attn_be, L0_attn_Wt, L0_attn_bt, L0_attn_Wd, L0_attn_bd, L0_attn_Wg, L0_attn_bg, L0_xattn_Wq, L0_xattn_bq, L0_xattn_Wk, L0_xattn_bk, L0_xattn_Wv, L0_xattn_bv, L0_xattn_Wo, L0_xattn_bo, L0_ffn_W1, L0_ffn_b1, L0_ffn_W2, L0_ffn_b2, L0_ffn_ln_gamma, L0_ffn_ln_beta, L0_ffn_Wr, L0_ffn_br, L1_attn_norm_g, L1_attn_norm_b, L1_attn_Wq, L1_attn_Wkv, L1_attn_q_scale, L1_attn_k_scale, L1_attn_null_kv, L1_attn_Wout, L1_xattn_g1, L1_xattn_b1, L1_xattn_g2, L1_xattn_b2, L1_xattn_Wq, L1_xattn_Wkv, L1_xattn_Wout, L1_xattn_bout, L1_ffn_ln1_weight, L1_ffn_ln1_bias, L1_ffn_ln2_weight, L1_ffn_ln2_bias, L1_ffn_qkv_weight, L1_ffn_proj_weight, L1_ffn_router_weight, L1_ffn_moe_w1, L1_ffn_moe_w2):
    import jax
    import jax.numpy as jnp

    def _L0_attn_ref(x, Wq, Wk, Wv, Wo, splat_positions, splat_scales, splat_importance, We, be, Wt, bt, Wd, bd, Wg, bg):
        import jax, jax.numpy as jnp
        import numpy as np
        H = 16
        SPLAT_RATIO = 0.4
        STD_RATIO = 1.0 - SPLAT_RATIO
        B, N, D = x.shape
        Dh = D // H
        q = (x @ Wq).reshape(B, N, H, Dh)
        k = (x @ Wk).reshape(B, N, H, Dh)
        v = (x @ Wv).reshape(B, N, H, Dh)
        scores = jnp.einsum('bqhd,bkhd->bhqk', q, k) * Dh ** (-0.5)
        attn = jax.nn.softmax(scores, axis=-1)
        std_out = jnp.einsum('bhqk,bkhd->bqhd', attn, v).reshape(B, N, D)
        x2 = jnp.sum(x * x, axis=-1, keepdims=True)
        s2 = jnp.sum(splat_positions * splat_positions, axis=-1)
        d2 = jnp.maximum(x2 + s2[None, None, :] - 2.0 * jnp.einsum('bnd,sd->bns', x, splat_positions), 0.0)
        scales = jnp.maximum(jnp.abs(splat_scales), 1e-06)
        infl = jnp.exp(-0.5 * d2 / (scales * scales)) * jnp.abs(splat_importance)
        total = jnp.maximum(jnp.sum(infl, axis=1), 1e-08)
        gathered = jnp.einsum('bns,bnd->bsd', infl, x) / total[..., None]
        enc = jax.nn.relu(gathered @ We + be)
        trans = jnp.einsum('bsd,sde->bse', enc, Wt) + bt
        dec = trans @ Wd + bd
        flow = jnp.einsum('bns,bsd->bnd', infl, dec)
        flow = flow * jax.nn.sigmoid(x @ Wg + bg)
        out = (STD_RATIO * std_out + SPLAT_RATIO * flow) @ Wo
        return out

    def _L0_xattn_ref(x, c, Wq, bq, Wk, bk, Wv, bv, Wo, bo):
        import jax, jax.numpy as jnp
        import numpy as np
        B, SQ, SK, D, H = (2, 256, 512, 128, 16)
        HD = D // H

        def _local_allowed_mask(num_q, num_k):
            kpq, extra = (num_k // num_q, num_k % num_q)
            i = jnp.arange(num_q)
            start = i * kpq + jnp.minimum(i, extra)
            end = start + kpq + (i < extra)
            j = jnp.arange(num_k)
            return (j[None, :] >= start[:, None]) & (j[None, :] < end[:, None])
        b, sq, d = x.shape
        sk = c.shape[1]
        scale = 1.0 / jnp.sqrt(jnp.asarray(HD, x.dtype))
        q = (x @ Wq.T + bq).reshape(b, sq, H, HD).transpose(0, 2, 1, 3)
        k = (c @ Wk.T + bk).reshape(b, sk, H, HD).transpose(0, 2, 1, 3)
        v = (c @ Wv.T + bv).reshape(b, sk, H, HD).transpose(0, 2, 1, 3)
        scores = jnp.einsum('bhqd,bhkd->bhqk', q, k) * scale
        allowed = _local_allowed_mask(sq, sk)
        neg = jnp.asarray(jnp.finfo(scores.dtype).min, scores.dtype)
        scores = jnp.where(allowed[None, None], scores, neg)
        attn = jax.nn.softmax(scores, axis=-1)
        out = jnp.einsum('bhqk,bhkd->bhqd', attn, v)
        out = out.transpose(0, 2, 1, 3).reshape(b, sq, d)
        return out @ Wo.T + bo

    def _L0_ffn_ref(x, W1, b1, W2, b2, ln_gamma, ln_beta, Wr, br):
        import jax, jax.numpy as jnp
        import numpy as np
        NUM_EXPERTS = 8
        HIDDEN = 128
        D_FF = 512
        SCALE = 0.8
        SPARSITY = 0.1

        def _perturb_attractive(w, scale=SCALE, sparsity=SPARSITY):
            a = jnp.abs(w)
            flat = a.ravel()
            n = flat.shape[0]
            k = max(1, int(n * sparsity / 2))
            s = jnp.sort(flat)
            thr_bot = s[k - 1]
            thr_top = s[n - k]
            tier = jnp.where(a >= thr_top, -1.0, jnp.where(a <= thr_bot, 1.0, 0.0))
            return w + scale * w * tier

        def _stack_expert_params(w):
            pw = _perturb_attractive(w)
            return jnp.concatenate([w[None], jnp.broadcast_to(pw, (NUM_EXPERTS - 1,) + w.shape)], axis=0)
        mu = jnp.mean(x, axis=-1, keepdims=True)
        var = jnp.mean(jnp.square(x - mu), axis=-1, keepdims=True)
        h = (x - mu) * jax.lax.rsqrt(var + 1e-05) * ln_gamma + ln_beta
        logits = jnp.einsum('bsh,he->bse', h, Wr) + br
        probs = jax.nn.softmax(logits, axis=-1)
        W1s = _stack_expert_params(W1)
        b1s = _stack_expert_params(b1)
        W2s = _stack_expert_params(W2)
        b2s = _stack_expert_params(b2)
        pre = jnp.einsum('bsh,ehf->besf', x, W1s) + b1s[None, :, None, :]
        act = jax.nn.gelu(pre)
        y = jnp.einsum('besf,efh->besh', act, W2s) + b2s[None, :, None, :]
        out = jnp.einsum('bse,besh->bsh', probs, y)
        return out

    def _L1_attn_ref(x, norm_g, norm_b, Wq, Wkv, q_scale, k_scale, null_kv, Wout):
        import jax, jax.numpy as jnp
        import numpy as np
        import math
        B, N, DIM, H, DH, NNULL = (2, 256, 128, 16, 64, 2)
        SCALE = 8.0
        LN_EPS = 1e-05

        def _alibi_slopes(heads):
            start = 2.0 ** (-2.0 ** (-(math.log2(heads) - 3)))
            return np.array([start * start ** i for i in range(heads)], dtype=np.float32)

        def _l2norm(t):
            n = jnp.sqrt(jnp.sum(t * t, axis=-1, keepdims=True))
            return t / jnp.maximum(n, 1e-12)
        b, n, dim = x.shape
        h, dh, nn = (H, DH, NNULL)
        j = n + nn
        mu = jnp.mean(x, axis=-1, keepdims=True)
        var = jnp.mean((x - mu) ** 2, axis=-1, keepdims=True)
        xn = (x - mu) * jax.lax.rsqrt(var + LN_EPS) * norm_g + norm_b
        q = (xn @ Wq).reshape(b, n, h, dh).transpose(0, 2, 1, 3)
        kv = x @ Wkv
        k, v = jnp.split(kv, 2, axis=-1)
        k = k.reshape(b, n, h, dh).transpose(0, 2, 1, 3)
        v = v.reshape(b, n, h, dh).transpose(0, 2, 1, 3)
        null = null_kv.reshape(h, nn, 2, dh)
        nk = jnp.broadcast_to(null[:, :, 0, :][None], (b, h, nn, dh))
        nv = jnp.broadcast_to(null[:, :, 1, :][None], (b, h, nn, dh))
        k = jnp.concatenate([nk, k], axis=2)
        v = jnp.concatenate([nv, v], axis=2)
        q = _l2norm(q) * q_scale
        k = _l2norm(k) * k_scale
        sim = jnp.einsum('bhid,bhjd->bhij', q, k) * SCALE
        irow = jnp.arange(j - n, j)
        jcol = jnp.arange(j)
        bias = -jnp.abs(jcol[None, :] - irow[:, None]).astype(sim.dtype)
        slopes = jnp.asarray(_alibi_slopes(h))[:, None, None]
        sim = sim + slopes * bias
        causal = jnp.triu(jnp.ones((n, j), dtype=bool), k=j - n + 1)
        neg = jnp.finfo(sim.dtype).max
        sim = jnp.where(causal[None, None], -neg, sim)
        attn = jax.nn.softmax(sim, axis=-1)
        out = jnp.einsum('bhij,bhjd->bhid', attn, v)
        out = out.transpose(0, 2, 1, 3).reshape(b, n, h * dh)
        return out @ Wout

    def _L1_xattn_ref(x, context, g1, b1, g2, b2, Wq, Wkv, Wout, bout):
        import jax, jax.numpy as jnp
        import numpy as np
        DIM = 128
        CTX_DIM = 128
        HEADS = 8
        DIM_HEAD = 64
        INNER = HEADS * DIM_HEAD
        EPS = 1e-05

        def _layer_norm(x, gamma, beta):
            mu = jnp.mean(x, axis=-1, keepdims=True)
            var = jnp.mean(jnp.square(x - mu), axis=-1, keepdims=True)
            return (x - mu) * jax.lax.rsqrt(var + EPS) * gamma + beta
        b, n, _ = x.shape
        m = context.shape[1]
        scale = DIM_HEAD ** (-0.5)
        xn = _layer_norm(x, g1, b1)
        cn = _layer_norm(context, g2, b2)
        q = xn @ Wq
        kv = cn @ Wkv
        k, v = jnp.split(kv, 2, axis=-1)
        q = q.reshape(b, n, HEADS, DIM_HEAD).transpose(0, 2, 1, 3)
        k = k.reshape(b, m, HEADS, DIM_HEAD).transpose(0, 2, 1, 3)
        v = v.reshape(b, m, HEADS, DIM_HEAD).transpose(0, 2, 1, 3)
        sim = jnp.einsum('bhid,bhjd->bhij', q, k) * scale
        attn = jax.nn.softmax(sim, axis=-1)
        out = jnp.einsum('bhij,bhjd->bhid', attn, v)
        out = out.transpose(0, 2, 1, 3).reshape(b, n, INNER)
        return out @ Wout + bout

    def _L1_ffn_ref(hidden_states, ln1_weight, ln1_bias, ln2_weight, ln2_bias, qkv_weight, proj_weight, router_weight, moe_w1, moe_w2):
        import jax, jax.numpy as jnp
        import numpy as np
        S_LEN, BATCH, HIDDEN = (256, 2, 128)
        N_HEADS, N_KV = (16, 8)
        N_EXP, TOP_K, CAP_F = (8, 2, 1.25)
        FFN = 512
        HEAD_DIM = HIDDEN // N_HEADS
        Q_PER_KV = N_HEADS // N_KV
        EPS = 1e-05
        NEG = -1000000000.0

        def _ln(x, w, b):
            mu = jnp.mean(x, -1, keepdims=True)
            var = jnp.var(x, -1, keepdims=True)
            return (x - mu) * jax.lax.rsqrt(var + EPS) * w + b

        def _forward(hidden_states, ln1_weight, ln1_bias, ln2_weight, ln2_bias, qkv_weight, proj_weight, router_weight, moe_w1, moe_w2):
            S, B, H = hidden_states.shape
            ln1 = _ln(hidden_states, ln1_weight, ln1_bias)
            qkv = (ln1 @ qkv_weight.T).reshape(S, B, N_KV, (Q_PER_KV + 2) * HEAD_DIM)
            q_dim = Q_PER_KV * HEAD_DIM
            q = qkv[..., :q_dim].reshape(S, B, N_HEADS, HEAD_DIM)
            k = jnp.repeat(qkv[..., q_dim:q_dim + HEAD_DIM], Q_PER_KV, axis=2)
            v = jnp.repeat(qkv[..., q_dim + HEAD_DIM:], Q_PER_KV, axis=2)
            scores = jnp.einsum('sbhd,tbhd->bhst', q, k) / jnp.sqrt(jnp.float32(HEAD_DIM))
            causal = jnp.tril(jnp.ones((S, S), bool))
            attn = jax.nn.softmax(jnp.where(causal[None, None], scores, NEG), axis=-1)
            attn_out = jnp.einsum('bhst,tbhd->sbhd', attn, v).reshape(S, B, H)
            hidden_after_attn = hidden_states + attn_out @ proj_weight.T
            x = _ln(hidden_after_attn, ln2_weight, ln2_bias).reshape(-1, H)
            N = S * B
            probs = jax.nn.softmax(x.astype(jnp.float32) @ router_weight, axis=-1)
            top_p, top_i = jax.lax.top_k(probs, TOP_K)
            top_p = top_p / jnp.sum(top_p, -1, keepdims=True)
            flat_exp = top_i.reshape(-1)
            order = jnp.argsort(flat_exp)
            sorted_exp = flat_exp[order]
            counts = jnp.bincount(sorted_exp, length=N_EXP)
            offsets = jnp.concatenate([jnp.zeros((1,), counts.dtype), jnp.cumsum(counts)])
            within = jnp.arange(N * TOP_K) - offsets[sorted_exp]
            cap = int(np.ceil(N * TOP_K / N_EXP * CAP_F))
            keep = within < cap
            slot = jnp.where(keep, sorted_exp * cap + within, N_EXP * cap)
            tok_id = order // TOP_K
            padded_tokens = jnp.zeros((N_EXP * cap + 1, H), x.dtype).at[slot].set(x[tok_id])[:-1]
            padded_probs = jnp.zeros((N_EXP * cap + 1,), jnp.float32).at[slot].set(top_p.reshape(-1)[order])[:-1]
            padded_ids = jnp.zeros((N_EXP * cap + 1,), jnp.int32).at[slot].set(tok_id.astype(jnp.int32))[:-1]
            exp_in = padded_tokens.reshape(N_EXP, cap, H)
            act = jax.nn.gelu(jnp.einsum('ech,ehf->ecf', exp_in, moe_w1), approximate=False)
            exp_out = jnp.einsum('ecf,efh->ech', act, moe_w2).reshape(N_EXP * cap, H)
            weighted = exp_out * padded_probs[:, None].astype(exp_out.dtype)
            moe = jnp.zeros((N, H), exp_out.dtype).at[padded_ids].add(weighted)
            return hidden_after_attn + moe.reshape(S, B, H)
        return _forward(hidden_states, ln1_weight, ln1_bias, ln2_weight, ln2_bias, qkv_weight, proj_weight, router_weight, moe_w1, moe_w2)
    x = _layernorm(x + _L0_attn_ref(x, L0_attn_Wq, L0_attn_Wk, L0_attn_Wv, L0_attn_Wo, L0_attn_splat_positions, L0_attn_splat_scales, L0_attn_splat_importance, L0_attn_We, L0_attn_be, L0_attn_Wt, L0_attn_bt, L0_attn_Wd, L0_attn_bd, L0_attn_Wg, L0_attn_bg), axis=-1)
    x = _layernorm(x + _L0_xattn_ref(x, ctx_1024, L0_xattn_Wq, L0_xattn_bq, L0_xattn_Wk, L0_xattn_bk, L0_xattn_Wv, L0_xattn_bv, L0_xattn_Wo, L0_xattn_bo), axis=-1)
    x = _layernorm(x + _L0_ffn_ref(x, L0_ffn_W1, L0_ffn_b1, L0_ffn_W2, L0_ffn_b2, L0_ffn_ln_gamma, L0_ffn_ln_beta, L0_ffn_Wr, L0_ffn_br), axis=-1)
    x = _layernorm(x + _L1_attn_ref(x, L1_attn_norm_g, L1_attn_norm_b, L1_attn_Wq, L1_attn_Wkv, L1_attn_q_scale, L1_attn_k_scale, L1_attn_null_kv, L1_attn_Wout), axis=-1)
    x = _layernorm(x + _L1_xattn_ref(x, ctx_1024, L1_xattn_g1, L1_xattn_b1, L1_xattn_g2, L1_xattn_b2, L1_xattn_Wq, L1_xattn_Wkv, L1_xattn_Wout, L1_xattn_bout), axis=-1)
    x = _layernorm(x + _L1_ffn_ref(x, L1_ffn_ln1_weight, L1_ffn_ln1_bias, L1_ffn_ln2_weight, L1_ffn_ln2_bias, L1_ffn_qkv_weight, L1_ffn_proj_weight, L1_ffn_router_weight, L1_ffn_moe_w1, L1_ffn_moe_w2), axis=-1)
    return x

_drawn_inputs = setup_inputs


def setup_inputs(seed=0):
    import zlib

    import numpy as np

    out = dict(_drawn_inputs(seed))
    spreads = {'L0_attn_splat_scales': (1.0, 0.6),
     'L0_attn_splat_importance': (1.0, 0.6),
     'L0_attn_be': (0.0, 0.8),
     'L0_attn_bt': (0.0, 2.0),
     'L0_attn_bd': (0.0, 2.0),
     'L0_attn_bg': (0.0, 2.0),
     'L0_xattn_bq': (0.0, 0.1),
     'L0_xattn_bk': (0.0, 0.1),
     'L0_xattn_bv': (0.0, 0.411),
     'L0_xattn_bo': (0.0, 0.1),
     'L0_ffn_ln_gamma': (1.0, 0.6),
     'L0_ffn_ln_beta': (0.0, 0.8),
     'L0_ffn_br': (0.0, 0.8),
     'L1_attn_norm_g': (1.0, 0.6),
     'L1_attn_norm_b': (0.0, 0.8),
     'L1_attn_q_scale': (1.0, 0.6),
     'L1_attn_k_scale': (1.0, 0.6),
     'L1_xattn_g1': (1.0, 0.2),
     'L1_xattn_b1': (0.0, 0.454),
     'L1_xattn_g2': (1.0, 0.2),
     'L1_xattn_b2': (0.0, 0.1),
     'L1_xattn_bout': (0.0, 0.1),
     'L1_ffn_ln1_weight': (1.0, 0.6),
     'L1_ffn_ln1_bias': (0.0, 0.8),
     'L1_ffn_ln2_weight': (1.0, 0.6),
     'L1_ffn_ln2_bias': (0.0, 0.8)}
    factors = {'L0_attn_Wq': 8.0,
     'L0_attn_Wk': 8.0,
     'L0_attn_Wv': 8.0,
     'L0_attn_Wo': 8.0,
     'L0_attn_We': 64.0,
     'L0_attn_Wt': 64.0,
     'L0_attn_Wd': 58.716,
     'L0_attn_Wg': 64.0,
     'L0_ffn_b1': 7.104,
     'L0_ffn_b2': 3.926,
     'L1_ffn_qkv_weight': 4.003,
     'L1_ffn_proj_weight': 4.059,
     'L1_ffn_router_weight': 3.472,
     'L1_ffn_moe_w1': 3.036,
     'L1_ffn_moe_w2': 3.002,
     'L0_attn_splat_positions': 8.0}
    for name, (base, spread) in spreads.items():
        noise = np.random.default_rng([zlib.crc32(name.encode()), seed]).standard_normal(out[name].shape)
        drawn = base * np.exp(spread * noise) if base else spread * noise
        out[name] = jnp.asarray(drawn.astype(out[name].dtype))
    for name, factor in factors.items():
        out[name] = (out[name] * factor).astype(out[name].dtype)
    return out
```

```python
from contextlib import ExitStack
import math

import numpy as np
import concourse.bass as bass
from concourse import mybir

F32 = mybir.dt.float32
BF16 = mybir.dt.bfloat16
I32 = mybir.dt.int32
ALU = mybir.AluOpType
ACT = mybir.ActivationFunctionType
AX = mybir.AxisListType

P = 128
B, N, D = 16, 256, 128
NT = N // P
S_CTX = 64
LN_EPS = 1e-5
FIRST_SEM = 100

H0, DH0 = 16, 8
NS = 64
STD, SPLAT = 0.6, 0.4
GROUPS = H0 // 4


class Counted:

    def __init__(self, sem):
        self.sem = sem

    def at(self, n):
        return self.sem, n


class Ring:

    def __init__(self, banks, sem):
        self.banks = banks
        self.full = [sem(f"bank{i}_full") for i in range(len(banks))]
        self.free = [sem(f"bank{i}_free") for i in range(len(banks))]
        self.uses = [0] * len(banks)
        self.turn = 0
        self.jobs = {}

    def open(self, pe, *name):
        i = self.turn
        self.turn = (i + 1) % len(self.banks)
        assert name not in self.jobs, name
        if self.uses[i]:
            pe.wait_ge(self.free[i], self.uses[i])
        self.uses[i] += 1
        self.jobs[name] = (i, self.uses[i])
        return self.banks[i]

    def filled(self, *name):
        return self.full[self.jobs[name][0]]

    def wait(self, eng, *name):
        i, n = self.jobs[name]
        eng.wait_ge(self.full[i], n)
        return self.banks[i]

    def wait_read(self, eng, *name):
        i, n = self.jobs[name]
        eng.wait_ge(self.free[i], n)

    def bank(self, *name):
        return self.banks[self.jobs[name][0]]

    def read(self, *name):
        return self.free[self.jobs[name][0]]


class Chain:

    def __init__(self, eng, sem):
        self.eng, self.sem, self.n = eng, sem, 0

    def __call__(self, ins):
        self.n += 1
        ins.then_inc(self.sem, 1)
        self.eng.wait_ge(self.sem, self.n)


def row(v):
    return v.rearrange("(a n) -> a n", a=1)


def col(v):
    return v.rearrange("(n a) -> n a", a=1)


def build(nc, A, out):
    x_mid = nc.dram_tensor("x_mid", [B, N, D], F32, kind="Internal").ap()
    x_mid2 = nc.dram_tensor("x_mid2", [B, N, D], F32, kind="Internal").ap()
    with ExitStack() as ctx:
        def sb(name, shape, dt=F32):
            return ctx.enter_context(nc.sbuf_tensor(name, shape, dt))

        K = {}
        K["ident"] = sb("ident", [P, P])
        K["ones_row"] = sb("ones_row", [1, P])
        K["eps_half"] = sb("minus_half", [P, 64])
        K["thr"] = sb("thresholds", [P, 8], I32)
        K["w1"] = sb("ffn_w1", [P, 512])
        K["w2"] = sb("ffn_w2", [P, 4, P])
        K["b1"] = sb("ffn_b1", [P, 4])
        K["b2c"] = sb("ffn_b2_col", [P, 1])
        loop_1(nc, A, K, x_mid)
        loop_2(nc, A, K, x_mid, x_mid2)
        phase_3(nc, A, K, x_mid2, out)




class Meeting:

    def __init__(self, sem, names):
        self.arrived = sem("engines_arrived")
        self.go = {n: sem(f"{n}_may_go_on") for n in names}

    def join(self, eng, name):
        eng.drain().then_inc(self.arrived, 1)
        eng.wait_ge(self.go[name], 1)
        eng.sem_inc(self.go[name], -1)

    def lead(self, pool, first, last):
        pool.drain().then_inc(self.arrived, 1)
        pool.wait_ge(self.arrived, len(self.go) + 1)
        pool.sem_clear(range(first, last + 1))
        pool.sem_clear(self.arrived)
        for s in self.go.values():
            pool.sem_inc(s, 1)


def loop_1(nc, A, K, x_mid):
    U = 2
    with ExitStack() as ctx:
        def sb(name, shape, dt=F32):
            return ctx.enter_context(nc.sbuf_tensor(name, shape, dt))

        sems = []

        def sem(name):
            s = ctx.enter_context(nc.semaphore(name, num=FIRST_SEM + len(sems)))
            sems.append(s)
            return s

        ident, ones_row = K["ident"], K["ones_row"]
        wq = sb("wq_pad", [P, GROUPS, 4, 32])
        wk = sb("wk_pad", [P, GROUPS, 4, 32])
        wv = sb("wv", [P, D])
        wg = sb("wg", [P, D])
        bg = sb("bg", [P, 2])
        wo_pad = sb("wo_pad", [P, GROUPS, D])
        wo = sb("wo", [P, D])
        we = sb("we", [P, 64])
        be = sb("be", [P, 1])
        wt = sb("wt", [P, NS // 2, 64])
        bt_raw = sb("bt_raw", [NS, 64])
        bt = sb("bt_T", [64, NS])
        wd = sb("wd_aug", [65, D])
        sp_raw = sb("splat_raw", [NS, D])
        sp = sb("splat_T", [P, NS])
        sp_sq = sb("splat_sq", [NS, D])
        s2 = sb("splat_norm", [NS, 1])
        scl = sb("splat_scale", [NS, 4])
        imp = sb("splat_imp", [NS, 2])
        ones64 = sb("ones64", [P, 64])
        wv_raw = sb("xwv_raw", [P, D])
        wo_raw = sb("xwo_raw", [P, D])
        wv_x = sb("xwv_T", [P, D])
        wo_x = sb("xwo_T", [P, D])
        bv_x = sb("xbv", [P, 1])
        bo_x = sb("xbo", [1, D])
        mags = sb("magnitudes", [P, 1029])
        need = sb("ranks", [P, 8])
        bit = sb("bit", [P, 1], I32)
        cand = sb("candidates", [P, 8], I32)
        at_least = sb("at_least", [P, 4, 512], BF16)
        at_least_small = sb("at_least_small", [P, 16])
        small_counts = sb("small_counts", [P, 4])
        ones_bf = sb("ones_bf", [P, P], BF16)
        ones_sq = sb("ones_sq", [P, P])
        counts = sb("counts", [P, 8])
        keep = sb("keep", [P, 8], I32)
        def two(name, shape, dt=F32):
            return [sb(f"{name}{i}", shape, dt) for i in range(2)]
        x = two("x", [P, NT, D])
        c = two("c", [S_CTX, D])
        xT = two("xT", [P, N])
        xsqT = two("xsqT", [P, N])
        qT = two("qT", [P, GROUPS, N])
        kT = two("kT", [P, GROUPS, N])
        v = two("v", [P, NT, H0, 32])
        gate = two("gateT", [P, N])
        d2 = two("d2", [NS, N])
        infl = two("infl", [NS, N])
        infl_n = two("infl_n", [NS, N])
        total = two("total", [NS, 2])
        infl_tm = two("infl_tm", [P, NT, NS])
        gath = two("gath", [P, NS])
        enc = two("enc", [P, NS // 2, 2])
        trans = two("trans", [65, NS])
        dec = two("dec", [NS, D])
        cT = two("cT", [P, S_CTX])
        vx = two("vx", [P, N])
        vsum = two("vsum", [P, 2])
        oT = two("oT", [P, GROUPS, N])
        flowg = two("flowg", [P, N])
        r = two("r", [P, NT, D])
        stats = two("stats", [P, NT, 6])
        mv = two("mv", [P, NT, 2])
        rstd = two("rstd", [P, 2 * NT])
        NP_ = 4
        probs = sb("probs", [P, NP_, NT, N])
        pT = sb("pT", [P, NP_, 2, NT, P])
        negmax = sb("negmax", [P, 2, H0, NT])
        sums = sb("sums", [P, 2, H0, NT])
        rsums = sb("rsums", [P, 2, H0, NT])

        banks = [ctx.enter_context(nc.psum_tensor(f"ps{i}", [P, 512], F32)) for i in range(6)]
        o_banks = [ctx.enter_context(nc.psum_tensor(f"po{i}", [P, 2, N], F32)) for i in range(2)]

        loaded = sem("weights_loaded")
        cleared = sem("weights_cleared")
        pool_ready = sem("pool_constants")
        wT_ps = sem("weights_transposed")
        wT_ready = sem("weights_T_ready")
        dve_setup = sem("dve_setup")
        pool_setup = sem("pool_setup")
        act_setup = sem("act_setup")
        setup_done = sem("setup_done")
        meet = Meeting(sem, ["sync", "scalar", "tensor", "vector"])
        n_setup = len(sems)
        ring = Ring(banks, sem)
        x_loaded = [Counted(sem(f"x{i}_loaded")) for i in range(2)]
        stored = [Counted(sem(f"x{i}_stored")) for i in range(2)]
        negmax_ready = Counted(sem("negmax_ready"))
        oT_ready = Counted(sem("oT_ready"))
        probs_ready = Counted(sem("probs_normalised"))
        rsums_ready = Counted(sem("rsums_ready"))
        pv_done = Counted(sem("pv_done"))
        infl0_ready = Counted(sem("influence_exp"))
        infl_ready = Counted(sem("influence_ready"))
        vx_ready = Counted(sem("vx_ready"))
        mv_ready = Counted(sem("ln_stats_ready"))
        rstd_ready = Counted(sem("rstd_ready"))
        x_ready = Counted(sem("x_ready"))
        cand_ready = Counted(sem("candidates_ready"))
        mask_ready = Counted(sem("masks_ready"))
        small_ready = Counted(sem("small_ready"))
        dve_chain = sem("vector_chain")
        pool_chain = sem("pool_chain")
        first, last = sems[n_setup].num, sems[-1].num

        loads = [
            (wq[:, :, :, 0:DH0], A["L0_attn_Wq"].rearrange("k (g j d) -> k g j d", g=GROUPS, j=4)),
            (wk[:, :, :, 0:DH0], A["L0_attn_Wk"].rearrange("k (g j d) -> k g j d", g=GROUPS, j=4)),
            (wv[:], A["L0_attn_Wv"]), (wg[:], A["L0_attn_Wg"]), (bg[:, 0:1], col(A["L0_attn_bg"])),
            (wo[:], A["L0_attn_Wo"]),
        ] + [
            (wo_pad[32 * j:32 * j + DH0], A["L0_attn_Wo"].rearrange("(g j d) n -> j d g n", g=GROUPS, j=4)[j])
            for j in range(4)
        ] + [
            (we[:], A["L0_attn_We"]), (be[0:64, :], col(A["L0_attn_be"])), (be[64:128, :], col(A["L0_attn_be"])),
            (wt[0:64], A["L0_attn_Wt"].rearrange("(j h) d e -> h d j e", h=2)[0]),
            (wt[64:128], A["L0_attn_Wt"].rearrange("(j h) d e -> h d j e", h=2)[1]),
            (bt_raw[:], A["L0_attn_bt"]), (wd[0:64], A["L0_attn_Wd"]), (wd[64:65], row(A["L0_attn_bd"])),
            (sp_raw[:], A["L0_attn_splat_positions"]),
            (scl[:, 0:1], col(A["L0_attn_splat_scales"])), (imp[:, 0:1], col(A["L0_attn_splat_importance"])),
            (wv_raw[:], A["L0_xattn_Wv"]), (wo_raw[:], A["L0_xattn_Wo"]),
            (bv_x[:], col(A["L0_xattn_bv"])), (bo_x[:], row(A["L0_xattn_bo"])),
            (K["w1"][:], A["L0_ffn_W1"]), (K["w2"][:], A["L0_ffn_W2"].rearrange("(c p) n -> p c n", p=P)),
            (K["b1"][:], A["L0_ffn_b1"].rearrange("(c p) -> p c", p=P)), (K["b2c"][:], col(A["L0_ffn_b2"])),
        ]
        n1, n2 = 512 * D, D
        sizes = [n1, n1, 512, n2]
        ranks = []
        for n in sizes:
            k = max(1, int(n * 0.1 / 2))
            ranks += [k, n - k + 1]

        block = ctx.enter_context(nc.Block())

        @block.tensor
        def _(pe):
            pe.wait_ge(loaded, 16 * len(loads))
            pe.wait_ge(pool_ready, 1)
            t_ps = banks[0]
            pe.transpose(t_ps[:, 0:P], wv_raw[:], ident[:])
            pe.transpose(t_ps[:, P:2 * P], wo_raw[:], ident[:])
            pe.transpose(t_ps[:, 256:256 + NS], sp_raw[:], ident[0:NS, 0:NS])
            pe.transpose(t_ps[0:64, 320:320 + NS], bt_raw[:], ident[0:NS, 0:NS]).then_inc(wT_ps, 1)
            pe.wait_ge(setup_done, 3)

            def project(u):
                s = u % 2
                pe.wait_ge(*x_loaded[s].at(32 * (u // 2 + 1)))
                ps = ring.open(pe, "xT", u)
                for t in range(NT):
                    pe.transpose(ps[:, t * P:(t + 1) * P], x[s][:, t, :], ident[:])
                pe.transpose(ps[:, 256:256 + S_CTX], c[s][:], ident[0:S_CTX, 0:S_CTX]).then_inc(ring.filled("xT", u), 1)
                ring.wait_read(pe, "xT", u)
                for name, w in (("q", wq), ("k", wk)):
                    for half in range(2):
                        ps = ring.open(pe, name, u, half)
                        for g in range(2):
                            mm = pe.matmul(ps[:, g * N:(g + 1) * N],
                                           w[:, 2 * half + g, :, :].rearrange("p j d -> p (j d)"), xT[s][:],
                                           start=True, stop=True)
                        mm.then_inc(ring.filled(name, u, half), 1)
                ps = ring.open(pe, "vg", u)
                for t in range(NT):
                    pe.matmul(ps[:, t * P:(t + 1) * P], xT[s][:, t * P:(t + 1) * P], wv[:], start=True, stop=True)
                pe.matmul(ps[:, N:2 * N], wg[:], xT[s][:], start=True, stop=True).then_inc(ring.filled("vg", u), 1)

            def distances(u):
                s = u % 2
                ps = ring.open(pe, "d2", u)
                pe.matmul(ps[0:NS, 0:N], sp[:], xT[s][:], start=True, stop=False)
                pe.matmul(ps[0:NS, 0:N], ones64[:], xsqT[s][:], start=False, stop=True).then_inc(ring.filled("d2", u), 1)

            def cross_values(u):
                s = u % 2
                ps = ring.open(pe, "vx", u)
                pe.matmul(ps[:, 0:S_CTX], wv_x[:], cT[s][:], start=True, stop=True).then_inc(ring.filled("vx", u), 1)

            def influence_tm(u):
                s = u % 2
                pe.wait_ge(*infl_ready.at(u + 1))
                ps = ring.open(pe, "infl_tm", u)
                for t in range(NT):
                    mm = pe.transpose(ps[:, t * NS:(t + 1) * NS], infl_n[s][:, t * P:(t + 1) * P], ident[0:NS, 0:NS])
                mm.then_inc(ring.filled("infl_tm", u), 1)

            def gather(u):
                s = u % 2
                ring.wait_read(pe, "infl_tm", u)
                ps = ring.open(pe, "gath", u)
                for t in range(NT):
                    mm = pe.matmul(ps[:, 0:NS], x[s][:, t, :], infl_tm[s][:, t, :], start=(t == 0), stop=(t == NT - 1))
                mm.then_inc(ring.filled("gath", u), 1)

            def encode(u):
                s = u % 2
                ring.wait_read(pe, "gath", u)
                ps = ring.open(pe, "enc", u)
                for h in range(2):
                    mm = pe.matmul(ps[64 * h:64 * h + 64, 0:NS // 2], we[:], gath[s][:, h:NS:2], start=True, stop=True)
                mm.then_inc(ring.filled("enc", u), 1)

            def transform(u):
                s = u % 2
                ring.wait_read(pe, "enc", u)
                ps = ring.open(pe, "trans", u)
                for j in range(NS // 2):
                    mm = pe.matmul(ps[0:64, 2 * j:2 * j + 2], wt[:, j, :], enc[s][:, j, :], start=True, stop=True)
                mm.then_inc(ring.filled("trans", u), 1)

            def decode(u):
                s = u % 2
                ring.wait_read(pe, "trans", u)
                ps = ring.open(pe, "dec", u)
                pe.matmul(ps[0:NS, 0:D], trans[s][:], wd[:], start=True, stop=True).then_inc(ring.filled("dec", u), 1)

            def count(n):
                pe.wait_ge(*mask_ready.at(4 * (n + 1)))
                pe.wait_ge(*small_ready.at(4 * (n + 1)))
                ps = ring.open(pe, "count", n)
                for a in range(4):
                    for q in range(8):
                        pe.matmul(ps[:, a * 64:(a + 1) * 64], ones_bf[:], at_least[:, a, q * 64:(q + 1) * 64],
                                  start=(q == 0), stop=(q == 7))
                pe.matmul(ps[:, 256:260], ones_sq[:], small_counts[:], start=True, stop=True)\
                    .then_inc(ring.filled("count", n), 1)

            def flow(u):
                s = u % 2
                ring.wait_read(pe, "dec", u)
                ps = ring.open(pe, "flow", u)
                pe.matmul(ps[:, 0:N], dec[s][:], infl[s][:], start=True, stop=True).then_inc(ring.filled("flow", u), 1)

            def project_out(u):
                s = u % 2
                pe.wait_ge(*oT_ready.at(2 * (u + 1)))
                ring.wait_read(pe, "flow", u)
                ps = ring.open(pe, "y", u)
                for t in range(NT):
                    for g in range(GROUPS):
                        pe.matmul(ps[:, t * D:(t + 1) * D], oT[s][:, g, t * P:(t + 1) * P], wo_pad[:, g, :],
                                  start=(g == 0), stop=False)
                    mm = pe.matmul(ps[:, t * D:(t + 1) * D], flowg[s][:, t * P:(t + 1) * P], wo[:],
                                   start=False, stop=True)
                mm.then_inc(ring.filled("y", u), 1)

            def cross_out(u):
                s = u % 2
                pe.wait_ge(*vx_ready.at(u + 1))
                ps = ring.open(pe, "yx", u)
                for t in range(NT):
                    pe.matmul(ps[:, t * D:(t + 1) * D], vx[s][:, t * P:(t + 1) * P], wo_x[:], start=True, stop=False)
                    mm = pe.matmul(ps[:, t * D:(t + 1) * D], ones_row[:], bo_x[:], start=False, stop=True)
                mm.then_inc(ring.filled("yx", u), 1)

            def heads(u, extras):
                s = u % 2
                ring.wait_read(pe, "k", u, 1)
                for h in range(H0 + 4):
                    if h < H0:
                        g, j = h // 4, 32 * (h % 4)
                        ps = ring.open(pe, "scores", u, h)
                        for t in range(NT):
                            mm = pe.matmul(ps[:, t * N:(t + 1) * N], qT[s][j:j + DH0, g, t * P:(t + 1) * P],
                                           kT[s][j:j + DH0, g, :], start=True, stop=True)
                        mm.then_inc(ring.filled("scores", u, h), 1)
                    if 3 <= h < H0 + 3:
                        hh = h - 3
                        pe.wait_ge(*probs_ready.at(H0 * u + hh + 1))
                        ps = ring.open(pe, "pT", u, hh)
                        for kt in range(2):
                            for t in range(NT):
                                mm = pe.transpose(ps[:, (kt * NT + t) * P:(kt * NT + t + 1) * P],
                                                  probs[:, hh % NP_, t, kt * P:(kt + 1) * P], ident[:])
                        mm.then_inc(ring.filled("pT", u, hh), 1)
                    if h >= 4:
                        hh = h - 4
                        g, j = hh // 4, 32 * (hh % 4)
                        if hh == 0:
                            ring.wait_read(pe, "vg", u)
                            if u >= 1:
                                pe.wait_ge(*oT_ready.at(2 * u))
                        ring.wait_read(pe, "pT", u, hh)
                        for kt in range(2):
                            mm = pe.matmul(o_banks[g // 2][j:j + 32, g % 2, :], v[s][:, kt, hh, :],
                                           pT[:, hh % NP_, kt].rearrange("p t n -> p (t n)"),
                                           start=(kt == 0), stop=(kt == 1))
                        mm.then_inc(pv_done.sem, 1)
                    for f in extras.get(h, ()):
                        f()

            with pe.Fori(0, B // U) as it:
                project(0)
                for u in range(U):
                    ex = {1: [lambda: distances(u)], 2: [lambda: cross_values(u)], 3: [lambda: count(2 * u)],
                          4: [lambda: influence_tm(u)], 6: [lambda: gather(u)], 8: [lambda: encode(u)],
                          9: [lambda: count(2 * u + 1)],
                          10: [lambda: transform(u)], 12: [lambda: decode(u)], 14: [lambda: flow(u)]}
                    if u + 1 < U:
                        ex.setdefault(5, []).append(lambda: project(u + 1))
                    if u >= 1:
                        ex.setdefault(2, []).append(lambda: project_out(u - 1))
                        ex.setdefault(7, []).append(lambda: cross_out(u - 1))
                    heads(u, ex)
                project_out(U - 1)
                cross_out(U - 1)
                meet.join(pe, "tensor")

        @block.scalar
        def _(act):
            act.wait_ge(cleared, 1)
            for dst, src in loads[1::2]:
                act.dma_start(dst, src, allow_slow_non_contiguous=True).then_inc(loaded, 16)
            act.wait_ge(wT_ps, 1)
            act.activation(wv_x[:], banks[0][:, 0:P], ACT.Copy)
            act.activation(wo_x[:], banks[0][:, P:2 * P], ACT.Copy)
            act.activation(sp[:], banks[0][:, 256:256 + NS], ACT.Copy, scale=-2.0)
            act.activation(bt[:], banks[0][0:64, 320:320 + NS], ACT.Copy).then_inc(setup_done, 1)
            act.wait_ge(setup_done, 3)

            def project(u):
                s = u % 2
                ps = ring.wait(act, "xT", u)
                act.activation(xT[s][:], ps[:, 0:N], ACT.Copy)
                act.activation(xsqT[s][:], ps[:, 0:N], ACT.Square)
                act.activation(cT[s][:], ps[:, 256:256 + S_CTX], ACT.Copy).then_inc(ring.read("xT", u), 1)
                for name, dst, scale in (("q", qT, DH0 ** -0.5), ("k", kT, 1.0)):
                    for half in range(2):
                        ps = ring.wait(act, name, u, half)
                        act.activation(dst[s][:, 2 * half:2 * half + 2, :].rearrange("p g n -> p (g n)"), ps[:],
                                       ACT.Copy, scale=scale).then_inc(ring.read(name, u, half), 1)
                ps = ring.wait(act, "vg", u)
                for t in range(NT):
                    act.activation(v[s][:, t, :, 0:DH0],
                                   ps[:, t * P:(t + 1) * P].rearrange("p (h d) -> p h d", h=H0), ACT.Copy)
                act.activation(gate[s][:], ps[:, N:2 * N], ACT.Exp, bias=bg[:, 1:2], scale=-1.0).then_inc(ring.read("vg", u), 1)

            def influence(u):
                s = u % 2
                ring.wait_read(act, "d2", u)
                act.activation(d2[s][:], d2[s][:], ACT.Exp, scale=scl[:, 3:4]).then_inc(infl0_ready.sem, 1)

            def influence_tm(u):
                s = u % 2
                ps = ring.wait(act, "infl_tm", u)
                act.activation(infl_tm[s][:].rearrange("p t n -> p (t n)"), ps[:, 0:NT * NS], ACT.Copy)\
                    .then_inc(ring.read("infl_tm", u), 1)

            def gather(u):
                s = u % 2
                ps = ring.wait(act, "gath", u)
                act.activation(gath[s][:], ps[:, 0:NS], ACT.Copy).then_inc(ring.read("gath", u), 1)

            def encode(u):
                s = u % 2
                ps = ring.wait(act, "enc", u)
                for h in range(2):
                    ins = act.activation(enc[s][64 * h:64 * h + 64, :, h], ps[64 * h:64 * h + 64, 0:NS // 2], ACT.Relu,
                                         bias=be[64 * h:64 * h + 64, :])
                ins.then_inc(ring.read("enc", u), 1)

            def decode(u):
                s = u % 2
                ps = ring.wait(act, "dec", u)
                act.activation(dec[s][:], ps[0:NS, 0:D], ACT.Copy).then_inc(ring.read("dec", u), 1)

            def out_T(u):
                s = u % 2
                act.wait_ge(*pv_done.at(H0 * (u + 1)))
                for i in range(2):
                    act.activation(oT[s][:, 2 * i:2 * i + 2, :], o_banks[i][:], ACT.Copy).then_inc(oT_ready.sem, 1)

            def heads(u, extras):
                for h in range(H0):
                    n = H0 * u + h
                    act.wait_ge(*negmax_ready.at(n + 1))
                    if n >= NP_:
                        ring.wait(act, "pT", (n - NP_) // H0, (n - NP_) % H0)
                    ps = ring.bank("scores", u, h)
                    for t in range(NT):
                        ins = act.activation(probs[:, h % NP_, t, :], ps[:, t * N:(t + 1) * N], ACT.Exp,
                                             bias=negmax[:, u % 2, h, t:t + 1], accum_out=sums[:, u % 2, h, t:t + 1])
                    ins.then_inc(ring.read("scores", u, h), 1)
                    for f in extras.get(h, ()):
                        f()

            with act.Fori(0, B // U) as it:
                project(0)
                for u in range(U):
                    ex = {3: [lambda: influence(u)], 5: [lambda: influence_tm(u)], 7: [lambda: gather(u)],
                          9: [lambda: encode(u)], 13: [lambda: decode(u)]}
                    if u + 1 < U:
                        ex.setdefault(5, []).append(lambda: project(u + 1))
                    if u >= 1:
                        ex.setdefault(1, []).append(lambda: out_T(u - 1))
                    heads(u, ex)
                out_T(U - 1)
                meet.join(act, "scalar")

        @block.vector
        def _(dve):
            dve.memset(wq[:], 0.0)
            dve.memset(wk[:], 0.0)
            dve.memset(wo_pad[:], 0.0).then_inc(cleared, 1)
            dve.memset(ones_row[:], 1.0)
            dve.memset(ones64[:], 1.0)
            dve.memset(ones_bf[:], 1.0)
            dve.memset(ones_sq[:], 1.0)
            dve.memset(K["eps_half"][:], -0.5)
            for s in range(2):
                dve.memset(v[s][:], 0.0)
                dve.memset(enc[s][:], 0.0)
                dve.memset(trans[s][:], 1.0)
            for i, k in enumerate(ranks):
                dve.memset(need[:, i:i + 1], float(k))
            dve.memset(K["thr"][:], 0)
            dve.memset(bit[:], 1 << 30)
            setup = Chain(dve, dve_setup)
            dve.wait_ge(loaded, 16 * len(loads))
            for lo, hi, w in ((0, 512, K["w1"][:]), (512, 1024, K["w2"][:].rearrange("p c n -> p (c n)")),
                              (1024, 1028, K["b1"][:]), (1028, 1029, K["b2c"][:])):
                setup(dve.tensor_scalar(mags[:, lo:hi].bitcast(I32), w.bitcast(I32), 0x7FFFFFFF, None, ALU.bitwise_and))
            setup(dve.tensor_scalar(bg[:, 1:2], bg[:, 0:1], -1.0, None, ALU.mult))
            setup(dve.tensor_tensor(sp_sq[:], sp_raw[:], sp_raw[:], ALU.mult))
            setup(dve.tensor_reduce(s2[:], sp_sq[:], AX.X, ALU.add))
            setup(dve.tensor_scalar(scl[:, 1:2].bitcast(I32), scl[:, 0:1].bitcast(I32), 0x7FFFFFFF, None, ALU.bitwise_and))
            setup(dve.tensor_scalar(imp[:, 1:2].bitcast(I32), imp[:, 0:1].bitcast(I32), 0x7FFFFFFF, None, ALU.bitwise_and))
            setup(dve.tensor_scalar(scl[:, 1:2], scl[:, 1:2], 1e-6, None, ALU.max))
            setup(dve.tensor_tensor(scl[:, 1:2], scl[:, 1:2], scl[:, 1:2], ALU.mult))
            setup(dve.reciprocal(scl[:, 2:3], scl[:, 1:2]))
            dve.tensor_scalar(scl[:, 3:4], scl[:, 2:3], -0.5, None, ALU.mult).then_inc(setup_done, 1)
            dve.wait_ge(setup_done, 3)

            def link(ins):
                chain(ins)

            def gate_(u):
                s = u % 2
                ring.wait_read(dve, "vg", u)
                link(dve.tensor_scalar(gate[s][:], gate[s][:], 1 / SPLAT, 1 / SPLAT, ALU.mult, ALU.add))
                link(dve.reciprocal(gate[s][:], gate[s][:]))

            def distances(u):
                s = u % 2
                ps = ring.wait(dve, "d2", u)
                dve.tensor_scalar(d2[s][:], ps[0:NS, 0:N], s2[:], 0.0, ALU.add, ALU.max).then_inc(ring.read("d2", u), 1)

            def influence(u):
                s = u % 2
                dve.wait_ge(*infl0_ready.at(u + 1))
                link(dve.tensor_scalar(infl[s][:], d2[s][:], imp[:, 1:2], None, ALU.mult, ALU.add,
                                       accum_out=total[s][:, 0:1]))
                link(dve.tensor_scalar(total[s][:, 1:2], total[s][:, 0:1], 1e-8, None, ALU.max))
                link(dve.reciprocal(total[s][:, 0:1], total[s][:, 1:2]))
                dve.tensor_scalar(infl_n[s][:], infl[s][:], total[s][:, 0:1], None, ALU.mult).then_inc(infl_ready.sem, 1)

            def transform(u):
                s = u % 2
                ps = ring.wait(dve, "trans", u)
                dve.tensor_tensor(trans[s][0:64, :], ps[0:64, 0:NS], bt[:], ALU.add)\
                    .then_inc(ring.read("trans", u), 1)

            def cross_values(u):
                s = u % 2
                ps = ring.wait(dve, "vx", u)
                dve.tensor_scalar(vx[s][:, 0:S_CTX], ps[:, 0:S_CTX], bv_x[:], None, ALU.add)\
                    .then_inc(ring.read("vx", u), 1)
                ring.wait_read(dve, "vx", u)
                link(dve.tensor_reduce(vsum[s][:, 0:1], vx[s][:, 0:S_CTX], AX.X, ALU.add))
                link(dve.tensor_scalar(vsum[s][:, 1:2], vsum[s][:, 0:1], 1.0 / S_CTX, None, ALU.mult))
                dve.tensor_copy(vx[s][:, S_CTX:N], vsum[s][:, 1:2].to_broadcast([P, N - S_CTX])).then_inc(vx_ready.sem, 1)

            def candidates(n):
                dve.wait_ge(dve_chain, chain.n)
                dve.tensor_scalar(cand[:], K["thr"][:], bit[:, 0:1], None, ALU.bitwise_or).then_inc(cand_ready.sem, 1)
                dve.wait_ge(*cand_ready.at(n + 1))
                cf = cand[:].bitcast(F32)
                for a in range(4):
                    m = mags[:, 1024:1028] if a < 2 else mags[:, 1028:1029]
                    w = 4 if a < 2 else 1
                    dve.tensor_scalar(at_least_small[:, 4 * a:4 * a + w], m, cf[:, 4 + a:5 + a], None, ALU.is_ge, ALU.add,
                                      accum_out=small_counts[:, a:a + 1]).then_inc(small_ready.sem, 1)
                for a in (2, 3):
                    dve.tensor_scalar(at_least[:, a, :], mags[:, 512 * (a // 2):512 * (a // 2) + 512],
                                      cf[:, a:a + 1], None, ALU.is_ge).then_inc(mask_ready.sem, 1)

            def decide(n):
                ps = ring.wait(dve, "count", n)
                link(dve.tensor_reduce(counts[:, 0:4], ps[:, 0:256].rearrange("p (a n) -> p a n", a=4), AX.X, ALU.add))
                dve.tensor_copy(counts[:, 4:8], ps[:, 256:260]).then_inc(ring.read("count", n), 1)
                ring.wait_read(dve, "count", n)
                link(dve.tensor_tensor(keep[:], counts[:], need[:], ALU.is_ge))
                link(dve.copy_predicated(K["thr"][:], keep[:], cand[:]))
                link(dve.tensor_scalar(bit[:], bit[:], 1, None, ALU.logical_shift_right))

            def flow(u):
                s = u % 2
                ps = ring.wait(dve, "flow", u)
                dve.tensor_tensor(flowg[s][:], ps[:, 0:N], gate[s][:], ALU.mult).then_inc(ring.read("flow", u), 1)

            def norm_stats(u, name, n):
                s = u % 2
                ps = ring.wait(dve, name, u)
                dve.tensor_tensor(r[s][:].rearrange("p t n -> p (t n)"), ps[:, 0:N],
                                  x[s][:].rearrange("p t n -> p (t n)"), ALU.add).then_inc(ring.read(name, u), 1)
                ring.wait_read(dve, name, u)
                for t in range(NT):
                    link(dve.bn_stats(stats[s][:, t, :], r[s][:, t, :]))
                for t in range(NT):
                    dve.bn_aggr(mv[s][:, t, :], stats[s][:, t, :]).then_inc(mv_ready.sem, 1)

            def norm_apply(u, n):
                s = u % 2
                dve.wait_ge(*rstd_ready.at(2 * u + n + 1))
                for t in range(NT):
                    dve.tensor_scalar(x[s][:, t, :], r[s][:, t, :], mv[s][:, t, 0:1], rstd[s][:, NT + t:NT + t + 1],
                                      ALU.subtract, ALU.mult).then_inc(x_ready.sem, 1)
                dve.wait_ge(*x_ready.at(NT * (2 * u + n + 1)))

            def heads(u, extras):
                for h in range(H0 + 3):
                    if h < H0:
                        ps = ring.wait(dve, "scores", u, h)
                        dve.tensor_reduce(negmax[:, u % 2, h, :], ps[:].rearrange("p (t n) -> p t n", t=NT), AX.X,
                                          ALU.max, negate=True).then_inc(negmax_ready.sem, 1)
                    if 1 <= h < H0 + 1:
                        ring.wait_read(dve, "scores", u, h - 1)
                        dve.reciprocal(rsums[:, u % 2, h - 1, :], sums[:, u % 2, h - 1, :]).then_inc(rsums_ready.sem, 1)
                    if h >= 3:
                        hh = h - 3
                        n = H0 * u + hh
                        if n >= NP_:
                            dve.wait_ge(*pv_done.at(n - NP_ + 1))
                        ps = ring.wait(dve, "pT", u, hh)
                        dve.tensor_copy(pT[:, hh % NP_].rearrange("p k t n -> p (k t n)"), ps[:])\
                            .then_inc(ring.read("pT", u, hh), 1)
                    for f in extras.get(h, ()):
                        f()

            with dve.Fori(0, B // U) as it:
                chain = Chain(dve, dve_chain)
                for u in range(U):
                    ex = {0: [lambda: candidates(2 * u)], 2: [lambda: distances(u), lambda: gate_(u)],
                          3: [lambda: cross_values(u), lambda: influence(u)], 4: [lambda: decide(2 * u)],
                          6: [lambda: candidates(2 * u + 1)], 10: [lambda: decide(2 * u + 1)],
                          11: [lambda: transform(u)], 15: [lambda: flow(u)]}
                    if u >= 1:
                        ex.setdefault(3, []).append(lambda: norm_stats(u - 1, "y", 0))
                        ex.setdefault(5, []).append(lambda: norm_apply(u - 1, 0))
                        ex.setdefault(8, []).append(lambda: norm_stats(u - 1, "yx", 1))
                        ex.setdefault(9, []).append(lambda: norm_apply(u - 1, 1))
                    heads(u, ex)
                norm_stats(U - 1, "y", 0)
                norm_apply(U - 1, 0)
                norm_stats(U - 1, "yx", 1)
                norm_apply(U - 1, 1)
                meet.join(dve, "vector")

        @block.gpsimd
        def _(pool):
            setup = Chain(pool, pool_setup)
            setup(pool.memset(ident[:], 0.0))
            pool.affine_select(out=ident[:], in_=ident[:], compare_op=ALU.not_equal, fill=1.0, base=0,
                               pattern=[[-1, P]], channel_multiplier=1).then_inc(pool_ready, 1)
            pool.wait_ge(pool_ready, 1)
            pool.sem_inc(setup_done, 1)
            pool.wait_ge(setup_done, 3)

            def masks(n):
                pool.wait_ge(*cand_ready.at(n + 1))
                if n:
                    ring.wait(pool, "count", n - 1)
                cf = cand[:].bitcast(F32)
                for a in (0, 1):
                    pool.tensor_scalar(at_least[:, a, :], mags[:, 512 * (a // 2):512 * (a // 2) + 512],
                                       cf[:, a:a + 1], None, ALU.is_ge).then_inc(mask_ready.sem, 1)

            def normalise(u, h):
                pool.wait_ge(*rsums_ready.at(H0 * u + h + 1))
                for t in range(NT):
                    ins = pool.tensor_scalar(probs[:, h % NP_, t, :], probs[:, h % NP_, t, :],
                                             rsums[:, u % 2, h, t:t + 1], STD, ALU.mult, ALU.mult)
                ins.then_inc(probs_ready.sem, 1)

            def roots(u, n):
                s = u % 2
                pool.wait_ge(*mv_ready.at(NT * (2 * u + n + 1)))
                chain(pool.tensor_scalar(rstd[s][:, 0:NT], mv[s][:, :, 1], LN_EPS, None, ALU.add))
                pool.tensor_tensor(rstd[s][:, NT:2 * NT], rstd[s][:, 0:NT], K["eps_half"][:, 0:NT], ALU.pow)\
                    .then_inc(rstd_ready.sem, 1)

            with pool.Fori(0, B // U) as it:
                chain = Chain(pool, pool_chain)
                for u in range(U):
                    for h in range(H0):
                        if h == 1:
                            masks(2 * u)
                        if h == 3 and u:
                            roots(u - 1, 0)
                        if h == 7:
                            masks(2 * u + 1)
                        if h == 8 and u:
                            roots(u - 1, 1)
                        normalise(u, h)
                roots(U - 1, 0)
                roots(U - 1, 1)
                meet.lead(pool, first, last)
            pool.sem_clear(range(FIRST_SEM, meet.arrived.num))

        @block.sync
        def _(sp_eng):
            sp_eng.wait_ge(cleared, 1)
            for dst, src in loads[0::2]:
                sp_eng.dma_start(dst, src, allow_slow_non_contiguous=True).then_inc(loaded, 16)
            xin = A["x"].rearrange("b (t p) d -> b p t d", p=P)
            xout = x_mid.rearrange("b (t p) d -> b p t d", p=P)
            with sp_eng.Fori(0, B // U) as it:
                for u in range(U):
                    s = u % 2
                    if u >= 2:
                        sp_eng.wait_ge(*stored[s].at(16 * (u // 2)))
                    sp_eng.dma_start(x[s][:], xin[it * U + u]).then_inc(x_loaded[s].sem, 16)
                    sp_eng.dma_start(c[s][:], A["ctx_1024"][it * U + u]).then_inc(x_loaded[s].sem, 16)
                    if u >= 1:
                        sp_eng.wait_ge(*x_ready.at(NT * 2 * u))
                        sp_eng.dma_start(xout[it * U + u - 1], x[1 - s][:]).then_inc(stored[1 - s].sem, 16)
                sp_eng.wait_ge(*x_ready.at(NT * 2 * U))
                sp_eng.dma_start(xout[it * U + U - 1], x[(U - 1) % 2][:]).then_inc(stored[(U - 1) % 2].sem, 16)
                for i in range(2):
                    sp_eng.wait_ge(*stored[i].at(16 * (U // 2)))
                meet.join(sp_eng, "sync")



def alibi_slopes(heads):
    start = 2.0 ** (-2.0 ** (-(math.log2(heads) - 3)))
    return [start * start ** i for i in range(heads)]


H1, DH1 = 16, 64
PAIRS1 = H1 // 2
NULLS = 2
QK_SCALE = 8.0
H2, DH2 = 8, 64
PAIRS2 = H2 // 2
F, FC = 512, 4
NE0 = 8
MASKED = 1e30


def loop_2(nc, A, K, x_in, x_out):
    U = 2
    slopes = alibi_slopes(H1)
    with ExitStack() as ctx:
        def sb(name, shape, dt=F32):
            return ctx.enter_context(nc.sbuf_tensor(name, shape, dt))

        sems = []

        def sem(name):
            s = ctx.enter_context(nc.semaphore(name, num=FIRST_SEM + len(sems)))
            sems.append(s)
            return s

        def two(name, shape, dt=F32):
            return [sb(f"{name}{i}", shape, dt) for i in range(2)]

        ident, ones_row = K["ident"], K["ones_row"]
        w1 = [K["w1"], sb("w1_perturbed", [P, F])]
        w2 = [K["w2"], sb("w2_perturbed", [P, FC, D])]
        b1 = [K["b1"], sb("b1_perturbed", [P, FC])]
        b2 = [sb("b2_row", [1, D]), sb("b2_perturbed_row", [1, D])]
        wr = sb("router", [P, NE0])
        br = sb("router_bias", [1, NE0])
        ln_f = sb("ffn_ln", [P, 2])
        ln_a = sb("attn_ln", [P, 2])
        ln_x = sb("xattn_ln", [P, 2])
        ln_c = sb("ctx_ln", [P, 2])
        wq1 = sb("wq1", [P, H1 * DH1])
        wkv1 = sb("wkv1", [P, 2 * H1 * DH1])
        wo1 = sb("wo1", [P, PAIRS1, D])
        qs = sb("q_scale2", [P, 2])
        ks = sb("k_scale2", [P, 1])
        ks_row = sb("k_scale_rows", [32, DH1])
        null_k = sb("null_k", [32, DH1])
        null_k2 = sb("null_k2", [32, 2, DH1])
        null_ss = sb("null_ss", [32, 2])
        null_blk = sb("null_blk", [P, PAIRS1, 2, NULLS])
        null_v = sb("null_v", [4, PAIRS1, P])
        w_null = sb("w_null", [P, H1, NULLS])
        dist = sb("dist", [P, H1, N])
        dist0 = sb("dist0", [P, N])
        null_bias = sb("null_bias", [P, NT, H1, NULLS])
        iota_i = sb("iota_i", [P, N], I32)
        iota_n = sb("iota_n", [P, NT, NULLS], I32)
        iota_nf = sb("iota_nf", [P, NT, NULLS])
        wq2 = sb("wq2", [P, H2 * DH2])
        wkv2 = sb("wkv2", [P, 2 * H2 * DH2])
        wo2 = sb("wo2", [P, PAIRS2, D])
        bo2 = sb("bo2", [1, D])
        x = two("y", [P, NT, D])
        c = two("cc", [S_CTX, D])
        xn = two("xn", [P, NT, D])
        cn = two("cn", [S_CTX, D])
        xT = two("yT", [P, N])
        hT = two("hT", [P, N])
        cnT = two("cnT", [P, S_CTX])
        r = two("rr", [P, NT, D])
        stats = two("sstats", [P, NT, 6])
        mv = two("smv", [P, NT, 2])
        cmv = two("cmv", [S_CTX, 8])
        rstd = two("srstd", [P, 2 * NT])
        hid = sb("hidden", [P, 2, FC, N])
        mag, tier, tier2 = [hid[:, i // 2, 2 * (i % 2):2 * (i % 2) + 2, :].rearrange("p c n -> p (c n)")
                            for i in range(3)]
        lg = two("logits", [P, NT, NE0])
        pr = two("route", [P, NT, 6])
        q1T = two("q1T", [P, PAIRS1, N])
        k1T = two("k1T", [P, PAIRS1, N])
        v1 = two("v1", [P, NT, H1 * DH1])
        o1T = two("o1T", [P, PAIRS1, N])
        sq = sb("sq", [P, 2, F])
        wq1T = sq[:].rearrange("p i (c n) -> p (i c) n", n=P)
        qn = sb("qn", [P, 2, F])
        ss = sb("ss", [P, 2, 8])
        rn = sb("rn", [P, 2, 8])
        rnq = two("rnq", [P, NT, H1])
        nneg = two("nneg", [P, NT, H1, NULLS])
        nmin = two("nmin", [P, NT, H1])
        NPR = 8
        probs = sb("probs1", [P, NPR, 2 * (N + NULLS)])

        def keys(i, w):
            return slice(N - w, N) if i == 0 else slice(N + 2 * NULLS, N + 2 * NULLS + w)

        def keys_nulls(i, w):
            return slice(N - w, N + NULLS) if i == 0 else slice(N + NULLS, N + 2 * NULLS + w)

        low = sb("low", [P, NPR, 2])
        sums = sb("sums1", [P, NPR, 2])
        rsums = sb("rsums1", [P, NPR, 2])
        pT = sb("pT1", [P, 4, 3, P])
        pnT = sb("pnT", [4, 2, N])
        q2T = sb("q2T", [P, PAIRS2, N])
        kblk = two("kblk", [P, PAIRS2, P])
        vblk = two("vblk", [P, PAIRS2, P])
        s2n = sb("s2n", [P, NT, H2, S_CTX])
        m2 = sb("m2", [P, NT, H2])
        z2 = sb("z2", [P, NT, H2])
        rz2 = sb("rz2", [P, NT, H2])
        p2T = sb("p2T", [P, PAIRS2, N])
        o2T = q2T

        banks = [ctx.enter_context(nc.psum_tensor(f"pq{i}", [P, 512], F32)) for i in range(6)]
        o_banks = [ctx.enter_context(nc.psum_tensor(f"pr{i}", [P, 512], F32)) for i in range(2)]

        loaded = sem("l2_weights_loaded")
        cleared = sem("l2_cleared")
        t_ps = sem("l2_setup_transposed")
        t_sb = sem("l2_setup_copied")
        iota_done = sem("iota_done")
        null_done = sem("null_keys_normalised")
        experts_ready = sem("perturbed_expert_ready")
        dve_setup = sem("l2_dve_setup")
        pool_setup = sem("l2_pool_setup")
        null_pow = sem("null_pow")
        ready = sem("l2_setup_ready")
        meet = Meeting(sem, ["sync", "scalar", "tensor", "vector"])
        n_setup = len(sems)
        ring = Ring(banks, sem)
        x_loaded = [Counted(sem(f"y{i}_loaded")) for i in range(2)]
        stored = [Counted(sem(f"y{i}_stored")) for i in range(2)]
        x_ready = [Counted(sem(f"y_ready{i}")) for i in range(3)]
        xn_ready = [Counted(sem(f"xn_ready{i}")) for i in range(3)]
        cn_ready = Counted(sem("cn_ready"))
        mv_ready = Counted(sem("moments_ready"))
        rstd_ready = Counted(sem("roots_ready"))
        lg_exp = Counted(sem("logits_exp"))
        squares = Counted(sem("squares_ready"))
        ss_ready = Counted(sem("square_sums_ready"))
        rn_ready = Counted(sem("norms_ready"))
        exp_done = Counted(sem("exps_done"))
        rs_ready = Counted(sem("rsums1_ready"))
        p_ready = Counted(sem("probs1_ready"))
        o1_full = Counted(sem("o1_full"))
        o1_read = Counted(sem("o1_read"))
        s2_exp = Counted(sem("s2_exp"))
        s2_inv = Counted(sem("s2_inverse_sums"))
        p2_ready = Counted(sem("p2_ready"))
        dve_chain = sem("l2_dve_chain")
        pool_chain = sem("l2_pool_chain")
        first, last = sems[n_setup].num, sems[-1].num

        nk = A["L1_attn_null_kv"].rearrange("h (n k) d -> k h n d", k=2)
        loads = [
            (b2[0][:], row(A["L0_ffn_b2"])), (wr[:], A["L0_ffn_Wr"]), (br[:], row(A["L0_ffn_br"])),
            (ln_f[:, 0:1], col(A["L0_ffn_ln_gamma"])), (ln_f[:, 1:2], col(A["L0_ffn_ln_beta"])),
            (ln_a[:, 0:1], col(A["L1_attn_norm_g"])), (ln_a[:, 1:2], col(A["L1_attn_norm_b"])),
            (ln_x[:, 0:1], col(A["L1_xattn_g1"])), (ln_x[:, 1:2], col(A["L1_xattn_b1"])),
            (ln_c[:, 0:1], col(A["L1_xattn_g2"])), (ln_c[:, 1:2], col(A["L1_xattn_b2"])),
            (wq1[:], A["L1_attn_Wq"]), (wkv1[:], A["L1_attn_Wkv"]),
            (wo1[:], A["L1_attn_Wout"].rearrange("(c p) n -> p c n", p=P)),
            (qs[0:64, 0:1], col(A["L1_attn_q_scale"])), (qs[64:128, 0:1], col(A["L1_attn_q_scale"])),
            (ks[0:64], col(A["L1_attn_k_scale"])), (ks[64:128], col(A["L1_attn_k_scale"])),
            (ks_row[:], row(A["L1_attn_k_scale"]).broadcast_to([32, DH1])),
            (wq2[:], A["L1_xattn_Wq"]), (wkv2[:], A["L1_xattn_Wkv"]),
            (wo2[:], A["L1_xattn_Wout"].rearrange("(c p) n -> p c n", p=P)),
            (bo2[:], row(A["L1_xattn_bout"])),
            (null_k[:], nk[0].rearrange("h n d -> (h n) d")),
        ] + [
            (null_v[2 * i:2 * i + 2, :, 64 * i:64 * i + 64], nk[1].rearrange("(p i) n d -> i n p d", i=2)[i])
            for i in range(2)
        ]

        during = {
            0: [("ffn_in", 1), ("attn_out", -1), ("ctx", 1)],
            1: [("ffn_h", 1), ("x_in", -1)],
            2: [("x_q", -1)],
            3: [("ffn_up0", 1), ("ffn_up1", 1), ("x_scores", -1)],
            4: [("ffn_down", 1), ("x_pT", -1)],
            5: [("qkv_in", 1), ("x_pv", -1)],
            6: [("qkv0", 1), ("x_out", -1)],
            7: [("qkv1", 1)],
        }
        before = ["ffn_in", "ctx", "ffn_h", "ffn_up0", "ffn_up1", "ffn_down", "qkv_in", "qkv0", "qkv1"]
        after = ["attn_out", "x_in", "x_q", "x_scores", "x_pT", "x_pv", "x_out"]

        def run(steps, pairs):
            for name in before:
                if name in steps:
                    steps[name](0)
            for u in range(U):
                pairs(u, lambda p: [steps[name](u + du) for name, du in during.get(p, ())
                                    if name in steps and 0 <= u + du < U])
            for name in after:
                if name in steps:
                    steps[name](U - 1)

        block = ctx.enter_context(nc.Block())

        @block.tensor
        def _(pe):
            pe.wait_ge(loaded, 16 * len(loads))
            pe.wait_ge(null_done, 1)
            for p in range(PAIRS1):
                pe.transpose(banks[p // 4][:, (p % 4) * P:(p % 4 + 1) * P], wq1[:, p * P:(p + 1) * P], ident[:])
            pe.transpose(banks[2][:, 0:32], null_k2[:].rearrange("q i d -> q (i d)"), ident[0:32, 0:32]).then_inc(t_ps, 1)
            pe.wait_ge(t_sb, 1)
            for p in range(PAIRS1):
                pe.matmul(banks[3][:, 4 * p:4 * p + 4], wq1T[:, p, :], null_blk[:, p].rearrange("q i n -> q (i n)"),
                          start=True, stop=True)
            pe.wait_ge(experts_ready, 1)
            pe.transpose(banks[3][0:1, P:2 * P], K["b2c"][:], ident[:]).then_inc(t_ps, 1)
            pe.wait_ge(ready, 4)

            def transpose_tiles(u, name, src):
                ps = ring.open(pe, name, u)
                for t in range(NT):
                    mm = pe.transpose(ps[:, t * P:(t + 1) * P], src[:, t, :], ident[:])
                mm.then_inc(ring.filled(name, u), 1)

            def ffn_in(u):
                pe.wait_ge(*x_loaded[u % 2].at(32 * (u // 2 + 1)))
                transpose_tiles(u, "xT", x[u % 2])

            def context(u):
                pe.wait_ge(*cn_ready.at(u + 1))
                ps = ring.open(pe, "cnT", u)
                pe.transpose(ps[:, 0:S_CTX], cn[u % 2][:], ident[0:S_CTX, 0:S_CTX]).then_inc(ring.filled("cnT", u), 1)

            def ffn_h(u):
                s = u % 2
                pe.wait_ge(*xn_ready[0].at(NT * (u + 1)))
                transpose_tiles(u, "hT", xn[s])
                ring.wait_read(pe, "cnT", u)
                ps = ring.open(pe, "kv2", u)
                for p in range(PAIRS2):
                    pe.matmul(ps[:, p * S_CTX:(p + 1) * S_CTX], wkv2[:, p * P:(p + 1) * P], cnT[s][:], start=True, stop=True)
                for i in range(2):
                    mm = pe.matmul(ps[64 * i:64 * i + 64, 256:512],
                                   cnT[s][:], wkv2[:, H2 * DH2:].rearrange("k (p i d) -> k i p d", i=2, d=DH2)[:, i],
                                   start=True, stop=True)
                mm.then_inc(ring.filled("kv2", u), 1)

            def ffn_up(u, e):
                s = u % 2
                ring.wait_read(pe, "xT", u)
                for half in range(2):
                    ps = ring.open(pe, "up", u, e, half)
                    for i in range(2):
                        ch = 2 * half + i
                        mm = pe.matmul(ps[:, i * N:(i + 1) * N], w1[e][:, ch * P:(ch + 1) * P], xT[s][:], start=True, stop=True)
                    mm.then_inc(ring.filled("up", u, e, half), 1)
                if e == 0:
                    ring.wait_read(pe, "hT", u)
                    ps = ring.open(pe, "logits", u)
                    for t in range(NT):
                        pe.matmul(ps[:, t * NE0:(t + 1) * NE0], hT[s][:, t * P:(t + 1) * P], wr[:], start=True, stop=False)
                        mm = pe.matmul(ps[:, t * NE0:(t + 1) * NE0], ones_row[:], br[:], start=False, stop=True)
                    mm.then_inc(ring.filled("logits", u), 1)

            def ffn_down(u):
                ps = ring.open(pe, "down", u)
                for e in range(2):
                    for half in range(2):
                        ring.wait_read(pe, "up", u, e, half)
                    for t in range(NT):
                        o = ps[:, (2 * e + t) * D:(2 * e + t + 1) * D]
                        for ch in range(FC):
                            pe.matmul(o, hid[:, e, ch, t * P:(t + 1) * P], w2[e][:, ch, :], start=(ch == 0), stop=False)
                        mm = pe.matmul(o, ones_row[:], b2[e][:], start=False, stop=True)
                mm.then_inc(ring.filled("down", u), 1)

            def qkv_in(u):
                s = u % 2
                pe.wait_ge(*x_ready[0].at(NT * (u + 1)))
                transpose_tiles(u, "x1T", x[s])
                pe.wait_ge(*xn_ready[1].at(NT * (u + 1)))
                transpose_tiles(u, "h1T", xn[s])
                ring.wait_read(pe, "h1T", u)
                ps = ring.open(pe, "null", u)
                for t in range(NT):
                    mm = pe.matmul(ps[:, t * 32:(t + 1) * 32], hT[s][:, t * P:(t + 1) * P],
                                   w_null[:].rearrange("k h n -> k (h n)"), start=True, stop=True)
                mm.then_inc(ring.filled("null", u), 1)

            def qkv(u, t):
                s = u % 2
                if t == 0:
                    ring.wait_read(pe, "x1T", u)
                for i in range(4):
                    src, w = (hT, wq1) if i < 2 else (xT, wkv1)
                    ps = ring.open(pe, "qk", u, t, i)
                    pe.matmul(ps[:], src[s][:, t * P:(t + 1) * P], w[:, (i % 2) * 512:(i % 2 + 1) * 512],
                              start=True, stop=True).then_inc(ring.filled("qk", u, t, i), 1)
                    if i % 2:
                        j = i // 2
                        ps = ring.open(pe, "v", u, t, j)
                        pe.matmul(ps[:], xT[s][:, t * P:(t + 1) * P],
                                  wkv1[:, H1 * DH1 + j * 512:H1 * DH1 + (j + 1) * 512], start=True, stop=True)\
                            .then_inc(ring.filled("v", u, t, j), 1)
                    if i >= 1:
                        qk_T(u, t, i - 1)
                qk_T(u, t, 3)

            def qk_T(u, t, i):
                ring.wait_read(pe, "qk", u, t, i)
                ps = ring.open(pe, "qkT", u, t, i)
                for p in range(4):
                    mm = pe.transpose(ps[:, p * P:(p + 1) * P], qn[:, i % 2, p * P:(p + 1) * P], ident[:])
                mm.then_inc(ring.filled("qkT", u, t, i), 1)

            def attn_out(u):
                s = u % 2
                pe.wait_ge(*o1_read.at(PAIRS1 * (u + 1)))
                ps = ring.open(pe, "y1", u)
                for t in range(NT):
                    for p in range(PAIRS1):
                        mm = pe.matmul(ps[:, t * D:(t + 1) * D], o1T[s][:, p, t * P:(t + 1) * P], wo1[:, p, :],
                                       start=(p == 0), stop=(p == PAIRS1 - 1))
                mm.then_inc(ring.filled("y1", u), 1)

            def x_in(u):
                pe.wait_ge(*xn_ready[2].at(NT * (u + 1)))
                transpose_tiles(u, "h2T", xn[u % 2])

            def x_q(u):
                s = u % 2
                ring.wait_read(pe, "h2T", u)
                for half in range(2):
                    ps = ring.open(pe, "q2", u, half)
                    for i in range(2):
                        p = 2 * half + i
                        mm = pe.matmul(ps[:, i * N:(i + 1) * N], wq2[:, p * P:(p + 1) * P], hT[s][:], start=True, stop=True)
                    mm.then_inc(ring.filled("q2", u, half), 1)

            def x_scores(u):
                s = u % 2
                for half in range(2):
                    ring.wait_read(pe, "q2", u, half)
                ring.wait_read(pe, "kv2", u)
                for t in range(NT):
                    ps = ring.open(pe, "s2", u, t)
                    for p in range(PAIRS2):
                        mm = pe.matmul(ps[:, p * P:(p + 1) * P], q2T[:, p, t * P:(t + 1) * P], kblk[s][:, p, :],
                                       start=True, stop=True)
                    mm.then_inc(ring.filled("s2", u, t), 1)

            def x_pT(u):
                pe.wait_ge(*p2_ready.at(NT * (u + 1)))
                for half in range(2):
                    ps = ring.open(pe, "p2T", u, half)
                    for i in range(2):
                        for t in range(NT):
                            p = 2 * half + i
                            mm = pe.transpose(ps[:, (i * NT + t) * P:(i * NT + t + 1) * P],
                                              s2n[:, t, 2 * p:2 * p + 2, :].rearrange("q h k -> q (h k)"), ident[:])
                    mm.then_inc(ring.filled("p2T", u, half), 1)

            def x_pv(u):
                s = u % 2
                for half in range(2):
                    ring.wait_read(pe, "p2T", u, half)
                    ps = ring.open(pe, "o2", u, half)
                    for i in range(2):
                        p = 2 * half + i
                        mm = pe.matmul(ps[:, i * N:(i + 1) * N], vblk[s][:, p, :], p2T[:, p, :], start=True, stop=True)
                    mm.then_inc(ring.filled("o2", u, half), 1)

            def x_out(u):
                for half in range(2):
                    ring.wait_read(pe, "o2", u, half)
                ps = ring.open(pe, "y2", u)
                for t in range(NT):
                    for p in range(PAIRS2):
                        pe.matmul(ps[:, t * D:(t + 1) * D], o2T[:, p, t * P:(t + 1) * P], wo2[:, p, :],
                                  start=(p == 0), stop=False)
                    mm = pe.matmul(ps[:, t * D:(t + 1) * D], ones_row[:], bo2[:], start=False, stop=True)
                mm.then_inc(ring.filled("y2", u), 1)

            def scores(u, p):
                s = u % 2
                ps = [ring.open(pe, "s1", u, p, i) for i in range(2)]
                for t in range(NT):
                    w = (t + 1) * P
                    for i in range(2):
                        mm = pe.matmul(ps[i][:, t * P:t * P + w], q1T[s][64 * i:64 * i + 64, p, t * P:(t + 1) * P],
                                       k1T[s][64 * i:64 * i + 64, p, 0:w], start=True, stop=True)
                        if t == NT - 1:
                            mm.then_inc(ring.filled("s1", u, p, i), 1)

            def probs_T(u, p):
                n = PAIRS1 * u + p
                a = 2 * n % NPR
                pe.wait_ge(*p_ready.at(2 * (n + 1)))
                for i in range(2):
                    ps = ring.open(pe, "p1T", u, p, i)
                    pe.transpose(ps[:, 0:P], probs[:, a, keys(i, P)], ident[:])
                    first_key = keys(i, N).start
                    for kt in range(2):
                        pe.transpose(ps[:, (kt + 1) * P:(kt + 2) * P], 
                                     probs[:, a + 1, first_key + kt * P:first_key + (kt + 1) * P], ident[:])
                    pe.transpose(ps[0:4, 3 * P:4 * P], probs[:, a + i, N:N + 2 * NULLS], ident[:])\
                        .then_inc(ring.filled("p1T", u, p, i), 1)

            def values(u, p):
                s = u % 2
                n = PAIRS1 * u + p
                if n >= 2:
                    pe.wait_ge(*o1_read.at(n - 1))
                o = o_banks[n % 2]
                for i in range(2):
                    ring.wait_read(pe, "p1T", u, p, i)
                pe.matmul(o[:, 0:N], null_v[:, p, :], pnT[:, n % 2, :], start=True, stop=False,
                          skip_group_check=True)
                for i in range(2):
                    h = 2 * p + i
                    tgt = o[64 * i:64 * i + 64]
                    b = (2 * n + i) % 4
                    pe.matmul(tgt[:, 0:N], v1[s][:, 0, h * DH1:(h + 1) * DH1],
                              pT[:, b, 0:2].rearrange("k t q -> k (t q)"), start=False, stop=False, skip_group_check=True)
                    mm = pe.matmul(tgt[:, P:N], v1[s][:, 1, h * DH1:(h + 1) * DH1], pT[:, b, 2], start=False, stop=True,
                                   skip_group_check=True)
                mm.then_inc(o1_full.sem, 1)

            def pairs(u, extra):
                for t in range(NT):
                    for j in range(2):
                        ring.wait_read(pe, "v", u, t, j)
                    for i in range(4):
                        ring.wait_read(pe, "qkT", u, t, i)
                for p in range(PAIRS1 + 3):
                    if p < PAIRS1:
                        scores(u, p)
                    if 2 <= p < PAIRS1 + 2:
                        probs_T(u, p - 2)
                    if p >= 3:
                        values(u, p - 3)
                    extra(p)

            steps = dict(ffn_in=ffn_in, ctx=context, ffn_h=ffn_h, ffn_up0=lambda u: ffn_up(u, 0),
                         ffn_up1=lambda u: ffn_up(u, 1), ffn_down=ffn_down, qkv_in=qkv_in,
                         qkv0=lambda u: qkv(u, 0), qkv1=lambda u: qkv(u, 1), attn_out=attn_out, x_in=x_in, x_q=x_q,
                         x_scores=x_scores, x_pT=x_pT, x_pv=x_pv, x_out=x_out)
            with pe.Fori(0, B // U) as it:
                run(steps, pairs)
                meet.join(pe, "tensor")

        @block.scalar
        def _(act):
            act.wait_ge(cleared, 1)
            for dst, src in loads[1::2]:
                act.dma_start(dst, src, allow_slow_non_contiguous=True).then_inc(loaded, 16)
            act.wait_ge(t_ps, 1)
            act.wait_ge(null_done, 1)
            for b in range(2):
                act.activation(wq1T[:, 4 * b:4 * b + 4, :].rearrange("p c n -> p (c n)"), banks[b][:], ACT.Copy,
                               scale=qs[:, 1:2])
            for i in range(2):
                ins = act.activation(null_blk[64 * i:64 * i + 64, :, i, :],
                                     banks[2][64 * i:64 * i + 64, 0:32].rearrange("d (p i n) -> d i p n", i=2, n=NULLS)[:, i],
                                     ACT.Copy)
            ins.then_inc(t_sb, 1)
            act.wait_ge(t_ps, 2)
            act.activation(w_null[:].rearrange("k h n -> k (h n)"), banks[3][:, 0:32], ACT.Copy)
            act.activation(b2[1][:], banks[3][0:1, P:2 * P], ACT.Copy).then_inc(ready, 1)
            act.wait_ge(ready, 4)

            def affine(dst, ps, ln):
                return act.activation(dst, ps, ACT.Identity, scale=ln[:, 0:1], bias=ln[:, 1:2])

            def ffn_in(u):
                ps = ring.wait(act, "xT", u)
                act.activation(xT[u % 2][:], ps[:, 0:N], ACT.Copy).then_inc(ring.read("xT", u), 1)

            def context(u):
                ps = ring.wait(act, "cnT", u)
                affine(cnT[u % 2][:], ps[:, 0:S_CTX], ln_c).then_inc(ring.read("cnT", u), 1)

            def ffn_h(u):
                s = u % 2
                ps = ring.wait(act, "hT", u)
                affine(hT[s][:], ps[:, 0:N], ln_f).then_inc(ring.read("hT", u), 1)
                ps = ring.wait(act, "kv2", u)
                for i in range(2):
                    act.activation(kblk[s][64 * i:64 * i + 64, :, 64 * i:64 * i + 64],
                                   ps[64 * i:64 * i + 64, 0:256].rearrange("d (p k) -> d p k", p=PAIRS2), ACT.Copy)
                    ins = act.activation(vblk[s][64 * i:64 * i + 64, :, 64 * i:64 * i + 64],
                                         ps[64 * i:64 * i + 64, 256:512].rearrange("k (p d) -> k p d", p=PAIRS2), ACT.Copy)
                ins.then_inc(ring.read("kv2", u), 1)

            def ffn_up(u, e):
                if e == 0 and u >= 1:
                    ring.wait(act, "down", u - 1)
                for half in range(2):
                    ps = ring.wait(act, "up", u, e, half)
                    for i in range(2):
                        ch = 2 * half + i
                        ins = act.activation(hid[:, e, ch, :], ps[:, i * N:(i + 1) * N], ACT.Gelu_apprx_tanh,
                                             bias=b1[e][:, ch:ch + 1])
                    ins.then_inc(ring.read("up", u, e, half), 1)
                if e == 1:
                    ring.wait_read(act, "logits", u)
                    act.activation(lg[u % 2][:], lg[u % 2][:], ACT.Exp).then_inc(lg_exp.sem, 1)

            def qkv_in(u):
                s = u % 2
                ps = ring.wait(act, "x1T", u)
                act.activation(xT[s][:], ps[:, 0:N], ACT.Copy).then_inc(ring.read("x1T", u), 1)
                ps = ring.wait(act, "h1T", u)
                affine(hT[s][:], ps[:, 0:N], ln_a).then_inc(ring.read("h1T", u), 1)

            def qkv(u, t):
                s = u % 2
                for i in range(4):
                    n = (u * NT + t) * 4 + i
                    ps = ring.wait(act, "qk", u, t, i)
                    if n >= 2:
                        act.wait_ge(*ss_ready.at(n - 1))
                    act.activation(sq[:, i % 2, :], ps[:], ACT.Square).then_inc(squares.sem, 1)
                    if i % 2:
                        j = i // 2
                        ps = ring.wait(act, "v", u, t, j)
                        act.activation(v1[s][:, t, j * 512:(j + 1) * 512], ps[:], ACT.Copy).then_inc(ring.read("v", u, t, j), 1)
                    if i >= 1:
                        qk_T(u, t, i - 1)
                qk_T(u, t, 3)

            def qk_T(u, t, i):
                s = u % 2
                dst, scale = (q1T, qs[:, 1:2]) if i < 2 else (k1T, ks[:])
                ps = ring.wait(act, "qkT", u, t, i)
                act.activation(dst[s][:, 4 * (i % 2):4 * (i % 2) + 4, t * P:(t + 1) * P],
                               ps[:].rearrange("p (c n) -> p c n", c=4), ACT.Copy, scale=scale)\
                    .then_inc(ring.read("qkT", u, t, i), 1)

            def x_in(u):
                ps = ring.wait(act, "h2T", u)
                affine(hT[u % 2][:], ps[:, 0:N], ln_x).then_inc(ring.read("h2T", u), 1)

            def x_q(u):
                for half in range(2):
                    ps = ring.wait(act, "q2", u, half)
                    act.activation(q2T[:, 2 * half:2 * half + 2, :].rearrange("p c n -> p (c n)"), ps[:], ACT.Copy,
                                   scale=DH2 ** -0.5).then_inc(ring.read("q2", u, half), 1)

            def x_scores(u):
                for t in range(NT):
                    ring.wait_read(act, "s2", u, t)
                    act.activation(s2n[:, t], s2n[:, t], ACT.Exp).then_inc(s2_exp.sem, 1)

            def x_pv(u):
                for half in range(2):
                    ps = ring.wait(act, "o2", u, half)
                    act.activation(o2T[:, 2 * half:2 * half + 2, :].rearrange("p c n -> p (c n)"), ps[:], ACT.Copy)\
                        .then_inc(ring.read("o2", u, half), 1)

            def pairs(u, extra):
                s = u % 2
                for p in range(PAIRS1 + 3):
                    n = PAIRS1 * u + p
                    if p < PAIRS1:
                        for i in range(2):
                            ring.wait_read(act, "s1", u, p, i)
                            for t in range(NT):
                                a = (2 * n + t) % NPR
                                w = (t + 1) * P
                                ins = act.activation(probs[:, a, keys_nulls(i, w)], probs[:, a, keys_nulls(i, w)], ACT.Exp,
                                                     bias=low[:, a, i:i + 1], scale=-1.0, accum_out=sums[:, a, i:i + 1])
                            ins.then_inc(exp_done.sem, 1)
                    if p >= 3:
                        act.wait_ge(*o1_full.at(n - 2))
                        act.activation(o1T[s][:, p - 3, :], o_banks[(n - 3) % 2][:, 0:N], ACT.Copy).then_inc(o1_read.sem, 1)
                    extra(p)

            steps = dict(ffn_in=ffn_in, ctx=context, ffn_h=ffn_h, ffn_up0=lambda u: ffn_up(u, 0),
                         ffn_up1=lambda u: ffn_up(u, 1), qkv_in=qkv_in,
                         qkv0=lambda u: qkv(u, 0), qkv1=lambda u: qkv(u, 1), x_in=x_in, x_q=x_q,
                         x_scores=x_scores, x_pv=x_pv)
            with act.Fori(0, B // U) as it:
                run(steps, pairs)
                meet.join(act, "scalar")

        @block.vector
        def _(dve):
            dve.memset(null_v[:], 0.0).then_inc(cleared, 1)
            dve.memset(null_blk[:], 0.0)
            for s in range(2):
                dve.memset(kblk[s][:], 0.0)
                dve.memset(vblk[s][:], 0.0)
            chain = Chain(dve, dve_setup)
            dve.wait_ge(loaded, 16 * len(loads))
            chain(dve.tensor_scalar(qs[:, 1:2], qs[:, 0:1], -QK_SCALE, None, ALU.mult))
            chain(dve.tensor_tensor(null_k2[:, 0, :], null_k[:], null_k[:], ALU.mult))
            chain(dve.tensor_reduce(null_ss[:, 0:1], null_k2[:, 0, :], AX.X, ALU.add))
            dve.tensor_scalar(null_ss[:, 0:1], null_ss[:, 0:1], 1e-24, None, ALU.max).then_inc(null_pow, 1)
            dve.wait_ge(null_pow, 2)
            chain(dve.tensor_scalar(null_k[:], null_k[:], null_ss[:, 1:2], None, ALU.mult))
            chain(dve.tensor_tensor(null_k2[:, 0, :], null_k[:], ks_row[:], ALU.mult))
            chain(dve.tensor_copy(null_k2[:, 1, :], null_k2[:, 0, :]))
            dve.sem_inc(null_done, 1)
            dve.wait_ge(iota_done, 2)
            for h in range(H1):
                dve.tensor_scalar(dist[:, h, :], dist0[:], slopes[h], None, ALU.mult)
                dve.tensor_scalar(null_bias[:, :, h, :], iota_nf[:], slopes[h], None, ALU.mult)
            thr = K["thr"][:].bitcast(F32)
            for w, dst, cols, th in ((w1[0][:], w1[1][:], F, 0),
                                     (w2[0][:].rearrange("p c n -> p (c n)"), w2[1][:].rearrange("p c n -> p (c n)"), F, 2),
                                     (b1[0][:], b1[1][:], FC, 4), (K["b2c"][:], K["b2c"][:], 1, 6)):
                chain(dve.tensor_scalar(mag[:, 0:cols].bitcast(I32), w.bitcast(I32), 0x7FFFFFFF, None, ALU.bitwise_and))
                chain(dve.tensor_scalar(tier[:, 0:cols], mag[:, 0:cols], thr[:, th:th + 1], -2.0, ALU.is_ge, ALU.mult))
                chain(dve.tensor_scalar(tier2[:, 0:cols], mag[:, 0:cols], thr[:, th + 1:th + 2], None, ALU.is_le))
                chain(dve.tensor_tensor(tier[:, 0:cols], tier[:, 0:cols], tier2[:, 0:cols], ALU.add))
                chain(dve.tensor_scalar(tier[:, 0:cols], tier[:, 0:cols], -1.0, None, ALU.max))
                chain(dve.tensor_scalar(tier2[:, 0:cols], w, 0.8, None, ALU.mult))
                chain(dve.tensor_tensor(tier[:, 0:cols], tier2[:, 0:cols], tier[:, 0:cols], ALU.mult))
                chain(dve.tensor_tensor(dst, w, tier[:, 0:cols], ALU.add))
            dve.sem_inc(experts_ready, 1)
            dve.sem_inc(ready, 1)
            dve.wait_ge(ready, 4)

            def moments(u, src, out, rows=P):
                for t in range(len(src)):
                    link(dve.bn_stats(stats[u % 2][0:rows, t, :], src[t]))
                for t in range(len(src)):
                    dve.bn_aggr(out[t], stats[u % 2][0:rows, t, :]).then_inc(mv_ready.sem, 1)
                waits["mv"] += len(src)

            def link(ins):
                chain(ins)

            waits = {"mv": 0, "root": 0, "x": 0}

            def normalise(u, src, dst, done):
                s = u % 2
                moments(u, [src[:, t, :] for t in range(NT)], [mv[s][:, t, :] for t in range(NT)])
                waits["root"] += 1
                dve.wait_ge(*rstd_ready.at(waits["root"]))
                for t in range(NT):
                    dve.tensor_scalar(dst[:, t, :], src[:, t, :], mv[s][:, t, 0:1], rstd[s][:, NT + t:NT + t + 1],
                                      ALU.subtract, ALU.mult).then_inc(done.sem, 1)

            def residual(u, name):
                s = u % 2
                ps = ring.wait(dve, name, u)
                dve.tensor_tensor(r[s][:].rearrange("p t n -> p (t n)"), ps[:, 0:N],
                                  x[s][:].rearrange("p t n -> p (t n)"), ALU.add).then_inc(ring.read(name, u), 1)
                ring.wait_read(dve, name, u)

            def ffn_in(u):
                s = u % 2
                dve.wait_ge(*x_loaded[s].at(32 * (u // 2 + 1)))
                normalise(u, x[s], xn[s], xn_ready[0])

            def context(u):
                s = u % 2
                link(dve.bn_stats(cmv[s][:, 0:6], c[s][:]))
                dve.bn_aggr(cmv[s][:, 6:8], cmv[s][:, 0:6]).then_inc(mv_ready.sem, 1)
                waits["root"] += 1
                dve.wait_ge(*rstd_ready.at(waits["root"]))
                dve.tensor_scalar(cn[s][:], c[s][:], cmv[s][:, 6:7], cmv[s][:, 1:2], ALU.subtract, ALU.mult)\
                    .then_inc(cn_ready.sem, 1)

            def ffn_up1(u):
                s = u % 2
                ps = ring.wait(dve, "logits", u)
                l = ps[:, 0:NT * NE0].rearrange("p (t e) -> p t e", t=NT)
                link(dve.tensor_reduce(pr[s][:, :, 0], l, AX.X, ALU.max))
                dve.tensor_tensor(lg[s][:], l, pr[s][:, :, 0:1].broadcast_to([P, NT, NE0]), ALU.subtract)\
                    .then_inc(ring.read("logits", u), 1)
                ring.wait_read(dve, "logits", u)
                dve.wait_ge(*lg_exp.at(u + 1))
                link(dve.tensor_reduce(pr[s][:, :, 1], lg[s][:], AX.X, ALU.add))
                link(dve.reciprocal(pr[s][:, :, 2], pr[s][:, :, 1]))
                link(dve.tensor_reduce(pr[s][:, :, 5], lg[s][:, :, 1:NE0], AX.X, ALU.add))
                link(dve.tensor_tensor(pr[s][:, :, 3], lg[s][:, :, 0], pr[s][:, :, 2], ALU.mult))
                link(dve.tensor_tensor(pr[s][:, :, 4], pr[s][:, :, 5], pr[s][:, :, 2], ALU.mult))

            def ffn_down(u):
                s = u % 2
                ps = ring.wait(dve, "down", u)
                for t in range(NT):
                    link(dve.scalar_tensor_tensor(r[s][:, t, :], ps[:, t * D:(t + 1) * D], pr[s][:, t, 3:4], x[s][:, t, :],
                                                  ALU.mult, ALU.add))
                for t in range(NT):
                    ins = dve.scalar_tensor_tensor(r[s][:, t, :], ps[:, (2 + t) * D:(3 + t) * D], pr[s][:, t, 4:5],
                                                   r[s][:, t, :], ALU.mult, ALU.add)
                ins.then_inc(ring.read("down", u), 1)
                ring.wait_read(dve, "down", u)
                normalise(u, r[s], x[s], x_ready[0])
                dve.wait_ge(*x_ready[0].at(NT * (u + 1)))
                normalise(u, x[s], xn[s], xn_ready[1])

            def qkv(u, t):
                s = u % 2
                def square_sums(i):
                    n = (u * NT + t) * 4 + i
                    dve.wait_ge(*squares.at(n + 1))
                    dve.tensor_reduce(ss[:, i % 2, :], sq[:, i % 2, :].rearrange("p (h d) -> p h d", d=DH1), AX.X, ALU.add)\
                        .then_inc(ss_ready.sem, 1)

                if t == 0:
                    ps = ring.wait(dve, "null", u)
                    dve.tensor_copy(nneg[s][:].rearrange("p t h n -> p (t h n)"), ps[:, 0:64])\
                        .then_inc(ring.read("null", u), 1)
                square_sums(0)
                for i in range(4):
                    if i < 3:
                        square_sums(i + 1)
                    dve.wait_ge(*rn_ready.at((u * NT + t) * 4 + i + 1))
                    ps = ring.bank("qk", u, t, i)
                    rr = rnq[s][:, t, 8 * i:8 * i + 8] if i < 2 else rn[:, i % 2, :]
                    if i >= 2:
                        ring.wait(dve, "qkT", u, t, i - 2)
                    elif t or u:
                        pu, pt = (u, t - 1) if t else (u - 1, NT - 1)
                        ring.wait(dve, "qkT", pu, pt, i + 2)
                    dve.tensor_tensor(qn[:, i % 2, :].rearrange("p (h d) -> p h d", d=DH1),
                                      ps[:].rearrange("p (h d) -> p h d", d=DH1),
                                      rr.unsqueeze(2).broadcast_to([P, 8, DH1]), ALU.mult)\
                        .then_inc(ring.read("qk", u, t, i), 1)
                if t == 1:
                    ring.wait_read(dve, "null", u)
                    link(dve.tensor_tensor(nneg[s][:], nneg[s][:],
                                           rnq[s][:].unsqueeze(3).broadcast_to([P, NT, H1, NULLS]), ALU.mult))
                    link(dve.tensor_tensor(nneg[s][:], nneg[s][:], null_bias[:], ALU.add))
                    link(dve.tensor_reduce(nmin[s][:], nneg[s][:], AX.X, ALU.min))

            def attn_out(u):
                s = u % 2
                residual(u, "y1")
                normalise(u, r[s], x[s], x_ready[1])
                dve.wait_ge(*x_ready[1].at(NT * (u + 1)))
                normalise(u, x[s], xn[s], xn_ready[2])

            def x_scores(u):
                for t in range(NT):
                    ps = ring.wait(dve, "s2", u, t)
                    sc = ps[:].rearrange("p (h k) -> p h k", h=H2)
                    link(dve.tensor_reduce(m2[:, t, :], sc, AX.X, ALU.max, negate=True))
                    dve.tensor_tensor(s2n[:, t], sc, m2[:, t, :].unsqueeze(2).broadcast_to([P, H2, S_CTX]), ALU.add)\
                        .then_inc(ring.read("s2", u, t), 1)
                    ring.wait_read(dve, "s2", u, t)
                for t in range(NT):
                    dve.wait_ge(*s2_exp.at(NT * u + t + 1))
                    link(dve.tensor_reduce(z2[:, t, :], s2n[:, t], AX.X, ALU.add))
                    dve.reciprocal(rz2[:, t, :], z2[:, t, :]).then_inc(s2_inv.sem, 1)

            def x_pT(u):
                for half in range(2):
                    ps = ring.wait(dve, "p2T", u, half)
                    dve.tensor_copy(p2T[:, 2 * half:2 * half + 2, :].rearrange("p c n -> p (c n)"), ps[:])\
                        .then_inc(ring.read("p2T", u, half), 1)

            def x_out(u):
                s = u % 2
                residual(u, "y2")
                normalise(u, r[s], x[s], x_ready[2])

            def pairs(u, extra):
                s = u % 2
                for p in range(PAIRS1 + 3):
                    n = PAIRS1 * u + p
                    if p < PAIRS1:
                        a = 2 * n % NPR
                        if 2 * n >= NPR:
                            m = n - NPR // 2
                            ring.wait(dve, "p1T", m // PAIRS1, m % PAIRS1, 1)
                        dve.tensor_copy(probs[:, a:a + NT, N:N + 2 * NULLS].rearrange("q t (h n) -> q t h n", n=NULLS),
                                        nneg[s][:, :, 2 * p:2 * p + 2, :])
                        for i in range(2):
                            h = 2 * p + i
                            ps = ring.wait(dve, "s1", u, p, i)
                            for t in range(NT):
                                w = (t + 1) * P
                                ins = dve.tensor_tensor_reduce(probs[:, a + t, keys(i, w)], dist[:, h, (1 - t) * P:N],
                                                               ps[:, t * P:t * P + w], 1.0, nmin[s][:, t, h:h + 1],
                                                               ALU.add, ALU.min, low[:, a + t, i:i + 1])
                            ins.then_inc(ring.read("s1", u, p, i), 1)
                    if 1 <= p < PAIRS1 + 1:
                        a = 2 * (n - 1) % NPR
                        for i in range(2):
                            dve.wait_ge(*exp_done.at(2 * (n - 1) + i + 1))
                            dve.reciprocal(rsums[:, a:a + NT, i], sums[:, a:a + NT, i]).then_inc(rs_ready.sem, 1)
                    if 2 <= p < PAIRS1 + 2:
                        m = n - 2
                        if m >= 2:
                            dve.wait_ge(*o1_full.at(m - 1))
                        for i in range(2):
                            ps = ring.wait(dve, "p1T", u, p - 2, i)
                            dve.tensor_copy(pnT[:, m % 2, i * P:(i + 1) * P], ps[0:4, 3 * P:4 * P])
                            dve.tensor_copy(pT[:, (2 * m + i) % 4].rearrange("k t q -> k (t q)"), ps[:, 0:3 * P])\
                                .then_inc(ring.read("p1T", u, p - 2, i), 1)
                    extra(p)

            steps = dict(ffn_in=ffn_in, ctx=context, ffn_up1=ffn_up1, ffn_down=ffn_down,
                         qkv0=lambda u: qkv(u, 0), qkv1=lambda u: qkv(u, 1), attn_out=attn_out,
                         x_scores=x_scores, x_pT=x_pT, x_out=x_out)
            with dve.Fori(0, B // U) as it:
                chain = Chain(dve, dve_chain)
                run(steps, pairs)
                meet.join(dve, "vector")

        @block.gpsimd
        def _(pool):
            chain = Chain(pool, pool_setup)
            chain(pool.iota(iota_i[:], pattern=[[-1, N]], base=P, channel_multiplier=1))
            chain(pool.tensor_copy(dist0[:], iota_i[:]))
            pool.affine_select(out=dist0[:], in_=dist0[:], compare_op=ALU.is_ge, fill=MASKED, base=P,
                               pattern=[[-1, N]], channel_multiplier=1).then_inc(iota_done, 1)
            chain(pool.iota(iota_n[:], pattern=[[P, NT], [-1, NULLS]], base=NULLS, channel_multiplier=1))
            pool.tensor_copy(iota_nf[:], iota_n[:]).then_inc(iota_done, 1)
            pool.wait_ge(null_pow, 1)
            pool.tensor_tensor(null_ss[:, 1:2], null_ss[:, 0:1], K["eps_half"][0:32, 0:1], ALU.pow).then_inc(null_pow, 1)
            pool.sem_inc(ready, 1)
            pool.wait_ge(ready, 4)
            count = {"mv": 0}

            def root(u):
                s = u % 2
                count["mv"] += NT
                pool.wait_ge(*mv_ready.at(count["mv"]))
                chain(pool.tensor_scalar(rstd[s][:, 0:NT], mv[s][:, :, 1], LN_EPS, None, ALU.add))
                pool.tensor_tensor(rstd[s][:, NT:2 * NT], rstd[s][:, 0:NT], K["eps_half"][:, 0:NT], ALU.pow)\
                    .then_inc(rstd_ready.sem, 1)

            def ctx_root(u):
                s = u % 2
                count["mv"] += 1
                pool.wait_ge(*mv_ready.at(count["mv"]))
                chain(pool.tensor_scalar(cmv[s][:, 0:1], cmv[s][:, 7:8], LN_EPS, None, ALU.add))
                pool.tensor_tensor(cmv[s][:, 1:2], cmv[s][:, 0:1], K["eps_half"][0:S_CTX, 0:1], ALU.pow)\
                    .then_inc(rstd_ready.sem, 1)

            def two_roots(u):
                root(u)
                root(u)

            def qkv(u, t):
                s = u % 2
                for i in range(4):
                    n = (u * NT + t) * 4 + i
                    pool.wait_ge(*ss_ready.at(n + 1))
                    rr = rnq[s][:, t, 8 * i:8 * i + 8] if i < 2 else rn[:, i % 2, :]
                    chain(pool.tensor_scalar(ss[:, i % 2, :], ss[:, i % 2, :], 1e-24, None, ALU.max))
                    pool.tensor_tensor(rr, ss[:, i % 2, :], K["eps_half"][:, 0:8], ALU.pow).then_inc(rn_ready.sem, 1)

            def x_scores(u):
                for t in range(NT):
                    pool.wait_ge(*s2_inv.at(NT * u + t + 1))
                    pool.tensor_tensor(s2n[:, t], s2n[:, t], rz2[:, t, :].unsqueeze(2).broadcast_to([P, H2, S_CTX]),
                                       ALU.mult).then_inc(p2_ready.sem, 1)

            def pairs(u, extra):
                for p in range(PAIRS1 + 3):
                    n = PAIRS1 * u + p
                    if 1 <= p < PAIRS1 + 1:
                        for i in range(2):
                            pool.wait_ge(*rs_ready.at(2 * (n - 1) + i + 1))
                            for t in range(NT):
                                a = (2 * (n - 1) + t) % NPR
                                w = (t + 1) * P
                                ins = pool.tensor_scalar(probs[:, a, keys_nulls(i, w)], probs[:, a, keys_nulls(i, w)], rsums[:, a, i:i + 1],
                                                         1.0, ALU.mult, ALU.mult)
                            ins.then_inc(p_ready.sem, 1)
                    extra(p)

            steps = dict(ffn_in=root, ctx=ctx_root, ffn_down=two_roots, qkv0=lambda u: qkv(u, 0),
                         qkv1=lambda u: qkv(u, 1), attn_out=two_roots, x_scores=x_scores, x_out=root)
            with pool.Fori(0, B // U) as it:
                chain = Chain(pool, pool_chain)
                run(steps, pairs)
                meet.lead(pool, first, last)
            pool.sem_clear(range(FIRST_SEM, meet.arrived.num))

        @block.sync
        def _(sy):
            sy.wait_ge(cleared, 1)
            for dst, src in loads[0::2]:
                sy.dma_start(dst, src, allow_slow_non_contiguous=True).then_inc(loaded, 16)
            sy.sem_inc(ready, 1)
            xin = x_in.rearrange("b (t p) d -> b p t d", p=P)
            xo = x_out.rearrange("b (t p) d -> b p t d", p=P)
            with sy.Fori(0, B // U) as it:
                for u in range(U):
                    s = u % 2
                    if u >= 2:
                        sy.wait_ge(*stored[s].at(16 * (u // 2)))
                    sy.dma_start(x[s][:], xin[it * U + u]).then_inc(x_loaded[s].sem, 16)
                    sy.dma_start(c[s][:], A["ctx_1024"][it * U + u]).then_inc(x_loaded[s].sem, 16)
                    if u >= 1:
                        sy.wait_ge(*x_ready[2].at(NT * u))
                        sy.dma_start(xo[it * U + u - 1], x[1 - s][:]).then_inc(stored[1 - s].sem, 16)
                sy.wait_ge(*x_ready[2].at(NT * U))
                sy.dma_start(xo[it * U + U - 1], x[(U - 1) % 2][:]).then_inc(stored[(U - 1) % 2].sem, 16)
                for i in range(2):
                    sy.wait_ge(*stored[i].at(16 * (U // 2)))
                meet.join(sy, "sync")


H3, DH3 = 16, 8
KV3 = 8
TC = B * N // P
TG = 4
NG = TC // TG
NE = 8
CAP = int(np.ceil(B * N * 2 / NE * 1.25))


def phase_3(nc, A, K, x_in, out):
    with ExitStack() as ctx:
        hT_all = ctx.enter_context(nc.sbuf_tensor("h2T_all", [P, TC, P], F32))
        acc_all = ctx.enter_context(nc.sbuf_tensor("acc_all", [P, TC, D], F32))
        column_attention(nc, A, K, x_in, hT_all, acc_all)
        experts(nc, A, K, hT_all, acc_all, out)


def column_attention(nc, A, K, x_in, hT_all, acc_all):
    U = 2
    PAIRS = H3 // 2
    with ExitStack() as ctx:
        def sb(name, shape, dt=F32):
            return ctx.enter_context(nc.sbuf_tensor(name, shape, dt))

        sems = []

        def sem(name):
            s = ctx.enter_context(nc.semaphore(name, num=FIRST_SEM + len(sems)))
            sems.append(s)
            return s

        def two(name, shape, dt=F32):
            return [sb(f"{name}{i}", shape, dt) for i in range(2)]

        ident = K["ident"]
        W = TG * P
        w_raw = sb("qkv_raw", [P, 2, P])
        wo_raw = sb("proj_raw", [P, P])
        wq = sb("cq_pad", [P, GROUPS, 4, 32])
        wk = sb("ck_pad", [P, GROUPS, 4, 32])
        wv = sb("cv", [P, KV3, DH3])
        woT = sb("c_woT", [P, D])
        wo_pad = sb("c_wo_pad", [P, GROUPS, D])
        ln1 = sb("c_ln1", [P, 2])
        ln2 = sb("c_ln2", [P, 2])
        ident_bf = sb("ident_bf", [P, P], BF16)
        iota = sb("c_iota", [P, P], I32)
        low_bits = sb("c_low_bits", [P, P], I32)
        mask_f = sb("c_mask_f", [P, P])
        mask = sb("c_mask", [P, TG, P], BF16)
        x = two("cx", [P, TG, D])
        xn = two("cxn", [P, TG, D])
        hn = two("chn", [P, TG, D])
        r = two("cr", [P, TG, D])
        stats = two("cstats", [P, TG, 6])
        mv = two("cmv3_", [P, TG, 2])
        rstd = two("crstd", [P, 2 * TG])
        lnT = two("clnT", [P, W])
        qT = two("cqT", [P, GROUPS, W])
        kT = two("ckT", [P, GROUPS, W])
        v = two("cv3_", [P, TG, KV3, 32])
        oT = two("coT", [P, GROUPS, W])
        NPR = 4
        probs = sb("cprobs", [P, NPR, TG, P])
        pT = sb("cpT", [P, NPR, TG, P])
        negmax = sb("cnegmax", [P, NPR, TG])
        sums = sb("csums", [P, NPR, TG])
        rsums = sb("crsums", [P, NPR, TG])
        banks = [ctx.enter_context(nc.psum_tensor(f"pc{i}", [P, 512], F32)) for i in range(6)]
        o_banks = [ctx.enter_context(nc.psum_tensor(f"pd{i}", [P, 512], F32)) for i in range(2)]

        loaded = sem("c_weights_loaded")
        cleared = sem("c_cleared")
        staged = sem("c_proj_staged")
        dve_setup = sem("c_dve_setup")
        pool_setup = sem("c_pool_setup")
        act_setup = sem("c_act_setup")
        t_ps = sem("c_setup_transposed")
        mask_iota = sem("c_mask_iota")
        ready = sem("c_setup_ready")
        meet = Meeting(sem, ["sync", "scalar", "tensor", "vector"])
        n_setup = len(sems)
        ring = Ring(banks, sem)
        x_loaded = [sem(f"cx{i}_loaded") for i in range(2)]
        mv_ready = Counted(sem("c_moments_ready"))
        rstd_ready = Counted(sem("c_roots_ready"))
        xn_ready = Counted(sem("c_xn_ready"))
        hn_ready = Counted(sem("c_hn_ready"))
        negmax_ready = Counted(sem("c_negmax_ready"))
        rs_ready = Counted(sem("c_rsums_ready"))
        p_ready = Counted(sem("c_probs_ready"))
        o_full = Counted(sem("c_o_full"))
        o_read = Counted(sem("c_o_read"))
        stored_hT = sem("c_hT_written")
        dve_chain = sem("c_dve_chain")
        pool_chain = sem("c_pool_chain")
        first, last = sems[n_setup].num, sems[-1].num

        loads = [
            (w_raw[:], A["L1_ffn_qkv_weight"].rearrange("(a p) k -> p a k", p=P)),
            (wo_raw[:], A["L1_ffn_proj_weight"]),
            (ln1[:, 0:1], col(A["L1_ffn_ln1_weight"])), (ln1[:, 1:2], col(A["L1_ffn_ln1_bias"])),
            (ln2[:, 0:1], col(A["L1_ffn_ln2_weight"])), (ln2[:, 1:2], col(A["L1_ffn_ln2_bias"])),
        ]
        during = {1: [("out", -1)], 3: [("norm1", 1)], 4: [("proj", 1)]}
        before = ["norm1", "proj"]
        after = ["out"]

        def run(steps, pairs):
            for name in before:
                if name in steps:
                    steps[name](0)
            for u in range(U):
                pairs(u, lambda p: [steps[name](u + du) for name, du in during.get(p, ())
                                    if name in steps and 0 <= u + du < U])
            for name in after:
                if name in steps:
                    steps[name](U - 1)

        block = ctx.enter_context(nc.Block())

        @block.tensor
        def _(pe):
            pe.wait_ge(loaded, 16 * len(loads))
            for a in range(2):
                pe.transpose(banks[0][:, a * P:(a + 1) * P], w_raw[:, a, :], ident[:])
            pe.transpose(banks[0][:, 2 * P:3 * P], wo_raw[:], ident[:]).then_inc(t_ps, 1)
            pe.wait_ge(ready, 4)

            def transposes(name, u, src):
                ps = ring.open(pe, name, u)
                for t in range(TG):
                    mm = pe.transpose(ps[:, t * P:(t + 1) * P], src[:, t, :], ident[:])
                mm.then_inc(ring.filled(name, u), 1)

            def norm1(u):
                pe.wait_ge(*xn_ready.at(TG * (u + 1)))
                transposes("lnT", u, xn[u % 2])

            def proj(u):
                s = u % 2
                ring.wait_read(pe, "lnT", u)
                for g in range(GROUPS):
                    for name, w in (("q", wq), ("k", wk)):
                        ps = ring.open(pe, name, u, g)
                        pe.matmul(ps[:], w[:, g].rearrange("p j d -> p (j d)"), lnT[s][:], start=True, stop=True)\
                            .then_inc(ring.filled(name, u, g), 1)
                ps = ring.open(pe, "v", u)
                for t in range(TG):
                    mm = pe.matmul(ps[:, t * 64:(t + 1) * 64], lnT[s][:, t * P:(t + 1) * P],
                                   wv[:].rearrange("p h d -> p (h d)"), start=True, stop=True)
                mm.then_inc(ring.filled("v", u), 1)

            def scores(u, p):
                s = u % 2
                ps = [ring.open(pe, "s", u, p, i) for i in range(2)]
                for i in range(2):
                    pe.matmul(ps[i][:], ident_bf[:], mask[:].rearrange("q t k -> q (t k)"), start=True, stop=False,
                              skip_group_check=True)
                for t in range(TG):
                    for i in range(2):
                        h = 2 * p + i
                        g, j = h // 4, 32 * (h % 4)
                        mm = pe.matmul(ps[i][:, t * P:(t + 1) * P], qT[s][j:j + DH3, g, t * P:(t + 1) * P],
                                       kT[s][j:j + DH3, g, t * P:(t + 1) * P], start=False, stop=True,
                                       skip_group_check=True)
                        if t == TG - 1:
                            mm.then_inc(ring.filled("s", u, p, i), 1)

            def probs_T(u, p):
                for i in range(2):
                    n = H3 * u + 2 * p + i
                    pe.wait_ge(*p_ready.at(n + 1))
                    ps = ring.open(pe, "pT", u, p, i)
                    for t in range(TG):
                        mm = pe.transpose(ps[:, t * P:(t + 1) * P], probs[:, n % NPR, t, :], ident[:])
                    mm.then_inc(ring.filled("pT", u, p, i), 1)

            def values(u, p):
                s = u % 2
                m = GROUPS * u + p // 2
                if p % 2 == 0 and m >= 2:
                    pe.wait_ge(*o_read.at(m - 1))
                for i in range(2):
                    h = 2 * p + i
                    n = H3 * u + h
                    j = 32 * (h % 4)
                    ring.wait_read(pe, "pT", u, p, i)
                    for t in range(TG):
                        mm = pe.matmul(o_banks[m % 2][j:j + 32, t * P:(t + 1) * P], v[s][:, t, h // 2, :],
                                       pT[:, n % NPR, t, :], start=True, stop=True)
                mm.then_inc(o_full.sem, 1)

            def pairs(u, extra):
                for g in range(GROUPS):
                    ring.wait_read(pe, "q", u, g)
                    ring.wait_read(pe, "k", u, g)
                ring.wait_read(pe, "v", u)
                for p in range(PAIRS + 3):
                    if p < PAIRS:
                        scores(u, p)
                    if 2 <= p < PAIRS + 2:
                        probs_T(u, p - 2)
                    if p >= 3:
                        values(u, p - 3)
                    extra(p)

            def project_out(u):
                s = u % 2
                pe.wait_ge(*o_read.at(GROUPS * (u + 1)))
                ps = ring.open(pe, "y", u)
                for t in range(TG):
                    for g in range(GROUPS):
                        mm = pe.matmul(ps[:, t * P:(t + 1) * P], oT[s][:, g, t * P:(t + 1) * P], wo_pad[:, g, :],
                                       start=(g == 0), stop=(g == GROUPS - 1))
                mm.then_inc(ring.filled("y", u), 1)
                pe.wait_ge(*hn_ready.at(TG * (u + 1)))
                transposes("hT", u, hn[s])

            steps = dict(norm1=norm1, proj=proj, out=project_out)
            with pe.Fori(0, NG // U) as it:
                run(steps, pairs)
                meet.join(pe, "tensor")

        @block.scalar
        def _(act):
            act.wait_ge(cleared, 4)
            act.wait_ge(t_ps, 1)
            w_ps = banks[0][:, 0:2 * P].rearrange("k (g a d) -> k g a d", g=GROUPS, a=2)
            for i in range(2):
                act.activation(wq[:, :, i::2, 0:DH3], w_ps[:, :, :, i * DH3:(i + 1) * DH3], ACT.Copy)
                act.activation(wk[:, :, i::2, 0:DH3], w_ps[:, :, :, 2 * DH3:3 * DH3], ACT.Copy)
            act.activation(wv[:].rearrange("k (g a) d -> k g a d", a=2), w_ps[:, :, :, 3 * DH3:4 * DH3], ACT.Copy)
            act.activation(woT[:], banks[0][:, 2 * P:3 * P], ACT.Copy).then_inc(act_setup, 1)
            act.wait_ge(act_setup, 1)
            for j in range(4):
                for g in range(GROUPS):
                    k = (4 * g + j) * DH3
                    act.dma_start(wo_pad[32 * j:32 * j + DH3, g, :], woT[k:k + DH3, :]).then_inc(staged, 16)
            act.wait_ge(staged, 16 * 4 * GROUPS)
            act.sem_inc(ready, 1)
            act.wait_ge(ready, 4)

            def affine(dst, ps, ln):
                return act.activation(dst, ps, ACT.Identity, scale=ln[:, 0:1], bias=ln[:, 1:2])

            def norm1(u):
                ps = ring.wait(act, "lnT", u)
                affine(lnT[u % 2][:], ps[:], ln1).then_inc(ring.read("lnT", u), 1)

            def proj(u):
                s = u % 2
                for g in range(GROUPS):
                    ps = ring.wait(act, "q", u, g)
                    act.activation(qT[s][:, g, :], ps[:], ACT.Copy, scale=1 / math.sqrt(DH3))\
                        .then_inc(ring.read("q", u, g), 1)
                ps = ring.wait(act, "v", u)
                act.activation(v[s][:, :, :, 0:DH3], ps[:, 0:TG * 64].rearrange("p (t h d) -> p t h d", t=TG, h=KV3),
                               ACT.Copy).then_inc(ring.read("v", u), 1)

            def pairs(u, extra):
                s = u % 2
                for p in range(PAIRS + 3):
                    if p < PAIRS:
                        for i in range(2):
                            n = H3 * u + 2 * p + i
                            ps = ring.wait(act, "s", u, p, i)
                            act.wait_ge(*negmax_ready.at(n + 1))
                            if n >= NPR:
                                m = n - NPR
                                ring.wait(act, "pT", m // H3, (m % H3) // 2, m % 2)
                            for t in range(TG):
                                ins = act.activation(probs[:, n % NPR, t, :], ps[:, t * P:(t + 1) * P], ACT.Exp,
                                                     bias=negmax[:, n % NPR, t:t + 1],
                                                     accum_out=sums[:, n % NPR, t:t + 1])
                            ins.then_inc(ring.read("s", u, p, i), 1)
                    if p >= 3 and p % 2 == 0:
                        g = (p - 4) // 2
                        act.wait_ge(*o_full.at(PAIRS * u + 2 * (g + 1)))
                        act.activation(oT[s][:, g, :], o_banks[(GROUPS * u + g) % 2][:], ACT.Copy).then_inc(o_read.sem, 1)
                    extra(p)

            def out_step(u):
                ps = ring.wait(act, "hT", u)
                affine(hT_all[:, bass.ds((it * U + u) * TG, TG), :].rearrange("p t n -> p (t n)"), ps[:], ln2)\
                    .then_inc(ring.read("hT", u), 1)

            steps = dict(norm1=norm1, proj=proj, out=out_step)
            with act.Fori(0, NG // U) as it:
                run(steps, pairs)
                meet.join(act, "scalar")

        @block.vector
        def _(dve):
            dve.memset(wq[:], 0.0).then_inc(cleared, 1)
            dve.memset(wk[:], 0.0).then_inc(cleared, 1)
            dve.memset(wo_pad[:], 0.0).then_inc(cleared, 1)
            dve.memset(v[0][:], 0.0)
            dve.memset(v[1][:], 0.0).then_inc(cleared, 1)
            chain = Chain(dve, dve_setup)
            dve.tensor_copy(ident_bf[:], ident[:])
            dve.wait_ge(mask_iota, 1)
            chain(dve.tensor_scalar(low_bits[:], iota[:], N // TC - 1, None, ALU.bitwise_and))
            chain(dve.tensor_copy(mask_f[:], low_bits[:]))
            chain(dve.tensor_scalar(mask_f[:], mask_f[:], 0.5, -MASKED, ALU.is_ge, ALU.mult))
            dve.sem_inc(mask_iota, 1)
            dve.wait_ge(mask_iota, 3)
            for t in range(TG):
                ins = dve.tensor_copy(mask[:, t, :], mask_f[:])
            chain(ins)
            dve.sem_inc(ready, 1)
            dve.wait_ge(ready, 4)
            roots = {"n": 0}

            def link(ins):
                chain(ins)

            def normalise(s, src, dst, done):
                for t in range(TG):
                    link(dve.bn_stats(stats[s][:, t, :], src[:, t, :]))
                for t in range(TG):
                    dve.bn_aggr(mv[s][:, t, :], stats[s][:, t, :]).then_inc(mv_ready.sem, 1)
                roots["n"] += 1
                dve.wait_ge(*rstd_ready.at(roots["n"]))
                for t in range(TG):
                    dve.tensor_scalar(dst[:, t, :], src[:, t, :], mv[s][:, t, 0:1], rstd[s][:, TG + t:TG + t + 1],
                                      ALU.subtract, ALU.mult).then_inc(done.sem, 1)

            def norm1(u):
                dve.wait_ge(x_loaded[u % 2], 16 * (u // 2 + 1))
                normalise(u % 2, x[u % 2], xn[u % 2], xn_ready)

            def proj(u):
                s = u % 2
                for g in range(GROUPS):
                    ps = ring.wait(dve, "k", u, g)
                    dve.tensor_copy(kT[s][:, g, :], ps[:]).then_inc(ring.read("k", u, g), 1)

            def out_step(u):
                s = u % 2
                ps = ring.wait(dve, "y", u)
                flat = lambda a: a.rearrange("p t n -> p (t n)")
                dve.tensor_tensor(flat(r[s][:]), ps[:], flat(x[s][:]), ALU.add).then_inc(ring.read("y", u), 1)
                ring.wait_read(dve, "y", u)
                normalise(s, r[s], hn[s], hn_ready)
                dve.tensor_tensor(flat(acc_all[:, bass.ds((it * U + u) * TG, TG), :]), flat(r[s][:]), flat(x[s][:]),
                                  ALU.add)

            def pairs(u, extra):
                for p in range(PAIRS + 3):
                    if p < PAIRS:
                        for i in range(2):
                            n = H3 * u + 2 * p + i
                            ps = ring.wait(dve, "s", u, p, i)
                            dve.tensor_reduce(negmax[:, n % NPR, :], ps[:].rearrange("q (t k) -> q t k", t=TG), AX.X,
                                              ALU.max, negate=True).then_inc(negmax_ready.sem, 1)
                    if 1 <= p < PAIRS + 1:
                        for i in range(2):
                            n = H3 * u + 2 * (p - 1) + i
                            ring.wait_read(dve, "s", u, p - 1, i)
                            dve.reciprocal(rsums[:, n % NPR, :], sums[:, n % NPR, :]).then_inc(rs_ready.sem, 1)
                    if 2 <= p < PAIRS + 2:
                        for i in range(2):
                            n = H3 * u + 2 * (p - 2) + i
                            ps = ring.wait(dve, "pT", u, p - 2, i)
                            if n >= NPR:
                                dve.wait_ge(*o_full.at((n - NPR) // 2 + 1))
                            dve.tensor_copy(pT[:, n % NPR].rearrange("k t q -> k (t q)"), ps[:])\
                                .then_inc(ring.read("pT", u, p - 2, i), 1)
                    extra(p)

            steps = dict(norm1=norm1, proj=proj, out=out_step)
            with dve.Fori(0, NG // U) as it:
                chain = Chain(dve, dve_chain)
                run(steps, pairs)
                meet.join(dve, "vector")

        @block.gpsimd
        def _(pool):
            pool.iota(iota[:], pattern=[[-1, P]], base=P, channel_multiplier=1).then_inc(mask_iota, 1)
            pool.wait_ge(mask_iota, 2)
            pool.affine_select(out=mask_f[:], in_=mask_f[:], compare_op=ALU.is_ge, fill=-MASKED, base=0,
                               pattern=[[-1, P]], channel_multiplier=1).then_inc(mask_iota, 1)
            pool.sem_inc(ready, 1)
            pool.wait_ge(ready, 4)
            count = {"mv": 0}

            def root(u):
                s = u % 2
                count["mv"] += TG
                pool.wait_ge(*mv_ready.at(count["mv"]))
                chain(pool.tensor_scalar(rstd[s][:, 0:TG], mv[s][:, :, 1], LN_EPS, None, ALU.add))
                pool.tensor_tensor(rstd[s][:, TG:2 * TG], rstd[s][:, 0:TG], K["eps_half"][:, 0:TG], ALU.pow)\
                    .then_inc(rstd_ready.sem, 1)

            def pairs(u, extra):
                for p in range(PAIRS + 3):
                    if 1 <= p < PAIRS + 1:
                        for i in range(2):
                            n = H3 * u + 2 * (p - 1) + i
                            pool.wait_ge(*rs_ready.at(n + 1))
                            for t in range(TG):
                                ins = pool.tensor_scalar(probs[:, n % NPR, t, :], probs[:, n % NPR, t, :],
                                                         rsums[:, n % NPR, t:t + 1], 1.0, ALU.mult, ALU.mult)
                            ins.then_inc(p_ready.sem, 1)
                    extra(p)

            steps = dict(norm1=root, out=root)
            with pool.Fori(0, NG // U) as it:
                chain = Chain(pool, pool_chain)
                run(steps, pairs)
                meet.lead(pool, first, last)
            pool.sem_clear(range(FIRST_SEM, meet.arrived.num))

        @block.sync
        def _(sy):
            for dst, src in loads:
                sy.dma_start(dst, src, allow_slow_non_contiguous=True).then_inc(loaded, 16)
            sy.sem_inc(ready, 1)
            xin = x_in.rearrange("b n d -> (b n) d").rearrange("(p g t) d -> g p t d", p=P, t=TG)
            with sy.Fori(0, NG // U) as it:
                for u in range(U):
                    sy.dma_start(x[u % 2][:], xin[it * U + u]).then_inc(x_loaded[u % 2], 16)
                meet.join(sy, "sync")


def experts(nc, A, K, hT_all, acc_all, out):
    U = 2
    with ExitStack() as ctx:
        def sb(name, shape, dt=F32):
            return ctx.enter_context(nc.sbuf_tensor(name, shape, dt))

        sems = []

        def sem(name):
            s = ctx.enter_context(nc.semaphore(name, num=FIRST_SEM + len(sems)))
            sems.append(s)
            return s

        def two(name, shape, dt=F32):
            return [sb(f"{name}{i}", shape, dt) for i in range(2)]

        W = TG * P
        wr = sb("e_router", [P, NE])
        w1 = sb("e_w1", [P, NE, F])
        w2 = sb("e_w2", [P, NE, FC, D])
        before = sb("e_before", [P, P])
        rev = sb("e_rev", [P, TC, NE])
        rev_i = sb("e_rev_i", [P, TC, NE], I32)
        small = sb("e_small", [P, 6, TC])
        prob = sb("e_prob", [P, TC, NE])
        work = [sb(f"e_work{i}", [P, TC, NE]) for i in range(4)]
        total = sb("e_total", [P, NE])
        wts = sb("e_weights", [P, TC, NE])
        hT = two("e_hT", [P, W])
        wg = two("e_wg", [P, TG, NE])
        hid = two("e_hid", [P, FC, W])
        r = two("e_r", [P, TG, D])
        y = two("e_y", [P, TG, D])
        stats = two("e_stats", [P, TG, 6])
        mv = two("e_mv", [P, TG, 2])
        rstd = two("e_rstd", [P, 2 * TG])
        banks = [ctx.enter_context(nc.psum_tensor(f"pe{i}", [P, 512], F32)) for i in range(8)]

        loaded = sem("e_loaded")
        rev_ready = sem("e_rev_ready")
        before_ready = sem("e_before_ready")
        logits_ready = sem("e_logits")
        step = sem("e_route_step")
        dve_setup = sem("e_dve_setup")
        pool_setup = sem("e_pool_setup")
        ready = sem("e_ready")
        meet = Meeting(sem, ["sync", "scalar", "tensor", "vector"])
        n_setup = len(sems)
        ring = Ring(banks, sem)
        in_ready = Counted(sem("e_inputs_ready"))
        mv_ready = Counted(sem("e_moments_ready"))
        rstd_ready = Counted(sem("e_roots_ready"))
        y_ready = Counted(sem("e_y_ready"))
        stored = Counted(sem("e_stored"))
        dve_chain = sem("e_dve_chain")
        pool_chain = sem("e_pool_chain")
        first, last = sems[n_setup].num, sems[-1].num
        loads = [(wr[:], A["L1_ffn_router_weight"])] + [
            (w1[:, e, :], A["L1_ffn_moe_w1"][e]) for e in range(NE)
        ] + [
            (w2[:, e], A["L1_ffn_moe_w2"][e].rearrange("(c p) n -> p c n", p=P)) for e in range(NE)
        ]

        block = ctx.enter_context(nc.Block())

        @block.tensor
        def _(pe):
            pe.wait_ge(loaded, 16 * len(loads))
            for c in range(TC):
                mm = pe.matmul(banks[0][:, c * NE:(c + 1) * NE], hT_all[:, c, :], wr[:], start=True, stop=True)
            mm.then_inc(logits_ready, 1)
            pe.wait_ge(step, 3)
            pe.wait_ge(before_ready, 1)
            pe.matmul(banks[1][:, 0:NE], before[:], total[:], start=True, stop=True).then_inc(step, 1)
            pe.wait_ge(ready, 3)

            def up(u, e):
                for c in range(FC):
                    ps = ring.open(pe, "up", u, e, c)
                    pe.matmul(ps[:], w1[:, e, c * P:(c + 1) * P], hT[u % 2][:], start=True, stop=True)\
                        .then_inc(ring.filled("up", u, e, c), 1)

            def down(u, e):
                b = e % 2
                for c in range(FC):
                    ring.wait_read(pe, "up", u, e, c)
                ps = ring.open(pe, "down", u, e)
                for t in range(TG):
                    for c in range(FC):
                        mm = pe.matmul(ps[:, t * P:(t + 1) * P], hid[b][:, c, t * P:(t + 1) * P], w2[:, e, c, :],
                                       start=(c == 0), stop=(c == FC - 1))
                mm.then_inc(ring.filled("down", u, e), 1)

            with pe.Fori(0, NG // U) as it:
                for n in range(U * NE + 1):
                    if n < U * NE:
                        if n % NE == 0:
                            pe.wait_ge(*in_ready.at(2 * (n // NE + 1)))
                        up(n // NE, n % NE)
                    if n >= 1:
                        down((n - 1) // NE, (n - 1) % NE)
                meet.join(pe, "tensor")

        @block.scalar
        def _(act):
            act.wait_ge(step, 1)
            act.activation(prob[:], prob[:], ACT.Exp).then_inc(step, 1)
            act.wait_ge(ready, 3)
            with act.Fori(0, NG // U) as it:
                for n in range(U * NE):
                    u, e = n // NE, n % NE
                    if n >= 2:
                        ring.wait(act, "down", (n - 2) // NE, (n - 2) % NE)
                    for c in range(FC):
                        ps = ring.wait(act, "up", u, e, c)
                        act.activation(hid[e % 2][:, c, :], ps[:], ACT.Gelu).then_inc(ring.read("up", u, e, c), 1)
                meet.join(act, "scalar")

        @block.vector
        def _(dve):
            chain = Chain(dve, dve_setup)

            def wide(a):
                return a.unsqueeze(2).broadcast_to([P, TC, NE])

            dve.wait_ge(logits_ready, 1)
            l = banks[0][:, 0:TC * NE].rearrange("p (c e) -> p c e", e=NE)
            chain(dve.tensor_reduce(small[:, 0, :], l, AX.X, ALU.max))
            dve.tensor_tensor(prob[:], l, wide(small[:, 0, :]), ALU.subtract).then_inc(step, 1)
            dve.wait_ge(step, 2)
            chain(dve.tensor_reduce(small[:, 1, :], prob[:], AX.X, ALU.add))
            chain(dve.reciprocal(small[:, 2, :], small[:, 1, :]))
            chain(dve.tensor_tensor(prob[:], prob[:], wide(small[:, 2, :]), ALU.mult))
            dve.wait_ge(rev_ready, 1)
            chain(dve.tensor_copy(rev[:], rev_i[:]))
            rest, pick, chosen, spare = (w[:] for w in work)
            src = prob[:]
            for k in range(2):
                chain(dve.tensor_reduce(small[:, 3 + k, :], src, AX.X, ALU.max))
                chain(dve.tensor_tensor(pick, src, wide(small[:, 3 + k, :]), ALU.is_equal))
                chain(dve.tensor_tensor(pick, pick, rev[:], ALU.mult))
                chain(dve.tensor_reduce(small[:, 5, :], pick, AX.X, ALU.max))
                if k == 0:
                    chain(dve.tensor_tensor(chosen, pick, wide(small[:, 5, :]), ALU.is_equal))
                    chain(dve.scalar_tensor_tensor(rest, chosen, -2.0, prob[:], ALU.mult, ALU.add))
                    src = rest
                else:
                    chain(dve.tensor_tensor(pick, pick, wide(small[:, 5, :]), ALU.is_equal))
                    chain(dve.tensor_tensor(chosen, chosen, pick, ALU.add))
            dve.tensor_reduce(total[:], chosen.rearrange("p c e -> p e c"), AX.X, ALU.add).then_inc(step, 1)
            a, b = rest, pick
            chain(dve.tensor_copy(a, chosen))
            k = 1
            while k < TC:
                chain(dve.tensor_copy(b[:, 0:k], a[:, 0:k]))
                chain(dve.tensor_tensor(b[:, k:TC], a[:, k:TC], a[:, 0:TC - k], ALU.add))
                a, b = b, a
                k *= 2
            chain(dve.tensor_tensor(b, a, chosen, ALU.subtract))
            dve.wait_ge(step, 4)
            chain(dve.tensor_copy(total[:], banks[1][:, 0:NE]))
            chain(dve.tensor_tensor(b, b, total[:].unsqueeze(1).broadcast_to([P, TC, NE]), ALU.add))
            chain(dve.tensor_scalar(b, b, CAP - 0.5, None, ALU.is_le))
            chain(dve.tensor_tensor(b, b, chosen, ALU.mult))
            chain(dve.tensor_tensor(small[:, 0, :], small[:, 3, :], small[:, 4, :], ALU.add))
            chain(dve.reciprocal(small[:, 1, :], small[:, 0, :]))
            chain(dve.tensor_tensor(wts[:], prob[:], wide(small[:, 1, :]), ALU.mult))
            chain(dve.tensor_tensor(wts[:], wts[:], b, ALU.mult))
            dve.sem_inc(ready, 1)
            dve.wait_ge(ready, 3)

            def finish(u):
                s = u % 2
                for t in range(TG):
                    chain(dve.bn_stats(stats[s][:, t, :], r[s][:, t, :]))
                for t in range(TG):
                    dve.bn_aggr(mv[s][:, t, :], stats[s][:, t, :]).then_inc(mv_ready.sem, 1)
                dve.wait_ge(*rstd_ready.at(u + 1))
                for t in range(TG):
                    dve.tensor_scalar(y[s][:, t, :], r[s][:, t, :], mv[s][:, t, 0:1], rstd[s][:, TG + t:TG + t + 1],
                                      ALU.subtract, ALU.mult).then_inc(y_ready.sem, 1)

            with dve.Fori(0, NG // U) as it:
                chain = Chain(dve, dve_chain)
                for u in range(U):
                    tiles = bass.ds((it * U + u) * TG, TG)
                    dve.tensor_copy(hT[u][:], hT_all[:, tiles, :].rearrange("p t n -> p (t n)")).then_inc(in_ready.sem, 1)
                    dve.tensor_copy(wg[u][:], wts[:, tiles, :])
                    dve.tensor_copy(r[u][:], acc_all[:, tiles, :]).then_inc(in_ready.sem, 1)
                dve.wait_ge(*in_ready.at(2 * U))
                for u in range(U):
                    for e in range(NE):
                        ps = ring.wait(dve, "down", u, e)
                        for t in range(TG):
                            ins = dve.scalar_tensor_tensor(r[u][:, t, :], ps[:, t * P:(t + 1) * P], wg[u][:, t, e:e + 1],
                                                           r[u][:, t, :], ALU.mult, ALU.add)
                        ins.then_inc(ring.read("down", u, e), 1)
                        ring.wait_read(dve, "down", u, e)
                    finish(u)
                meet.join(dve, "vector")

        @block.gpsimd
        def _(pool):
            pool.iota(rev_i[:], pattern=[[0, TC], [-1, NE]], base=NE, channel_multiplier=0).then_inc(rev_ready, 1)
            pool.memset(before[:], 1.0).then_inc(pool_setup, 1)
            pool.wait_ge(pool_setup, 1)
            pool.affine_select(out=before[:], in_=before[:], compare_op=ALU.is_ge, fill=0.0, base=-1,
                               pattern=[[1, P]], channel_multiplier=-1).then_inc(before_ready, 1)
            pool.sem_inc(ready, 1)
            pool.wait_ge(ready, 3)
            with pool.Fori(0, NG // U) as it:
                chain = Chain(pool, pool_chain)
                for u in range(U):
                    pool.wait_ge(*mv_ready.at(TG * (u + 1)))
                    chain(pool.tensor_scalar(rstd[u][:, 0:TG], mv[u][:, :, 1], LN_EPS, None, ALU.add))
                    pool.tensor_tensor(rstd[u][:, TG:2 * TG], rstd[u][:, 0:TG], K["eps_half"][:, 0:TG], ALU.pow)\
                        .then_inc(rstd_ready.sem, 1)
                meet.lead(pool, first, last)
            pool.sem_clear(range(FIRST_SEM, meet.arrived.num))

        @block.sync
        def _(sy):
            for dst, src in loads:
                sy.dma_start(dst, src).then_inc(loaded, 16)
            sy.sem_inc(ready, 1)
            xo = out.rearrange("b n d -> (b n) d").rearrange("(p g t) d -> g p t d", p=P, t=TG)
            with sy.Fori(0, NG // U) as it:
                for u in range(U):
                    sy.wait_ge(*y_ready.at(TG * (u + 1)))
                    sy.dma_start(xo[it * U + u], y[u][:]).then_inc(stored.sem, 16)
                sy.wait_ge(*stored.at(16 * U))
                meet.join(sy, "sync")


def kernel(**inputs):
    import concourse.bacc as bacc
    from concourse.bass_utils import run_bass_kernel_spmd

    nc = bacc.Bacc("TRN2", target_bir_lowering=False, num_devices=1)
    arrays, A = {}, {}
    for name, a in inputs.items():
        a = np.ascontiguousarray(a)
        arrays[f"in_{name}_dram"] = a
        A[name] = nc.dram_tensor(f"in_{name}_dram", a.shape, mybir.dt.from_np(a.dtype), kind="ExternalInput").ap()
    out = nc.dram_tensor("out_0_dram", (B, N, D), F32, kind="ExternalOutput").ap()
    build(nc, A, out)
    r = run_bass_kernel_spmd(nc, [arrays], core_ids=[0])
    return r.results[0]["out_0_dram"]
```

```python
from contextlib import ExitStack
import math

import numpy as np
import concourse.bass as bass
from concourse import mybir

F32 = mybir.dt.float32
F32R = mybir.dt.float32r
BF16 = mybir.dt.bfloat16
I32 = mybir.dt.int32
ALU = mybir.AluOpType
ACT = mybir.ActivationFunctionType
AX = mybir.AxisListType

P = 128
B, N, D = 16, 256, 128
NT = N // P
S_CTX = 64
LN_EPS = 1e-5
FIRST_SEM = 100

H0, DH0 = 16, 8
NS = 64
STD, SPLAT = 0.6, 0.4
GROUPS = H0 // 4


class Counted:

    def __init__(self, sem):
        self.sem = sem

    def at(self, n):
        return self.sem, n


class Ring:

    def __init__(self, banks, sem):
        self.banks = banks
        self.full = [sem(f"bank{i}_full") for i in range(len(banks))]
        self.free = [sem(f"bank{i}_free") for i in range(len(banks))]
        self.uses = [0] * len(banks)
        self.turn = 0
        self.jobs = {}

    def open(self, pe, *name):
        i = self.turn
        self.turn = (i + 1) % len(self.banks)
        assert name not in self.jobs, name
        if self.uses[i]:
            pe.wait_ge(self.free[i], self.uses[i])
        self.uses[i] += 1
        self.jobs[name] = (i, self.uses[i])
        return self.banks[i]

    def filled(self, *name):
        return self.full[self.jobs[name][0]]

    def wait(self, eng, *name):
        i, n = self.jobs[name]
        eng.wait_ge(self.full[i], n)
        return self.banks[i]

    def wait_read(self, eng, *name):
        i, n = self.jobs[name]
        eng.wait_ge(self.free[i], n)

    def bank(self, *name):
        return self.banks[self.jobs[name][0]]

    def read(self, *name):
        return self.free[self.jobs[name][0]]


class Chain:

    def __init__(self, eng, sem):
        self.eng, self.sem, self.n = eng, sem, 0

    def __call__(self, ins):
        self.n += 1
        ins.then_inc(self.sem, 1)
        self.eng.wait_ge(self.sem, self.n)


def run_steps(stages, per_item, items, drain, steps, pipeline_step):
    for g in range(min(o for o, _ in stages), per_item * (items - 1) + max(o for o, _ in stages) + 1):
        if 0 <= g < per_item * items + drain:
            pipeline_step(g)
        for offset, name in sorted(stages, key=lambda stage: -stage[0]):
            u, rest = divmod(g - offset, per_item)
            if rest == 0 and 0 <= u < items and name in steps:
                steps[name](u)


class Sets:

    def __init__(self, items):
        self.items = items

    def __getitem__(self, u):
        return self.items[u % len(self.items)]


def row(v):
    return v.rearrange("(a n) -> a n", a=1)


def col(v):
    return v.rearrange("(n a) -> n a", a=1)


def build(nc, A, out):
    x_mid = nc.dram_tensor("x_mid", [B, N, D], F32, kind="Internal").ap()
    x_mid2 = nc.dram_tensor("x_mid2", [B, N, D], F32, kind="Internal").ap()
    with ExitStack() as ctx:
        def sb(name, shape, dt=F32):
            return ctx.enter_context(nc.sbuf_tensor(name, shape, dt))

        K = {}
        K["ident"] = sb("ident", [P, P])
        K["ones_row"] = sb("ones_row", [1, P])
        K["eps_half"] = sb("minus_half", [P, 64])
        K["split"] = sb("split_rows", [P, 2])
        K["thr"] = sb("thresholds", [P, 8], I32)
        K["w1"] = sb("ffn_w1", [P, 512])
        K["w2"] = sb("ffn_w2", [P, 4, P])
        K["b1"] = sb("ffn_b1", [P, 4])
        K["b2c"] = sb("ffn_b2_col", [P, 1])
        loop_1(nc, A, K, x_mid)
        loop_2(nc, A, K, x_mid, x_mid2)
        phase_3(nc, A, K, x_mid2, out)




class Meeting:

    def __init__(self, sem, names):
        self.arrived = sem("engines_arrived")
        self.go = {n: sem(f"{n}_may_go_on") for n in names}

    def join(self, eng, name):
        eng.drain().then_inc(self.arrived, 1)
        eng.wait_ge(self.go[name], 1)
        eng.sem_inc(self.go[name], -1)

    def lead(self, pool, first, last):
        pool.drain().then_inc(self.arrived, 1)
        pool.wait_ge(self.arrived, len(self.go) + 1)
        pool.sem_clear(range(first, last + 1))
        pool.sem_clear(self.arrived)
        for s in self.go.values():
            pool.sem_inc(s, 1)


def loop_1(nc, A, K, x_mid):
    U = 8
    with ExitStack() as ctx:
        def sb(name, shape, dt=F32):
            return ctx.enter_context(nc.sbuf_tensor(name, shape, dt))

        sems = []

        def sem(name):
            s = ctx.enter_context(nc.semaphore(name, num=FIRST_SEM + len(sems)))
            sems.append(s)
            return s

        ident, ones_row = K["ident"], K["ones_row"]
        wq = sb("wq_pad", [P, GROUPS, 4, 32])
        wk = sb("wk_pad", [P, GROUPS, 4, 32])
        split_i = sb("split_iota", [P, 2], I32)
        split = K["split"]
        wv = sb("wv", [P, D])
        wg = sb("wg", [P, D])
        bg = sb("bg", [P, 2])
        wo_pad = sb("wo_pad", [P, GROUPS, D])
        wo = sb("wo", [P, D])
        we = sb("we", [P, 64])
        be = sb("be", [P, 1])
        wt = sb("wt", [P, NS // 2, 64])
        bt_raw = sb("bt_raw", [NS, 64])
        bt = sb("bt_T", [64, NS])
        wd = sb("wd_aug", [65, D])
        sp_raw = sb("splat_raw", [NS, D])
        sp = sb("splat_T", [P, NS])
        sp_sq = sb("splat_sq", [NS, D])
        s2 = sb("splat_norm", [NS, 1])
        scl = sb("splat_scale", [NS, 4])
        imp = sb("splat_imp", [NS, 2])
        ones64 = sb("ones64", [P, 64])
        wv_raw = sb("xwv_raw", [P, D])
        wo_raw = sb("xwo_raw", [P, D])
        wv_x = sb("xwv_T", [P, D])
        wo_x = sb("xwo_T", [P, D])
        bv_x = sb("xbv", [P, 1])
        bo_x = sb("xbo", [1, D])
        mags = sb("magnitudes", [P, 1029])
        need = sb("ranks", [P, 8])
        bit = sb("bit", [P, 1], I32)
        cand = sb("candidates", [P, 8], I32)
        at_least = sb("at_least", [P, 4, 512], BF16)
        at_least_small = sb("at_least_small", [P, 16])
        small_counts = sb("small_counts", [P, 4])
        ones_bf = sb("ones_bf", [P, P], BF16)
        ones_sq = sb("ones_sq", [P, P])
        counts = sb("counts", [P, 8])
        keep = sb("keep", [P, 8], I32)
        def two(name, shape, dt=F32):
            return Sets([sb(f"{name}{i}", shape, dt) for i in range(2)])

        SETS = 3
        x = Sets([sb(f"x{i}", [P, NT, D]) for i in range(SETS)])
        c = Sets([sb(f"c{i}", [S_CTX, D]) for i in range(SETS)])
        xT = two("xT", [P, N])
        xsqT = two("xsqT", [P, N])
        rounded = two("qk_rounded", [P, 2 * N], F32R)
        qT = two("qT", [P, GROUPS, N], F32R)
        kT = two("kT", [P, GROUPS, N], F32R)
        v = two("v", [P, NT, H0, 32])
        gate = two("gateT", [P, N])
        d2 = two("d2", [NS, N])
        infl = two("infl", [NS, N])
        infl_n = two("infl_n", [NS, N])
        total = two("total", [NS, 2])
        infl_tm = two("infl_tm", [P, NT, NS])
        gath = two("gath", [P, NS])
        enc = two("enc", [P, NS // 2, 2])
        trans = two("trans", [65, NS])
        dec = two("dec", [NS, D])
        cT = two("cT", [P, S_CTX])
        vx = two("vx", [P, N])
        vsum = two("vsum", [P, 2])
        oT = two("oT", [P, GROUPS, N])
        flowg = two("flowg", [P, N])
        r = two("r", [P, NT, D])
        stats = two("stats", [P, NT, 6])
        mv = two("mv", [P, NT, 2])
        rstd = two("rstd", [P, 2 * NT])
        NP_ = 8
        probs = sb("probs", [P, NP_, NT, N])
        pT = sb("pT", [P, NP_, 2, NT, P])
        negmax = sb("negmax", [P, 2, H0, NT])
        sums = sb("sums", [P, 2, H0, NT])
        rsums = sb("rsums", [P, 2, H0, NT])

        banks = [ctx.enter_context(nc.psum_tensor(f"ps{i}", [P, 512], F32)) for i in range(6)]
        o_banks = [ctx.enter_context(nc.psum_tensor(f"po{i}", [P, 2, N], F32)) for i in range(2)]

        loaded = sem("weights_loaded")
        cleared = sem("weights_cleared")
        pool_ready = sem("pool_constants")
        wT_ps = sem("weights_transposed")
        wT_ready = sem("weights_T_ready")
        dve_setup = sem("dve_setup")
        pool_setup = sem("pool_setup")
        act_setup = sem("act_setup")
        setup_done = sem("setup_done")
        meet = Meeting(sem, ["sync", "scalar", "tensor", "vector"])
        n_setup = len(sems)
        ring = Ring(banks, sem)
        x_loaded = [Counted(sem(f"x{i}_loaded")) for i in range(SETS)]
        stored = [Counted(sem(f"x{i}_stored")) for i in range(SETS)]
        negmax_ready = Counted(sem("negmax_ready"))
        rounded_ready = Counted(sem("rounded_ready"))
        oT_ready = Counted(sem("oT_ready"))
        probs_ready = Counted(sem("probs_normalised"))
        rsums_ready = Counted(sem("rsums_ready"))
        pv_done = Counted(sem("pv_done"))
        infl0_ready = Counted(sem("influence_exp"))
        infl_ready = Counted(sem("influence_ready"))
        vx_ready = Counted(sem("vx_ready"))
        mv_ready = Counted(sem("ln_stats_ready"))
        rstd_ready = Counted(sem("rstd_ready"))
        x_ready = Counted(sem("x_ready"))
        cand_ready = Counted(sem("candidates_ready"))
        mask_ready = Counted(sem("masks_ready"))
        small_ready = Counted(sem("small_ready"))
        dve_chain = sem("vector_chain")
        pool_chain = sem("pool_chain")
        first, last = sems[n_setup].num, sems[-1].num

        loads = [
            (w[:, :, :, DH0 * i:DH0 * (i + 1)], A[name].rearrange("k (g j d) -> k g j d", g=GROUPS, j=4))
            for i in range(3) for w, name in ((wq, "L0_attn_Wq"), (wk, "L0_attn_Wk"))
        ] + [
            (wv[:], A["L0_attn_Wv"]), (wg[:], A["L0_attn_Wg"]), (bg[:, 0:1], col(A["L0_attn_bg"])),
            (wo[:], A["L0_attn_Wo"]),
        ] + [
            (wo_pad[32 * j:32 * j + DH0], A["L0_attn_Wo"].rearrange("(g j d) n -> j d g n", g=GROUPS, j=4)[j])
            for j in range(4)
        ] + [
            (we[:], A["L0_attn_We"]), (be[0:64, :], col(A["L0_attn_be"])), (be[64:128, :], col(A["L0_attn_be"])),
            (wt[0:64], A["L0_attn_Wt"].rearrange("(j h) d e -> h d j e", h=2)[0]),
            (wt[64:128], A["L0_attn_Wt"].rearrange("(j h) d e -> h d j e", h=2)[1]),
            (bt_raw[:], A["L0_attn_bt"]), (wd[0:64], A["L0_attn_Wd"]), (wd[64:65], row(A["L0_attn_bd"])),
            (sp_raw[:], A["L0_attn_splat_positions"]),
            (scl[:, 0:1], col(A["L0_attn_splat_scales"])), (imp[:, 0:1], col(A["L0_attn_splat_importance"])),
            (wv_raw[:], A["L0_xattn_Wv"]), (wo_raw[:], A["L0_xattn_Wo"]),
            (bv_x[:], col(A["L0_xattn_bv"])), (bo_x[:], row(A["L0_xattn_bo"])),
            (K["w1"][:], A["L0_ffn_W1"]), (K["w2"][:], A["L0_ffn_W2"].rearrange("(c p) n -> p c n", p=P)),
            (K["b1"][:], A["L0_ffn_b1"].rearrange("(c p) -> p c", p=P)), (K["b2c"][:], col(A["L0_ffn_b2"])),
        ]
        n1, n2 = 512 * D, D
        sizes = [n1, n1, 512, n2]
        ranks = []
        for n in sizes:
            k = max(1, int(n * 0.1 / 2))
            ranks += [k, n - k + 1]

        stages = [
            (-11, "project"), (0, "candidates0"), (0, "masks0"), (1, "distances"), (2, "cross_values"),
            (2, "read_distances"), (2, "gate"), (3, "count0"), (3, "read_cross"), (3, "influence"),
            (4, "influence_tm"), (4, "decide0"), (5, "read_influence_tm"), (6, "gather"), (6, "candidates1"),
            (6, "masks1"), (7, "read_gather"), (8, "encode"), (9, "read_encode"), (9, "count1"), (10, "transform"),
            (10, "decide1"), (11, "read_transform"), (12, "decode"), (13, "out_T0"), (13, "read_decode"),
            (14, "flow"), (15, "read_flow"), (20, "out_T1"), (21, "project_out"), (23, "norm0"), (24, "cross_out"),
            (26, "norm1"),
        ]

        block = ctx.enter_context(nc.Block())

        @block.tensor
        def _(pe):
            pe.wait_ge(loaded, 16 * len(loads))
            pe.wait_ge(pool_ready, 1)
            t_ps = banks[0]
            pe.transpose(t_ps[:, 0:P], wv_raw[:], ident[:])
            pe.transpose(t_ps[:, P:2 * P], wo_raw[:], ident[:])
            pe.transpose(t_ps[:, 256:256 + NS], sp_raw[:], ident[0:NS, 0:NS])
            pe.transpose(t_ps[0:64, 320:320 + NS], bt_raw[:], ident[0:NS, 0:NS]).then_inc(wT_ps, 1)
            pe.wait_ge(setup_done, 3)

            def project(u):
                s = u
                pe.wait_ge(*x_loaded[u % SETS].at(32 * (u // SETS + 1)))
                ps = ring.open(pe, "xT", u)
                for t in range(NT):
                    pe.transpose(ps[:, t * P:(t + 1) * P], x[s][:, t, :], ident[:])
                pe.transpose(ps[:, 256:256 + S_CTX], c[s][:], ident[0:S_CTX, 0:S_CTX]).then_inc(ring.filled("xT", u), 1)
                ring.wait_read(pe, "xT", u)
                for name, w in (("q", wq), ("k", wk)):
                    for half in range(2):
                        ps = ring.open(pe, name, u, half)
                        for g in range(2):
                            mm = pe.matmul(ps[:, g * N:(g + 1) * N],
                                           w[:, 2 * half + g, :, :].rearrange("p j d -> p (j d)"), xT[s][:],
                                           start=True, stop=True)
                        mm.then_inc(ring.filled(name, u, half), 1)
                ps = ring.open(pe, "vg", u)
                for t in range(NT):
                    pe.matmul(ps[:, t * P:(t + 1) * P], xT[s][:, t * P:(t + 1) * P], wv[:], start=True, stop=True)
                pe.matmul(ps[:, N:2 * N], wg[:], xT[s][:], start=True, stop=True).then_inc(ring.filled("vg", u), 1)

            def distances(u):
                s = u
                ps = ring.open(pe, "d2", u)
                pe.matmul(ps[0:NS, 0:N], sp[:], xT[s][:], start=True, stop=False)
                pe.matmul(ps[0:NS, 0:N], ones64[:], xsqT[s][:], start=False, stop=True).then_inc(ring.filled("d2", u), 1)

            def cross_values(u):
                s = u
                ps = ring.open(pe, "vx", u)
                pe.matmul(ps[:, 0:S_CTX], wv_x[:], cT[s][:], start=True, stop=True).then_inc(ring.filled("vx", u), 1)

            def influence_tm(u):
                s = u
                pe.wait_ge(*infl_ready.at(u + 1))
                ps = ring.open(pe, "infl_tm", u)
                for t in range(NT):
                    mm = pe.transpose(ps[:, t * NS:(t + 1) * NS], infl_n[s][:, t * P:(t + 1) * P], ident[0:NS, 0:NS])
                mm.then_inc(ring.filled("infl_tm", u), 1)

            def gather(u):
                s = u
                ring.wait_read(pe, "infl_tm", u)
                ps = ring.open(pe, "gath", u)
                for t in range(NT):
                    mm = pe.matmul(ps[:, 0:NS], x[s][:, t, :], infl_tm[s][:, t, :], start=(t == 0), stop=(t == NT - 1))
                mm.then_inc(ring.filled("gath", u), 1)

            def encode(u):
                s = u
                ring.wait_read(pe, "gath", u)
                ps = ring.open(pe, "enc", u)
                for h in range(2):
                    mm = pe.matmul(ps[64 * h:64 * h + 64, 0:NS // 2], we[:], gath[s][:, h:NS:2], start=True, stop=True)
                mm.then_inc(ring.filled("enc", u), 1)

            def transform(u):
                s = u
                ring.wait_read(pe, "enc", u)
                ps = ring.open(pe, "trans", u)
                for j in range(NS // 2):
                    mm = pe.matmul(ps[0:64, 2 * j:2 * j + 2], wt[:, j, :], enc[s][:, j, :], start=True, stop=True)
                mm.then_inc(ring.filled("trans", u), 1)

            def decode(u):
                s = u
                ring.wait_read(pe, "trans", u)
                ps = ring.open(pe, "dec", u)
                pe.matmul(ps[0:NS, 0:D], trans[s][:], wd[:], start=True, stop=True).then_inc(ring.filled("dec", u), 1)

            def count(n):
                pe.wait_ge(*mask_ready.at(4 * (n + 1)))
                pe.wait_ge(*small_ready.at(4 * (n + 1)))
                ps = ring.open(pe, "count", n)
                for a in range(4):
                    for q in range(8):
                        pe.matmul(ps[:, a * 64:(a + 1) * 64], ones_bf[:], at_least[:, a, q * 64:(q + 1) * 64],
                                  start=(q == 0), stop=(q == 7))
                pe.matmul(ps[:, 256:260], ones_sq[:], small_counts[:], start=True, stop=True)\
                    .then_inc(ring.filled("count", n), 1)

            def flow(u):
                s = u
                ring.wait_read(pe, "dec", u)
                ps = ring.open(pe, "flow", u)
                pe.matmul(ps[:, 0:N], dec[s][:], infl[s][:], start=True, stop=True).then_inc(ring.filled("flow", u), 1)

            def project_out(u):
                s = u
                pe.wait_ge(*oT_ready.at(2 * (u + 1)))
                ring.wait_read(pe, "flow", u)
                ps = ring.open(pe, "y", u)
                for t in range(NT):
                    for g in range(GROUPS):
                        pe.matmul(ps[:, t * D:(t + 1) * D], oT[s][:, g, t * P:(t + 1) * P], wo_pad[:, g, :],
                                  start=(g == 0), stop=False)
                    mm = pe.matmul(ps[:, t * D:(t + 1) * D], flowg[s][:, t * P:(t + 1) * P], wo[:],
                                   start=False, stop=True)
                mm.then_inc(ring.filled("y", u), 1)

            def cross_out(u):
                s = u
                pe.wait_ge(*vx_ready.at(u + 1))
                ps = ring.open(pe, "yx", u)
                for t in range(NT):
                    pe.matmul(ps[:, t * D:(t + 1) * D], vx[s][:, t * P:(t + 1) * P], wo_x[:], start=True, stop=False)
                    mm = pe.matmul(ps[:, t * D:(t + 1) * D], ones_row[:], bo_x[:], start=False, stop=True)
                mm.then_inc(ring.filled("yx", u), 1)

            def head_step(g):
                u, h = divmod(g, H0)
                if u < U:
                    if h == 0:
                        ring.wait_read(pe, "k", u, 1)
                    q, j = h // 4, 32 * (h % 4)
                    ps = ring.open(pe, "scores", u, h)
                    for t in range(NT):
                        mm = pe.matmul(ps[:, t * N:(t + 1) * N], qT[u][j:j + 3 * DH0, q, t * P:(t + 1) * P],
                                       kT[u][j:j + 3 * DH0, q, :], start=True, stop=True)
                    mm.then_inc(ring.filled("scores", u, h), 1)
                if 4 <= g < H0 * U + 4:
                    n = g - 4
                    pe.wait_ge(*probs_ready.at(n + 1))
                    ps = ring.open(pe, "pT", n)
                    for kt in range(2):
                        for t in range(NT):
                            mm = pe.transpose(ps[:, (kt * NT + t) * P:(kt * NT + t + 1) * P],
                                              probs[:, n % NP_, t, kt * P:(kt + 1) * P], ident[:])
                    mm.then_inc(ring.filled("pT", n), 1)
                if g >= 5:
                    n = g - 5
                    u, h = divmod(n, H0)
                    q, j = h // 4, 32 * (h % 4)
                    if h == 0:
                        ring.wait_read(pe, "vg", u)
                    if u >= 1 and h % 8 == 0:
                        pe.wait_ge(*oT_ready.at(2 * (u - 1) + h // 8 + 1))
                    ring.wait_read(pe, "pT", n)
                    for kt in range(2):
                        mm = pe.matmul(o_banks[q // 2][j:j + 32, q % 2, :], v[u][:, kt, h, :],
                                       pT[:, n % NP_, kt].rearrange("p t n -> p (t n)"),
                                       start=(kt == 0), stop=(kt == 1))
                    mm.then_inc(pv_done.sem, 1)

            steps = dict(project=project, distances=distances, cross_values=cross_values,
                         count0=lambda u: count(2 * u), influence_tm=influence_tm, gather=gather, encode=encode,
                         count1=lambda u: count(2 * u + 1), transform=transform, decode=decode, flow=flow,
                         project_out=project_out, cross_out=cross_out)
            with pe.Fori(0, B // U) as it:
                run_steps(stages, H0, U, 5, steps, head_step)
                meet.join(pe, "tensor")

        @block.scalar
        def _(act):
            act.wait_ge(cleared, 1)
            for dst, src in loads[1::2]:
                act.dma_start(dst, src, allow_slow_non_contiguous=True).then_inc(loaded, 16)
            act.wait_ge(wT_ps, 1)
            act.activation(wv_x[:], banks[0][:, 0:P], ACT.Copy)
            act.activation(wo_x[:], banks[0][:, P:2 * P], ACT.Copy)
            act.activation(sp[:], banks[0][:, 256:256 + NS], ACT.Copy, scale=-2.0)
            act.activation(bt[:], banks[0][0:64, 320:320 + NS], ACT.Copy).then_inc(setup_done, 1)
            act.wait_ge(setup_done, 3)

            def project(u):
                s = u
                ps = ring.wait(act, "xT", u)
                act.activation(xT[s][:], ps[:, 0:N], ACT.Copy)
                act.activation(xsqT[s][:], ps[:, 0:N], ACT.Square)
                act.activation(cT[s][:], ps[:, 256:256 + S_CTX], ACT.Copy).then_inc(ring.read("xT", u), 1)
                halves = [("q", 0), ("q", 1), ("k", 0), ("k", 1)]
                for i, (name, half) in enumerate(halves):
                    ps = ring.wait(act, name, u, half)
                    if i >= 2:
                        ring.wait_read(act, halves[i - 2][0], u, halves[i - 2][1])
                    act.activation(rounded[i][:], ps[:], ACT.Copy).then_inc(rounded_ready.sem, 1)
                ps = ring.wait(act, "vg", u)
                for t in range(NT):
                    act.activation(v[s][:, t, :, 0:DH0],
                                   ps[:, t * P:(t + 1) * P].rearrange("p (h d) -> p h d", h=H0), ACT.Copy)
                act.activation(gate[s][:], ps[:, N:2 * N], ACT.Exp, bias=bg[:, 1:2], scale=-1.0).then_inc(ring.read("vg", u), 1)

            def influence(u):
                s = u
                ring.wait_read(act, "d2", u)
                act.activation(d2[s][:], d2[s][:], ACT.Exp, scale=scl[:, 3:4]).then_inc(infl0_ready.sem, 1)

            def influence_tm(u):
                s = u
                ps = ring.wait(act, "infl_tm", u)
                act.activation(infl_tm[s][:].rearrange("p t n -> p (t n)"), ps[:, 0:NT * NS], ACT.Copy)\
                    .then_inc(ring.read("infl_tm", u), 1)

            def gather(u):
                s = u
                ps = ring.wait(act, "gath", u)
                act.activation(gath[s][:], ps[:, 0:NS], ACT.Copy).then_inc(ring.read("gath", u), 1)

            def encode(u):
                s = u
                ps = ring.wait(act, "enc", u)
                for h in range(2):
                    ins = act.activation(enc[s][64 * h:64 * h + 64, :, h], ps[64 * h:64 * h + 64, 0:NS // 2], ACT.Relu,
                                         bias=be[64 * h:64 * h + 64, :])
                ins.then_inc(ring.read("enc", u), 1)

            def decode(u):
                s = u
                ps = ring.wait(act, "dec", u)
                act.activation(dec[s][:], ps[0:NS, 0:D], ACT.Copy).then_inc(ring.read("dec", u), 1)

            def out_T(u, i):
                act.wait_ge(*pv_done.at(H0 * u + 8 * (i + 1)))
                act.activation(oT[u][:, 2 * i:2 * i + 2, :], o_banks[i][:], ACT.Copy).then_inc(oT_ready.sem, 1)

            def head_step(g):
                u, h = divmod(g, H0)
                if u < U:
                    act.wait_ge(*negmax_ready.at(g + 1))
                    if g >= NP_:
                        ring.wait(act, "pT", g - NP_)
                    ps = ring.bank("scores", u, h)
                    for t in range(NT):
                        ins = act.activation(probs[:, g % NP_, t, :], ps[:, t * N:(t + 1) * N], ACT.Exp,
                                             bias=negmax[:, u % 2, h, t:t + 1], accum_out=sums[:, u % 2, h, t:t + 1])
                    ins.then_inc(ring.read("scores", u, h), 1)

            steps = dict(project=project, influence=influence, read_influence_tm=influence_tm, read_gather=gather,
                         read_encode=encode, read_decode=decode, out_T0=lambda u: out_T(u, 0),
                         out_T1=lambda u: out_T(u, 1))
            with act.Fori(0, B // U) as it:
                run_steps(stages, H0, U, 5, steps, head_step)
                meet.join(act, "scalar")

        @block.vector
        def _(dve):
            dve.memset(wq[:], 0.0)
            dve.memset(wk[:], 0.0)
            dve.memset(wo_pad[:], 0.0).then_inc(cleared, 1)
            dve.memset(ones_row[:], 1.0)
            dve.memset(ones64[:], 1.0)
            dve.memset(ones_bf[:], 1.0)
            dve.memset(ones_sq[:], 1.0)
            dve.memset(K["eps_half"][:], -0.5)
            for s in range(2):
                dve.memset(v[s][:], 0.0)
                dve.memset(enc[s][:], 0.0)
                dve.memset(trans[s][:], 1.0)
            for i, k in enumerate(ranks):
                dve.memset(need[:, i:i + 1], float(k))
            dve.memset(K["thr"][:], 0)
            dve.memset(bit[:], 1 << 30)
            setup = Chain(dve, dve_setup)
            dve.wait_ge(pool_ready, 1)
            setup(dve.tensor_scalar(split_i[:, 1:2], split_i[:, 0:1], 3 * DH0, None, ALU.bitwise_and))
            setup(dve.tensor_copy(split[:], split_i[:, 1:2].broadcast_to([P, 2])))
            setup(dve.tensor_scalar(split[:, 0:1], split[:, 0:1], float(DH0), -1.0, ALU.is_equal, ALU.mult))
            setup(dve.tensor_scalar(split[:, 1:2], split[:, 1:2], float(2 * DH0), -1.0, ALU.is_equal, ALU.mult))
            dve.wait_ge(loaded, 16 * len(loads))
            setup(dve.tensor_scalar(wq[:], wq[:], DH0 ** -0.5, None, ALU.mult))
            for lo, hi, w in ((0, 512, K["w1"][:]), (512, 1024, K["w2"][:].rearrange("p c n -> p (c n)")),
                              (1024, 1028, K["b1"][:]), (1028, 1029, K["b2c"][:])):
                setup(dve.tensor_scalar(mags[:, lo:hi].bitcast(I32), w.bitcast(I32), 0x7FFFFFFF, None, ALU.bitwise_and))
            setup(dve.tensor_scalar(bg[:, 1:2], bg[:, 0:1], -1.0, None, ALU.mult))
            setup(dve.tensor_tensor(sp_sq[:], sp_raw[:], sp_raw[:], ALU.mult))
            setup(dve.tensor_reduce(s2[:], sp_sq[:], AX.X, ALU.add))
            setup(dve.tensor_scalar(scl[:, 1:2].bitcast(I32), scl[:, 0:1].bitcast(I32), 0x7FFFFFFF, None, ALU.bitwise_and))
            setup(dve.tensor_scalar(imp[:, 1:2].bitcast(I32), imp[:, 0:1].bitcast(I32), 0x7FFFFFFF, None, ALU.bitwise_and))
            setup(dve.tensor_scalar(scl[:, 1:2], scl[:, 1:2], 1e-6, None, ALU.max))
            setup(dve.tensor_tensor(scl[:, 1:2], scl[:, 1:2], scl[:, 1:2], ALU.mult))
            setup(dve.reciprocal(scl[:, 2:3], scl[:, 1:2]))
            dve.tensor_scalar(scl[:, 3:4], scl[:, 2:3], -0.5, None, ALU.mult).then_inc(setup_done, 1)
            dve.wait_ge(setup_done, 3)

            def link(ins):
                chain(ins)

            def split_qk(u):
                for i, (name, dst, half) in enumerate((("q", qT, 0), ("q", qT, 1), ("k", kT, 0), ("k", kT, 1))):
                    ps = ring.bank(name, u, half)
                    dve.wait_ge(*rounded_ready.at(4 * u + i + 1))
                    dve.scalar_tensor_tensor(dst[u][:, 2 * half:2 * half + 2, :].rearrange("p g n -> p (g n)"),
                                             rounded[i][:].bitcast(F32), split[:, i // 2:i // 2 + 1], ps[:],
                                             ALU.mult, ALU.add).then_inc(ring.read(name, u, half), 1)

            def gate_(u):
                s = u
                ring.wait_read(dve, "vg", u)
                link(dve.tensor_scalar(gate[s][:], gate[s][:], 1 / SPLAT, 1 / SPLAT, ALU.mult, ALU.add))
                link(dve.reciprocal(gate[s][:], gate[s][:]))

            def distances(u):
                s = u
                ps = ring.wait(dve, "d2", u)
                dve.tensor_scalar(d2[s][:], ps[0:NS, 0:N], s2[:], 0.0, ALU.add, ALU.max).then_inc(ring.read("d2", u), 1)

            def influence(u):
                s = u
                dve.wait_ge(*infl0_ready.at(u + 1))
                link(dve.tensor_scalar(infl[s][:], d2[s][:], imp[:, 1:2], None, ALU.mult, ALU.add,
                                       accum_out=total[s][:, 0:1]))
                link(dve.tensor_scalar(total[s][:, 1:2], total[s][:, 0:1], 1e-8, None, ALU.max))
                link(dve.reciprocal(total[s][:, 0:1], total[s][:, 1:2]))
                dve.tensor_scalar(infl_n[s][:], infl[s][:], total[s][:, 0:1], None, ALU.mult).then_inc(infl_ready.sem, 1)

            def transform(u):
                s = u
                ps = ring.wait(dve, "trans", u)
                dve.tensor_tensor(trans[s][0:64, :], ps[0:64, 0:NS], bt[:], ALU.add)\
                    .then_inc(ring.read("trans", u), 1)

            def cross_values(u):
                s = u
                ps = ring.wait(dve, "vx", u)
                dve.tensor_scalar(vx[s][:, 0:S_CTX], ps[:, 0:S_CTX], bv_x[:], None, ALU.add)\
                    .then_inc(ring.read("vx", u), 1)
                ring.wait_read(dve, "vx", u)
                link(dve.tensor_reduce(vsum[s][:, 0:1], vx[s][:, 0:S_CTX], AX.X, ALU.add))
                link(dve.tensor_scalar(vsum[s][:, 1:2], vsum[s][:, 0:1], 1.0 / S_CTX, None, ALU.mult))
                dve.tensor_copy(vx[s][:, S_CTX:N], vsum[s][:, 1:2].to_broadcast([P, N - S_CTX])).then_inc(vx_ready.sem, 1)

            def candidates(n):
                dve.wait_ge(dve_chain, chain.n)
                dve.tensor_scalar(cand[:], K["thr"][:], bit[:, 0:1], None, ALU.bitwise_or).then_inc(cand_ready.sem, 1)
                dve.wait_ge(*cand_ready.at(n + 1))
                cf = cand[:].bitcast(F32)
                for a in range(4):
                    m = mags[:, 1024:1028] if a < 2 else mags[:, 1028:1029]
                    w = 4 if a < 2 else 1
                    dve.tensor_scalar(at_least_small[:, 4 * a:4 * a + w], m, cf[:, 4 + a:5 + a], None, ALU.is_ge, ALU.add,
                                      accum_out=small_counts[:, a:a + 1]).then_inc(small_ready.sem, 1)
                for a in (2, 3):
                    dve.tensor_scalar(at_least[:, a, :], mags[:, 512 * (a // 2):512 * (a // 2) + 512],
                                      cf[:, a:a + 1], None, ALU.is_ge).then_inc(mask_ready.sem, 1)

            def decide(n):
                ps = ring.wait(dve, "count", n)
                link(dve.tensor_reduce(counts[:, 0:4], ps[:, 0:256].rearrange("p (a n) -> p a n", a=4), AX.X, ALU.add))
                dve.tensor_copy(counts[:, 4:8], ps[:, 256:260]).then_inc(ring.read("count", n), 1)
                ring.wait_read(dve, "count", n)
                link(dve.tensor_tensor(keep[:], counts[:], need[:], ALU.is_ge))
                link(dve.copy_predicated(K["thr"][:], keep[:], cand[:]))
                link(dve.tensor_scalar(bit[:], bit[:], 1, None, ALU.logical_shift_right))

            def flow(u):
                s = u
                ps = ring.wait(dve, "flow", u)
                dve.tensor_tensor(flowg[s][:], ps[:, 0:N], gate[s][:], ALU.mult).then_inc(ring.read("flow", u), 1)

            def norm_stats(u, name, n):
                s = u
                ps = ring.wait(dve, name, u)
                dve.tensor_tensor(r[s][:].rearrange("p t n -> p (t n)"), ps[:, 0:N],
                                  x[s][:].rearrange("p t n -> p (t n)"), ALU.add).then_inc(ring.read(name, u), 1)
                ring.wait_read(dve, name, u)
                for t in range(NT):
                    link(dve.bn_stats(stats[s][:, t, :], r[s][:, t, :]))
                for t in range(NT):
                    dve.bn_aggr(mv[s][:, t, :], stats[s][:, t, :]).then_inc(mv_ready.sem, 1)

            def norm_apply(u, n):
                s = u
                dve.wait_ge(*rstd_ready.at(2 * u + n + 1))
                for t in range(NT):
                    dve.tensor_scalar(x[s][:, t, :], r[s][:, t, :], mv[s][:, t, 0:1], rstd[s][:, NT + t:NT + t + 1],
                                      ALU.subtract, ALU.mult).then_inc(x_ready.sem, 1)
                dve.wait_ge(*x_ready.at(NT * (2 * u + n + 1)))

            def head_step(g):
                u, h = divmod(g, H0)
                if u < U:
                    ps = ring.wait(dve, "scores", u, h)
                    dve.tensor_reduce(negmax[:, u % 2, h, :], ps[:].rearrange("p (t n) -> p t n", t=NT), AX.X,
                                      ALU.max, negate=True).then_inc(negmax_ready.sem, 1)
                if 1 <= g < H0 * U + 1:
                    u, h = divmod(g - 1, H0)
                    ring.wait_read(dve, "scores", u, h)
                    dve.reciprocal(rsums[:, u % 2, h, :], sums[:, u % 2, h, :]).then_inc(rsums_ready.sem, 1)
                if 4 <= g < H0 * U + 4:
                    n = g - 4
                    if n >= NP_:
                        dve.wait_ge(*pv_done.at(n - NP_ + 1))
                    ps = ring.wait(dve, "pT", n)
                    dve.tensor_copy(pT[:, n % NP_].rearrange("p k t n -> p (k t n)"), ps[:]).then_inc(ring.read("pT", n), 1)

            steps = dict(project=split_qk, candidates0=lambda u: candidates(2 * u), candidates1=lambda u: candidates(2 * u + 1),
                         decide0=lambda u: decide(2 * u), decide1=lambda u: decide(2 * u + 1),
                         read_distances=distances, gate=gate_, read_cross=cross_values, influence=influence,
                         read_transform=transform, read_flow=flow,
                         project_out=lambda u: norm_stats(u, "y", 0), norm0=lambda u: norm_apply(u, 0),
                         cross_out=lambda u: norm_stats(u, "yx", 1), norm1=lambda u: norm_apply(u, 1))
            with dve.Fori(0, B // U) as it:
                chain = Chain(dve, dve_chain)
                run_steps(stages, H0, U, 5, steps, head_step)
                meet.join(dve, "vector")

        @block.gpsimd
        def _(pool):
            setup = Chain(pool, pool_setup)
            setup(pool.iota(split_i[:, 0:1], pattern=[[0, 1]], base=0, channel_multiplier=1))
            setup(pool.memset(ident[:], 0.0))
            pool.affine_select(out=ident[:], in_=ident[:], compare_op=ALU.not_equal, fill=1.0, base=0,
                               pattern=[[-1, P]], channel_multiplier=1).then_inc(pool_ready, 1)
            pool.wait_ge(pool_ready, 1)
            pool.sem_inc(setup_done, 1)
            pool.wait_ge(setup_done, 3)

            def masks(n):
                pool.wait_ge(*cand_ready.at(n + 1))
                if n:
                    ring.wait(pool, "count", n - 1)
                cf = cand[:].bitcast(F32)
                for a in (0, 1):
                    pool.tensor_scalar(at_least[:, a, :], mags[:, 512 * (a // 2):512 * (a // 2) + 512],
                                       cf[:, a:a + 1], None, ALU.is_ge).then_inc(mask_ready.sem, 1)

            def normalise(u, h):
                pool.wait_ge(*rsums_ready.at(H0 * u + h + 1))
                for t in range(NT):
                    ins = pool.tensor_scalar(probs[:, h % NP_, t, :], probs[:, h % NP_, t, :],
                                             rsums[:, u % 2, h, t:t + 1], STD, ALU.mult, ALU.mult)
                ins.then_inc(probs_ready.sem, 1)

            def roots(u, n):
                s = u
                pool.wait_ge(*mv_ready.at(NT * (2 * u + n + 1)))
                chain(pool.tensor_scalar(rstd[s][:, 0:NT], mv[s][:, :, 1], LN_EPS, None, ALU.add))
                pool.tensor_tensor(rstd[s][:, NT:2 * NT], rstd[s][:, 0:NT], K["eps_half"][:, 0:NT], ALU.pow)\
                    .then_inc(rstd_ready.sem, 1)

            def head_step(g):
                if 1 <= g < H0 * U + 1:
                    normalise(*divmod(g - 1, H0))

            steps = dict(masks0=lambda u: masks(2 * u), masks1=lambda u: masks(2 * u + 1),
                         project_out=lambda u: roots(u, 0), cross_out=lambda u: roots(u, 1))
            with pool.Fori(0, B // U) as it:
                chain = Chain(pool, pool_chain)
                run_steps(stages, H0, U, 5, steps, head_step)
                meet.lead(pool, first, last)
            pool.sem_clear(range(FIRST_SEM, meet.arrived.num))

        @block.sync
        def _(sp_eng):
            sp_eng.wait_ge(cleared, 1)
            for dst, src in loads[0::2]:
                sp_eng.dma_start(dst, src, allow_slow_non_contiguous=True).then_inc(loaded, 16)
            xin = A["x"].rearrange("b (t p) d -> b p t d", p=P)
            xout = x_mid.rearrange("b (t p) d -> b p t d", p=P)
            with sp_eng.Fori(0, B // U) as it:
                def load(u):
                    if u >= SETS:
                        sp_eng.wait_ge(*stored[u % SETS].at(16 * (u // SETS)))
                    sp_eng.dma_start(x[u][:], xin[it * U + u]).then_inc(x_loaded[u % SETS].sem, 16)
                    sp_eng.dma_start(c[u][:], A["ctx_1024"][it * U + u]).then_inc(x_loaded[u % SETS].sem, 16)

                def store(u):
                    sp_eng.wait_ge(*x_ready.at(NT * 2 * (u + 1)))
                    sp_eng.dma_start(xout[it * U + u], x[u][:]).then_inc(stored[u % SETS].sem, 16)

                for u in range(U):
                    if u >= SETS:
                        store(u - SETS)
                    load(u)
                for u in range(U - SETS, U):
                    store(u)
                for i in range(SETS):
                    sp_eng.wait_ge(*stored[i].at(16 * ((U - 1 - i) // SETS + 1)))
                meet.join(sp_eng, "sync")



def alibi_slopes(heads):
    start = 2.0 ** (-2.0 ** (-(math.log2(heads) - 3)))
    return [start * start ** i for i in range(heads)]


H1, DH1 = 16, 64
PAIRS1 = H1 // 2
NULLS = 2
QK_SCALE = 8.0
H2, DH2 = 8, 64
PAIRS2 = H2 // 2
F, FC = 512, 4
NE0 = 8
MASKED = 1e30


def loop_2(nc, A, K, x_in, x_out):
    U = 8
    slopes = alibi_slopes(H1)
    with ExitStack() as ctx:
        def sb(name, shape, dt=F32):
            return ctx.enter_context(nc.sbuf_tensor(name, shape, dt))

        sems = []

        def sem(name):
            s = ctx.enter_context(nc.semaphore(name, num=FIRST_SEM + len(sems)))
            sems.append(s)
            return s

        def two(name, shape, dt=F32):
            return Sets([sb(f"{name}{i}", shape, dt) for i in range(2)])

        def three(name, shape, dt=F32):
            return Sets([sb(f"{name}{i}", shape, dt) for i in range(SETS)])

        SETS = 4

        ident, ones_row = K["ident"], K["ones_row"]
        w1 = [K["w1"], sb("w1_perturbed", [P, F])]
        w2 = [K["w2"], sb("w2_perturbed", [P, FC, D])]
        b1 = [K["b1"], sb("b1_perturbed", [P, FC])]
        b2 = [sb("b2_row", [1, D]), sb("b2_perturbed_row", [1, D])]
        wr = sb("router", [P, NE0])
        br = sb("router_bias", [1, NE0])
        ln_f = sb("ffn_ln", [P, 2])
        ln_a = sb("attn_ln", [P, 2])
        ln_x = sb("xattn_ln", [P, 2])
        ln_c = sb("ctx_ln", [P, 2])
        wq1 = sb("wq1", [P, H1 * DH1])
        wkv1 = sb("wkv1", [P, 2 * H1 * DH1])
        wo1 = sb("wo1", [P, PAIRS1, D])
        qs = sb("q_scale2", [P, 2])
        ks = sb("k_scale2", [P, 1])
        ks_row = sb("k_scale_rows", [32, DH1])
        null_k = sb("null_k", [32, DH1])
        null_k2 = sb("null_k2", [32, 2, DH1])
        null_ss = sb("null_ss", [32, 2])
        null_blk = sb("null_blk", [P, PAIRS1, 2, NULLS])
        null_v = sb("null_v", [4, PAIRS1, P])
        w_null = sb("w_null", [P, H1, NULLS])
        dist = sb("dist", [P, H1, N])
        null_bias = sb("null_bias", [P, NT, H1, NULLS])
        iota_n = sb("iota_n", [P, NT, NULLS], I32)
        iota_nf = sb("iota_nf", [P, NT, NULLS])
        wq2 = sb("wq2", [P, H2 * DH2])
        wkv2 = sb("wkv2", [P, 2 * H2 * DH2])
        wo2 = sb("wo2", [P, PAIRS2, D])
        bo2 = sb("bo2", [1, D])
        x = three("y", [P, NT, D])
        c = three("cc", [S_CTX, D])
        xn = three("xn", [P, NT, D])
        cn = three("cn", [S_CTX, D])
        xT = three("yT", [P, N])
        hT = three("hT", [P, N])
        cnT = three("cnT", [P, S_CTX])
        r = sb("rr", [P, NT, D])
        stats = three("sstats", [P, NT, 6])
        mv = three("smv", [P, NT, 2])
        cmv = three("cmv", [S_CTX, 8])
        rstd = three("srstd", [P, 2 * NT])
        hid = sb("hidden", [P, 2, FC, N])
        mag, tier, tier2 = [hid[:, i // 2, 2 * (i % 2):2 * (i % 2) + 2, :].rearrange("p c n -> p (c n)")
                            for i in range(3)]
        lg = three("logits", [P, NT, NE0])
        pr = three("route", [P, NT, 6])
        q1T = two("q1T", [P, PAIRS1, N])
        k1T = two("k1T", [P, PAIRS1, N])
        v1 = two("v1", [P, NT, H1 * DH1])
        o1T = sb("o1T", [P, PAIRS1, N])
        sq = sb("sq", [P, 2, F])
        wq1T = sq[:].rearrange("p i (c n) -> p (i c) n", n=P)
        qn = sb("qn", [P, 4, F])
        ss = sb("ss", [P, 4, 8])
        rn = sb("rn", [P, 2, 8])
        rnq = two("rnq", [P, NT, H1])
        nneg = two("nneg", [P, NT, H1, NULLS])
        nmin = two("nmin", [P, NT, H1])
        NPR = 6
        probs = sb("probs1", [P, NPR, 2 * (N + NULLS)])

        def keys(i, w):
            return slice(N - w, N) if i == 0 else slice(N + 2 * NULLS, N + 2 * NULLS + w)

        def keys_nulls(i, w):
            return slice(N - w, N + NULLS) if i == 0 else slice(N + NULLS, N + 2 * NULLS + w)

        low = sb("low", [P, NPR, 2])
        sums = sb("sums1", [P, NPR, 2])
        rsums = sb("rsums1", [P, NPR, 2])
        pT = sb("pT1", [P, 4, 3, P])
        pnT = sb("pnT", [4, 2, N])
        q2T = sb("q2T", [P, PAIRS2, N])
        kblk = three("kblk", [P, PAIRS2, P])
        vblk = three("vblk", [P, PAIRS2, P])
        s2n = sb("s2n", [P, NT, H2, S_CTX])
        dist0 = s2n[:, 0].rearrange("p h k -> p (h k)")[:, 0:N]
        iota_i = s2n[:, 1].rearrange("p h k -> p (h k)")[:, 0:N].bitcast(I32)
        m2 = sb("m2", [P, NT, H2])
        z2 = sb("z2", [P, NT, H2])
        rz2 = sb("rz2", [P, NT, H2])
        p2T = sb("p2T", [P, PAIRS2, N])
        o2T = q2T

        banks = [ctx.enter_context(nc.psum_tensor(f"pq{i}", [P, 512], F32)) for i in range(6)]
        o_banks = [ctx.enter_context(nc.psum_tensor(f"pr{i}", [P, 512], F32)) for i in range(2)]

        loaded = sem("l2_weights_loaded")
        cleared = sem("l2_cleared")
        t_ps = sem("l2_setup_transposed")
        t_sb = sem("l2_setup_copied")
        iota_done = sem("iota_done")
        null_done = sem("null_keys_normalised")
        experts_ready = sem("perturbed_expert_ready")
        dve_setup = sem("l2_dve_setup")
        pool_setup = sem("l2_pool_setup")
        null_pow = sem("null_pow")
        ready = sem("l2_setup_ready")
        meet = Meeting(sem, ["sync", "scalar", "tensor", "vector"])
        n_setup = len(sems)
        ring = Ring(banks, sem)
        x_loaded = [Counted(sem(f"y{i}_loaded")) for i in range(SETS)]
        stored = [Counted(sem(f"y{i}_stored")) for i in range(SETS)]
        x_ready = [Counted(sem(f"y_ready{i}")) for i in range(3)]
        xn_ready = [Counted(sem(f"xn_ready{i}")) for i in range(3)]
        cn_ready = Counted(sem("cn_ready"))
        mv_ready = Counted(sem("moments_ready"))
        rstd_ready = Counted(sem("roots_ready"))
        lg_exp = Counted(sem("logits_exp"))
        qk_copied = Counted(sem("q_k_copied"))
        qn_ready = Counted(sem("q_k_normalised"))
        ss_ready = Counted(sem("square_sums_ready"))
        rn_ready = Counted(sem("norms_ready"))
        exp_done = Counted(sem("exps_done"))
        rs_ready = Counted(sem("rsums1_ready"))
        p_ready = Counted(sem("probs1_ready"))
        o1_full = Counted(sem("o1_full"))
        o1_read = Counted(sem("o1_read"))
        s2_exp = Counted(sem("s2_exp"))
        s2_inv = Counted(sem("s2_inverse_sums"))
        p2_ready = Counted(sem("p2_ready"))
        dve_chain = sem("l2_dve_chain")
        pool_chain = sem("l2_pool_chain")
        first, last = sems[n_setup].num, sems[-1].num

        nk = A["L1_attn_null_kv"].rearrange("h (n k) d -> k h n d", k=2)
        loads = [
            (b2[0][:], row(A["L0_ffn_b2"])), (wr[:], A["L0_ffn_Wr"]), (br[:], row(A["L0_ffn_br"])),
            (ln_f[:, 0:1], col(A["L0_ffn_ln_gamma"])), (ln_f[:, 1:2], col(A["L0_ffn_ln_beta"])),
            (ln_a[:, 0:1], col(A["L1_attn_norm_g"])), (ln_a[:, 1:2], col(A["L1_attn_norm_b"])),
            (ln_x[:, 0:1], col(A["L1_xattn_g1"])), (ln_x[:, 1:2], col(A["L1_xattn_b1"])),
            (ln_c[:, 0:1], col(A["L1_xattn_g2"])), (ln_c[:, 1:2], col(A["L1_xattn_b2"])),
            (wq1[:], A["L1_attn_Wq"]), (wkv1[:], A["L1_attn_Wkv"]),
            (wo1[:], A["L1_attn_Wout"].rearrange("(c p) n -> p c n", p=P)),
            (qs[0:64, 0:1], col(A["L1_attn_q_scale"])), (qs[64:128, 0:1], col(A["L1_attn_q_scale"])),
            (ks[0:64], col(A["L1_attn_k_scale"])), (ks[64:128], col(A["L1_attn_k_scale"])),
            (ks_row[:], row(A["L1_attn_k_scale"]).broadcast_to([32, DH1])),
            (wq2[:], A["L1_xattn_Wq"]), (wkv2[:], A["L1_xattn_Wkv"]),
            (wo2[:], A["L1_xattn_Wout"].rearrange("(c p) n -> p c n", p=P)),
            (bo2[:], row(A["L1_xattn_bout"])),
            (null_k[:], nk[0].rearrange("h n d -> (h n) d")),
        ] + [
            (null_v[2 * i:2 * i + 2, :, 64 * i:64 * i + 64], nk[1].rearrange("(p i) n d -> i n p d", i=2)[i])
            for i in range(2)
        ]

        stages = [
            (-12, "ffn_in"), (-12, "ctx"), (-11, "ffn_h"), (-10, "kv2"), (-10, "ffn_up0"), (-9, "ffn_up1"), (-8, "ffn_down"), (-6, "qkv_in"), (-5, "null"), (-5, "qkv_a0"), (-4, "qkv_b0"), (-3, "qkv_a1"), (-2, "qkv_b1"),
            (11, "attn_out"), (13, "x_in"), (14, "x_q"), (15, "x_scores"), (17, "x_pT"), (18, "x_pv"), (19, "x_out"),
        ]

        block = ctx.enter_context(nc.Block())

        @block.tensor
        def _(pe):
            pe.wait_ge(loaded, 16 * len(loads))
            pe.wait_ge(null_done, 1)
            for p in range(PAIRS1):
                pe.transpose(banks[p // 4][:, (p % 4) * P:(p % 4 + 1) * P], wq1[:, p * P:(p + 1) * P], ident[:])
            pe.transpose(banks[2][:, 0:32], null_k2[:].rearrange("q i d -> q (i d)"), ident[0:32, 0:32]).then_inc(t_ps, 1)
            pe.wait_ge(t_sb, 1)
            for p in range(PAIRS1):
                pe.matmul(banks[3][:, 4 * p:4 * p + 4], wq1T[:, p, :], null_blk[:, p].rearrange("q i n -> q (i n)"),
                          start=True, stop=True)
            pe.wait_ge(experts_ready, 1)
            pe.transpose(banks[3][0:1, P:2 * P], K["b2c"][:], ident[:]).then_inc(t_ps, 1)
            pe.wait_ge(ready, 4)

            def transpose_tiles(u, name, src):
                ps = ring.open(pe, name, u)
                for t in range(NT):
                    mm = pe.transpose(ps[:, t * P:(t + 1) * P], src[:, t, :], ident[:])
                mm.then_inc(ring.filled(name, u), 1)

            def ffn_in(u):
                pe.wait_ge(*x_loaded[u % SETS].at(32 * (u // SETS + 1)))
                transpose_tiles(u, "xT", x[u])

            def ffn_h(u):
                s = u
                pe.wait_ge(*xn_ready[0].at(NT * (u + 1)))
                transpose_tiles(u, "hT", xn[s])
                pe.wait_ge(*cn_ready.at(u + 1))
                ps = ring.open(pe, "cnT", u)
                pe.transpose(ps[:, 0:S_CTX], cn[u][:], ident[0:S_CTX, 0:S_CTX]).then_inc(ring.filled("cnT", u), 1)

            def kv2(u):
                s = u
                ring.wait_read(pe, "cnT", u)
                ps = ring.open(pe, "kv2", u)
                for p in range(PAIRS2):
                    pe.matmul(ps[:, p * S_CTX:(p + 1) * S_CTX], wkv2[:, p * P:(p + 1) * P], cnT[s][:], start=True, stop=True)
                for i in range(2):
                    mm = pe.matmul(ps[64 * i:64 * i + 64, 256:512],
                                   cnT[s][:], wkv2[:, H2 * DH2:].rearrange("k (p i d) -> k i p d", i=2, d=DH2)[:, i],
                                   start=True, stop=True)
                mm.then_inc(ring.filled("kv2", u), 1)

            def ffn_up(u, e):
                s = u
                ring.wait_read(pe, "xT", u)
                for half in range(2):
                    ps = ring.open(pe, "up", u, e, half)
                    for i in range(2):
                        ch = 2 * half + i
                        mm = pe.matmul(ps[:, i * N:(i + 1) * N], w1[e][:, ch * P:(ch + 1) * P], xT[s][:], start=True, stop=True)
                    mm.then_inc(ring.filled("up", u, e, half), 1)
                if e == 0:
                    ring.wait_read(pe, "hT", u)
                    ps = ring.open(pe, "logits", u)
                    for t in range(NT):
                        pe.matmul(ps[:, t * NE0:(t + 1) * NE0], hT[s][:, t * P:(t + 1) * P], wr[:], start=True, stop=False)
                        mm = pe.matmul(ps[:, t * NE0:(t + 1) * NE0], ones_row[:], br[:], start=False, stop=True)
                    mm.then_inc(ring.filled("logits", u), 1)

            def ffn_down(u):
                ps = ring.open(pe, "down", u)
                for e in range(2):
                    for half in range(2):
                        ring.wait_read(pe, "up", u, e, half)
                    for t in range(NT):
                        o = ps[:, (2 * e + t) * D:(2 * e + t + 1) * D]
                        for ch in range(FC):
                            pe.matmul(o, hid[:, e, ch, t * P:(t + 1) * P], w2[e][:, ch, :], start=(ch == 0), stop=False)
                        mm = pe.matmul(o, ones_row[:], b2[e][:], start=False, stop=True)
                mm.then_inc(ring.filled("down", u), 1)

            def qkv_in(u):
                s = u
                pe.wait_ge(*x_ready[0].at(NT * (u + 1)))
                transpose_tiles(u, "x1T", x[s])
                pe.wait_ge(*xn_ready[1].at(NT * (u + 1)))
                transpose_tiles(u, "h1T", xn[s])

            def null(u):
                s = u
                ring.wait_read(pe, "h1T", u)
                ps = ring.open(pe, "null", u)
                for t in range(NT):
                    mm = pe.matmul(ps[:, t * 32:(t + 1) * 32], hT[s][:, t * P:(t + 1) * P],
                                   w_null[:].rearrange("k h n -> k (h n)"), start=True, stop=True)
                mm.then_inc(ring.filled("null", u), 1)

            def qkv_a(u, t):
                s = u
                if t == 0:
                    ring.wait_read(pe, "x1T", u)
                for i in range(4):
                    src, w = (hT, wq1) if i < 2 else (xT, wkv1)
                    ps = ring.open(pe, "qk", u, t, i)
                    pe.matmul(ps[:], src[s][:, t * P:(t + 1) * P], w[:, (i % 2) * 512:(i % 2 + 1) * 512],
                              start=True, stop=True).then_inc(ring.filled("qk", u, t, i), 1)
                for j in range(2):
                    ps = ring.open(pe, "v", u, t, j)
                    pe.matmul(ps[:], xT[s][:, t * P:(t + 1) * P],
                              wkv1[:, H1 * DH1 + j * 512:H1 * DH1 + (j + 1) * 512], start=True, stop=True)\
                        .then_inc(ring.filled("v", u, t, j), 1)

            def qkv_b(u, t):
                for i in range(4):
                    pe.wait_ge(*qn_ready.at((u * NT + t) * 4 + i + 1))
                    ps = ring.open(pe, "qkT", u, t, i)
                    for p in range(4):
                        mm = pe.transpose(ps[:, p * P:(p + 1) * P], qn[:, i, p * P:(p + 1) * P], ident[:])
                    mm.then_inc(ring.filled("qkT", u, t, i), 1)

            def attn_out(u):
                s = u
                pe.wait_ge(*o1_read.at(PAIRS1 * (u + 1)))
                ps = ring.open(pe, "y1", u)
                for t in range(NT):
                    for p in range(PAIRS1):
                        mm = pe.matmul(ps[:, t * D:(t + 1) * D], o1T[:, p, t * P:(t + 1) * P], wo1[:, p, :],
                                       start=(p == 0), stop=(p == PAIRS1 - 1))
                mm.then_inc(ring.filled("y1", u), 1)

            def x_in(u):
                pe.wait_ge(*xn_ready[2].at(NT * (u + 1)))
                transpose_tiles(u, "h2T", xn[u])

            def x_q(u):
                s = u
                ring.wait_read(pe, "h2T", u)
                for half in range(2):
                    ps = ring.open(pe, "q2", u, half)
                    for i in range(2):
                        p = 2 * half + i
                        mm = pe.matmul(ps[:, i * N:(i + 1) * N], wq2[:, p * P:(p + 1) * P], hT[s][:], start=True, stop=True)
                    mm.then_inc(ring.filled("q2", u, half), 1)

            def x_scores(u):
                s = u
                for half in range(2):
                    ring.wait_read(pe, "q2", u, half)
                ring.wait_read(pe, "kv2", u)
                for t in range(NT):
                    ps = ring.open(pe, "s2", u, t)
                    for p in range(PAIRS2):
                        mm = pe.matmul(ps[:, p * P:(p + 1) * P], q2T[:, p, t * P:(t + 1) * P], kblk[s][:, p, :],
                                       start=True, stop=True)
                    mm.then_inc(ring.filled("s2", u, t), 1)

            def x_pT(u):
                pe.wait_ge(*p2_ready.at(NT * (u + 1)))
                for half in range(2):
                    ps = ring.open(pe, "p2T", u, half)
                    for i in range(2):
                        for t in range(NT):
                            p = 2 * half + i
                            mm = pe.transpose(ps[:, (i * NT + t) * P:(i * NT + t + 1) * P],
                                              s2n[:, t, 2 * p:2 * p + 2, :].rearrange("q h k -> q (h k)"), ident[:])
                    mm.then_inc(ring.filled("p2T", u, half), 1)

            def x_pv(u):
                s = u
                for half in range(2):
                    ring.wait_read(pe, "p2T", u, half)
                    ps = ring.open(pe, "o2", u, half)
                    for i in range(2):
                        p = 2 * half + i
                        mm = pe.matmul(ps[:, i * N:(i + 1) * N], vblk[s][:, p, :], p2T[:, p, :], start=True, stop=True)
                    mm.then_inc(ring.filled("o2", u, half), 1)

            def x_out(u):
                for half in range(2):
                    ring.wait_read(pe, "o2", u, half)
                ps = ring.open(pe, "y2", u)
                for t in range(NT):
                    for p in range(PAIRS2):
                        pe.matmul(ps[:, t * D:(t + 1) * D], o2T[:, p, t * P:(t + 1) * P], wo2[:, p, :],
                                  start=(p == 0), stop=False)
                    mm = pe.matmul(ps[:, t * D:(t + 1) * D], ones_row[:], bo2[:], start=False, stop=True)
                mm.then_inc(ring.filled("y2", u), 1)

            def scores(u, p):
                s = u
                ps = [ring.open(pe, "s1", u, p, i) for i in range(2)]
                for t in range(NT):
                    w = (t + 1) * P
                    for i in range(2):
                        mm = pe.matmul(ps[i][:, t * P:t * P + w], q1T[s][64 * i:64 * i + 64, p, t * P:(t + 1) * P],
                                       k1T[s][64 * i:64 * i + 64, p, 0:w], start=True, stop=True)
                        if t == NT - 1:
                            mm.then_inc(ring.filled("s1", u, p, i), 1)

            def probs_T(u, p):
                n = PAIRS1 * u + p
                a = 2 * n % NPR
                pe.wait_ge(*p_ready.at(2 * (n + 1)))
                for i in range(2):
                    ps = ring.open(pe, "p1T", u, p, i)
                    pe.transpose(ps[:, 0:P], probs[:, a, keys(i, P)], ident[:])
                    first_key = keys(i, N).start
                    for kt in range(2):
                        pe.transpose(ps[:, (kt + 1) * P:(kt + 2) * P], 
                                     probs[:, a + 1, first_key + kt * P:first_key + (kt + 1) * P], ident[:])
                    pe.transpose(ps[0:4, 3 * P:4 * P], probs[:, a + i, N:N + 2 * NULLS], ident[:])\
                        .then_inc(ring.filled("p1T", u, p, i), 1)

            def values(u, p):
                s = u
                n = PAIRS1 * u + p
                if n >= 2:
                    pe.wait_ge(*o1_read.at(n - 1))
                o = o_banks[n % 2]
                for i in range(2):
                    ring.wait_read(pe, "p1T", u, p, i)
                pe.matmul(o[:, 0:N], null_v[:, p, :], pnT[:, n % 2, :], start=True, stop=False,
                          skip_group_check=True)
                for i in range(2):
                    h = 2 * p + i
                    tgt = o[64 * i:64 * i + 64]
                    b = (2 * n + i) % 4
                    pe.matmul(tgt[:, 0:N], v1[s][:, 0, h * DH1:(h + 1) * DH1],
                              pT[:, b, 0:2].rearrange("k t q -> k (t q)"), start=False, stop=False, skip_group_check=True)
                    mm = pe.matmul(tgt[:, P:N], v1[s][:, 1, h * DH1:(h + 1) * DH1], pT[:, b, 2], start=False, stop=True,
                                   skip_group_check=True)
                mm.then_inc(o1_full.sem, 1)

            def pair_step(g):
                u, p = divmod(g, PAIRS1)
                if u < U:
                    if p == 0:
                        for t in range(NT):
                            for j in range(2):
                                ring.wait_read(pe, "v", u, t, j)
                            for i in range(4):
                                ring.wait_read(pe, "qkT", u, t, i)
                    scores(u, p)
                if 2 <= g < PAIRS1 * U + 2:
                    probs_T(*divmod(g - 2, PAIRS1))
                if 3 <= g < PAIRS1 * U + 3:
                    values(*divmod(g - 3, PAIRS1))

            steps = dict(ffn_in=ffn_in, ffn_h=ffn_h, kv2=kv2, ffn_up0=lambda u: ffn_up(u, 0),
                         ffn_up1=lambda u: ffn_up(u, 1), ffn_down=ffn_down, qkv_in=qkv_in, null=null,
                         qkv_a0=lambda u: qkv_a(u, 0), qkv_b0=lambda u: qkv_b(u, 0),
                         qkv_a1=lambda u: qkv_a(u, 1), qkv_b1=lambda u: qkv_b(u, 1), attn_out=attn_out, x_in=x_in, x_q=x_q,
                         x_scores=x_scores, x_pT=x_pT, x_pv=x_pv, x_out=x_out)
            with pe.Fori(0, B // U) as it:
                run_steps(stages, PAIRS1, U, 4, steps, pair_step)
                meet.join(pe, "tensor")

        @block.scalar
        def _(act):
            act.wait_ge(cleared, 1)
            for dst, src in loads[1::2]:
                act.dma_start(dst, src, allow_slow_non_contiguous=True).then_inc(loaded, 16)
            act.wait_ge(t_ps, 1)
            act.wait_ge(null_done, 1)
            for b in range(2):
                act.activation(wq1T[:, 4 * b:4 * b + 4, :].rearrange("p c n -> p (c n)"), banks[b][:], ACT.Copy,
                               scale=qs[:, 1:2])
            for i in range(2):
                ins = act.activation(null_blk[64 * i:64 * i + 64, :, i, :],
                                     banks[2][64 * i:64 * i + 64, 0:32].rearrange("d (p i n) -> d i p n", i=2, n=NULLS)[:, i],
                                     ACT.Copy)
            ins.then_inc(t_sb, 1)
            act.wait_ge(t_ps, 2)
            act.activation(w_null[:].rearrange("k h n -> k (h n)"), banks[3][:, 0:32], ACT.Copy)
            act.activation(b2[1][:], banks[3][0:1, P:2 * P], ACT.Copy).then_inc(ready, 1)
            act.wait_ge(ready, 4)

            def affine(dst, ps, ln):
                return act.activation(dst, ps, ACT.Identity, scale=ln[:, 0:1], bias=ln[:, 1:2])

            def ffn_in(u):
                ps = ring.wait(act, "xT", u)
                act.activation(xT[u][:], ps[:, 0:N], ACT.Copy).then_inc(ring.read("xT", u), 1)

            def ffn_h(u):
                s = u
                ps = ring.wait(act, "hT", u)
                affine(hT[s][:], ps[:, 0:N], ln_f).then_inc(ring.read("hT", u), 1)
                ps = ring.wait(act, "cnT", u)
                affine(cnT[u][:], ps[:, 0:S_CTX], ln_c).then_inc(ring.read("cnT", u), 1)

            def kv2(u):
                s = u
                ps = ring.wait(act, "kv2", u)
                for i in range(2):
                    act.activation(kblk[s][64 * i:64 * i + 64, :, 64 * i:64 * i + 64],
                                   ps[64 * i:64 * i + 64, 0:256].rearrange("d (p k) -> d p k", p=PAIRS2), ACT.Copy)
                    ins = act.activation(vblk[s][64 * i:64 * i + 64, :, 64 * i:64 * i + 64],
                                         ps[64 * i:64 * i + 64, 256:512].rearrange("k (p d) -> k p d", p=PAIRS2), ACT.Copy)
                ins.then_inc(ring.read("kv2", u), 1)

            def ffn_up(u, e):
                if e == 0 and u >= 1:
                    ring.wait(act, "down", u - 1)
                for half in range(2):
                    ps = ring.wait(act, "up", u, e, half)
                    for i in range(2):
                        ch = 2 * half + i
                        ins = act.activation(hid[:, e, ch, :], ps[:, i * N:(i + 1) * N], ACT.Gelu_apprx_tanh,
                                             bias=b1[e][:, ch:ch + 1])
                    ins.then_inc(ring.read("up", u, e, half), 1)
                if e == 1:
                    ring.wait_read(act, "logits", u)
                    act.activation(lg[u][:], lg[u][:], ACT.Exp).then_inc(lg_exp.sem, 1)

            def qkv_in(u):
                s = u
                ps = ring.wait(act, "x1T", u)
                act.activation(xT[s][:], ps[:, 0:N], ACT.Copy).then_inc(ring.read("x1T", u), 1)
                ps = ring.wait(act, "h1T", u)
                affine(hT[s][:], ps[:, 0:N], ln_a).then_inc(ring.read("h1T", u), 1)

            def qkv_a(u, t):
                for i in range(4):
                    n = (u * NT + t) * 4 + i
                    ps = ring.wait(act, "qk", u, t, i)
                    act.activation(qn[:, i, :], ps[:], ACT.Copy).then_inc(qk_copied.sem, 1)
                    if n >= 2:
                        act.wait_ge(*ss_ready.at(n - 1))
                    act.activation(sq[:, i % 2, :], ps[:], ACT.Square).then_inc(ring.read("qk", u, t, i), 1)
                for j in range(2):
                    ps = ring.wait(act, "v", u, t, j)
                    act.activation(v1[u][:, t, j * 512:(j + 1) * 512], ps[:], ACT.Copy).then_inc(ring.read("v", u, t, j), 1)

            def qkv_b(u, t):
                for i in range(4):
                    dst, scale = (q1T, qs[:, 1:2]) if i < 2 else (k1T, ks[:])
                    ps = ring.wait(act, "qkT", u, t, i)
                    act.activation(dst[u][:, 4 * (i % 2):4 * (i % 2) + 4, t * P:(t + 1) * P],
                                   ps[:].rearrange("p (c n) -> p c n", c=4), ACT.Copy, scale=scale)\
                        .then_inc(ring.read("qkT", u, t, i), 1)

            def x_in(u):
                ps = ring.wait(act, "h2T", u)
                affine(hT[u][:], ps[:, 0:N], ln_x).then_inc(ring.read("h2T", u), 1)

            def x_q(u):
                for half in range(2):
                    ps = ring.wait(act, "q2", u, half)
                    act.activation(q2T[:, 2 * half:2 * half + 2, :].rearrange("p c n -> p (c n)"), ps[:], ACT.Copy,
                                   scale=DH2 ** -0.5).then_inc(ring.read("q2", u, half), 1)

            def x_scores(u):
                for t in range(NT):
                    ring.wait_read(act, "s2", u, t)
                    act.activation(s2n[:, t], s2n[:, t], ACT.Exp).then_inc(s2_exp.sem, 1)

            def x_pv(u):
                for half in range(2):
                    ps = ring.wait(act, "o2", u, half)
                    act.activation(o2T[:, 2 * half:2 * half + 2, :].rearrange("p c n -> p (c n)"), ps[:], ACT.Copy)\
                        .then_inc(ring.read("o2", u, half), 1)

            def pair_step(g):
                if g >= 4:
                    n = g - 4
                    act.wait_ge(*o1_full.at(n + 1))
                    if n >= PAIRS1 and n % PAIRS1 == 0:
                        ring.wait(act, "y1", n // PAIRS1 - 1)
                    act.activation(o1T[:, n % PAIRS1, :], o_banks[n % 2][:, 0:N], ACT.Copy).then_inc(o1_read.sem, 1)
                u, p = divmod(g, PAIRS1)
                if u < U:
                    for i in range(2):
                        ring.wait_read(act, "s1", u, p, i)
                        for t in range(NT):
                            a = (2 * g + t) % NPR
                            w = (t + 1) * P
                            ins = act.activation(probs[:, a, keys_nulls(i, w)], probs[:, a, keys_nulls(i, w)], ACT.Exp,
                                                 bias=low[:, a, i:i + 1], scale=-1.0, accum_out=sums[:, a, i:i + 1])
                        ins.then_inc(exp_done.sem, 1)

            steps = dict(ffn_in=ffn_in, ffn_h=ffn_h, kv2=kv2, ffn_up0=lambda u: ffn_up(u, 0),
                         ffn_up1=lambda u: ffn_up(u, 1), qkv_in=qkv_in,
                         qkv_a0=lambda u: qkv_a(u, 0), qkv_b0=lambda u: qkv_b(u, 0),
                         qkv_a1=lambda u: qkv_a(u, 1), qkv_b1=lambda u: qkv_b(u, 1), x_in=x_in, x_q=x_q,
                         x_scores=x_scores, x_pv=x_pv)
            with act.Fori(0, B // U) as it:
                run_steps(stages, PAIRS1, U, 4, steps, pair_step)
                meet.join(act, "scalar")

        @block.vector
        def _(dve):
            dve.memset(null_v[:], 0.0).then_inc(cleared, 1)
            dve.memset(null_blk[:], 0.0)
            for s in range(SETS):
                dve.memset(kblk[s][:], 0.0)
                dve.memset(vblk[s][:], 0.0)
            chain = Chain(dve, dve_setup)
            dve.wait_ge(loaded, 16 * len(loads))
            chain(dve.tensor_scalar(qs[:, 1:2], qs[:, 0:1], -QK_SCALE, None, ALU.mult))
            chain(dve.tensor_tensor(null_k2[:, 0, :], null_k[:], null_k[:], ALU.mult))
            chain(dve.tensor_reduce(null_ss[:, 0:1], null_k2[:, 0, :], AX.X, ALU.add))
            dve.tensor_scalar(null_ss[:, 0:1], null_ss[:, 0:1], 1e-24, None, ALU.max).then_inc(null_pow, 1)
            dve.wait_ge(null_pow, 2)
            chain(dve.tensor_scalar(null_k[:], null_k[:], null_ss[:, 1:2], None, ALU.mult))
            chain(dve.tensor_tensor(null_k2[:, 0, :], null_k[:], ks_row[:], ALU.mult))
            chain(dve.tensor_copy(null_k2[:, 1, :], null_k2[:, 0, :]))
            dve.sem_inc(null_done, 1)
            dve.wait_ge(iota_done, 2)
            for h in range(H1):
                dve.tensor_scalar(dist[:, h, :], dist0, slopes[h], None, ALU.mult)
                dve.tensor_scalar(null_bias[:, :, h, :], iota_nf[:], slopes[h], None, ALU.mult)
            thr = K["thr"][:].bitcast(F32)
            for w, dst, cols, th in ((w1[0][:], w1[1][:], F, 0),
                                     (w2[0][:].rearrange("p c n -> p (c n)"), w2[1][:].rearrange("p c n -> p (c n)"), F, 2),
                                     (b1[0][:], b1[1][:], FC, 4), (K["b2c"][:], K["b2c"][:], 1, 6)):
                chain(dve.tensor_scalar(mag[:, 0:cols].bitcast(I32), w.bitcast(I32), 0x7FFFFFFF, None, ALU.bitwise_and))
                chain(dve.tensor_scalar(tier[:, 0:cols], mag[:, 0:cols], thr[:, th:th + 1], -2.0, ALU.is_ge, ALU.mult))
                chain(dve.tensor_scalar(tier2[:, 0:cols], mag[:, 0:cols], thr[:, th + 1:th + 2], None, ALU.is_le))
                chain(dve.tensor_tensor(tier[:, 0:cols], tier[:, 0:cols], tier2[:, 0:cols], ALU.add))
                chain(dve.tensor_scalar(tier[:, 0:cols], tier[:, 0:cols], -1.0, None, ALU.max))
                chain(dve.tensor_scalar(tier2[:, 0:cols], w, 0.8, None, ALU.mult))
                chain(dve.tensor_tensor(tier[:, 0:cols], tier2[:, 0:cols], tier[:, 0:cols], ALU.mult))
                chain(dve.tensor_tensor(dst, w, tier[:, 0:cols], ALU.add))
            dve.sem_inc(experts_ready, 1)
            dve.sem_inc(ready, 1)
            dve.wait_ge(ready, 4)

            def moments(u, src, out, rows=P):
                for t in range(len(src)):
                    link(dve.bn_stats(stats[u][0:rows, t, :], src[t]))
                for t in range(len(src)):
                    dve.bn_aggr(out[t], stats[u][0:rows, t, :]).then_inc(mv_ready.sem, 1)
                waits["mv"] += len(src)

            def link(ins):
                chain(ins)

            waits = {"mv": 0, "root": 0, "x": 0}

            def normalise(u, src, dst, done):
                s = u
                moments(u, [src[:, t, :] for t in range(NT)], [mv[s][:, t, :] for t in range(NT)])
                waits["root"] += 1
                dve.wait_ge(*rstd_ready.at(waits["root"]))
                for t in range(NT):
                    dve.tensor_scalar(dst[:, t, :], src[:, t, :], mv[s][:, t, 0:1], rstd[s][:, NT + t:NT + t + 1],
                                      ALU.subtract, ALU.mult).then_inc(done.sem, 1)

            def residual(u, name):
                s = u
                ps = ring.wait(dve, name, u)
                dve.tensor_tensor(r[:].rearrange("p t n -> p (t n)"), ps[:, 0:N],
                                  x[s][:].rearrange("p t n -> p (t n)"), ALU.add).then_inc(ring.read(name, u), 1)
                ring.wait_read(dve, name, u)

            def ffn_in(u):
                s = u
                dve.wait_ge(*x_loaded[u % SETS].at(32 * (u // SETS + 1)))
                normalise(u, x[s], xn[s], xn_ready[0])

            def context(u):
                s = u
                dve.wait_ge(*x_loaded[u % SETS].at(32 * (u // SETS + 1)))
                link(dve.bn_stats(cmv[s][:, 0:6], c[s][:]))
                dve.bn_aggr(cmv[s][:, 6:8], cmv[s][:, 0:6]).then_inc(mv_ready.sem, 1)
                waits["root"] += 1
                dve.wait_ge(*rstd_ready.at(waits["root"]))
                dve.tensor_scalar(cn[s][:], c[s][:], cmv[s][:, 6:7], cmv[s][:, 1:2], ALU.subtract, ALU.mult)\
                    .then_inc(cn_ready.sem, 1)

            def ffn_up0(u):
                s = u
                ps = ring.wait(dve, "logits", u)
                l = ps[:, 0:NT * NE0].rearrange("p (t e) -> p t e", t=NT)
                link(dve.tensor_reduce(pr[s][:, :, 0], l, AX.X, ALU.max))
                dve.tensor_tensor(lg[s][:], l, pr[s][:, :, 0:1].broadcast_to([P, NT, NE0]), ALU.subtract)\
                    .then_inc(ring.read("logits", u), 1)

            def ffn_up1(u):
                s = u
                dve.wait_ge(*lg_exp.at(u + 1))
                link(dve.tensor_reduce(pr[s][:, :, 1], lg[s][:], AX.X, ALU.add))
                link(dve.reciprocal(pr[s][:, :, 2], pr[s][:, :, 1]))
                link(dve.tensor_reduce(pr[s][:, :, 5], lg[s][:, :, 1:NE0], AX.X, ALU.add))
                link(dve.tensor_tensor(pr[s][:, :, 3], lg[s][:, :, 0], pr[s][:, :, 2], ALU.mult))
                link(dve.tensor_tensor(pr[s][:, :, 4], pr[s][:, :, 5], pr[s][:, :, 2], ALU.mult))

            def ffn_down(u):
                s = u
                ps = ring.wait(dve, "down", u)
                for t in range(NT):
                    link(dve.scalar_tensor_tensor(r[:, t, :], ps[:, t * D:(t + 1) * D], pr[s][:, t, 3:4], x[s][:, t, :],
                                                  ALU.mult, ALU.add))
                for t in range(NT):
                    ins = dve.scalar_tensor_tensor(r[:, t, :], ps[:, (2 + t) * D:(3 + t) * D], pr[s][:, t, 4:5],
                                                   r[:, t, :], ALU.mult, ALU.add)
                ins.then_inc(ring.read("down", u), 1)
                ring.wait_read(dve, "down", u)
                normalise(u, r, x[s], x_ready[0])
                dve.wait_ge(*x_ready[0].at(NT * (u + 1)))
                normalise(u, x[s], xn[s], xn_ready[1])

            def null(u):
                ps = ring.wait(dve, "null", u)
                dve.tensor_copy(nneg[u][:].rearrange("p t h n -> p (t h n)"), ps[:, 0:64])\
                    .then_inc(ring.read("null", u), 1)

            def qkv_a(u, t):
                for i in range(4):
                    n = (u * NT + t) * 4 + i
                    ring.wait_read(dve, "qk", u, t, i)
                    if n >= 4:
                        dve.wait_ge(*rn_ready.at(n - 3))
                    dve.tensor_reduce(ss[:, i, :], sq[:, i % 2, :].rearrange("p (h d) -> p h d", d=DH1), AX.X, ALU.add)\
                        .then_inc(ss_ready.sem, 1)

            def qkv_b(u, t):
                s = u
                for i in range(4):
                    n = (u * NT + t) * 4 + i
                    dve.wait_ge(*rn_ready.at(n + 1))
                    rr = rnq[s][:, t, 8 * i:8 * i + 8] if i < 2 else rn[:, i % 2, :]
                    rows = qn[:, i, :].rearrange("p (h d) -> p h d", d=DH1)
                    dve.wait_ge(*qk_copied.at(n + 1))
                    dve.tensor_tensor(rows, rows, rr.unsqueeze(2).broadcast_to([P, 8, DH1]), ALU.mult)\
                        .then_inc(qn_ready.sem, 1)
                if t == 1:
                    ring.wait_read(dve, "null", u)
                    link(dve.tensor_tensor(nneg[s][:], nneg[s][:],
                                           rnq[s][:].unsqueeze(3).broadcast_to([P, NT, H1, NULLS]), ALU.mult))
                    link(dve.tensor_tensor(nneg[s][:], nneg[s][:], null_bias[:], ALU.add))
                    link(dve.tensor_reduce(nmin[s][:], nneg[s][:], AX.X, ALU.min))

            def attn_out(u):
                s = u
                residual(u, "y1")
                normalise(u, r, x[s], x_ready[1])
                dve.wait_ge(*x_ready[1].at(NT * (u + 1)))
                normalise(u, x[s], xn[s], xn_ready[2])

            def x_scores(u):
                for t in range(NT):
                    ps = ring.wait(dve, "s2", u, t)
                    sc = ps[:].rearrange("p (h k) -> p h k", h=H2)
                    link(dve.tensor_reduce(m2[:, t, :], sc, AX.X, ALU.max, negate=True))
                    dve.tensor_tensor(s2n[:, t], sc, m2[:, t, :].unsqueeze(2).broadcast_to([P, H2, S_CTX]), ALU.add)\
                        .then_inc(ring.read("s2", u, t), 1)
                    ring.wait_read(dve, "s2", u, t)
                for t in range(NT):
                    dve.wait_ge(*s2_exp.at(NT * u + t + 1))
                    link(dve.tensor_reduce(z2[:, t, :], s2n[:, t], AX.X, ALU.add))
                    dve.reciprocal(rz2[:, t, :], z2[:, t, :]).then_inc(s2_inv.sem, 1)

            def x_pT(u):
                for half in range(2):
                    ps = ring.wait(dve, "p2T", u, half)
                    dve.tensor_copy(p2T[:, 2 * half:2 * half + 2, :].rearrange("p c n -> p (c n)"), ps[:])\
                        .then_inc(ring.read("p2T", u, half), 1)

            def x_out(u):
                s = u
                residual(u, "y2")
                normalise(u, r, x[s], x_ready[2])
                dve.wait_ge(*x_ready[2].at(NT * (u + 1)))

            def pair_step(g):
                u, p = divmod(g, PAIRS1)
                if u < U:
                    a = 2 * g % NPR
                    if 2 * g >= NPR:
                        m = g - NPR // 2
                        ring.wait(dve, "p1T", m // PAIRS1, m % PAIRS1, 1)
                    dve.tensor_copy(probs[:, a:a + NT, N:N + 2 * NULLS].rearrange("q t (h n) -> q t h n", n=NULLS),
                                    nneg[u][:, :, 2 * p:2 * p + 2, :])
                    for i in range(2):
                        h = 2 * p + i
                        ps = ring.wait(dve, "s1", u, p, i)
                        for t in range(NT):
                            w = (t + 1) * P
                            ins = dve.tensor_tensor_reduce(probs[:, a + t, keys(i, w)], dist[:, h, (1 - t) * P:N],
                                                           ps[:, t * P:t * P + w], 1.0, nmin[u][:, t, h:h + 1],
                                                           ALU.add, ALU.min, low[:, a + t, i:i + 1])
                        ins.then_inc(ring.read("s1", u, p, i), 1)
                if 1 <= g < PAIRS1 * U + 1:
                    a = 2 * (g - 1) % NPR
                    for i in range(2):
                        dve.wait_ge(*exp_done.at(2 * (g - 1) + i + 1))
                        dve.reciprocal(rsums[:, a:a + NT, i], sums[:, a:a + NT, i]).then_inc(rs_ready.sem, 1)
                if 2 <= g < PAIRS1 * U + 2:
                    m = g - 2
                    if m >= 2:
                        dve.wait_ge(*o1_full.at(m - 1))
                    for i in range(2):
                        ps = ring.wait(dve, "p1T", m // PAIRS1, m % PAIRS1, i)
                        dve.tensor_copy(pnT[:, m % 2, i * P:(i + 1) * P], ps[0:4, 3 * P:4 * P])
                        dve.tensor_copy(pT[:, (2 * m + i) % 4].rearrange("k t q -> k (t q)"), ps[:, 0:3 * P])\
                            .then_inc(ring.read("p1T", m // PAIRS1, m % PAIRS1, i), 1)

            steps = dict(ffn_in=ffn_in, ctx=context, ffn_up0=ffn_up0, ffn_up1=ffn_up1, ffn_down=ffn_down, null=null,
                         qkv_a0=lambda u: qkv_a(u, 0), qkv_b0=lambda u: qkv_b(u, 0),
                         qkv_a1=lambda u: qkv_a(u, 1), qkv_b1=lambda u: qkv_b(u, 1), attn_out=attn_out,
                         x_scores=x_scores, x_pT=x_pT, x_out=x_out)
            with dve.Fori(0, B // U) as it:
                chain = Chain(dve, dve_chain)
                run_steps(stages, PAIRS1, U, 4, steps, pair_step)
                meet.join(dve, "vector")

        @block.gpsimd
        def _(pool):
            chain = Chain(pool, pool_setup)
            chain(pool.iota(iota_i, pattern=[[-1, N]], base=P, channel_multiplier=1))
            chain(pool.tensor_copy(dist0, iota_i))
            pool.affine_select(out=dist0, in_=dist0, compare_op=ALU.is_ge, fill=MASKED, base=P,
                               pattern=[[-1, N]], channel_multiplier=1).then_inc(iota_done, 1)
            chain(pool.iota(iota_n[:], pattern=[[P, NT], [-1, NULLS]], base=NULLS, channel_multiplier=1))
            pool.tensor_copy(iota_nf[:], iota_n[:]).then_inc(iota_done, 1)
            pool.wait_ge(null_pow, 1)
            pool.tensor_tensor(null_ss[:, 1:2], null_ss[:, 0:1], K["eps_half"][0:32, 0:1], ALU.pow).then_inc(null_pow, 1)
            pool.sem_inc(ready, 1)
            pool.wait_ge(ready, 4)
            count = {"mv": 0}

            def root(u):
                s = u
                count["mv"] += NT
                pool.wait_ge(*mv_ready.at(count["mv"]))
                chain(pool.tensor_scalar(rstd[s][:, 0:NT], mv[s][:, :, 1], LN_EPS, None, ALU.add))
                pool.tensor_tensor(rstd[s][:, NT:2 * NT], rstd[s][:, 0:NT], K["eps_half"][:, 0:NT], ALU.pow)\
                    .then_inc(rstd_ready.sem, 1)

            def ctx_root(u):
                s = u
                count["mv"] += 1
                pool.wait_ge(*mv_ready.at(count["mv"]))
                chain(pool.tensor_scalar(cmv[s][:, 0:1], cmv[s][:, 7:8], LN_EPS, None, ALU.add))
                pool.tensor_tensor(cmv[s][:, 1:2], cmv[s][:, 0:1], K["eps_half"][0:S_CTX, 0:1], ALU.pow)\
                    .then_inc(rstd_ready.sem, 1)

            def two_roots(u):
                root(u)
                root(u)

            def qkv_a(u, t):
                s = u
                for i in range(4):
                    n = (u * NT + t) * 4 + i
                    pool.wait_ge(*ss_ready.at(n + 1))
                    rr = rnq[s][:, t, 8 * i:8 * i + 8] if i < 2 else rn[:, i % 2, :]
                    chain(pool.tensor_scalar(ss[:, i, :], ss[:, i, :], 1e-24, None, ALU.max))
                    pool.tensor_tensor(rr, ss[:, i, :], K["eps_half"][:, 0:8], ALU.pow).then_inc(rn_ready.sem, 1)

            def x_scores(u):
                for t in range(NT):
                    pool.wait_ge(*s2_inv.at(NT * u + t + 1))
                    pool.tensor_tensor(s2n[:, t], s2n[:, t], rz2[:, t, :].unsqueeze(2).broadcast_to([P, H2, S_CTX]),
                                       ALU.mult).then_inc(p2_ready.sem, 1)

            def pair_step(g):
                if 1 <= g < PAIRS1 * U + 1:
                    for i in range(2):
                        pool.wait_ge(*rs_ready.at(2 * (g - 1) + i + 1))
                        for t in range(NT):
                            a = (2 * (g - 1) + t) % NPR
                            w = (t + 1) * P
                            ins = pool.tensor_scalar(probs[:, a, keys_nulls(i, w)], probs[:, a, keys_nulls(i, w)],
                                                     rsums[:, a, i:i + 1], 1.0, ALU.mult, ALU.mult)
                        ins.then_inc(p_ready.sem, 1)

            steps = dict(ffn_in=root, ctx=ctx_root, ffn_down=two_roots, qkv_a0=lambda u: qkv_a(u, 0),
                         qkv_a1=lambda u: qkv_a(u, 1), attn_out=two_roots, x_scores=x_scores, x_out=root)
            with pool.Fori(0, B // U) as it:
                chain = Chain(pool, pool_chain)
                run_steps(stages, PAIRS1, U, 4, steps, pair_step)
                meet.lead(pool, first, last)
            pool.sem_clear(range(FIRST_SEM, meet.arrived.num))

        @block.sync
        def _(sy):
            sy.wait_ge(cleared, 1)
            for dst, src in loads[0::2]:
                sy.dma_start(dst, src, allow_slow_non_contiguous=True).then_inc(loaded, 16)
            sy.sem_inc(ready, 1)
            xin = x_in.rearrange("b (t p) d -> b p t d", p=P)
            xo = x_out.rearrange("b (t p) d -> b p t d", p=P)
            with sy.Fori(0, B // U) as it:
                def load(u):
                    if u >= SETS:
                        sy.wait_ge(*stored[u % SETS].at(16 * (u // SETS)))
                    sy.dma_start(x[u][:], xin[it * U + u]).then_inc(x_loaded[u % SETS].sem, 16)
                    sy.dma_start(c[u][:], A["ctx_1024"][it * U + u]).then_inc(x_loaded[u % SETS].sem, 16)

                def store(u):
                    sy.wait_ge(*x_ready[2].at(NT * (u + 1)))
                    sy.dma_start(xo[it * U + u], x[u][:]).then_inc(stored[u % SETS].sem, 16)

                for u in range(U):
                    if u >= SETS:
                        store(u - SETS)
                    load(u)
                for u in range(U - SETS, U):
                    store(u)
                for i in range(min(SETS, U)):
                    sy.wait_ge(*stored[i].at(16 * ((U - 1 - i) // SETS + 1)))
                meet.join(sy, "sync")


H3, DH3 = 16, 8
KV3 = 8
TC = B * N // P
TG = 4
NG = TC // TG
NE = 8
CAP = int(np.ceil(B * N * 2 / NE * 1.25))


def phase_3(nc, A, K, x_in, out):
    with ExitStack() as ctx:
        hT_all = ctx.enter_context(nc.sbuf_tensor("h2T_all", [P, TC, P], F32))
        acc_all = ctx.enter_context(nc.sbuf_tensor("acc_all", [P, TC, D], F32))
        column_attention(nc, A, K, x_in, hT_all, acc_all)
        experts(nc, A, K, hT_all, acc_all, out)


def column_attention(nc, A, K, x_in, hT_all, acc_all):
    U = 4
    PAIRS = H3 // 2
    with ExitStack() as ctx:
        def sb(name, shape, dt=F32):
            return ctx.enter_context(nc.sbuf_tensor(name, shape, dt))

        sems = []

        def sem(name):
            s = ctx.enter_context(nc.semaphore(name, num=FIRST_SEM + len(sems)))
            sems.append(s)
            return s

        def two(name, shape, dt=F32):
            return Sets([sb(f"{name}{i}", shape, dt) for i in range(2)])

        XS = 3

        ident = K["ident"]
        W = TG * P
        w_raw = sb("qkv_raw", [P, 2, P])
        wo_raw = sb("proj_raw", [P, P])
        split = K["split"]
        wq = sb("cq_pad", [P, GROUPS, 4, 32])
        wk = sb("ck_pad", [P, GROUPS, 4, 32])
        wv = sb("cv", [P, KV3, DH3])
        woT = sb("c_woT", [P, D])
        wo_pad = sb("c_wo_pad", [P, GROUPS, D])
        ln1 = sb("c_ln1", [P, 2])
        ln2 = sb("c_ln2", [P, 2])
        ident_bf = sb("ident_bf", [P, P], BF16)
        iota = sb("c_iota", [P, P], I32)
        low_bits = sb("c_low_bits", [P, P], I32)
        mask_f = sb("c_mask_f", [P, P])
        mask = sb("c_mask", [P, TG, P], BF16)
        x = Sets([sb(f"cx{i}", [P, TG, D]) for i in range(XS)])
        xn = two("cxn", [P, TG, D])
        hn = two("chn", [P, TG, D])
        r = two("cr", [P, TG, D])
        stats = two("cstats", [P, TG, 6])
        mv = two("cmv3_", [P, TG, 2])
        rstd = two("crstd", [P, 2 * TG])
        lnT = two("clnT", [P, W])
        rounded = two("c_rounded", [P, W], F32R)
        qT = two("cqT", [P, GROUPS, W], F32R)
        kT = two("ckT", [P, GROUPS, W], F32R)
        v = two("cv3_", [P, TG, KV3, 32])
        oT = two("coT", [P, GROUPS, W])
        NPR = 8
        probs = sb("cprobs", [P, NPR, TG, P])
        pT = sb("cpT", [P, NPR, TG, P])
        negmax = sb("cnegmax", [P, NPR, TG])
        sums = sb("csums", [P, NPR, TG])
        rsums = sb("crsums", [P, NPR, TG])
        banks = [ctx.enter_context(nc.psum_tensor(f"pc{i}", [P, 512], F32)) for i in range(6)]
        o_banks = [ctx.enter_context(nc.psum_tensor(f"pd{i}", [P, 512], F32)) for i in range(2)]

        loaded = sem("c_weights_loaded")
        cleared = sem("c_cleared")
        staged = sem("c_proj_staged")
        dve_setup = sem("c_dve_setup")
        pool_setup = sem("c_pool_setup")
        act_setup = sem("c_act_setup")
        t_ps = sem("c_setup_transposed")
        mask_iota = sem("c_mask_iota")
        ready = sem("c_setup_ready")
        meet = Meeting(sem, ["sync", "scalar", "tensor", "vector"])
        n_setup = len(sems)
        ring = Ring(banks, sem)
        x_loaded = [sem(f"cx{i}_loaded") for i in range(XS)]
        mv_ready = Counted(sem("c_moments_ready"))
        rstd_ready = Counted(sem("c_roots_ready"))
        xn_ready = Counted(sem("c_xn_ready"))
        rounded_ready = Counted(sem("c_rounded_ready"))
        hn_ready = Counted(sem("c_hn_ready"))
        negmax_ready = Counted(sem("c_negmax_ready"))
        rs_ready = Counted(sem("c_rsums_ready"))
        p_ready = Counted(sem("c_probs_ready"))
        o_full = Counted(sem("c_o_full"))
        o_read = Counted(sem("c_o_read"))
        acc_ready = Counted(sem("c_acc_ready"))
        dve_chain = sem("c_dve_chain")
        pool_chain = sem("c_pool_chain")
        first, last = sems[n_setup].num, sems[-1].num

        loads = [
            (w_raw[:], A["L1_ffn_qkv_weight"].rearrange("(a p) k -> p a k", p=P)),
            (wo_raw[:], A["L1_ffn_proj_weight"]),
            (ln1[:, 0:1], col(A["L1_ffn_ln1_weight"])), (ln1[:, 1:2], col(A["L1_ffn_ln1_bias"])),
            (ln2[:, 0:1], col(A["L1_ffn_ln2_weight"])), (ln2[:, 1:2], col(A["L1_ffn_ln2_bias"])),
        ]
        stages = [(-9, "norm1"), (-6, "lnT"), (-5, "qk01"), (-4, "qk23"), (-3, "v"), (13, "out"), (16, "hT")]

        block = ctx.enter_context(nc.Block())

        @block.tensor
        def _(pe):
            pe.wait_ge(loaded, 16 * len(loads))
            for a in range(2):
                pe.transpose(banks[0][:, a * P:(a + 1) * P], w_raw[:, a, :], ident[:])
            pe.transpose(banks[0][:, 2 * P:3 * P], wo_raw[:], ident[:]).then_inc(t_ps, 1)
            pe.wait_ge(ready, 4)

            def transposes(name, u, src):
                ps = ring.open(pe, name, u)
                for t in range(TG):
                    mm = pe.transpose(ps[:, t * P:(t + 1) * P], src[:, t, :], ident[:])
                mm.then_inc(ring.filled(name, u), 1)

            def ln_T(u):
                pe.wait_ge(*xn_ready.at(TG * (u + 1)))
                transposes("lnT", u, xn[u])

            def qk(u, groups):
                ring.wait_read(pe, "lnT", u)
                for g in groups:
                    for name, w in (("q", wq), ("k", wk)):
                        ps = ring.open(pe, name, u, g)
                        pe.matmul(ps[:], w[:, g].rearrange("p j d -> p (j d)"), lnT[u][:], start=True, stop=True)\
                            .then_inc(ring.filled(name, u, g), 1)

            def v_(u):
                ps = ring.open(pe, "v", u)
                for t in range(TG):
                    mm = pe.matmul(ps[:, t * 64:(t + 1) * 64], lnT[u][:, t * P:(t + 1) * P],
                                   wv[:].rearrange("p h d -> p (h d)"), start=True, stop=True)
                mm.then_inc(ring.filled("v", u), 1)

            def scores(u, p):
                s = u
                ps = [ring.open(pe, "s", u, p, i) for i in range(2)]
                for i in range(2):
                    pe.matmul(ps[i][:], ident_bf[:], mask[:].rearrange("q t k -> q (t k)"), start=True, stop=False,
                              skip_group_check=True)
                for t in range(TG):
                    for i in range(2):
                        h = 2 * p + i
                        g, j = h // 4, 32 * (h % 4)
                        mm = pe.matmul(ps[i][:, t * P:(t + 1) * P], qT[s][j:j + 3 * DH3, g, t * P:(t + 1) * P],
                                       kT[s][j:j + 3 * DH3, g, t * P:(t + 1) * P], start=False, stop=True,
                                       skip_group_check=True)
                        if t == TG - 1:
                            mm.then_inc(ring.filled("s", u, p, i), 1)

            def probs_T(u, p):
                for i in range(2):
                    n = H3 * u + 2 * p + i
                    pe.wait_ge(*p_ready.at(n + 1))
                    ps = ring.open(pe, "pT", u, p, i)
                    for t in range(TG):
                        mm = pe.transpose(ps[:, t * P:(t + 1) * P], probs[:, n % NPR, t, :], ident[:])
                    mm.then_inc(ring.filled("pT", u, p, i), 1)

            def values(u, p):
                s = u
                m = GROUPS * u + p // 2
                if p % 2 == 0 and m >= 2:
                    pe.wait_ge(*o_read.at(m - 1))
                for i in range(2):
                    h = 2 * p + i
                    n = H3 * u + h
                    j = 32 * (h % 4)
                    ring.wait_read(pe, "pT", u, p, i)
                    for t in range(TG):
                        mm = pe.matmul(o_banks[m % 2][j:j + 32, t * P:(t + 1) * P], v[s][:, t, h // 2, :],
                                       pT[:, n % NPR, t, :], start=True, stop=True)
                mm.then_inc(o_full.sem, 1)

            def pair_step(g):
                u, p = divmod(g, PAIRS)
                if u < U:
                    if p == 0:
                        for q in range(GROUPS):
                            ring.wait_read(pe, "q", u, q)
                            ring.wait_read(pe, "k", u, q)
                        ring.wait_read(pe, "v", u)
                    scores(u, p)
                if 3 <= g < PAIRS * U + 3:
                    probs_T(*divmod(g - 3, PAIRS))
                if 4 <= g < PAIRS * U + 4:
                    values(*divmod(g - 4, PAIRS))

            def project_out(u):
                s = u
                pe.wait_ge(*o_read.at(GROUPS * (u + 1)))
                ps = ring.open(pe, "y", u)
                for t in range(TG):
                    for g in range(GROUPS):
                        mm = pe.matmul(ps[:, t * P:(t + 1) * P], oT[s][:, g, t * P:(t + 1) * P], wo_pad[:, g, :],
                                       start=(g == 0), stop=(g == GROUPS - 1))
                mm.then_inc(ring.filled("y", u), 1)

            def h_T(u):
                pe.wait_ge(*hn_ready.at(TG * (u + 1)))
                transposes("hT", u, hn[u])

            steps = dict(lnT=ln_T, qk01=lambda u: qk(u, (0, 1)), qk23=lambda u: qk(u, (2, 3)), v=v_, out=project_out,
                         hT=h_T)
            with pe.Fori(0, NG // U) as it:
                run_steps(stages, PAIRS, U, 5, steps, pair_step)
                meet.join(pe, "tensor")

        @block.scalar
        def _(act):
            act.wait_ge(cleared, 4)
            act.wait_ge(t_ps, 1)
            w_ps = banks[0][:, 0:2 * P].rearrange("k (g a d) -> k g a d", g=GROUPS, a=2)
            for i in range(2):
                for n in range(3):
                    act.activation(wq[:, :, i::2, n * DH3:(n + 1) * DH3], w_ps[:, :, :, i * DH3:(i + 1) * DH3],
                                   ACT.Copy, scale=1 / math.sqrt(DH3))
                    act.activation(wk[:, :, i::2, n * DH3:(n + 1) * DH3], w_ps[:, :, :, 2 * DH3:3 * DH3], ACT.Copy)
            act.activation(wv[:].rearrange("k (g a) d -> k g a d", a=2), w_ps[:, :, :, 3 * DH3:4 * DH3], ACT.Copy)
            act.activation(woT[:], banks[0][:, 2 * P:3 * P], ACT.Copy).then_inc(act_setup, 1)
            act.wait_ge(act_setup, 1)
            for j in range(4):
                for g in range(GROUPS):
                    k = (4 * g + j) * DH3
                    act.dma_start(wo_pad[32 * j:32 * j + DH3, g, :], woT[k:k + DH3, :]).then_inc(staged, 16)
            act.wait_ge(staged, 16 * 4 * GROUPS)
            act.sem_inc(ready, 1)
            act.wait_ge(ready, 4)

            def affine(dst, ps, ln):
                return act.activation(dst, ps, ACT.Identity, scale=ln[:, 0:1], bias=ln[:, 1:2])

            def norm1(u):
                ps = ring.wait(act, "lnT", u)
                affine(lnT[u][:], ps[:], ln1).then_inc(ring.read("lnT", u), 1)

            def round_qk(u, groups):
                for g in groups:
                    for i, name in enumerate("qk"):
                        ps = ring.wait(act, name, u, g)
                        n = 2 * (GROUPS * u + g) + i
                        if n >= 2:
                            ring.wait_read(act, name, (n // 2 - 1) // GROUPS, (n // 2 - 1) % GROUPS)
                        act.activation(rounded[i][:], ps[:], ACT.Copy).then_inc(rounded_ready.sem, 1)

            def read_v(u):
                ps = ring.wait(act, "v", u)
                act.activation(v[u][:, :, :, 0:DH3], ps[:, 0:TG * 64].rearrange("p (t h d) -> p t h d", t=TG, h=KV3),
                               ACT.Copy).then_inc(ring.read("v", u), 1)

            def pair_step(g):
                if g >= 6 and g % 2 == 0:
                    m = (g - 6) // 2
                    act.wait_ge(*o_full.at(2 * (m + 1)))
                    act.activation(oT[m // GROUPS][:, m % GROUPS, :], o_banks[m % 2][:], ACT.Copy)\
                        .then_inc(o_read.sem, 1)
                u, p = divmod(g, PAIRS)
                if u < U:
                    for i in range(2):
                        n = 2 * g + i
                        ps = ring.wait(act, "s", u, p, i)
                        act.wait_ge(*negmax_ready.at(n + 1))
                        if n >= NPR:
                            m = n - NPR
                            ring.wait(act, "pT", m // H3, (m % H3) // 2, m % 2)
                        for t in range(TG):
                            ins = act.activation(probs[:, n % NPR, t, :], ps[:, t * P:(t + 1) * P], ACT.Exp,
                                                 bias=negmax[:, n % NPR, t:t + 1],
                                                 accum_out=sums[:, n % NPR, t:t + 1])
                        ins.then_inc(ring.read("s", u, p, i), 1)

            def out_step(u):
                ps = ring.wait(act, "hT", u)
                affine(hT_all[:, bass.ds((it * U + u) * TG, TG), :].rearrange("p t n -> p (t n)"), ps[:], ln2)\
                    .then_inc(ring.read("hT", u), 1)

            steps = dict(lnT=norm1, qk01=lambda u: round_qk(u, (0, 1)), qk23=lambda u: round_qk(u, (2, 3)), v=read_v,
                         hT=out_step)
            with act.Fori(0, NG // U) as it:
                run_steps(stages, PAIRS, U, 5, steps, pair_step)
                meet.join(act, "scalar")

        @block.vector
        def _(dve):
            dve.memset(wq[:], 0.0).then_inc(cleared, 1)
            dve.memset(wk[:], 0.0).then_inc(cleared, 1)
            dve.memset(wo_pad[:], 0.0).then_inc(cleared, 1)
            dve.memset(v[0][:], 0.0)
            dve.memset(v[1][:], 0.0).then_inc(cleared, 1)
            chain = Chain(dve, dve_setup)
            dve.tensor_copy(ident_bf[:], ident[:])
            dve.wait_ge(mask_iota, 1)
            chain(dve.tensor_scalar(low_bits[:], iota[:], N // TC - 1, None, ALU.bitwise_and))
            chain(dve.tensor_copy(mask_f[:], low_bits[:]))
            chain(dve.tensor_scalar(mask_f[:], mask_f[:], 0.5, -MASKED, ALU.is_ge, ALU.mult))
            dve.sem_inc(mask_iota, 1)
            dve.wait_ge(mask_iota, 3)
            for t in range(TG):
                ins = dve.tensor_copy(mask[:, t, :], mask_f[:])
            chain(ins)
            dve.sem_inc(ready, 1)
            dve.wait_ge(ready, 4)
            roots = {"n": 0}

            def link(ins):
                chain(ins)

            def normalise(s, src, dst, done):
                for t in range(TG):
                    link(dve.bn_stats(stats[s][:, t, :], src[:, t, :]))
                for t in range(TG):
                    dve.bn_aggr(mv[s][:, t, :], stats[s][:, t, :]).then_inc(mv_ready.sem, 1)
                roots["n"] += 1
                dve.wait_ge(*rstd_ready.at(roots["n"]))
                for t in range(TG):
                    dve.tensor_scalar(dst[:, t, :], src[:, t, :], mv[s][:, t, 0:1], rstd[s][:, TG + t:TG + t + 1],
                                      ALU.subtract, ALU.mult).then_inc(done.sem, 1)

            def norm1(u):
                dve.wait_ge(x_loaded[u % XS], 16 * (u // XS + 1))
                normalise(u % 2, x[u], xn[u], xn_ready)

            def split_qk(u, groups):
                for g in groups:
                    for i, (name, dst) in enumerate((("q", qT), ("k", kT))):
                        ps = ring.bank(name, u, g)
                        dve.wait_ge(*rounded_ready.at(2 * (GROUPS * u + g) + i + 1))
                        dve.scalar_tensor_tensor(dst[u][:, g, :], rounded[i][:].bitcast(F32), split[:, i:i + 1], ps[:],
                                                 ALU.mult, ALU.add).then_inc(ring.read(name, u, g), 1)

            def out_step(u):
                s = u
                ps = ring.wait(dve, "y", u)
                flat = lambda a: a.rearrange("p t n -> p (t n)")
                dve.tensor_tensor(flat(r[s][:]), ps[:], flat(x[s][:]), ALU.add).then_inc(ring.read("y", u), 1)
                ring.wait_read(dve, "y", u)
                normalise(s, r[s], hn[s], hn_ready)
                dve.tensor_tensor(flat(acc_all[:, bass.ds((it * U + u) * TG, TG), :]), flat(r[s][:]), flat(x[s][:]),
                                  ALU.add).then_inc(acc_ready.sem, 1)

            def pair_step(g):
                u, p = divmod(g, PAIRS)
                if u < U:
                    for i in range(2):
                        ps = ring.wait(dve, "s", u, p, i)
                        dve.tensor_reduce(negmax[:, (2 * g + i) % NPR, :], ps[:].rearrange("q (t k) -> q t k", t=TG),
                                          AX.X, ALU.max, negate=True).then_inc(negmax_ready.sem, 1)
                if 1 <= g < PAIRS * U + 1:
                    u, p = divmod(g - 1, PAIRS)
                    for i in range(2):
                        n = 2 * (g - 1) + i
                        ring.wait_read(dve, "s", u, p, i)
                        dve.reciprocal(rsums[:, n % NPR, :], sums[:, n % NPR, :]).then_inc(rs_ready.sem, 1)
                if 3 <= g < PAIRS * U + 3:
                    u, p = divmod(g - 3, PAIRS)
                    for i in range(2):
                        n = 2 * (g - 3) + i
                        ps = ring.wait(dve, "pT", u, p, i)
                        if n >= NPR:
                            dve.wait_ge(*o_full.at((n - NPR) // 2 + 1))
                        dve.tensor_copy(pT[:, n % NPR].rearrange("k t q -> k (t q)"), ps[:])\
                            .then_inc(ring.read("pT", u, p, i), 1)

            steps = dict(norm1=norm1, qk01=lambda u: split_qk(u, (0, 1)), qk23=lambda u: split_qk(u, (2, 3)), out=out_step)
            with dve.Fori(0, NG // U) as it:
                chain = Chain(dve, dve_chain)
                run_steps(stages, PAIRS, U, 5, steps, pair_step)
                meet.join(dve, "vector")

        @block.gpsimd
        def _(pool):
            pool.iota(iota[:], pattern=[[-1, P]], base=P, channel_multiplier=1).then_inc(mask_iota, 1)
            pool.wait_ge(mask_iota, 2)
            pool.affine_select(out=mask_f[:], in_=mask_f[:], compare_op=ALU.is_ge, fill=-MASKED, base=0,
                               pattern=[[-1, P]], channel_multiplier=1).then_inc(mask_iota, 1)
            pool.sem_inc(ready, 1)
            pool.wait_ge(ready, 4)
            count = {"mv": 0}

            def root(u):
                s = u
                count["mv"] += TG
                pool.wait_ge(*mv_ready.at(count["mv"]))
                chain(pool.tensor_scalar(rstd[s][:, 0:TG], mv[s][:, :, 1], LN_EPS, None, ALU.add))
                pool.tensor_tensor(rstd[s][:, TG:2 * TG], rstd[s][:, 0:TG], K["eps_half"][:, 0:TG], ALU.pow)\
                    .then_inc(rstd_ready.sem, 1)

            def pair_step(g):
                if 1 <= g < PAIRS * U + 1:
                    for i in range(2):
                        n = 2 * (g - 1) + i
                        pool.wait_ge(*rs_ready.at(n + 1))
                        for t in range(TG):
                            ins = pool.tensor_scalar(probs[:, n % NPR, t, :], probs[:, n % NPR, t, :],
                                                     rsums[:, n % NPR, t:t + 1], 1.0, ALU.mult, ALU.mult)
                        ins.then_inc(p_ready.sem, 1)

            steps = dict(norm1=root, out=root)
            with pool.Fori(0, NG // U) as it:
                chain = Chain(pool, pool_chain)
                run_steps(stages, PAIRS, U, 5, steps, pair_step)
                meet.lead(pool, first, last)
            pool.sem_clear(range(FIRST_SEM, meet.arrived.num))

        @block.sync
        def _(sy):
            for dst, src in loads:
                sy.dma_start(dst, src, allow_slow_non_contiguous=True).then_inc(loaded, 16)
            sy.sem_inc(ready, 1)
            xin = x_in.rearrange("b n d -> (b n) d").rearrange("(p g t) d -> g p t d", p=P, t=TG)
            with sy.Fori(0, NG // U) as it:
                for u in range(U):
                    if u >= XS:
                        sy.wait_ge(*acc_ready.at(u - XS + 1))
                    sy.dma_start(x[u][:], xin[it * U + u]).then_inc(x_loaded[u % XS], 16)
                meet.join(sy, "sync")


def experts(nc, A, K, hT_all, acc_all, out):
    U = 2
    with ExitStack() as ctx:
        def sb(name, shape, dt=F32):
            return ctx.enter_context(nc.sbuf_tensor(name, shape, dt))

        sems = []

        def sem(name):
            s = ctx.enter_context(nc.semaphore(name, num=FIRST_SEM + len(sems)))
            sems.append(s)
            return s

        def two(name, shape, dt=F32):
            return [sb(f"{name}{i}", shape, dt) for i in range(2)]

        W = TG * P
        wr = sb("e_router", [P, NE])
        w1 = sb("e_w1", [P, NE, F])
        w2 = sb("e_w2", [P, NE, FC, D])
        before = sb("e_before", [P, P])
        rev = sb("e_rev", [P, TC, NE])
        rev_i = sb("e_rev_i", [P, TC, NE], I32)
        small = sb("e_small", [P, 6, TC])
        prob = sb("e_prob", [P, TC, NE])
        work = [sb(f"e_work{i}", [P, TC, NE]) for i in range(4)]
        total = sb("e_total", [P, NE])
        wts = sb("e_weights", [P, TC, NE])
        hT = two("e_hT", [P, W])
        wg = two("e_wg", [P, TG, NE])
        hid = two("e_hid", [P, FC, W])
        r = two("e_r", [P, TG, D])
        y = two("e_y", [P, TG, D])
        stats = two("e_stats", [P, TG, 6])
        mv = two("e_mv", [P, TG, 2])
        rstd = two("e_rstd", [P, 2 * TG])
        banks = [ctx.enter_context(nc.psum_tensor(f"pe{i}", [P, 512], F32)) for i in range(8)]

        loaded = sem("e_loaded")
        rev_ready = sem("e_rev_ready")
        before_ready = sem("e_before_ready")
        logits_ready = sem("e_logits")
        step = sem("e_route_step")
        dve_setup = sem("e_dve_setup")
        pool_setup = sem("e_pool_setup")
        ready = sem("e_ready")
        meet = Meeting(sem, ["sync", "scalar", "tensor", "vector"])
        n_setup = len(sems)
        ring = Ring(banks, sem)
        in_ready = Counted(sem("e_inputs_ready"))
        mv_ready = Counted(sem("e_moments_ready"))
        rstd_ready = Counted(sem("e_roots_ready"))
        y_ready = Counted(sem("e_y_ready"))
        stored = Counted(sem("e_stored"))
        dve_chain = sem("e_dve_chain")
        pool_chain = sem("e_pool_chain")
        first, last = sems[n_setup].num, sems[-1].num
        loads = [(wr[:], A["L1_ffn_router_weight"])] + [
            (w1[:, e, :], A["L1_ffn_moe_w1"][e]) for e in range(NE)
        ] + [
            (w2[:, e], A["L1_ffn_moe_w2"][e].rearrange("(c p) n -> p c n", p=P)) for e in range(NE)
        ]

        block = ctx.enter_context(nc.Block())

        @block.tensor
        def _(pe):
            pe.wait_ge(loaded, 16 * len(loads))
            for c in range(TC):
                mm = pe.matmul(banks[0][:, c * NE:(c + 1) * NE], hT_all[:, c, :], wr[:], start=True, stop=True)
            mm.then_inc(logits_ready, 1)
            pe.wait_ge(step, 3)
            pe.wait_ge(before_ready, 1)
            pe.matmul(banks[1][:, 0:NE], before[:], total[:], start=True, stop=True).then_inc(step, 1)
            pe.wait_ge(ready, 3)

            def up(u, e):
                for c in range(FC):
                    ps = ring.open(pe, "up", u, e, c)
                    pe.matmul(ps[:], w1[:, e, c * P:(c + 1) * P], hT[u % 2][:], start=True, stop=True)\
                        .then_inc(ring.filled("up", u, e, c), 1)

            def down(u, e):
                b = e % 2
                for c in range(FC):
                    ring.wait_read(pe, "up", u, e, c)
                ps = ring.open(pe, "down", u, e)
                for t in range(TG):
                    for c in range(FC):
                        mm = pe.matmul(ps[:, t * P:(t + 1) * P], hid[b][:, c, t * P:(t + 1) * P], w2[:, e, c, :],
                                       start=(c == 0), stop=(c == FC - 1))
                mm.then_inc(ring.filled("down", u, e), 1)

            with pe.Fori(0, NG // U) as it:
                for n in range(U * NE + 1):
                    if n < U * NE:
                        if n % NE == 0:
                            pe.wait_ge(*in_ready.at(2 * (n // NE + 1)))
                        up(n // NE, n % NE)
                    if n >= 1:
                        down((n - 1) // NE, (n - 1) % NE)
                meet.join(pe, "tensor")

        @block.scalar
        def _(act):
            act.wait_ge(step, 1)
            act.activation(prob[:], prob[:], ACT.Exp).then_inc(step, 1)
            act.wait_ge(ready, 3)
            with act.Fori(0, NG // U) as it:
                for n in range(U * NE):
                    u, e = n // NE, n % NE
                    if n >= 2:
                        ring.wait(act, "down", (n - 2) // NE, (n - 2) % NE)
                    for c in range(FC):
                        ps = ring.wait(act, "up", u, e, c)
                        act.activation(hid[e % 2][:, c, :], ps[:], ACT.Gelu).then_inc(ring.read("up", u, e, c), 1)
                meet.join(act, "scalar")

        @block.vector
        def _(dve):
            chain = Chain(dve, dve_setup)

            def wide(a):
                return a.unsqueeze(2).broadcast_to([P, TC, NE])

            dve.wait_ge(logits_ready, 1)
            l = banks[0][:, 0:TC * NE].rearrange("p (c e) -> p c e", e=NE)
            chain(dve.tensor_reduce(small[:, 0, :], l, AX.X, ALU.max))
            dve.tensor_tensor(prob[:], l, wide(small[:, 0, :]), ALU.subtract).then_inc(step, 1)
            dve.wait_ge(step, 2)
            chain(dve.tensor_reduce(small[:, 1, :], prob[:], AX.X, ALU.add))
            chain(dve.reciprocal(small[:, 2, :], small[:, 1, :]))
            chain(dve.tensor_tensor(prob[:], prob[:], wide(small[:, 2, :]), ALU.mult))
            dve.wait_ge(rev_ready, 1)
            chain(dve.tensor_copy(rev[:], rev_i[:]))
            rest, pick, chosen, spare = (w[:] for w in work)
            src = prob[:]
            for k in range(2):
                chain(dve.tensor_reduce(small[:, 3 + k, :], src, AX.X, ALU.max))
                chain(dve.tensor_tensor(pick, src, wide(small[:, 3 + k, :]), ALU.is_equal))
                chain(dve.tensor_tensor(pick, pick, rev[:], ALU.mult))
                chain(dve.tensor_reduce(small[:, 5, :], pick, AX.X, ALU.max))
                if k == 0:
                    chain(dve.tensor_tensor(chosen, pick, wide(small[:, 5, :]), ALU.is_equal))
                    chain(dve.scalar_tensor_tensor(rest, chosen, -2.0, prob[:], ALU.mult, ALU.add))
                    src = rest
                else:
                    chain(dve.tensor_tensor(pick, pick, wide(small[:, 5, :]), ALU.is_equal))
                    chain(dve.tensor_tensor(chosen, chosen, pick, ALU.add))
            dve.tensor_reduce(total[:], chosen.rearrange("p c e -> p e c"), AX.X, ALU.add).then_inc(step, 1)
            a, b = rest, pick
            chain(dve.tensor_copy(a, chosen))
            k = 1
            while k < TC:
                chain(dve.tensor_copy(b[:, 0:k], a[:, 0:k]))
                chain(dve.tensor_tensor(b[:, k:TC], a[:, k:TC], a[:, 0:TC - k], ALU.add))
                a, b = b, a
                k *= 2
            chain(dve.tensor_tensor(b, a, chosen, ALU.subtract))
            dve.wait_ge(step, 4)
            chain(dve.tensor_copy(total[:], banks[1][:, 0:NE]))
            chain(dve.tensor_tensor(b, b, total[:].unsqueeze(1).broadcast_to([P, TC, NE]), ALU.add))
            chain(dve.tensor_scalar(b, b, CAP - 0.5, None, ALU.is_le))
            chain(dve.tensor_tensor(b, b, chosen, ALU.mult))
            chain(dve.tensor_tensor(small[:, 0, :], small[:, 3, :], small[:, 4, :], ALU.add))
            chain(dve.reciprocal(small[:, 1, :], small[:, 0, :]))
            chain(dve.tensor_tensor(wts[:], prob[:], wide(small[:, 1, :]), ALU.mult))
            chain(dve.tensor_tensor(wts[:], wts[:], b, ALU.mult))
            dve.sem_inc(ready, 1)
            dve.wait_ge(ready, 3)

            def finish(u):
                s = u % 2
                for t in range(TG):
                    chain(dve.bn_stats(stats[s][:, t, :], r[s][:, t, :]))
                for t in range(TG):
                    dve.bn_aggr(mv[s][:, t, :], stats[s][:, t, :]).then_inc(mv_ready.sem, 1)
                dve.wait_ge(*rstd_ready.at(u + 1))
                for t in range(TG):
                    dve.tensor_scalar(y[s][:, t, :], r[s][:, t, :], mv[s][:, t, 0:1], rstd[s][:, TG + t:TG + t + 1],
                                      ALU.subtract, ALU.mult).then_inc(y_ready.sem, 1)

            with dve.Fori(0, NG // U) as it:
                chain = Chain(dve, dve_chain)
                for u in range(U):
                    tiles = bass.ds((it * U + u) * TG, TG)
                    dve.tensor_copy(hT[u][:], hT_all[:, tiles, :].rearrange("p t n -> p (t n)")).then_inc(in_ready.sem, 1)
                    dve.tensor_copy(wg[u][:], wts[:, tiles, :])
                    dve.tensor_copy(r[u][:], acc_all[:, tiles, :]).then_inc(in_ready.sem, 1)
                dve.wait_ge(*in_ready.at(2 * U))
                for u in range(U):
                    for e in range(NE):
                        ps = ring.wait(dve, "down", u, e)
                        for t in range(TG):
                            ins = dve.scalar_tensor_tensor(r[u][:, t, :], ps[:, t * P:(t + 1) * P], wg[u][:, t, e:e + 1],
                                                           r[u][:, t, :], ALU.mult, ALU.add)
                        ins.then_inc(ring.read("down", u, e), 1)
                        ring.wait_read(dve, "down", u, e)
                    finish(u)
                meet.join(dve, "vector")

        @block.gpsimd
        def _(pool):
            pool.iota(rev_i[:], pattern=[[0, TC], [-1, NE]], base=NE, channel_multiplier=0).then_inc(rev_ready, 1)
            pool.memset(before[:], 1.0).then_inc(pool_setup, 1)
            pool.wait_ge(pool_setup, 1)
            pool.affine_select(out=before[:], in_=before[:], compare_op=ALU.is_ge, fill=0.0, base=-1,
                               pattern=[[1, P]], channel_multiplier=-1).then_inc(before_ready, 1)
            pool.sem_inc(ready, 1)
            pool.wait_ge(ready, 3)
            with pool.Fori(0, NG // U) as it:
                chain = Chain(pool, pool_chain)
                for u in range(U):
                    pool.wait_ge(*mv_ready.at(TG * (u + 1)))
                    chain(pool.tensor_scalar(rstd[u][:, 0:TG], mv[u][:, :, 1], LN_EPS, None, ALU.add))
                    pool.tensor_tensor(rstd[u][:, TG:2 * TG], rstd[u][:, 0:TG], K["eps_half"][:, 0:TG], ALU.pow)\
                        .then_inc(rstd_ready.sem, 1)
                meet.lead(pool, first, last)
            pool.sem_clear(range(FIRST_SEM, meet.arrived.num))

        @block.sync
        def _(sy):
            for dst, src in loads:
                sy.dma_start(dst, src).then_inc(loaded, 16)
            sy.sem_inc(ready, 1)
            xo = out.rearrange("b n d -> (b n) d").rearrange("(p g t) d -> g p t d", p=P, t=TG)
            with sy.Fori(0, NG // U) as it:
                for u in range(U):
                    sy.wait_ge(*y_ready.at(TG * (u + 1)))
                    sy.dma_start(xo[it * U + u], y[u][:]).then_inc(stored.sem, 16)
                sy.wait_ge(*stored.at(16 * U))
                meet.join(sy, "sync")


def kernel(**inputs):
    import concourse.bacc as bacc
    from concourse.bass_utils import run_bass_kernel_spmd

    nc = bacc.Bacc("TRN2", target_bir_lowering=False, num_devices=1)
    arrays, A = {}, {}
    for name, a in inputs.items():
        a = np.ascontiguousarray(a)
        arrays[f"in_{name}_dram"] = a
        A[name] = nc.dram_tensor(f"in_{name}_dram", a.shape, mybir.dt.from_np(a.dtype), kind="ExternalInput").ap()
    out = nc.dram_tensor("out_0_dram", (B, N, D), F32, kind="ExternalOutput").ap()
    build(nc, A, out)
    r = run_bass_kernel_spmd(nc, [arrays], core_ids=[0])
    return r.results[0]["out_0_dram"]
```

```python
from contextlib import ExitStack
import math

import numpy as np
import concourse.bass as bass
from concourse import mybir

F32 = mybir.dt.float32
F32R = mybir.dt.float32r
BF16 = mybir.dt.bfloat16
I32 = mybir.dt.int32
ALU = mybir.AluOpType
ACT = mybir.ActivationFunctionType
AX = mybir.AxisListType

P = 128
B, N, D = 16, 256, 128
NT = N // P
S_CTX = 64
LN_EPS = 1e-5
FIRST_SEM = 100

H0, DH0 = 16, 8
NS = 64
STD, SPLAT = 0.6, 0.4
GROUPS = H0 // 4


class Counted:

    def __init__(self, sem):
        self.sem = sem

    def at(self, n):
        return self.sem, n


class Ring:

    def __init__(self, banks, sem):
        self.banks = banks
        self.full = [sem(f"bank{i}_full") for i in range(len(banks))]
        self.free = [sem(f"bank{i}_free") for i in range(len(banks))]
        self.uses = [0] * len(banks)
        self.turn = 0
        self.jobs = {}

    def open(self, pe, *name):
        i = self.turn
        self.turn = (i + 1) % len(self.banks)
        assert name not in self.jobs, name
        if self.uses[i]:
            pe.wait_ge(self.free[i], self.uses[i])
        self.uses[i] += 1
        self.jobs[name] = (i, self.uses[i])
        return self.banks[i]

    def filled(self, *name):
        return self.full[self.jobs[name][0]]

    def wait(self, eng, *name):
        i, n = self.jobs[name]
        eng.wait_ge(self.full[i], n)
        return self.banks[i]

    def wait_read(self, eng, *name):
        i, n = self.jobs[name]
        eng.wait_ge(self.free[i], n)

    def bank(self, *name):
        return self.banks[self.jobs[name][0]]

    def read(self, *name):
        return self.free[self.jobs[name][0]]


class Chain:

    def __init__(self, eng, sem):
        self.eng, self.sem, self.n = eng, sem, 0

    def __call__(self, ins):
        self.n += 1
        ins.then_inc(self.sem, 1)
        self.eng.wait_ge(self.sem, self.n)


def run_steps(stages, per_item, items, drain, steps, pipeline_step):
    for g in range(min(o for o, _ in stages), per_item * (items - 1) + max(o for o, _ in stages) + 1):
        if 0 <= g < per_item * items + drain:
            pipeline_step(g)
        for offset, name in sorted(stages, key=lambda stage: -stage[0]):
            u, rest = divmod(g - offset, per_item)
            if rest == 0 and 0 <= u < items and name in steps:
                steps[name](u)


class Sets:

    def __init__(self, items):
        self.items = items

    def __getitem__(self, u):
        return self.items[u % len(self.items)]


def row(v):
    return v.rearrange("(a n) -> a n", a=1)


def col(v):
    return v.rearrange("(n a) -> n a", a=1)


def build(nc, A, out):
    x_mid = nc.dram_tensor("x_mid", [B, N, D], F32, kind="Internal").ap()
    x_mid2 = nc.dram_tensor("x_mid2", [B, N, D], F32, kind="Internal").ap()
    with ExitStack() as ctx:
        def sb(name, shape, dt=F32):
            return ctx.enter_context(nc.sbuf_tensor(name, shape, dt))

        K = {}
        K["ident"] = sb("ident", [P, P])
        K["ones_row"] = sb("ones_row", [1, P])
        K["eps_half"] = sb("minus_half", [P, 64])
        K["split"] = sb("split_rows", [P, 2])
        K["thr"] = sb("thresholds", [P, 8], I32)
        K["w1"] = sb("ffn_w1", [P, 512])
        K["w2"] = sb("ffn_w2", [P, 4, P])
        K["b1"] = sb("ffn_b1", [P, 4])
        K["b2c"] = sb("ffn_b2_col", [P, 1])
        loop_1(nc, A, K, x_mid)
        loop_2(nc, A, K, x_mid, x_mid2)
        phase_3(nc, A, K, x_mid2, out)




class Meeting:

    def __init__(self, sem, names):
        self.arrived = sem("engines_arrived")
        self.go = {n: sem(f"{n}_may_go_on") for n in names}

    def join(self, eng, name):
        eng.drain().then_inc(self.arrived, 1)
        eng.wait_ge(self.go[name], 1)
        eng.sem_inc(self.go[name], -1)

    def lead(self, pool, first, last):
        pool.drain().then_inc(self.arrived, 1)
        pool.wait_ge(self.arrived, len(self.go) + 1)
        pool.sem_clear(range(first, last + 1))
        pool.sem_clear(self.arrived)
        for s in self.go.values():
            pool.sem_inc(s, 1)


def loop_1(nc, A, K, x_mid):
    U = 8
    with ExitStack() as ctx:
        def sb(name, shape, dt=F32):
            return ctx.enter_context(nc.sbuf_tensor(name, shape, dt))

        sems = []

        def sem(name):
            s = ctx.enter_context(nc.semaphore(name, num=FIRST_SEM + len(sems)))
            sems.append(s)
            return s

        ident, ones_row = K["ident"], K["ones_row"]
        wq = sb("wq_pad", [P, GROUPS, 4, 32])
        wk = sb("wk_pad", [P, GROUPS, 4, 32])
        split_i = sb("split_iota", [P, 2], I32)
        split = K["split"]
        wv = sb("wv", [P, D])
        wg = sb("wg", [P, D])
        bg = sb("bg", [P, 2])
        wo_pad = sb("wo_pad", [P, GROUPS, D])
        wo = sb("wo", [P, D])
        we = sb("we", [P, 64])
        be = sb("be", [P, 1])
        wt = sb("wt", [P, NS // 2, 64])
        bt_raw = sb("bt_raw", [NS, 64])
        bt = sb("bt_T", [64, NS])
        wd = sb("wd_aug", [65, D])
        sp_raw = sb("splat_raw", [NS, D])
        sp = sb("splat_T", [P, NS])
        sp_sq = sb("splat_sq", [NS, D])
        s2 = sb("splat_norm", [NS, 1])
        scl = sb("splat_scale", [NS, 4])
        imp = sb("splat_imp", [NS, 2])
        ones64 = sb("ones64", [P, 64])
        wv_raw = sb("xwv_raw", [P, D])
        wo_raw = sb("xwo_raw", [P, D])
        wv_x = sb("xwv_T", [P, D])
        wo_x = sb("xwo_T", [P, D])
        bv_x = sb("xbv", [P, 1])
        bo_x = sb("xbo", [1, D])
        mags = sb("magnitudes", [P, 1029])
        need = sb("ranks", [P, 8])
        bit = sb("bit", [P, 1], I32)
        cand = sb("candidates", [P, 8], I32)
        at_least = sb("at_least", [P, 4, 512], BF16)
        at_least_small = sb("at_least_small", [P, 16])
        small_counts = sb("small_counts", [P, 4])
        ones_bf = sb("ones_bf", [P, P], BF16)
        ones_sq = sb("ones_sq", [P, P])
        counts = sb("counts", [P, 8])
        keep = sb("keep", [P, 8], I32)
        def two(name, shape, dt=F32):
            return Sets([sb(f"{name}{i}", shape, dt) for i in range(2)])

        SETS = 3
        x = Sets([sb(f"x{i}", [P, NT, D]) for i in range(SETS)])
        c = Sets([sb(f"c{i}", [S_CTX, D]) for i in range(SETS)])
        xT = two("xT", [P, N])
        xsqT = two("xsqT", [P, N])
        rounded = two("qk_rounded", [P, 2 * N], F32R)
        qT = two("qT", [P, GROUPS, N], F32R)
        kT = two("kT", [P, GROUPS, N], F32R)
        v = two("v", [P, NT, H0, 32])
        gate = two("gateT", [P, N])
        d2 = two("d2", [NS, N])
        infl = two("infl", [NS, N])
        infl_n = two("infl_n", [NS, N])
        total = two("total", [NS, 2])
        infl_tm = two("infl_tm", [P, NT, NS])
        gath = two("gath", [P, NS])
        enc = two("enc", [P, NS // 2, 2])
        trans = two("trans", [65, NS])
        dec = two("dec", [NS, D])
        cT = two("cT", [P, S_CTX])
        vx = two("vx", [P, N])
        vsum = two("vsum", [P, 2])
        oT = two("oT", [P, GROUPS, N])
        flowg = two("flowg", [P, N])
        r = two("r", [P, NT, D])
        stats = two("stats", [P, NT, 6])
        mv = two("mv", [P, NT, 2])
        rstd = two("rstd", [P, 2 * NT])
        NP_ = 8
        probs = sb("probs", [P, NP_, NT, N])
        pT = sb("pT", [P, NP_, 2, NT, P])
        negmax = sb("negmax", [P, 2, H0, NT])
        sums = sb("sums", [P, 2, H0, NT])
        rsums = sb("rsums", [P, 2, H0, NT])

        banks = [ctx.enter_context(nc.psum_tensor(f"ps{i}", [P, 512], F32)) for i in range(6)]
        o_banks = [ctx.enter_context(nc.psum_tensor(f"po{i}", [P, 2, N], F32)) for i in range(2)]

        loaded = sem("weights_loaded")
        cleared = sem("weights_cleared")
        pool_ready = sem("pool_constants")
        wT_ps = sem("weights_transposed")
        wT_ready = sem("weights_T_ready")
        dve_setup = sem("dve_setup")
        pool_setup = sem("pool_setup")
        act_setup = sem("act_setup")
        setup_done = sem("setup_done")
        meet = Meeting(sem, ["sync", "scalar", "tensor", "vector"])
        n_setup = len(sems)
        ring = Ring(banks, sem)
        x_loaded = [Counted(sem(f"x{i}_loaded")) for i in range(SETS)]
        stored = [Counted(sem(f"x{i}_stored")) for i in range(SETS)]
        negmax_ready = Counted(sem("negmax_ready"))
        rounded_ready = Counted(sem("rounded_ready"))
        oT_ready = Counted(sem("oT_ready"))
        probs_ready = Counted(sem("probs_normalised"))
        rsums_ready = Counted(sem("rsums_ready"))
        pv_done = Counted(sem("pv_done"))
        infl0_ready = Counted(sem("influence_exp"))
        infl_ready = Counted(sem("influence_ready"))
        vx_ready = Counted(sem("vx_ready"))
        mv_ready = Counted(sem("ln_stats_ready"))
        rstd_ready = Counted(sem("rstd_ready"))
        x_ready = Counted(sem("x_ready"))
        cand_ready = Counted(sem("candidates_ready"))
        mask_ready = Counted(sem("masks_ready"))
        small_ready = Counted(sem("small_ready"))
        dve_chain = sem("vector_chain")
        pool_chain = sem("pool_chain")
        first, last = sems[n_setup].num, sems[-1].num

        loads = [
            (w[:, :, :, DH0 * i:DH0 * (i + 1)], A[name].rearrange("k (g j d) -> k g j d", g=GROUPS, j=4))
            for i in range(3) for w, name in ((wq, "L0_attn_Wq"), (wk, "L0_attn_Wk"))
        ] + [
            (wv[:], A["L0_attn_Wv"]), (wg[:], A["L0_attn_Wg"]), (bg[:, 0:1], col(A["L0_attn_bg"])),
            (wo[:], A["L0_attn_Wo"]),
        ] + [
            (wo_pad[32 * j:32 * j + DH0], A["L0_attn_Wo"].rearrange("(g j d) n -> j d g n", g=GROUPS, j=4)[j])
            for j in range(4)
        ] + [
            (we[:], A["L0_attn_We"]), (be[0:64, :], col(A["L0_attn_be"])), (be[64:128, :], col(A["L0_attn_be"])),
            (wt[0:64], A["L0_attn_Wt"].rearrange("(j h) d e -> h d j e", h=2)[0]),
            (wt[64:128], A["L0_attn_Wt"].rearrange("(j h) d e -> h d j e", h=2)[1]),
            (bt_raw[:], A["L0_attn_bt"]), (wd[0:64], A["L0_attn_Wd"]), (wd[64:65], row(A["L0_attn_bd"])),
            (sp_raw[:], A["L0_attn_splat_positions"]),
            (scl[:, 0:1], col(A["L0_attn_splat_scales"])), (imp[:, 0:1], col(A["L0_attn_splat_importance"])),
            (wv_raw[:], A["L0_xattn_Wv"]), (wo_raw[:], A["L0_xattn_Wo"]),
            (bv_x[:], col(A["L0_xattn_bv"])), (bo_x[:], row(A["L0_xattn_bo"])),
            (K["w1"][:], A["L0_ffn_W1"]), (K["w2"][:], A["L0_ffn_W2"].rearrange("(c p) n -> p c n", p=P)),
            (K["b1"][:], A["L0_ffn_b1"].rearrange("(c p) -> p c", p=P)), (K["b2c"][:], col(A["L0_ffn_b2"])),
        ]
        n1, n2 = 512 * D, D
        sizes = [n1, n1, 512, n2]
        ranks = []
        for n in sizes:
            k = max(1, int(n * 0.1 / 2))
            ranks += [k, n - k + 1]

        stages = [
            (-11, "project"), (0, "candidates0"), (0, "masks0"), (1, "distances"), (2, "cross_values"),
            (2, "read_distances"), (2, "gate"), (3, "count0"), (3, "read_cross"), (3, "influence"),
            (4, "influence_tm"), (4, "decide0"), (5, "read_influence_tm"), (6, "gather"), (6, "candidates1"),
            (6, "masks1"), (7, "read_gather"), (8, "encode"), (9, "read_encode"), (9, "count1"), (10, "transform"),
            (10, "decide1"), (11, "read_transform"), (12, "decode"), (13, "out_T0"), (13, "read_decode"),
            (14, "flow"), (15, "read_flow"), (20, "out_T1"), (21, "project_out"), (23, "norm0"), (24, "cross_out"),
            (26, "norm1"),
        ]

        block = ctx.enter_context(nc.Block())

        @block.tensor
        def _(pe):
            pe.wait_ge(loaded, 16 * len(loads))
            pe.wait_ge(pool_ready, 1)
            t_ps = banks[0]
            pe.transpose(t_ps[:, 0:P], wv_raw[:], ident[:])
            pe.transpose(t_ps[:, P:2 * P], wo_raw[:], ident[:])
            pe.transpose(t_ps[:, 256:256 + NS], sp_raw[:], ident[0:NS, 0:NS])
            pe.transpose(t_ps[0:64, 320:320 + NS], bt_raw[:], ident[0:NS, 0:NS]).then_inc(wT_ps, 1)
            pe.wait_ge(setup_done, 3)

            def project(u):
                s = u
                pe.wait_ge(*x_loaded[u % SETS].at(32 * (u // SETS + 1)))
                ps = ring.open(pe, "xT", u)
                for t in range(NT):
                    pe.transpose(ps[:, t * P:(t + 1) * P], x[s][:, t, :], ident[:])
                pe.transpose(ps[:, 256:256 + S_CTX], c[s][:], ident[0:S_CTX, 0:S_CTX]).then_inc(ring.filled("xT", u), 1)
                ring.wait_read(pe, "xT", u)
                for name, w in (("q", wq), ("k", wk)):
                    for half in range(2):
                        ps = ring.open(pe, name, u, half)
                        for g in range(2):
                            mm = pe.matmul(ps[:, g * N:(g + 1) * N],
                                           w[:, 2 * half + g, :, :].rearrange("p j d -> p (j d)"), xT[s][:],
                                           start=True, stop=True)
                        mm.then_inc(ring.filled(name, u, half), 1)
                ps = ring.open(pe, "vg", u)
                for t in range(NT):
                    pe.matmul(ps[:, t * P:(t + 1) * P], xT[s][:, t * P:(t + 1) * P], wv[:], start=True, stop=True)
                pe.matmul(ps[:, N:2 * N], wg[:], xT[s][:], start=True, stop=True).then_inc(ring.filled("vg", u), 1)

            def distances(u):
                s = u
                ps = ring.open(pe, "d2", u)
                pe.matmul(ps[0:NS, 0:N], sp[:], xT[s][:], start=True, stop=False)
                pe.matmul(ps[0:NS, 0:N], ones64[:], xsqT[s][:], start=False, stop=True).then_inc(ring.filled("d2", u), 1)

            def cross_values(u):
                s = u
                ps = ring.open(pe, "vx", u)
                pe.matmul(ps[:, 0:S_CTX], wv_x[:], cT[s][:], start=True, stop=True).then_inc(ring.filled("vx", u), 1)

            def influence_tm(u):
                s = u
                pe.wait_ge(*infl_ready.at(u + 1))
                ps = ring.open(pe, "infl_tm", u)
                for t in range(NT):
                    mm = pe.transpose(ps[:, t * NS:(t + 1) * NS], infl_n[s][:, t * P:(t + 1) * P], ident[0:NS, 0:NS])
                mm.then_inc(ring.filled("infl_tm", u), 1)

            def gather(u):
                s = u
                ring.wait_read(pe, "infl_tm", u)
                ps = ring.open(pe, "gath", u)
                for t in range(NT):
                    mm = pe.matmul(ps[:, 0:NS], x[s][:, t, :], infl_tm[s][:, t, :], start=(t == 0), stop=(t == NT - 1))
                mm.then_inc(ring.filled("gath", u), 1)

            def encode(u):
                s = u
                ring.wait_read(pe, "gath", u)
                ps = ring.open(pe, "enc", u)
                for h in range(2):
                    mm = pe.matmul(ps[64 * h:64 * h + 64, 0:NS // 2], we[:], gath[s][:, h:NS:2], start=True, stop=True)
                mm.then_inc(ring.filled("enc", u), 1)

            def transform(u):
                s = u
                ring.wait_read(pe, "enc", u)
                ps = ring.open(pe, "trans", u)
                for j in range(NS // 2):
                    mm = pe.matmul(ps[0:64, 2 * j:2 * j + 2], wt[:, j, :], enc[s][:, j, :], start=True, stop=True)
                mm.then_inc(ring.filled("trans", u), 1)

            def decode(u):
                s = u
                ring.wait_read(pe, "trans", u)
                ps = ring.open(pe, "dec", u)
                pe.matmul(ps[0:NS, 0:D], trans[s][:], wd[:], start=True, stop=True).then_inc(ring.filled("dec", u), 1)

            def count(n):
                pe.wait_ge(*mask_ready.at(4 * (n + 1)))
                pe.wait_ge(*small_ready.at(4 * (n + 1)))
                ps = ring.open(pe, "count", n)
                for a in range(4):
                    for q in range(8):
                        pe.matmul(ps[:, a * 64:(a + 1) * 64], ones_bf[:], at_least[:, a, q * 64:(q + 1) * 64],
                                  start=(q == 0), stop=(q == 7))
                pe.matmul(ps[:, 256:260], ones_sq[:], small_counts[:], start=True, stop=True)\
                    .then_inc(ring.filled("count", n), 1)

            def flow(u):
                s = u
                ring.wait_read(pe, "dec", u)
                ps = ring.open(pe, "flow", u)
                pe.matmul(ps[:, 0:N], dec[s][:], infl[s][:], start=True, stop=True).then_inc(ring.filled("flow", u), 1)

            def project_out(u):
                s = u
                pe.wait_ge(*oT_ready.at(2 * (u + 1)))
                ring.wait_read(pe, "flow", u)
                ps = ring.open(pe, "y", u)
                for t in range(NT):
                    for g in range(GROUPS):
                        pe.matmul(ps[:, t * D:(t + 1) * D], oT[s][:, g, t * P:(t + 1) * P], wo_pad[:, g, :],
                                  start=(g == 0), stop=False)
                    mm = pe.matmul(ps[:, t * D:(t + 1) * D], flowg[s][:, t * P:(t + 1) * P], wo[:],
                                   start=False, stop=True)
                mm.then_inc(ring.filled("y", u), 1)

            def cross_out(u):
                s = u
                pe.wait_ge(*vx_ready.at(u + 1))
                ps = ring.open(pe, "yx", u)
                for t in range(NT):
                    pe.matmul(ps[:, t * D:(t + 1) * D], vx[s][:, t * P:(t + 1) * P], wo_x[:], start=True, stop=False)
                    mm = pe.matmul(ps[:, t * D:(t + 1) * D], ones_row[:], bo_x[:], start=False, stop=True)
                mm.then_inc(ring.filled("yx", u), 1)

            def head_step(g):
                u, h = divmod(g, H0)
                if u < U:
                    if h == 0:
                        ring.wait_read(pe, "k", u, 1)
                    q, j = h // 4, 32 * (h % 4)
                    ps = ring.open(pe, "scores", u, h)
                    for t in range(NT):
                        mm = pe.matmul(ps[:, t * N:(t + 1) * N], qT[u][j:j + 3 * DH0, q, t * P:(t + 1) * P],
                                       kT[u][j:j + 3 * DH0, q, :], start=True, stop=True)
                    mm.then_inc(ring.filled("scores", u, h), 1)
                if 4 <= g < H0 * U + 4:
                    n = g - 4
                    pe.wait_ge(*probs_ready.at(n + 1))
                    ps = ring.open(pe, "pT", n)
                    for kt in range(2):
                        for t in range(NT):
                            mm = pe.transpose(ps[:, (kt * NT + t) * P:(kt * NT + t + 1) * P],
                                              probs[:, n % NP_, t, kt * P:(kt + 1) * P], ident[:])
                    mm.then_inc(ring.filled("pT", n), 1)
                if g >= 5:
                    n = g - 5
                    u, h = divmod(n, H0)
                    q, j = h // 4, 32 * (h % 4)
                    if h == 0:
                        ring.wait_read(pe, "vg", u)
                    if u >= 1 and h % 8 == 0:
                        pe.wait_ge(*oT_ready.at(2 * (u - 1) + h // 8 + 1))
                    ring.wait_read(pe, "pT", n)
                    for kt in range(2):
                        mm = pe.matmul(o_banks[q // 2][j:j + 32, q % 2, :], v[u][:, kt, h, :],
                                       pT[:, n % NP_, kt].rearrange("p t n -> p (t n)"),
                                       start=(kt == 0), stop=(kt == 1))
                    mm.then_inc(pv_done.sem, 1)

            steps = dict(project=project, distances=distances, cross_values=cross_values,
                         count0=lambda u: count(2 * u), influence_tm=influence_tm, gather=gather, encode=encode,
                         count1=lambda u: count(2 * u + 1), transform=transform, decode=decode, flow=flow,
                         project_out=project_out, cross_out=cross_out)
            with pe.Fori(0, B // U) as it:
                run_steps(stages, H0, U, 5, steps, head_step)
                meet.join(pe, "tensor")

        @block.scalar
        def _(act):
            act.wait_ge(cleared, 1)
            for dst, src in loads[1::2]:
                act.dma_start(dst, src, allow_slow_non_contiguous=True).then_inc(loaded, 16)
            act.wait_ge(wT_ps, 1)
            act.activation(wv_x[:], banks[0][:, 0:P], ACT.Copy)
            act.activation(wo_x[:], banks[0][:, P:2 * P], ACT.Copy)
            act.activation(sp[:], banks[0][:, 256:256 + NS], ACT.Copy, scale=-2.0)
            act.activation(bt[:], banks[0][0:64, 320:320 + NS], ACT.Copy).then_inc(setup_done, 1)
            act.wait_ge(setup_done, 3)

            def project(u):
                s = u
                ps = ring.wait(act, "xT", u)
                act.activation(xT[s][:], ps[:, 0:N], ACT.Copy)
                act.activation(xsqT[s][:], ps[:, 0:N], ACT.Square)
                act.activation(cT[s][:], ps[:, 256:256 + S_CTX], ACT.Copy).then_inc(ring.read("xT", u), 1)
                halves = [("q", 0), ("q", 1), ("k", 0), ("k", 1)]
                for i, (name, half) in enumerate(halves):
                    ps = ring.wait(act, name, u, half)
                    if i >= 2:
                        ring.wait_read(act, halves[i - 2][0], u, halves[i - 2][1])
                    act.activation(rounded[i][:], ps[:], ACT.Copy).then_inc(rounded_ready.sem, 1)
                ps = ring.wait(act, "vg", u)
                for t in range(NT):
                    act.activation(v[s][:, t, :, 0:DH0],
                                   ps[:, t * P:(t + 1) * P].rearrange("p (h d) -> p h d", h=H0), ACT.Copy)
                act.activation(gate[s][:], ps[:, N:2 * N], ACT.Exp, bias=bg[:, 1:2], scale=-1.0).then_inc(ring.read("vg", u), 1)

            def influence(u):
                s = u
                ring.wait_read(act, "d2", u)
                act.activation(d2[s][:], d2[s][:], ACT.Exp, scale=scl[:, 3:4]).then_inc(infl0_ready.sem, 1)

            def influence_tm(u):
                s = u
                ps = ring.wait(act, "infl_tm", u)
                act.activation(infl_tm[s][:].rearrange("p t n -> p (t n)"), ps[:, 0:NT * NS], ACT.Copy)\
                    .then_inc(ring.read("infl_tm", u), 1)

            def gather(u):
                s = u
                ps = ring.wait(act, "gath", u)
                act.activation(gath[s][:], ps[:, 0:NS], ACT.Copy).then_inc(ring.read("gath", u), 1)

            def encode(u):
                s = u
                ps = ring.wait(act, "enc", u)
                for h in range(2):
                    ins = act.activation(enc[s][64 * h:64 * h + 64, :, h], ps[64 * h:64 * h + 64, 0:NS // 2], ACT.Relu,
                                         bias=be[64 * h:64 * h + 64, :])
                ins.then_inc(ring.read("enc", u), 1)

            def decode(u):
                s = u
                ps = ring.wait(act, "dec", u)
                act.activation(dec[s][:], ps[0:NS, 0:D], ACT.Copy).then_inc(ring.read("dec", u), 1)

            def out_T(u, i):
                act.wait_ge(*pv_done.at(H0 * u + 8 * (i + 1)))
                act.activation(oT[u][:, 2 * i:2 * i + 2, :], o_banks[i][:], ACT.Copy).then_inc(oT_ready.sem, 1)

            def head_step(g):
                u, h = divmod(g, H0)
                if u < U:
                    act.wait_ge(*negmax_ready.at(g + 1))
                    if g >= NP_:
                        ring.wait(act, "pT", g - NP_)
                    ps = ring.bank("scores", u, h)
                    for t in range(NT):
                        ins = act.activation(probs[:, g % NP_, t, :], ps[:, t * N:(t + 1) * N], ACT.Exp,
                                             bias=negmax[:, u % 2, h, t:t + 1], accum_out=sums[:, u % 2, h, t:t + 1])
                    ins.then_inc(ring.read("scores", u, h), 1)

            steps = dict(project=project, influence=influence, read_influence_tm=influence_tm, read_gather=gather,
                         read_encode=encode, read_decode=decode, out_T0=lambda u: out_T(u, 0),
                         out_T1=lambda u: out_T(u, 1))
            with act.Fori(0, B // U) as it:
                run_steps(stages, H0, U, 5, steps, head_step)
                meet.join(act, "scalar")

        @block.vector
        def _(dve):
            dve.memset(wq[:], 0.0)
            dve.memset(wk[:], 0.0)
            dve.memset(wo_pad[:], 0.0).then_inc(cleared, 1)
            dve.memset(ones_row[:], 1.0)
            dve.memset(ones64[:], 1.0)
            dve.memset(ones_bf[:], 1.0)
            dve.memset(ones_sq[:], 1.0)
            dve.memset(K["eps_half"][:], -0.5)
            for s in range(2):
                dve.memset(v[s][:], 0.0)
                dve.memset(enc[s][:], 0.0)
                dve.memset(trans[s][:], 1.0)
            for i, k in enumerate(ranks):
                dve.memset(need[:, i:i + 1], float(k))
            dve.memset(K["thr"][:], 0)
            dve.memset(bit[:], 1 << 30)
            setup = Chain(dve, dve_setup)
            dve.wait_ge(pool_ready, 1)
            setup(dve.tensor_scalar(split_i[:, 1:2], split_i[:, 0:1], 3 * DH0, None, ALU.bitwise_and))
            setup(dve.tensor_copy(split[:], split_i[:, 1:2].broadcast_to([P, 2])))
            setup(dve.tensor_scalar(split[:, 0:1], split[:, 0:1], float(DH0), -1.0, ALU.is_equal, ALU.mult))
            setup(dve.tensor_scalar(split[:, 1:2], split[:, 1:2], float(2 * DH0), -1.0, ALU.is_equal, ALU.mult))
            dve.wait_ge(loaded, 16 * len(loads))
            setup(dve.tensor_scalar(wq[:], wq[:], DH0 ** -0.5, None, ALU.mult))
            for lo, hi, w in ((0, 512, K["w1"][:]), (512, 1024, K["w2"][:].rearrange("p c n -> p (c n)")),
                              (1024, 1028, K["b1"][:]), (1028, 1029, K["b2c"][:])):
                setup(dve.tensor_scalar(mags[:, lo:hi].bitcast(I32), w.bitcast(I32), 0x7FFFFFFF, None, ALU.bitwise_and))
            setup(dve.tensor_scalar(bg[:, 1:2], bg[:, 0:1], -1.0, None, ALU.mult))
            setup(dve.tensor_tensor(sp_sq[:], sp_raw[:], sp_raw[:], ALU.mult))
            setup(dve.tensor_reduce(s2[:], sp_sq[:], AX.X, ALU.add))
            setup(dve.tensor_scalar(scl[:, 1:2].bitcast(I32), scl[:, 0:1].bitcast(I32), 0x7FFFFFFF, None, ALU.bitwise_and))
            setup(dve.tensor_scalar(imp[:, 1:2].bitcast(I32), imp[:, 0:1].bitcast(I32), 0x7FFFFFFF, None, ALU.bitwise_and))
            setup(dve.tensor_scalar(scl[:, 1:2], scl[:, 1:2], 1e-6, None, ALU.max))
            setup(dve.tensor_tensor(scl[:, 1:2], scl[:, 1:2], scl[:, 1:2], ALU.mult))
            setup(dve.reciprocal(scl[:, 2:3], scl[:, 1:2]))
            dve.tensor_scalar(scl[:, 3:4], scl[:, 2:3], -0.5, None, ALU.mult).then_inc(setup_done, 1)
            dve.wait_ge(setup_done, 3)

            def link(ins):
                chain(ins)

            def split_qk(u):
                for i, (name, dst, half) in enumerate((("q", qT, 0), ("q", qT, 1), ("k", kT, 0), ("k", kT, 1))):
                    ps = ring.bank(name, u, half)
                    dve.wait_ge(*rounded_ready.at(4 * u + i + 1))
                    dve.scalar_tensor_tensor(dst[u][:, 2 * half:2 * half + 2, :].rearrange("p g n -> p (g n)"),
                                             rounded[i][:].bitcast(F32), split[:, i // 2:i // 2 + 1], ps[:],
                                             ALU.mult, ALU.add).then_inc(ring.read(name, u, half), 1)

            def gate_(u):
                s = u
                ring.wait_read(dve, "vg", u)
                link(dve.tensor_scalar(gate[s][:], gate[s][:], 1 / SPLAT, 1 / SPLAT, ALU.mult, ALU.add))
                link(dve.reciprocal(gate[s][:], gate[s][:]))

            def distances(u):
                s = u
                ps = ring.wait(dve, "d2", u)
                dve.tensor_scalar(d2[s][:], ps[0:NS, 0:N], s2[:], 0.0, ALU.add, ALU.max).then_inc(ring.read("d2", u), 1)

            def influence(u):
                s = u
                dve.wait_ge(*infl0_ready.at(u + 1))
                link(dve.tensor_scalar(infl[s][:], d2[s][:], imp[:, 1:2], None, ALU.mult, ALU.add,
                                       accum_out=total[s][:, 0:1]))
                link(dve.tensor_scalar(total[s][:, 1:2], total[s][:, 0:1], 1e-8, None, ALU.max))
                link(dve.reciprocal(total[s][:, 0:1], total[s][:, 1:2]))
                dve.tensor_scalar(infl_n[s][:], infl[s][:], total[s][:, 0:1], None, ALU.mult).then_inc(infl_ready.sem, 1)

            def transform(u):
                s = u
                ps = ring.wait(dve, "trans", u)
                dve.tensor_tensor(trans[s][0:64, :], ps[0:64, 0:NS], bt[:], ALU.add)\
                    .then_inc(ring.read("trans", u), 1)

            def cross_values(u):
                s = u
                ps = ring.wait(dve, "vx", u)
                dve.tensor_scalar(vx[s][:, 0:S_CTX], ps[:, 0:S_CTX], bv_x[:], None, ALU.add)\
                    .then_inc(ring.read("vx", u), 1)
                ring.wait_read(dve, "vx", u)
                link(dve.tensor_reduce(vsum[s][:, 0:1], vx[s][:, 0:S_CTX], AX.X, ALU.add))
                link(dve.tensor_scalar(vsum[s][:, 1:2], vsum[s][:, 0:1], 1.0 / S_CTX, None, ALU.mult))
                dve.tensor_copy(vx[s][:, S_CTX:N], vsum[s][:, 1:2].to_broadcast([P, N - S_CTX])).then_inc(vx_ready.sem, 1)

            def candidates(n):
                dve.wait_ge(dve_chain, chain.n)
                dve.tensor_scalar(cand[:], K["thr"][:], bit[:, 0:1], None, ALU.bitwise_or).then_inc(cand_ready.sem, 1)
                dve.wait_ge(*cand_ready.at(n + 1))
                cf = cand[:].bitcast(F32)
                for a in range(4):
                    m = mags[:, 1024:1028] if a < 2 else mags[:, 1028:1029]
                    w = 4 if a < 2 else 1
                    dve.tensor_scalar(at_least_small[:, 4 * a:4 * a + w], m, cf[:, 4 + a:5 + a], None, ALU.is_ge, ALU.add,
                                      accum_out=small_counts[:, a:a + 1]).then_inc(small_ready.sem, 1)
                for a in (2, 3):
                    dve.tensor_scalar(at_least[:, a, :], mags[:, 512 * (a // 2):512 * (a // 2) + 512],
                                      cf[:, a:a + 1], None, ALU.is_ge).then_inc(mask_ready.sem, 1)

            def decide(n):
                ps = ring.wait(dve, "count", n)
                link(dve.tensor_reduce(counts[:, 0:4], ps[:, 0:256].rearrange("p (a n) -> p a n", a=4), AX.X, ALU.add))
                dve.tensor_copy(counts[:, 4:8], ps[:, 256:260]).then_inc(ring.read("count", n), 1)
                ring.wait_read(dve, "count", n)
                link(dve.tensor_tensor(keep[:], counts[:], need[:], ALU.is_ge))
                link(dve.copy_predicated(K["thr"][:], keep[:], cand[:]))
                link(dve.tensor_scalar(bit[:], bit[:], 1, None, ALU.logical_shift_right))

            def flow(u):
                s = u
                ps = ring.wait(dve, "flow", u)
                dve.tensor_tensor(flowg[s][:], ps[:, 0:N], gate[s][:], ALU.mult).then_inc(ring.read("flow", u), 1)

            def norm_stats(u, name, n):
                s = u
                ps = ring.wait(dve, name, u)
                dve.tensor_tensor(r[s][:].rearrange("p t n -> p (t n)"), ps[:, 0:N],
                                  x[s][:].rearrange("p t n -> p (t n)"), ALU.add).then_inc(ring.read(name, u), 1)
                ring.wait_read(dve, name, u)
                for t in range(NT):
                    link(dve.bn_stats(stats[s][:, t, :], r[s][:, t, :]))
                for t in range(NT):
                    dve.bn_aggr(mv[s][:, t, :], stats[s][:, t, :]).then_inc(mv_ready.sem, 1)

            def norm_apply(u, n):
                s = u
                dve.wait_ge(*rstd_ready.at(2 * u + n + 1))
                for t in range(NT):
                    dve.tensor_scalar(x[s][:, t, :], r[s][:, t, :], mv[s][:, t, 0:1], rstd[s][:, NT + t:NT + t + 1],
                                      ALU.subtract, ALU.mult).then_inc(x_ready.sem, 1)
                dve.wait_ge(*x_ready.at(NT * (2 * u + n + 1)))

            def head_step(g):
                u, h = divmod(g, H0)
                if u < U:
                    ps = ring.wait(dve, "scores", u, h)
                    dve.tensor_reduce(negmax[:, u % 2, h, :], ps[:].rearrange("p (t n) -> p t n", t=NT), AX.X,
                                      ALU.max, negate=True).then_inc(negmax_ready.sem, 1)
                if 1 <= g < H0 * U + 1:
                    u, h = divmod(g - 1, H0)
                    ring.wait_read(dve, "scores", u, h)
                    dve.reciprocal(rsums[:, u % 2, h, :], sums[:, u % 2, h, :]).then_inc(rsums_ready.sem, 1)
                if 4 <= g < H0 * U + 4:
                    n = g - 4
                    if n >= NP_:
                        dve.wait_ge(*pv_done.at(n - NP_ + 1))
                    ps = ring.wait(dve, "pT", n)
                    dve.tensor_copy(pT[:, n % NP_].rearrange("p k t n -> p (k t n)"), ps[:]).then_inc(ring.read("pT", n), 1)

            steps = dict(project=split_qk, candidates0=lambda u: candidates(2 * u), candidates1=lambda u: candidates(2 * u + 1),
                         decide0=lambda u: decide(2 * u), decide1=lambda u: decide(2 * u + 1),
                         read_distances=distances, gate=gate_, read_cross=cross_values, influence=influence,
                         read_transform=transform, read_flow=flow,
                         project_out=lambda u: norm_stats(u, "y", 0), norm0=lambda u: norm_apply(u, 0),
                         cross_out=lambda u: norm_stats(u, "yx", 1), norm1=lambda u: norm_apply(u, 1))
            with dve.Fori(0, B // U) as it:
                chain = Chain(dve, dve_chain)
                run_steps(stages, H0, U, 5, steps, head_step)
                meet.join(dve, "vector")

        @block.gpsimd
        def _(pool):
            setup = Chain(pool, pool_setup)
            setup(pool.iota(split_i[:, 0:1], pattern=[[0, 1]], base=0, channel_multiplier=1))
            setup(pool.memset(ident[:], 0.0))
            pool.affine_select(out=ident[:], in_=ident[:], compare_op=ALU.not_equal, fill=1.0, base=0,
                               pattern=[[-1, P]], channel_multiplier=1).then_inc(pool_ready, 1)
            pool.wait_ge(pool_ready, 1)
            pool.sem_inc(setup_done, 1)
            pool.wait_ge(setup_done, 3)

            def masks(n):
                pool.wait_ge(*cand_ready.at(n + 1))
                if n:
                    ring.wait(pool, "count", n - 1)
                cf = cand[:].bitcast(F32)
                for a in (0, 1):
                    pool.tensor_scalar(at_least[:, a, :], mags[:, 512 * (a // 2):512 * (a // 2) + 512],
                                       cf[:, a:a + 1], None, ALU.is_ge).then_inc(mask_ready.sem, 1)

            def normalise(u, h):
                pool.wait_ge(*rsums_ready.at(H0 * u + h + 1))
                for t in range(NT):
                    ins = pool.tensor_scalar(probs[:, h % NP_, t, :], probs[:, h % NP_, t, :],
                                             rsums[:, u % 2, h, t:t + 1], STD, ALU.mult, ALU.mult)
                ins.then_inc(probs_ready.sem, 1)

            def roots(u, n):
                s = u
                pool.wait_ge(*mv_ready.at(NT * (2 * u + n + 1)))
                chain(pool.tensor_scalar(rstd[s][:, 0:NT], mv[s][:, :, 1], LN_EPS, None, ALU.add))
                pool.tensor_tensor(rstd[s][:, NT:2 * NT], rstd[s][:, 0:NT], K["eps_half"][:, 0:NT], ALU.pow)\
                    .then_inc(rstd_ready.sem, 1)

            def head_step(g):
                if 1 <= g < H0 * U + 1:
                    normalise(*divmod(g - 1, H0))

            steps = dict(masks0=lambda u: masks(2 * u), masks1=lambda u: masks(2 * u + 1),
                         project_out=lambda u: roots(u, 0), cross_out=lambda u: roots(u, 1))
            with pool.Fori(0, B // U) as it:
                chain = Chain(pool, pool_chain)
                run_steps(stages, H0, U, 5, steps, head_step)
                meet.lead(pool, first, last)
            pool.sem_clear(range(FIRST_SEM, meet.arrived.num))

        @block.sync
        def _(sp_eng):
            sp_eng.wait_ge(cleared, 1)
            for dst, src in loads[0::2]:
                sp_eng.dma_start(dst, src, allow_slow_non_contiguous=True).then_inc(loaded, 16)
            xin = A["x"].rearrange("b (t p) d -> b p t d", p=P)
            xout = x_mid.rearrange("b (t p) d -> b p t d", p=P)
            with sp_eng.Fori(0, B // U) as it:
                def load(u):
                    if u >= SETS:
                        sp_eng.wait_ge(*stored[u % SETS].at(16 * (u // SETS)))
                    sp_eng.dma_start(x[u][:], xin[it * U + u]).then_inc(x_loaded[u % SETS].sem, 16)
                    sp_eng.dma_start(c[u][:], A["ctx_1024"][it * U + u]).then_inc(x_loaded[u % SETS].sem, 16)

                def store(u):
                    sp_eng.wait_ge(*x_ready.at(NT * 2 * (u + 1)))
                    sp_eng.dma_start(xout[it * U + u], x[u][:]).then_inc(stored[u % SETS].sem, 16)

                for u in range(U):
                    if u >= SETS:
                        store(u - SETS)
                    load(u)
                for u in range(U - SETS, U):
                    store(u)
                for i in range(SETS):
                    sp_eng.wait_ge(*stored[i].at(16 * ((U - 1 - i) // SETS + 1)))
                meet.join(sp_eng, "sync")



def alibi_slopes(heads):
    start = 2.0 ** (-2.0 ** (-(math.log2(heads) - 3)))
    return [start * start ** i for i in range(heads)]


H1, DH1 = 16, 64
PAIRS1 = H1 // 2
NULLS = 2
QK_SCALE = 8.0
H2, DH2 = 8, 64
PAIRS2 = H2 // 2
F, FC = 512, 4
NE0 = 8
MASKED = 1e30


def loop_2(nc, A, K, x_in, x_out):
    U = 8
    slopes = alibi_slopes(H1)
    with ExitStack() as ctx:
        def sb(name, shape, dt=F32):
            return ctx.enter_context(nc.sbuf_tensor(name, shape, dt))

        sems = []

        def sem(name):
            s = ctx.enter_context(nc.semaphore(name, num=FIRST_SEM + len(sems)))
            sems.append(s)
            return s

        def two(name, shape, dt=F32):
            return Sets([sb(f"{name}{i}", shape, dt) for i in range(2)])

        def three(name, shape, dt=F32):
            return Sets([sb(f"{name}{i}", shape, dt) for i in range(SETS)])

        SETS = 4

        ident, ones_row = K["ident"], K["ones_row"]
        w1 = [K["w1"], sb("w1_perturbed", [P, F])]
        w2 = [K["w2"], sb("w2_perturbed", [P, FC, D])]
        b1 = [K["b1"], sb("b1_perturbed", [P, FC])]
        b2 = [sb("b2_row", [1, D]), sb("b2_perturbed_row", [1, D])]
        wr = sb("router", [P, NE0])
        br = sb("router_bias", [1, NE0])
        ln_f = sb("ffn_ln", [P, 2])
        ln_a = sb("attn_ln", [P, 2])
        ln_x = sb("xattn_ln", [P, 2])
        ln_c = sb("ctx_ln", [P, 2])
        wq1 = sb("wq1", [P, H1 * DH1])
        wkv1 = sb("wkv1", [P, 2 * H1 * DH1])
        wo1 = sb("wo1", [P, PAIRS1, D])
        qs = sb("q_scale2", [P, 2])
        ks = sb("k_scale2", [P, 1])
        ks_row = sb("k_scale_rows", [32, DH1])
        null_k = sb("null_k", [32, DH1])
        null_k2 = sb("null_k2", [32, 2, DH1])
        null_ss = sb("null_ss", [32, 2])
        null_blk = sb("null_blk", [P, PAIRS1, 2, NULLS])
        null_v = sb("null_v", [4, PAIRS1, P])
        w_null = sb("w_null", [P, H1, NULLS])
        dist = sb("dist", [P, H1, N])
        null_bias = sb("null_bias", [P, NT, H1, NULLS])
        iota_n = sb("iota_n", [P, NT, NULLS], I32)
        iota_nf = sb("iota_nf", [P, NT, NULLS])
        wq2 = sb("wq2", [P, H2 * DH2])
        wkv2 = sb("wkv2", [P, 2 * H2 * DH2])
        wo2 = sb("wo2", [P, PAIRS2, D])
        bo2 = sb("bo2", [1, D])
        x = three("y", [P, NT, D])
        c = three("cc", [S_CTX, D])
        xn = three("xn", [P, NT, D])
        cn = three("cn", [S_CTX, D])
        xT = three("yT", [P, N])
        hT = three("hT", [P, N])
        cnT = three("cnT", [P, S_CTX])
        r = sb("rr", [P, NT, D])
        stats = three("sstats", [P, NT, 6])
        mv = three("smv", [P, NT, 2])
        cmv = three("cmv", [S_CTX, 8])
        rstd = three("srstd", [P, 2 * NT])
        hid = sb("hidden", [P, 2, FC, N])
        mag, tier, tier2 = [hid[:, i // 2, 2 * (i % 2):2 * (i % 2) + 2, :].rearrange("p c n -> p (c n)")
                            for i in range(3)]
        lg = three("logits", [P, NT, NE0])
        pr = three("route", [P, NT, 6])
        q1T = two("q1T", [P, PAIRS1, N])
        k1T = two("k1T", [P, PAIRS1, N])
        v1 = two("v1", [P, NT, H1 * DH1])
        o1T = sb("o1T", [P, PAIRS1, N])
        sq = sb("sq", [P, 2, F])
        wq1T = sq[:].rearrange("p i (c n) -> p (i c) n", n=P)
        qn = sb("qn", [P, 4, F])
        ss = sb("ss", [P, 4, 8])
        rn = sb("rn", [P, 2, 8])
        rnq = two("rnq", [P, NT, H1])
        nneg = two("nneg", [P, NT, H1, NULLS])
        nmin = two("nmin", [P, NT, H1])
        NPR = 6
        probs = sb("probs1", [P, NPR, 2 * (N + NULLS)])

        def keys(i, w):
            return slice(N - w, N) if i == 0 else slice(N + 2 * NULLS, N + 2 * NULLS + w)

        def keys_nulls(i, w):
            return slice(N - w, N + NULLS) if i == 0 else slice(N + NULLS, N + 2 * NULLS + w)

        low = sb("low", [P, NPR, 2])
        sums = sb("sums1", [P, NPR, 2])
        rsums = sb("rsums1", [P, NPR, 2])
        pT = sb("pT1", [P, 4, 3, P])
        pnT = sb("pnT", [4, 2, N])
        q2T = sb("q2T", [P, PAIRS2, N])
        kblk = three("kblk", [P, PAIRS2, P])
        vblk = three("vblk", [P, PAIRS2, P])
        s2n = sb("s2n", [P, NT, H2, S_CTX])
        dist0 = s2n[:, 0].rearrange("p h k -> p (h k)")[:, 0:N]
        iota_i = s2n[:, 1].rearrange("p h k -> p (h k)")[:, 0:N].bitcast(I32)
        m2 = sb("m2", [P, NT, H2])
        z2 = sb("z2", [P, NT, H2])
        rz2 = sb("rz2", [P, NT, H2])
        p2T = sb("p2T", [P, PAIRS2, N])
        o2T = q2T

        banks = [ctx.enter_context(nc.psum_tensor(f"pq{i}", [P, 512], F32)) for i in range(6)]
        o_banks = [ctx.enter_context(nc.psum_tensor(f"pr{i}", [P, 512], F32)) for i in range(2)]

        loaded = sem("l2_weights_loaded")
        cleared = sem("l2_cleared")
        t_ps = sem("l2_setup_transposed")
        t_sb = sem("l2_setup_copied")
        iota_done = sem("iota_done")
        null_done = sem("null_keys_normalised")
        experts_ready = sem("perturbed_expert_ready")
        dve_setup = sem("l2_dve_setup")
        pool_setup = sem("l2_pool_setup")
        null_pow = sem("null_pow")
        ready = sem("l2_setup_ready")
        meet = Meeting(sem, ["sync", "scalar", "tensor", "vector"])
        n_setup = len(sems)
        ring = Ring(banks, sem)
        x_loaded = [Counted(sem(f"y{i}_loaded")) for i in range(SETS)]
        stored = [Counted(sem(f"y{i}_stored")) for i in range(SETS)]
        x_ready = [Counted(sem(f"y_ready{i}")) for i in range(3)]
        xn_ready = [Counted(sem(f"xn_ready{i}")) for i in range(3)]
        cn_ready = Counted(sem("cn_ready"))
        mv_ready = Counted(sem("moments_ready"))
        rstd_ready = Counted(sem("roots_ready"))
        lg_exp = Counted(sem("logits_exp"))
        qk_copied = Counted(sem("q_k_copied"))
        qn_ready = Counted(sem("q_k_normalised"))
        ss_ready = Counted(sem("square_sums_ready"))
        rn_ready = Counted(sem("norms_ready"))
        exp_done = Counted(sem("exps_done"))
        rs_ready = Counted(sem("rsums1_ready"))
        p_ready = Counted(sem("probs1_ready"))
        o1_full = Counted(sem("o1_full"))
        o1_read = Counted(sem("o1_read"))
        s2_exp = Counted(sem("s2_exp"))
        s2_inv = Counted(sem("s2_inverse_sums"))
        p2_ready = Counted(sem("p2_ready"))
        dve_chain = sem("l2_dve_chain")
        pool_chain = sem("l2_pool_chain")
        first, last = sems[n_setup].num, sems[-1].num

        nk = A["L1_attn_null_kv"].rearrange("h (n k) d -> k h n d", k=2)
        loads = [
            (b2[0][:], row(A["L0_ffn_b2"])), (wr[:], A["L0_ffn_Wr"]), (br[:], row(A["L0_ffn_br"])),
            (ln_f[:, 0:1], col(A["L0_ffn_ln_gamma"])), (ln_f[:, 1:2], col(A["L0_ffn_ln_beta"])),
            (ln_a[:, 0:1], col(A["L1_attn_norm_g"])), (ln_a[:, 1:2], col(A["L1_attn_norm_b"])),
            (ln_x[:, 0:1], col(A["L1_xattn_g1"])), (ln_x[:, 1:2], col(A["L1_xattn_b1"])),
            (ln_c[:, 0:1], col(A["L1_xattn_g2"])), (ln_c[:, 1:2], col(A["L1_xattn_b2"])),
            (wq1[:], A["L1_attn_Wq"]), (wkv1[:], A["L1_attn_Wkv"]),
            (wo1[:], A["L1_attn_Wout"].rearrange("(c p) n -> p c n", p=P)),
            (qs[0:64, 0:1], col(A["L1_attn_q_scale"])), (qs[64:128, 0:1], col(A["L1_attn_q_scale"])),
            (ks[0:64], col(A["L1_attn_k_scale"])), (ks[64:128], col(A["L1_attn_k_scale"])),
            (ks_row[:], row(A["L1_attn_k_scale"]).broadcast_to([32, DH1])),
            (wq2[:], A["L1_xattn_Wq"]), (wkv2[:], A["L1_xattn_Wkv"]),
            (wo2[:], A["L1_xattn_Wout"].rearrange("(c p) n -> p c n", p=P)),
            (bo2[:], row(A["L1_xattn_bout"])),
            (null_k[:], nk[0].rearrange("h n d -> (h n) d")),
        ] + [
            (null_v[2 * i:2 * i + 2, :, 64 * i:64 * i + 64], nk[1].rearrange("(p i) n d -> i n p d", i=2)[i])
            for i in range(2)
        ]

        stages = [
            (-12, "ffn_in"), (-12, "ctx"), (-11, "ffn_h"), (-10, "kv2"), (-10, "ffn_up0"), (-9, "ffn_up1"), (-8, "ffn_down"), (-6, "qkv_in"), (-5, "null"), (-5, "qkv_a0"), (-4, "qkv_b0"), (-3, "qkv_a1"), (-2, "qkv_b1"),
            (11, "attn_out"), (13, "x_in"), (14, "x_q"), (15, "x_scores"), (17, "x_pT"), (17, "x_pv"), (18, "x_out"),
        ]

        block = ctx.enter_context(nc.Block())

        @block.tensor
        def _(pe):
            pe.wait_ge(loaded, 16 * len(loads))
            pe.wait_ge(null_done, 1)
            for p in range(PAIRS1):
                pe.transpose(banks[p // 4][:, (p % 4) * P:(p % 4 + 1) * P], wq1[:, p * P:(p + 1) * P], ident[:])
            pe.transpose(banks[2][:, 0:32], null_k2[:].rearrange("q i d -> q (i d)"), ident[0:32, 0:32]).then_inc(t_ps, 1)
            pe.wait_ge(t_sb, 1)
            for p in range(PAIRS1):
                pe.matmul(banks[3][:, 4 * p:4 * p + 4], wq1T[:, p, :], null_blk[:, p].rearrange("q i n -> q (i n)"),
                          start=True, stop=True)
            pe.wait_ge(experts_ready, 1)
            pe.transpose(banks[3][0:1, P:2 * P], K["b2c"][:], ident[:]).then_inc(t_ps, 1)
            pe.wait_ge(ready, 4)

            def transpose_tiles(u, name, src):
                ps = ring.open(pe, name, u)
                for t in range(NT):
                    mm = pe.transpose(ps[:, t * P:(t + 1) * P], src[:, t, :], ident[:])
                mm.then_inc(ring.filled(name, u), 1)

            def ffn_in(u):
                pe.wait_ge(*x_loaded[u % SETS].at(32 * (u // SETS + 1)))
                transpose_tiles(u, "xT", x[u])

            def ffn_h(u):
                s = u
                pe.wait_ge(*xn_ready[0].at(NT * (u + 1)))
                transpose_tiles(u, "hT", xn[s])
                pe.wait_ge(*cn_ready.at(u + 1))
                ps = ring.open(pe, "cnT", u)
                pe.transpose(ps[:, 0:S_CTX], cn[u][:], ident[0:S_CTX, 0:S_CTX]).then_inc(ring.filled("cnT", u), 1)

            def kv2(u):
                s = u
                ring.wait_read(pe, "cnT", u)
                ps = ring.open(pe, "kv2", u)
                for p in range(PAIRS2):
                    pe.matmul(ps[:, p * S_CTX:(p + 1) * S_CTX], wkv2[:, p * P:(p + 1) * P], cnT[s][:], start=True, stop=True)
                for i in range(2):
                    mm = pe.matmul(ps[64 * i:64 * i + 64, 256:512],
                                   cnT[s][:], wkv2[:, H2 * DH2:].rearrange("k (p i d) -> k i p d", i=2, d=DH2)[:, i],
                                   start=True, stop=True)
                mm.then_inc(ring.filled("kv2", u), 1)

            def ffn_up(u, e):
                s = u
                ring.wait_read(pe, "xT", u)
                for half in range(2):
                    ps = ring.open(pe, "up", u, e, half)
                    for i in range(2):
                        ch = 2 * half + i
                        mm = pe.matmul(ps[:, i * N:(i + 1) * N], w1[e][:, ch * P:(ch + 1) * P], xT[s][:], start=True, stop=True)
                    mm.then_inc(ring.filled("up", u, e, half), 1)
                if e == 0:
                    ring.wait_read(pe, "hT", u)
                    ps = ring.open(pe, "logits", u)
                    for t in range(NT):
                        pe.matmul(ps[:, t * NE0:(t + 1) * NE0], hT[s][:, t * P:(t + 1) * P], wr[:], start=True, stop=False)
                        mm = pe.matmul(ps[:, t * NE0:(t + 1) * NE0], ones_row[:], br[:], start=False, stop=True)
                    mm.then_inc(ring.filled("logits", u), 1)

            def ffn_down(u):
                ps = ring.open(pe, "down", u)
                for e in range(2):
                    for half in range(2):
                        ring.wait_read(pe, "up", u, e, half)
                    for t in range(NT):
                        o = ps[:, (2 * e + t) * D:(2 * e + t + 1) * D]
                        for ch in range(FC):
                            pe.matmul(o, hid[:, e, ch, t * P:(t + 1) * P], w2[e][:, ch, :], start=(ch == 0), stop=False)
                        mm = pe.matmul(o, ones_row[:], b2[e][:], start=False, stop=True)
                mm.then_inc(ring.filled("down", u), 1)

            def qkv_in(u):
                s = u
                pe.wait_ge(*x_ready[0].at(NT * (u + 1)))
                transpose_tiles(u, "x1T", x[s])
                pe.wait_ge(*xn_ready[1].at(NT * (u + 1)))
                transpose_tiles(u, "h1T", xn[s])

            def null(u):
                s = u
                ring.wait_read(pe, "h1T", u)
                ps = ring.open(pe, "null", u)
                for t in range(NT):
                    mm = pe.matmul(ps[:, t * 32:(t + 1) * 32], hT[s][:, t * P:(t + 1) * P],
                                   w_null[:].rearrange("k h n -> k (h n)"), start=True, stop=True)
                mm.then_inc(ring.filled("null", u), 1)

            def qkv_a(u, t):
                s = u
                if t == 0:
                    ring.wait_read(pe, "x1T", u)
                for i in range(4):
                    src, w = (hT, wq1) if i < 2 else (xT, wkv1)
                    ps = ring.open(pe, "qk", u, t, i)
                    pe.matmul(ps[:], src[s][:, t * P:(t + 1) * P], w[:, (i % 2) * 512:(i % 2 + 1) * 512],
                              start=True, stop=True).then_inc(ring.filled("qk", u, t, i), 1)
                for j in range(2):
                    ps = ring.open(pe, "v", u, t, j)
                    pe.matmul(ps[:], xT[s][:, t * P:(t + 1) * P],
                              wkv1[:, H1 * DH1 + j * 512:H1 * DH1 + (j + 1) * 512], start=True, stop=True)\
                        .then_inc(ring.filled("v", u, t, j), 1)

            def qkv_b(u, t):
                for i in range(4):
                    pe.wait_ge(*qn_ready.at((u * NT + t) * 4 + i + 1))
                    ps = ring.open(pe, "qkT", u, t, i)
                    for p in range(4):
                        mm = pe.transpose(ps[:, p * P:(p + 1) * P], qn[:, i, p * P:(p + 1) * P], ident[:])
                    mm.then_inc(ring.filled("qkT", u, t, i), 1)

            def attn_out(u):
                s = u
                pe.wait_ge(*o1_read.at(PAIRS1 * (u + 1)))
                ps = ring.open(pe, "y1", u)
                for t in range(NT):
                    for p in range(PAIRS1):
                        mm = pe.matmul(ps[:, t * D:(t + 1) * D], o1T[:, p, t * P:(t + 1) * P], wo1[:, p, :],
                                       start=(p == 0), stop=(p == PAIRS1 - 1))
                mm.then_inc(ring.filled("y1", u), 1)

            def x_in(u):
                pe.wait_ge(*xn_ready[2].at(NT * (u + 1)))
                transpose_tiles(u, "h2T", xn[u])

            def x_q(u):
                s = u
                ring.wait_read(pe, "h2T", u)
                for half in range(2):
                    ps = ring.open(pe, "q2", u, half)
                    for i in range(2):
                        p = 2 * half + i
                        mm = pe.matmul(ps[:, i * N:(i + 1) * N], wq2[:, p * P:(p + 1) * P], hT[s][:], start=True, stop=True)
                    mm.then_inc(ring.filled("q2", u, half), 1)

            def x_scores(u):
                s = u
                for half in range(2):
                    ring.wait_read(pe, "q2", u, half)
                ring.wait_read(pe, "kv2", u)
                for t in range(NT):
                    ps = ring.open(pe, "s2", u, t)
                    for p in range(PAIRS2):
                        mm = pe.matmul(ps[:, p * P:(p + 1) * P], q2T[:, p, t * P:(t + 1) * P], kblk[s][:, p, :],
                                       start=True, stop=True)
                    mm.then_inc(ring.filled("s2", u, t), 1)

            def x_pT(u):
                pe.wait_ge(*p2_ready.at(NT * (u + 1)))
                for half in range(2):
                    ps = ring.open(pe, "p2T", u, half)
                    for i in range(2):
                        for t in range(NT):
                            p = 2 * half + i
                            mm = pe.transpose(ps[:, (i * NT + t) * P:(i * NT + t + 1) * P],
                                              s2n[:, t, 2 * p:2 * p + 2, :].rearrange("q h k -> q (h k)"), ident[:])
                    mm.then_inc(ring.filled("p2T", u, half), 1)

            def x_pv(u):
                s = u
                for half in range(2):
                    ring.wait_read(pe, "p2T", u, half)
                    ps = ring.open(pe, "o2", u, half)
                    for i in range(2):
                        p = 2 * half + i
                        mm = pe.matmul(ps[:, i * N:(i + 1) * N], vblk[s][:, p, :], p2T[:, p, :], start=True, stop=True)
                    mm.then_inc(ring.filled("o2", u, half), 1)

            def x_out(u):
                for half in range(2):
                    ring.wait_read(pe, "o2", u, half)
                ps = ring.open(pe, "y2", u)
                for t in range(NT):
                    for p in range(PAIRS2):
                        pe.matmul(ps[:, t * D:(t + 1) * D], o2T[:, p, t * P:(t + 1) * P], wo2[:, p, :],
                                  start=(p == 0), stop=False)
                    mm = pe.matmul(ps[:, t * D:(t + 1) * D], ones_row[:], bo2[:], start=False, stop=True)
                mm.then_inc(ring.filled("y2", u), 1)

            def scores(u, p):
                s = u
                ps = [ring.open(pe, "s1", u, p, i) for i in range(2)]
                for t in range(NT):
                    w = (t + 1) * P
                    for i in range(2):
                        mm = pe.matmul(ps[i][:, t * P:t * P + w], q1T[s][64 * i:64 * i + 64, p, t * P:(t + 1) * P],
                                       k1T[s][64 * i:64 * i + 64, p, 0:w], start=True, stop=True)
                        if t == NT - 1:
                            mm.then_inc(ring.filled("s1", u, p, i), 1)

            def probs_T(u, p):
                n = PAIRS1 * u + p
                a = 2 * n % NPR
                pe.wait_ge(*p_ready.at(2 * (n + 1)))
                for i in range(2):
                    ps = ring.open(pe, "p1T", u, p, i)
                    pe.transpose(ps[:, 0:P], probs[:, a, keys(i, P)], ident[:])
                    first_key = keys(i, N).start
                    for kt in range(2):
                        pe.transpose(ps[:, (kt + 1) * P:(kt + 2) * P], 
                                     probs[:, a + 1, first_key + kt * P:first_key + (kt + 1) * P], ident[:])
                    pe.transpose(ps[0:4, 3 * P:4 * P], probs[:, a + i, N:N + 2 * NULLS], ident[:])\
                        .then_inc(ring.filled("p1T", u, p, i), 1)

            def values(u, p):
                s = u
                n = PAIRS1 * u + p
                if n >= 2:
                    pe.wait_ge(*o1_read.at(n - 1))
                o = o_banks[n % 2]
                for i in range(2):
                    ring.wait_read(pe, "p1T", u, p, i)
                pe.matmul(o[:, 0:N], null_v[:, p, :], pnT[:, n % 2, :], start=True, stop=False,
                          skip_group_check=True)
                for i in range(2):
                    h = 2 * p + i
                    tgt = o[64 * i:64 * i + 64]
                    b = (2 * n + i) % 4
                    pe.matmul(tgt[:, 0:N], v1[s][:, 0, h * DH1:(h + 1) * DH1],
                              pT[:, b, 0:2].rearrange("k t q -> k (t q)"), start=False, stop=False, skip_group_check=True)
                    mm = pe.matmul(tgt[:, P:N], v1[s][:, 1, h * DH1:(h + 1) * DH1], pT[:, b, 2], start=False, stop=True,
                                   skip_group_check=True)
                mm.then_inc(o1_full.sem, 1)

            def pair_step(g):
                u, p = divmod(g, PAIRS1)
                if u < U:
                    if p == 0:
                        for t in range(NT):
                            for j in range(2):
                                ring.wait_read(pe, "v", u, t, j)
                            for i in range(4):
                                ring.wait_read(pe, "qkT", u, t, i)
                    scores(u, p)
                if 2 <= g < PAIRS1 * U + 2:
                    probs_T(*divmod(g - 2, PAIRS1))
                if 3 <= g < PAIRS1 * U + 3:
                    values(*divmod(g - 3, PAIRS1))

            steps = dict(ffn_in=ffn_in, ffn_h=ffn_h, kv2=kv2, ffn_up0=lambda u: ffn_up(u, 0),
                         ffn_up1=lambda u: ffn_up(u, 1), ffn_down=ffn_down, qkv_in=qkv_in, null=null,
                         qkv_a0=lambda u: qkv_a(u, 0), qkv_b0=lambda u: qkv_b(u, 0),
                         qkv_a1=lambda u: qkv_a(u, 1), qkv_b1=lambda u: qkv_b(u, 1), attn_out=attn_out, x_in=x_in, x_q=x_q,
                         x_scores=x_scores, x_pT=x_pT, x_pv=x_pv, x_out=x_out)
            with pe.Fori(0, B // U) as it:
                run_steps(stages, PAIRS1, U, 4, steps, pair_step)
                meet.join(pe, "tensor")

        @block.scalar
        def _(act):
            act.wait_ge(cleared, 1)
            for dst, src in loads[1::2]:
                act.dma_start(dst, src, allow_slow_non_contiguous=True).then_inc(loaded, 16)
            act.wait_ge(t_ps, 1)
            act.wait_ge(null_done, 1)
            for b in range(2):
                act.activation(wq1T[:, 4 * b:4 * b + 4, :].rearrange("p c n -> p (c n)"), banks[b][:], ACT.Copy,
                               scale=qs[:, 1:2])
            for i in range(2):
                ins = act.activation(null_blk[64 * i:64 * i + 64, :, i, :],
                                     banks[2][64 * i:64 * i + 64, 0:32].rearrange("d (p i n) -> d i p n", i=2, n=NULLS)[:, i],
                                     ACT.Copy)
            ins.then_inc(t_sb, 1)
            act.wait_ge(t_ps, 2)
            act.activation(w_null[:].rearrange("k h n -> k (h n)"), banks[3][:, 0:32], ACT.Copy)
            act.activation(b2[1][:], banks[3][0:1, P:2 * P], ACT.Copy).then_inc(ready, 1)
            act.wait_ge(ready, 4)

            def affine(dst, ps, ln):
                return act.activation(dst, ps, ACT.Identity, scale=ln[:, 0:1], bias=ln[:, 1:2])

            def ffn_in(u):
                ps = ring.wait(act, "xT", u)
                act.activation(xT[u][:], ps[:, 0:N], ACT.Copy).then_inc(ring.read("xT", u), 1)

            def ffn_h(u):
                s = u
                ps = ring.wait(act, "hT", u)
                affine(hT[s][:], ps[:, 0:N], ln_f).then_inc(ring.read("hT", u), 1)
                ps = ring.wait(act, "cnT", u)
                affine(cnT[u][:], ps[:, 0:S_CTX], ln_c).then_inc(ring.read("cnT", u), 1)

            def kv2(u):
                s = u
                ps = ring.wait(act, "kv2", u)
                for i in range(2):
                    act.activation(kblk[s][64 * i:64 * i + 64, :, 64 * i:64 * i + 64],
                                   ps[64 * i:64 * i + 64, 0:256].rearrange("d (p k) -> d p k", p=PAIRS2), ACT.Copy)
                    ins = act.activation(vblk[s][64 * i:64 * i + 64, :, 64 * i:64 * i + 64],
                                         ps[64 * i:64 * i + 64, 256:512].rearrange("k (p d) -> k p d", p=PAIRS2), ACT.Copy)
                ins.then_inc(ring.read("kv2", u), 1)

            def ffn_up(u, e):
                if e == 0 and u >= 1:
                    ring.wait(act, "down", u - 1)
                for half in range(2):
                    ps = ring.wait(act, "up", u, e, half)
                    for i in range(2):
                        ch = 2 * half + i
                        ins = act.activation(hid[:, e, ch, :], ps[:, i * N:(i + 1) * N], ACT.Gelu_apprx_tanh,
                                             bias=b1[e][:, ch:ch + 1])
                    ins.then_inc(ring.read("up", u, e, half), 1)
                if e == 1:
                    ring.wait_read(act, "logits", u)
                    act.activation(lg[u][:], lg[u][:], ACT.Exp).then_inc(lg_exp.sem, 1)

            def qkv_in(u):
                s = u
                ps = ring.wait(act, "x1T", u)
                act.activation(xT[s][:], ps[:, 0:N], ACT.Copy).then_inc(ring.read("x1T", u), 1)
                ps = ring.wait(act, "h1T", u)
                affine(hT[s][:], ps[:, 0:N], ln_a).then_inc(ring.read("h1T", u), 1)

            def qkv_a(u, t):
                for i in range(4):
                    n = (u * NT + t) * 4 + i
                    ps = ring.wait(act, "qk", u, t, i)
                    act.activation(qn[:, i, :], ps[:], ACT.Copy).then_inc(qk_copied.sem, 1)
                    if n >= 2:
                        act.wait_ge(*ss_ready.at(n - 1))
                    act.activation(sq[:, i % 2, :], ps[:], ACT.Square).then_inc(ring.read("qk", u, t, i), 1)
                for j in range(2):
                    ps = ring.wait(act, "v", u, t, j)
                    act.activation(v1[u][:, t, j * 512:(j + 1) * 512], ps[:], ACT.Copy).then_inc(ring.read("v", u, t, j), 1)

            def qkv_b(u, t):
                for i in range(4):
                    dst, scale = (q1T, qs[:, 1:2]) if i < 2 else (k1T, ks[:])
                    ps = ring.wait(act, "qkT", u, t, i)
                    act.activation(dst[u][:, 4 * (i % 2):4 * (i % 2) + 4, t * P:(t + 1) * P],
                                   ps[:].rearrange("p (c n) -> p c n", c=4), ACT.Copy, scale=scale)\
                        .then_inc(ring.read("qkT", u, t, i), 1)

            def x_in(u):
                ps = ring.wait(act, "h2T", u)
                affine(hT[u][:], ps[:, 0:N], ln_x).then_inc(ring.read("h2T", u), 1)

            def x_q(u):
                for half in range(2):
                    ps = ring.wait(act, "q2", u, half)
                    act.activation(q2T[:, 2 * half:2 * half + 2, :].rearrange("p c n -> p (c n)"), ps[:], ACT.Copy,
                                   scale=DH2 ** -0.5).then_inc(ring.read("q2", u, half), 1)

            def x_scores(u):
                for t in range(NT):
                    ring.wait_read(act, "s2", u, t)
                    act.activation(s2n[:, t], s2n[:, t], ACT.Exp).then_inc(s2_exp.sem, 1)

            def x_pv(u):
                for half in range(2):
                    ps = ring.wait(act, "o2", u, half)
                    act.activation(o2T[:, 2 * half:2 * half + 2, :].rearrange("p c n -> p (c n)"), ps[:], ACT.Copy)\
                        .then_inc(ring.read("o2", u, half), 1)

            def pair_step(g):
                if g >= 4:
                    n = g - 4
                    act.wait_ge(*o1_full.at(n + 1))
                    if n >= PAIRS1 and n % PAIRS1 == 0:
                        ring.wait(act, "y1", n // PAIRS1 - 1)
                    act.activation(o1T[:, n % PAIRS1, :], o_banks[n % 2][:, 0:N], ACT.Copy).then_inc(o1_read.sem, 1)
                u, p = divmod(g, PAIRS1)
                if u < U:
                    for i in range(2):
                        ring.wait_read(act, "s1", u, p, i)
                        for t in range(NT):
                            a = (2 * g + t) % NPR
                            w = (t + 1) * P
                            ins = act.activation(probs[:, a, keys_nulls(i, w)], probs[:, a, keys_nulls(i, w)], ACT.Exp,
                                                 bias=low[:, a, i:i + 1], scale=-1.0, accum_out=sums[:, a, i:i + 1])
                        ins.then_inc(exp_done.sem, 1)

            steps = dict(ffn_in=ffn_in, ffn_h=ffn_h, kv2=kv2, ffn_up0=lambda u: ffn_up(u, 0),
                         ffn_up1=lambda u: ffn_up(u, 1), qkv_in=qkv_in,
                         qkv_a0=lambda u: qkv_a(u, 0), qkv_b0=lambda u: qkv_b(u, 0),
                         qkv_a1=lambda u: qkv_a(u, 1), qkv_b1=lambda u: qkv_b(u, 1), x_in=x_in, x_q=x_q,
                         x_scores=x_scores, x_pv=x_pv)
            with act.Fori(0, B // U) as it:
                run_steps(stages, PAIRS1, U, 4, steps, pair_step)
                meet.join(act, "scalar")

        @block.vector
        def _(dve):
            dve.memset(null_v[:], 0.0).then_inc(cleared, 1)
            dve.memset(null_blk[:], 0.0)
            for s in range(SETS):
                dve.memset(kblk[s][:], 0.0)
                dve.memset(vblk[s][:], 0.0)
            chain = Chain(dve, dve_setup)
            dve.wait_ge(loaded, 16 * len(loads))
            chain(dve.tensor_scalar(qs[:, 1:2], qs[:, 0:1], -QK_SCALE, None, ALU.mult))
            chain(dve.tensor_tensor(null_k2[:, 0, :], null_k[:], null_k[:], ALU.mult))
            chain(dve.tensor_reduce(null_ss[:, 0:1], null_k2[:, 0, :], AX.X, ALU.add))
            dve.tensor_scalar(null_ss[:, 0:1], null_ss[:, 0:1], 1e-24, None, ALU.max).then_inc(null_pow, 1)
            dve.wait_ge(null_pow, 2)
            chain(dve.tensor_scalar(null_k[:], null_k[:], null_ss[:, 1:2], None, ALU.mult))
            chain(dve.tensor_tensor(null_k2[:, 0, :], null_k[:], ks_row[:], ALU.mult))
            chain(dve.tensor_copy(null_k2[:, 1, :], null_k2[:, 0, :]))
            dve.sem_inc(null_done, 1)
            dve.wait_ge(iota_done, 2)
            for h in range(H1):
                dve.tensor_scalar(dist[:, h, :], dist0, slopes[h], None, ALU.mult)
                dve.tensor_scalar(null_bias[:, :, h, :], iota_nf[:], slopes[h], None, ALU.mult)
            thr = K["thr"][:].bitcast(F32)
            for w, dst, cols, th in ((w1[0][:], w1[1][:], F, 0),
                                     (w2[0][:].rearrange("p c n -> p (c n)"), w2[1][:].rearrange("p c n -> p (c n)"), F, 2),
                                     (b1[0][:], b1[1][:], FC, 4), (K["b2c"][:], K["b2c"][:], 1, 6)):
                chain(dve.tensor_scalar(mag[:, 0:cols].bitcast(I32), w.bitcast(I32), 0x7FFFFFFF, None, ALU.bitwise_and))
                chain(dve.tensor_scalar(tier[:, 0:cols], mag[:, 0:cols], thr[:, th:th + 1], -2.0, ALU.is_ge, ALU.mult))
                chain(dve.tensor_scalar(tier2[:, 0:cols], mag[:, 0:cols], thr[:, th + 1:th + 2], None, ALU.is_le))
                chain(dve.tensor_tensor(tier[:, 0:cols], tier[:, 0:cols], tier2[:, 0:cols], ALU.add))
                chain(dve.tensor_scalar(tier[:, 0:cols], tier[:, 0:cols], -1.0, None, ALU.max))
                chain(dve.tensor_scalar(tier2[:, 0:cols], w, 0.8, None, ALU.mult))
                chain(dve.tensor_tensor(tier[:, 0:cols], tier2[:, 0:cols], tier[:, 0:cols], ALU.mult))
                chain(dve.tensor_tensor(dst, w, tier[:, 0:cols], ALU.add))
            dve.sem_inc(experts_ready, 1)
            dve.sem_inc(ready, 1)
            dve.wait_ge(ready, 4)

            def moments(u, src, out, rows=P):
                for t in range(len(src)):
                    link(dve.bn_stats(stats[u][0:rows, t, :], src[t]))
                for t in range(len(src)):
                    dve.bn_aggr(out[t], stats[u][0:rows, t, :]).then_inc(mv_ready.sem, 1)
                waits["mv"] += len(src)

            def link(ins):
                chain(ins)

            waits = {"mv": 0, "root": 0}

            def normalise(u, src, dst, done):
                s = u
                moments(u, [src[:, t, :] for t in range(NT)], [mv[s][:, t, :] for t in range(NT)])
                waits["root"] += 1
                dve.wait_ge(*rstd_ready.at(waits["root"]))
                for t in range(NT):
                    dve.tensor_scalar(dst[:, t, :], src[:, t, :], mv[s][:, t, 0:1], rstd[s][:, NT + t:NT + t + 1],
                                      ALU.subtract, ALU.mult).then_inc(done.sem, 1)

            def residual(u, name):
                s = u
                ps = ring.wait(dve, name, u)
                dve.tensor_tensor(r[:].rearrange("p t n -> p (t n)"), ps[:, 0:N],
                                  x[s][:].rearrange("p t n -> p (t n)"), ALU.add).then_inc(ring.read(name, u), 1)
                ring.wait_read(dve, name, u)

            def ffn_in(u):
                s = u
                dve.wait_ge(*x_loaded[u % SETS].at(32 * (u // SETS + 1)))
                normalise(u, x[s], xn[s], xn_ready[0])

            def context(u):
                s = u
                dve.wait_ge(*x_loaded[u % SETS].at(32 * (u // SETS + 1)))
                link(dve.bn_stats(cmv[s][:, 0:6], c[s][:]))
                dve.bn_aggr(cmv[s][:, 6:8], cmv[s][:, 0:6]).then_inc(mv_ready.sem, 1)
                waits["root"] += 1
                dve.wait_ge(*rstd_ready.at(waits["root"]))
                dve.tensor_scalar(cn[s][:], c[s][:], cmv[s][:, 6:7], cmv[s][:, 1:2], ALU.subtract, ALU.mult)\
                    .then_inc(cn_ready.sem, 1)

            def ffn_up0(u):
                s = u
                ps = ring.wait(dve, "logits", u)
                l = ps[:, 0:NT * NE0].rearrange("p (t e) -> p t e", t=NT)
                link(dve.tensor_reduce(pr[s][:, :, 0], l, AX.X, ALU.max))
                dve.tensor_tensor(lg[s][:], l, pr[s][:, :, 0:1].broadcast_to([P, NT, NE0]), ALU.subtract)\
                    .then_inc(ring.read("logits", u), 1)

            def ffn_up1(u):
                s = u
                dve.wait_ge(*lg_exp.at(u + 1))
                link(dve.tensor_reduce(pr[s][:, :, 1], lg[s][:], AX.X, ALU.add))
                link(dve.reciprocal(pr[s][:, :, 2], pr[s][:, :, 1]))
                link(dve.tensor_reduce(pr[s][:, :, 5], lg[s][:, :, 1:NE0], AX.X, ALU.add))
                link(dve.tensor_tensor(pr[s][:, :, 3], lg[s][:, :, 0], pr[s][:, :, 2], ALU.mult))
                link(dve.tensor_tensor(pr[s][:, :, 4], pr[s][:, :, 5], pr[s][:, :, 2], ALU.mult))

            def ffn_down(u):
                s = u
                ps = ring.wait(dve, "down", u)
                for t in range(NT):
                    link(dve.scalar_tensor_tensor(r[:, t, :], ps[:, t * D:(t + 1) * D], pr[s][:, t, 3:4], x[s][:, t, :],
                                                  ALU.mult, ALU.add))
                for t in range(NT):
                    ins = dve.scalar_tensor_tensor(r[:, t, :], ps[:, (2 + t) * D:(3 + t) * D], pr[s][:, t, 4:5],
                                                   r[:, t, :], ALU.mult, ALU.add)
                ins.then_inc(ring.read("down", u), 1)
                ring.wait_read(dve, "down", u)
                normalise(u, r, x[s], x_ready[0])
                dve.wait_ge(*x_ready[0].at(NT * (u + 1)))
                normalise(u, x[s], xn[s], xn_ready[1])

            def null(u):
                ps = ring.wait(dve, "null", u)
                dve.tensor_copy(nneg[u][:].rearrange("p t h n -> p (t h n)"), ps[:, 0:64])\
                    .then_inc(ring.read("null", u), 1)

            def qkv_a(u, t):
                for i in range(4):
                    n = (u * NT + t) * 4 + i
                    ring.wait_read(dve, "qk", u, t, i)
                    if n >= 4:
                        dve.wait_ge(*rn_ready.at(n - 3))
                    dve.tensor_reduce(ss[:, i, :], sq[:, i % 2, :].rearrange("p (h d) -> p h d", d=DH1), AX.X, ALU.add)\
                        .then_inc(ss_ready.sem, 1)

            def qkv_b(u, t):
                s = u
                for i in range(4):
                    n = (u * NT + t) * 4 + i
                    dve.wait_ge(*rn_ready.at(n + 1))
                    rr = rnq[s][:, t, 8 * i:8 * i + 8] if i < 2 else rn[:, i % 2, :]
                    rows = qn[:, i, :].rearrange("p (h d) -> p h d", d=DH1)
                    dve.wait_ge(*qk_copied.at(n + 1))
                    dve.tensor_tensor(rows, rows, rr.unsqueeze(2).broadcast_to([P, 8, DH1]), ALU.mult)\
                        .then_inc(qn_ready.sem, 1)
                if t == 1:
                    ring.wait_read(dve, "null", u)
                    link(dve.tensor_tensor(nneg[s][:], nneg[s][:],
                                           rnq[s][:].unsqueeze(3).broadcast_to([P, NT, H1, NULLS]), ALU.mult))
                    link(dve.tensor_tensor(nneg[s][:], nneg[s][:], null_bias[:], ALU.add))
                    link(dve.tensor_reduce(nmin[s][:], nneg[s][:], AX.X, ALU.min))

            def attn_out(u):
                s = u
                residual(u, "y1")
                normalise(u, r, x[s], x_ready[1])
                dve.wait_ge(*x_ready[1].at(NT * (u + 1)))
                normalise(u, x[s], xn[s], xn_ready[2])

            def x_scores(u):
                for t in range(NT):
                    ps = ring.wait(dve, "s2", u, t)
                    sc = ps[:].rearrange("p (h k) -> p h k", h=H2)
                    link(dve.tensor_reduce(m2[:, t, :], sc, AX.X, ALU.max, negate=True))
                    dve.tensor_tensor(s2n[:, t], sc, m2[:, t, :].unsqueeze(2).broadcast_to([P, H2, S_CTX]), ALU.add)\
                        .then_inc(ring.read("s2", u, t), 1)
                    ring.wait_read(dve, "s2", u, t)
                for t in range(NT):
                    dve.wait_ge(*s2_exp.at(NT * u + t + 1))
                    link(dve.tensor_reduce(z2[:, t, :], s2n[:, t], AX.X, ALU.add))
                    dve.reciprocal(rz2[:, t, :], z2[:, t, :]).then_inc(s2_inv.sem, 1)

            def x_pT(u):
                for half in range(2):
                    ps = ring.wait(dve, "p2T", u, half)
                    dve.tensor_copy(p2T[:, 2 * half:2 * half + 2, :].rearrange("p c n -> p (c n)"), ps[:])\
                        .then_inc(ring.read("p2T", u, half), 1)

            def x_out(u):
                s = u
                residual(u, "y2")
                normalise(u, r, x[s], x_ready[2])
                dve.wait_ge(*x_ready[2].at(NT * (u + 1)))

            def pair_step(g):
                u, p = divmod(g, PAIRS1)
                if u < U:
                    a = 2 * g % NPR
                    if 2 * g >= NPR:
                        m = g - NPR // 2
                        ring.wait(dve, "p1T", m // PAIRS1, m % PAIRS1, 1)
                    dve.tensor_copy(probs[:, a:a + NT, N:N + 2 * NULLS].rearrange("q t (h n) -> q t h n", n=NULLS),
                                    nneg[u][:, :, 2 * p:2 * p + 2, :])
                    for i in range(2):
                        h = 2 * p + i
                        ps = ring.wait(dve, "s1", u, p, i)
                        for t in range(NT):
                            w = (t + 1) * P
                            ins = dve.tensor_tensor_reduce(probs[:, a + t, keys(i, w)], dist[:, h, (1 - t) * P:N],
                                                           ps[:, t * P:t * P + w], 1.0, nmin[u][:, t, h:h + 1],
                                                           ALU.add, ALU.min, low[:, a + t, i:i + 1])
                        ins.then_inc(ring.read("s1", u, p, i), 1)
                if 1 <= g < PAIRS1 * U + 1:
                    a = 2 * (g - 1) % NPR
                    for i in range(2):
                        dve.wait_ge(*exp_done.at(2 * (g - 1) + i + 1))
                        dve.reciprocal(rsums[:, a:a + NT, i], sums[:, a:a + NT, i]).then_inc(rs_ready.sem, 1)
                if 2 <= g < PAIRS1 * U + 2:
                    m = g - 2
                    if m >= 2:
                        dve.wait_ge(*o1_full.at(m - 1))
                    for i in range(2):
                        ps = ring.wait(dve, "p1T", m // PAIRS1, m % PAIRS1, i)
                        dve.tensor_copy(pnT[:, m % 2, i * P:(i + 1) * P], ps[0:4, 3 * P:4 * P])
                        dve.tensor_copy(pT[:, (2 * m + i) % 4].rearrange("k t q -> k (t q)"), ps[:, 0:3 * P])\
                            .then_inc(ring.read("p1T", m // PAIRS1, m % PAIRS1, i), 1)

            steps = dict(ffn_in=ffn_in, ctx=context, ffn_up0=ffn_up0, ffn_up1=ffn_up1, ffn_down=ffn_down, null=null,
                         qkv_a0=lambda u: qkv_a(u, 0), qkv_b0=lambda u: qkv_b(u, 0),
                         qkv_a1=lambda u: qkv_a(u, 1), qkv_b1=lambda u: qkv_b(u, 1), attn_out=attn_out,
                         x_scores=x_scores, x_pT=x_pT, x_out=x_out)
            with dve.Fori(0, B // U) as it:
                chain = Chain(dve, dve_chain)
                run_steps(stages, PAIRS1, U, 4, steps, pair_step)
                meet.join(dve, "vector")

        @block.gpsimd
        def _(pool):
            chain = Chain(pool, pool_setup)
            chain(pool.iota(iota_i, pattern=[[-1, N]], base=P, channel_multiplier=1))
            chain(pool.tensor_copy(dist0, iota_i))
            pool.affine_select(out=dist0, in_=dist0, compare_op=ALU.is_ge, fill=MASKED, base=P,
                               pattern=[[-1, N]], channel_multiplier=1).then_inc(iota_done, 1)
            chain(pool.iota(iota_n[:], pattern=[[P, NT], [-1, NULLS]], base=NULLS, channel_multiplier=1))
            pool.tensor_copy(iota_nf[:], iota_n[:]).then_inc(iota_done, 1)
            pool.wait_ge(null_pow, 1)
            pool.tensor_tensor(null_ss[:, 1:2], null_ss[:, 0:1], K["eps_half"][0:32, 0:1], ALU.pow).then_inc(null_pow, 1)
            pool.sem_inc(ready, 1)
            pool.wait_ge(ready, 4)
            count = {"mv": 0}

            def root(u):
                s = u
                count["mv"] += NT
                pool.wait_ge(*mv_ready.at(count["mv"]))
                chain(pool.tensor_scalar(rstd[s][:, 0:NT], mv[s][:, :, 1], LN_EPS, None, ALU.add))
                pool.tensor_tensor(rstd[s][:, NT:2 * NT], rstd[s][:, 0:NT], K["eps_half"][:, 0:NT], ALU.pow)\
                    .then_inc(rstd_ready.sem, 1)

            def ctx_root(u):
                s = u
                count["mv"] += 1
                pool.wait_ge(*mv_ready.at(count["mv"]))
                chain(pool.tensor_scalar(cmv[s][:, 0:1], cmv[s][:, 7:8], LN_EPS, None, ALU.add))
                pool.tensor_tensor(cmv[s][:, 1:2], cmv[s][:, 0:1], K["eps_half"][0:S_CTX, 0:1], ALU.pow)\
                    .then_inc(rstd_ready.sem, 1)

            def two_roots(u):
                root(u)
                root(u)

            def qkv_a(u, t):
                s = u
                for i in range(4):
                    n = (u * NT + t) * 4 + i
                    pool.wait_ge(*ss_ready.at(n + 1))
                    rr = rnq[s][:, t, 8 * i:8 * i + 8] if i < 2 else rn[:, i % 2, :]
                    chain(pool.tensor_scalar(ss[:, i, :], ss[:, i, :], 1e-24, None, ALU.max))
                    pool.tensor_tensor(rr, ss[:, i, :], K["eps_half"][:, 0:8], ALU.pow).then_inc(rn_ready.sem, 1)

            def x_scores(u):
                for t in range(NT):
                    pool.wait_ge(*s2_inv.at(NT * u + t + 1))
                    pool.tensor_tensor(s2n[:, t], s2n[:, t], rz2[:, t, :].unsqueeze(2).broadcast_to([P, H2, S_CTX]),
                                       ALU.mult).then_inc(p2_ready.sem, 1)

            def pair_step(g):
                if 1 <= g < PAIRS1 * U + 1:
                    for i in range(2):
                        pool.wait_ge(*rs_ready.at(2 * (g - 1) + i + 1))
                        for t in range(NT):
                            a = (2 * (g - 1) + t) % NPR
                            w = (t + 1) * P
                            ins = pool.tensor_scalar(probs[:, a, keys_nulls(i, w)], probs[:, a, keys_nulls(i, w)],
                                                     rsums[:, a, i:i + 1], 1.0, ALU.mult, ALU.mult)
                        ins.then_inc(p_ready.sem, 1)

            steps = dict(ffn_in=root, ctx=ctx_root, ffn_down=two_roots, qkv_a0=lambda u: qkv_a(u, 0),
                         qkv_a1=lambda u: qkv_a(u, 1), attn_out=two_roots, x_scores=x_scores, x_out=root)
            with pool.Fori(0, B // U) as it:
                chain = Chain(pool, pool_chain)
                run_steps(stages, PAIRS1, U, 4, steps, pair_step)
                meet.lead(pool, first, last)
            pool.sem_clear(range(FIRST_SEM, meet.arrived.num))

        @block.sync
        def _(sy):
            sy.wait_ge(cleared, 1)
            for dst, src in loads[0::2]:
                sy.dma_start(dst, src, allow_slow_non_contiguous=True).then_inc(loaded, 16)
            sy.sem_inc(ready, 1)
            xin = x_in.rearrange("b (t p) d -> b p t d", p=P)
            xo = x_out.rearrange("b (t p) d -> b p t d", p=P)
            with sy.Fori(0, B // U) as it:
                def load(u):
                    if u >= SETS:
                        sy.wait_ge(*stored[u % SETS].at(16 * (u // SETS)))
                    sy.dma_start(x[u][:], xin[it * U + u]).then_inc(x_loaded[u % SETS].sem, 16)
                    sy.dma_start(c[u][:], A["ctx_1024"][it * U + u]).then_inc(x_loaded[u % SETS].sem, 16)

                def store(u):
                    sy.wait_ge(*x_ready[2].at(NT * (u + 1)))
                    sy.dma_start(xo[it * U + u], x[u][:]).then_inc(stored[u % SETS].sem, 16)

                for u in range(U):
                    if u >= SETS:
                        store(u - SETS)
                    load(u)
                for u in range(U - SETS, U):
                    store(u)
                for i in range(min(SETS, U)):
                    sy.wait_ge(*stored[i].at(16 * ((U - 1 - i) // SETS + 1)))
                meet.join(sy, "sync")


H3, DH3 = 16, 8
KV3 = 8
TC = B * N // P
TG = 4
NG = TC // TG
NE = 8
CAP = int(np.ceil(B * N * 2 / NE * 1.25))


def phase_3(nc, A, K, x_in, out):
    xs = nc.dram_tensor("expert_rows", [SLOTS + 2 * B * N, D], F32, kind="Internal").ap()
    ys = nc.dram_tensor("expert_answers", [SLOTS, D], F32, kind="Internal").ap()
    with ExitStack() as ctx:
        acc_all = ctx.enter_context(nc.sbuf_tensor("acc_all", [P, TC, D], F32))
        idx_get = ctx.enter_context(nc.sbuf_tensor("idx_get", [P, 2, TC], I32))
        gate_w = ctx.enter_context(nc.sbuf_tensor("gate_w", [P, 2, TC], F32))
        with ExitStack() as rows:
            hT_all = rows.enter_context(nc.sbuf_tensor("h2T_all", [P, TC, P], F32))
            hn_all = rows.enter_context(nc.sbuf_tensor("hn_all", [P, TC, D], F32))
            column_attention(nc, A, K, x_in, hT_all, hn_all, acc_all, xs)
            route(nc, A, hT_all, hn_all, idx_get, gate_w, xs)
        experts(nc, A, K, xs, ys)
        combine(nc, K, acc_all, idx_get, gate_w, ys, out)


def column_attention(nc, A, K, x_in, hT_all, hn_all, acc_all, xs):
    U = 4
    PAIRS = H3 // 2
    with ExitStack() as ctx:
        def sb(name, shape, dt=F32):
            return ctx.enter_context(nc.sbuf_tensor(name, shape, dt))

        sems = []

        def sem(name):
            s = ctx.enter_context(nc.semaphore(name, num=FIRST_SEM + len(sems)))
            sems.append(s)
            return s

        def two(name, shape, dt=F32):
            return Sets([sb(f"{name}{i}", shape, dt) for i in range(2)])

        XS = 3

        ident = K["ident"]
        W = TG * P
        w_raw = sb("qkv_raw", [P, 2, P])
        wo_raw = sb("proj_raw", [P, P])
        split = K["split"]
        wq = sb("cq_pad", [P, GROUPS, 4, 32])
        wk = sb("ck_pad", [P, GROUPS, 4, 32])
        wv = sb("cv", [P, KV3, DH3])
        woT = sb("c_woT", [P, D])
        wo_pad = sb("c_wo_pad", [P, GROUPS, D])
        ln1 = sb("c_ln1", [P, 2])
        ln2 = sb("c_ln2", [P, 2])
        zeros = sb("c_zeros", [P, 1, D])
        ident_bf = sb("ident_bf", [P, P], BF16)
        iota = sb("c_iota", [P, P], I32)
        low_bits = sb("c_low_bits", [P, P], I32)
        mask_f = sb("c_mask_f", [P, P])
        mask = sb("c_mask", [P, TG, P], BF16)
        x = Sets([sb(f"cx{i}", [P, TG, D]) for i in range(XS)])
        xn = two("cxn", [P, TG, D])
        hn = two("chn", [P, TG, D])
        r = two("cr", [P, TG, D])
        stats = two("cstats", [P, TG, 6])
        mv = two("cmv3_", [P, TG, 2])
        rstd = two("crstd", [P, 2 * TG])
        lnT = two("clnT", [P, W])
        rounded = two("c_rounded", [P, W], F32R)
        qT = two("cqT", [P, GROUPS, W], F32R)
        kT = two("ckT", [P, GROUPS, W], F32R)
        v = two("cv3_", [P, TG, KV3, 32])
        oT = two("coT", [P, GROUPS, W])
        NPR = 8
        probs = sb("cprobs", [P, NPR, TG, P])
        pT = sb("cpT", [P, NPR, TG, P])
        negmax = sb("cnegmax", [P, NPR, TG])
        sums = sb("csums", [P, NPR, TG])
        rsums = sb("crsums", [P, NPR, TG])
        banks = [ctx.enter_context(nc.psum_tensor(f"pc{i}", [P, 512], F32)) for i in range(6)]
        o_banks = [ctx.enter_context(nc.psum_tensor(f"pd{i}", [P, 512], F32)) for i in range(2)]

        loaded = sem("c_weights_loaded")
        cleared = sem("c_cleared")
        staged = sem("c_proj_staged")
        zeroed = sem("c_slots_zeroed")
        dve_setup = sem("c_dve_setup")
        pool_setup = sem("c_pool_setup")
        act_setup = sem("c_act_setup")
        t_ps = sem("c_setup_transposed")
        mask_iota = sem("c_mask_iota")
        ready = sem("c_setup_ready")
        meet = Meeting(sem, ["sync", "scalar", "tensor", "vector"])
        n_setup = len(sems)
        ring = Ring(banks, sem)
        x_loaded = [sem(f"cx{i}_loaded") for i in range(XS)]
        mv_ready = Counted(sem("c_moments_ready"))
        rstd_ready = Counted(sem("c_roots_ready"))
        xn_ready = Counted(sem("c_xn_ready"))
        rounded_ready = Counted(sem("c_rounded_ready"))
        hn_ready = Counted(sem("c_hn_ready"))
        negmax_ready = Counted(sem("c_negmax_ready"))
        rs_ready = Counted(sem("c_rsums_ready"))
        p_ready = Counted(sem("c_probs_ready"))
        o_full = Counted(sem("c_o_full"))
        o_read = Counted(sem("c_o_read"))
        acc_ready = Counted(sem("c_acc_ready"))
        dve_chain = sem("c_dve_chain")
        pool_chain = sem("c_pool_chain")
        first, last = sems[n_setup].num, sems[-1].num

        loads = [
            (w_raw[:], A["L1_ffn_qkv_weight"].rearrange("(a p) k -> p a k", p=P)),
            (wo_raw[:], A["L1_ffn_proj_weight"]),
            (ln1[:, 0:1], col(A["L1_ffn_ln1_weight"])), (ln1[:, 1:2], col(A["L1_ffn_ln1_bias"])),
            (ln2[:, 0:1], col(A["L1_ffn_ln2_weight"])), (ln2[:, 1:2], col(A["L1_ffn_ln2_bias"])),
        ]
        stages = [(-9, "norm1"), (-6, "lnT"), (-5, "qk01"), (-4, "qk23"), (-4, "v"), (13, "out"), (17, "hT")]

        block = ctx.enter_context(nc.Block())

        @block.tensor
        def _(pe):
            pe.wait_ge(loaded, 16 * len(loads))
            for a in range(2):
                pe.transpose(banks[0][:, a * P:(a + 1) * P], w_raw[:, a, :], ident[:])
            pe.transpose(banks[0][:, 2 * P:3 * P], wo_raw[:], ident[:]).then_inc(t_ps, 1)
            pe.wait_ge(ready, 4)

            def transposes(name, u, src):
                ps = ring.open(pe, name, u)
                for t in range(TG):
                    mm = pe.transpose(ps[:, t * P:(t + 1) * P], src[:, t, :], ident[:])
                mm.then_inc(ring.filled(name, u), 1)

            def ln_T(u):
                pe.wait_ge(*xn_ready.at(TG * (u + 1)))
                transposes("lnT", u, xn[u])

            def qk(u, groups):
                ring.wait_read(pe, "lnT", u)
                for g in groups:
                    for name, w in (("q", wq), ("k", wk)):
                        ps = ring.open(pe, name, u, g)
                        pe.matmul(ps[:], w[:, g].rearrange("p j d -> p (j d)"), lnT[u][:], start=True, stop=True)\
                            .then_inc(ring.filled(name, u, g), 1)

            def v_(u):
                ps = ring.open(pe, "v", u)
                for t in range(TG):
                    mm = pe.matmul(ps[:, t * 64:(t + 1) * 64], lnT[u][:, t * P:(t + 1) * P],
                                   wv[:].rearrange("p h d -> p (h d)"), start=True, stop=True)
                mm.then_inc(ring.filled("v", u), 1)

            def scores(u, p):
                s = u
                ps = [ring.open(pe, "s", u, p, i) for i in range(2)]
                for i in range(2):
                    pe.matmul(ps[i][:], ident_bf[:], mask[:].rearrange("q t k -> q (t k)"), start=True, stop=False,
                              skip_group_check=True)
                for t in range(TG):
                    for i in range(2):
                        h = 2 * p + i
                        g, j = h // 4, 32 * (h % 4)
                        mm = pe.matmul(ps[i][:, t * P:(t + 1) * P], qT[s][j:j + 3 * DH3, g, t * P:(t + 1) * P],
                                       kT[s][j:j + 3 * DH3, g, t * P:(t + 1) * P], start=False, stop=True,
                                       skip_group_check=True)
                        if t == TG - 1:
                            mm.then_inc(ring.filled("s", u, p, i), 1)

            def probs_T(u, p):
                for i in range(2):
                    n = H3 * u + 2 * p + i
                    pe.wait_ge(*p_ready.at(n + 1))
                    ps = ring.open(pe, "pT", u, p, i)
                    for t in range(TG):
                        mm = pe.transpose(ps[:, t * P:(t + 1) * P], probs[:, n % NPR, t, :], ident[:])
                    mm.then_inc(ring.filled("pT", u, p, i), 1)

            def values(u, p):
                s = u
                m = GROUPS * u + p // 2
                if p % 2 == 0 and m >= 2:
                    pe.wait_ge(*o_read.at(m - 1))
                for i in range(2):
                    h = 2 * p + i
                    n = H3 * u + h
                    j = 32 * (h % 4)
                    ring.wait_read(pe, "pT", u, p, i)
                    for t in range(TG):
                        mm = pe.matmul(o_banks[m % 2][j:j + 32, t * P:(t + 1) * P], v[s][:, t, h // 2, :],
                                       pT[:, n % NPR, t, :], start=True, stop=True)
                mm.then_inc(o_full.sem, 1)

            def pair_step(g):
                u, p = divmod(g, PAIRS)
                if u < U:
                    if p == 0:
                        for q in range(GROUPS):
                            ring.wait_read(pe, "q", u, q)
                            ring.wait_read(pe, "k", u, q)
                        ring.wait_read(pe, "v", u)
                    scores(u, p)
                if 3 <= g < PAIRS * U + 3:
                    probs_T(*divmod(g - 3, PAIRS))
                if 4 <= g < PAIRS * U + 4:
                    values(*divmod(g - 4, PAIRS))

            def project_out(u):
                s = u
                pe.wait_ge(*o_read.at(GROUPS * (u + 1)))
                ps = ring.open(pe, "y", u)
                for t in range(TG):
                    for g in range(GROUPS):
                        mm = pe.matmul(ps[:, t * P:(t + 1) * P], oT[s][:, g, t * P:(t + 1) * P], wo_pad[:, g, :],
                                       start=(g == 0), stop=(g == GROUPS - 1))
                mm.then_inc(ring.filled("y", u), 1)

            def h_T(u):
                pe.wait_ge(*hn_ready.at(TG * (u + 1)))
                transposes("hT", u, hn[u])

            steps = dict(lnT=ln_T, qk01=lambda u: qk(u, (0, 1)), qk23=lambda u: qk(u, (2, 3)), v=v_, out=project_out,
                         hT=h_T)
            with pe.Fori(0, NG // U) as it:
                run_steps(stages, PAIRS, U, 5, steps, pair_step)
                meet.join(pe, "tensor")

        @block.scalar
        def _(act):
            act.wait_ge(cleared, 4)
            act.wait_ge(t_ps, 1)
            w_ps = banks[0][:, 0:2 * P].rearrange("k (g a d) -> k g a d", g=GROUPS, a=2)
            for i in range(2):
                for n in range(3):
                    act.activation(wq[:, :, i::2, n * DH3:(n + 1) * DH3], w_ps[:, :, :, i * DH3:(i + 1) * DH3],
                                   ACT.Copy, scale=1 / math.sqrt(DH3))
                    act.activation(wk[:, :, i::2, n * DH3:(n + 1) * DH3], w_ps[:, :, :, 2 * DH3:3 * DH3], ACT.Copy)
            act.activation(wv[:].rearrange("k (g a) d -> k g a d", a=2), w_ps[:, :, :, 3 * DH3:4 * DH3], ACT.Copy)
            act.activation(woT[:], banks[0][:, 2 * P:3 * P], ACT.Copy).then_inc(act_setup, 1)
            act.wait_ge(act_setup, 1)
            for j in range(4):
                for g in range(GROUPS):
                    k = (4 * g + j) * DH3
                    act.dma_start(wo_pad[32 * j:32 * j + DH3, g, :], woT[k:k + DH3, :]).then_inc(staged, 16)
            act.wait_ge(staged, 16 * 4 * GROUPS)
            act.sem_inc(ready, 1)
            act.wait_ge(ready, 4)

            def affine(dst, ps, ln):
                return act.activation(dst, ps, ACT.Identity, scale=ln[:, 0:1], bias=ln[:, 1:2])

            def norm1(u):
                ps = ring.wait(act, "lnT", u)
                affine(lnT[u][:], ps[:], ln1).then_inc(ring.read("lnT", u), 1)

            def round_qk(u, groups):
                for g in groups:
                    for i, name in enumerate("qk"):
                        ps = ring.wait(act, name, u, g)
                        n = 2 * (GROUPS * u + g) + i
                        if n >= 2:
                            ring.wait_read(act, name, (n // 2 - 1) // GROUPS, (n // 2 - 1) % GROUPS)
                        act.activation(rounded[i][:], ps[:], ACT.Copy).then_inc(rounded_ready.sem, 1)

            def read_v(u):
                ps = ring.wait(act, "v", u)
                act.activation(v[u][:, :, :, 0:DH3], ps[:, 0:TG * 64].rearrange("p (t h d) -> p t h d", t=TG, h=KV3),
                               ACT.Copy).then_inc(ring.read("v", u), 1)

            def pair_step(g):
                if g >= 6 and g % 2 == 0:
                    m = (g - 6) // 2
                    act.wait_ge(*o_full.at(2 * (m + 1)))
                    act.activation(oT[m // GROUPS][:, m % GROUPS, :], o_banks[m % 2][:], ACT.Copy)\
                        .then_inc(o_read.sem, 1)
                u, p = divmod(g, PAIRS)
                if u < U:
                    for i in range(2):
                        n = 2 * g + i
                        ps = ring.wait(act, "s", u, p, i)
                        act.wait_ge(*negmax_ready.at(n + 1))
                        if n >= NPR:
                            m = n - NPR
                            ring.wait(act, "pT", m // H3, (m % H3) // 2, m % 2)
                        for t in range(TG):
                            ins = act.activation(probs[:, n % NPR, t, :], ps[:, t * P:(t + 1) * P], ACT.Exp,
                                                 bias=negmax[:, n % NPR, t:t + 1],
                                                 accum_out=sums[:, n % NPR, t:t + 1])
                        ins.then_inc(ring.read("s", u, p, i), 1)

            def out_step(u):
                ps = ring.wait(act, "hT", u)
                affine(hT_all[:, bass.ds((it * U + u) * TG, TG), :].rearrange("p t n -> p (t n)"), ps[:], ln2)\
                    .then_inc(ring.read("hT", u), 1)

            steps = dict(lnT=norm1, qk01=lambda u: round_qk(u, (0, 1)), qk23=lambda u: round_qk(u, (2, 3)), v=read_v,
                         hT=out_step)
            with act.Fori(0, NG // U) as it:
                run_steps(stages, PAIRS, U, 5, steps, pair_step)
                meet.join(act, "scalar")

        @block.vector
        def _(dve):
            dve.memset(wq[:], 0.0).then_inc(cleared, 1)
            dve.memset(wk[:], 0.0).then_inc(cleared, 1)
            dve.memset(wo_pad[:], 0.0).then_inc(cleared, 1)
            dve.memset(v[0][:], 0.0)
            dve.memset(v[1][:], 0.0).then_inc(cleared, 1)
            dve.memset(zeros[:], 0.0).then_inc(cleared, 1)
            chain = Chain(dve, dve_setup)
            dve.tensor_copy(ident_bf[:], ident[:])
            dve.wait_ge(mask_iota, 1)
            chain(dve.tensor_scalar(low_bits[:], iota[:], N // TC - 1, None, ALU.bitwise_and))
            chain(dve.tensor_copy(mask_f[:], low_bits[:]))
            chain(dve.tensor_scalar(mask_f[:], mask_f[:], 0.5, -MASKED, ALU.is_ge, ALU.mult))
            dve.sem_inc(mask_iota, 1)
            dve.wait_ge(mask_iota, 3)
            for t in range(TG):
                ins = dve.tensor_copy(mask[:, t, :], mask_f[:])
            chain(ins)
            dve.sem_inc(ready, 1)
            dve.wait_ge(ready, 4)
            roots = {"n": 0}

            def link(ins):
                chain(ins)

            def normalise(s, src, dst, done):
                for t in range(TG):
                    link(dve.bn_stats(stats[s][:, t, :], src[:, t, :]))
                for t in range(TG):
                    dve.bn_aggr(mv[s][:, t, :], stats[s][:, t, :]).then_inc(mv_ready.sem, 1)
                roots["n"] += 1
                dve.wait_ge(*rstd_ready.at(roots["n"]))
                for t in range(TG):
                    dve.tensor_scalar(dst[:, t, :], src[:, t, :], mv[s][:, t, 0:1], rstd[s][:, TG + t:TG + t + 1],
                                      ALU.subtract, ALU.mult).then_inc(done.sem, 1)

            def norm1(u):
                dve.wait_ge(x_loaded[u % XS], 16 * (u // XS + 1))
                normalise(u % 2, x[u], xn[u], xn_ready)

            def split_qk(u, groups):
                for g in groups:
                    for i, (name, dst) in enumerate((("q", qT), ("k", kT))):
                        ps = ring.bank(name, u, g)
                        dve.wait_ge(*rounded_ready.at(2 * (GROUPS * u + g) + i + 1))
                        dve.scalar_tensor_tensor(dst[u][:, g, :], rounded[i][:].bitcast(F32), split[:, i:i + 1], ps[:],
                                                 ALU.mult, ALU.add).then_inc(ring.read(name, u, g), 1)

            def out_step(u):
                s = u
                ps = ring.wait(dve, "y", u)
                flat = lambda a: a.rearrange("p t n -> p (t n)")
                dve.tensor_tensor(flat(r[s][:]), ps[:], flat(x[s][:]), ALU.add).then_inc(ring.read("y", u), 1)
                ring.wait_read(dve, "y", u)
                normalise(s, r[s], hn[s], hn_ready)
                dve.wait_ge(*hn_ready.at(TG * (u + 1)))
                dve.tensor_copy(hn_all[:, bass.ds((it * U + u) * TG, TG), :], hn[s][:])
                dve.tensor_tensor(flat(acc_all[:, bass.ds((it * U + u) * TG, TG), :]), flat(r[s][:]), flat(x[s][:]),
                                  ALU.add).then_inc(acc_ready.sem, 1)

            def pair_step(g):
                u, p = divmod(g, PAIRS)
                if u < U:
                    for i in range(2):
                        ps = ring.wait(dve, "s", u, p, i)
                        dve.tensor_reduce(negmax[:, (2 * g + i) % NPR, :], ps[:].rearrange("q (t k) -> q t k", t=TG),
                                          AX.X, ALU.max, negate=True).then_inc(negmax_ready.sem, 1)
                if 1 <= g < PAIRS * U + 1:
                    u, p = divmod(g - 1, PAIRS)
                    for i in range(2):
                        n = 2 * (g - 1) + i
                        ring.wait_read(dve, "s", u, p, i)
                        dve.reciprocal(rsums[:, n % NPR, :], sums[:, n % NPR, :]).then_inc(rs_ready.sem, 1)
                if 3 <= g < PAIRS * U + 3:
                    u, p = divmod(g - 3, PAIRS)
                    for i in range(2):
                        n = 2 * (g - 3) + i
                        ps = ring.wait(dve, "pT", u, p, i)
                        if n >= NPR:
                            dve.wait_ge(*o_full.at((n - NPR) // 2 + 1))
                        dve.tensor_copy(pT[:, n % NPR].rearrange("k t q -> k (t q)"), ps[:])\
                            .then_inc(ring.read("pT", u, p, i), 1)

            steps = dict(norm1=norm1, qk01=lambda u: split_qk(u, (0, 1)), qk23=lambda u: split_qk(u, (2, 3)), out=out_step)
            with dve.Fori(0, NG // U) as it:
                chain = Chain(dve, dve_chain)
                run_steps(stages, PAIRS, U, 5, steps, pair_step)
                meet.join(dve, "vector")

        @block.gpsimd
        def _(pool):
            pool.iota(iota[:], pattern=[[-1, P]], base=P, channel_multiplier=1).then_inc(mask_iota, 1)
            pool.wait_ge(mask_iota, 2)
            pool.affine_select(out=mask_f[:], in_=mask_f[:], compare_op=ALU.is_ge, fill=-MASKED, base=0,
                               pattern=[[-1, P]], channel_multiplier=1).then_inc(mask_iota, 1)
            pool.sem_inc(ready, 1)
            pool.wait_ge(ready, 4)
            count = {"mv": 0}

            def root(u):
                s = u
                count["mv"] += TG
                pool.wait_ge(*mv_ready.at(count["mv"]))
                chain(pool.tensor_scalar(rstd[s][:, 0:TG], mv[s][:, :, 1], LN_EPS, None, ALU.add))
                pool.tensor_tensor(rstd[s][:, TG:2 * TG], rstd[s][:, 0:TG], K["eps_half"][:, 0:TG], ALU.pow)\
                    .then_inc(rstd_ready.sem, 1)

            def pair_step(g):
                if 1 <= g < PAIRS * U + 1:
                    for i in range(2):
                        n = 2 * (g - 1) + i
                        pool.wait_ge(*rs_ready.at(n + 1))
                        for t in range(TG):
                            ins = pool.tensor_scalar(probs[:, n % NPR, t, :], probs[:, n % NPR, t, :],
                                                     rsums[:, n % NPR, t:t + 1], 1.0, ALU.mult, ALU.mult)
                        ins.then_inc(p_ready.sem, 1)

            steps = dict(norm1=root, out=root)
            with pool.Fori(0, NG // U) as it:
                chain = Chain(pool, pool_chain)
                run_steps(stages, PAIRS, U, 5, steps, pair_step)
                meet.lead(pool, first, last)
            pool.sem_clear(range(FIRST_SEM, meet.arrived.num))

        @block.sync
        def _(sy):
            for dst, src in loads:
                sy.dma_start(dst, src, allow_slow_non_contiguous=True).then_inc(loaded, 16)
            sy.wait_ge(cleared, 5)
            spare = xs[0:SLOTS].rearrange("(a p) d -> p a d", p=P)
            parts = 4
            size = SLOTS // P // parts
            for i in range(parts):
                sy.dma_start(spare[:, i * size:(i + 1) * size, :], zeros[:].broadcast_to([P, size, D])).then_inc(zeroed, 16)
            sy.sem_inc(ready, 1)
            xin = x_in.rearrange("b n d -> (b n) d").rearrange("(p g t) d -> g p t d", p=P, t=TG)
            with sy.Fori(0, NG // U) as it:
                for u in range(U):
                    if u >= XS:
                        sy.wait_ge(*acc_ready.at(u - XS + 1))
                    sy.dma_start(x[u][:], xin[it * U + u]).then_inc(x_loaded[u % XS], 16)
                sy.wait_ge(zeroed, 16 * parts)
                meet.join(sy, "sync")


ROUTE_SEMS = 16
EXPERT_SEMS = 64
SLOTS = NE * CAP


def route(nc, A, hT_all, hn_all, idx_get, gate_w, xs):
    with ExitStack() as ctx:
        def sb(name, shape, dt=F32):
            return ctx.enter_context(nc.sbuf_tensor(name, shape, dt))

        sems = []

        def sem(name):
            s = ctx.enter_context(nc.semaphore(name, num=FIRST_SEM + len(sems)))
            sems.append(s)
            return s

        wr = sb("e_router", [P, NE])
        before = sb("e_before", [P, P])
        rev = sb("e_rev", [P, TC, NE])
        rev_i = sb("e_rev_i", [P, TC, NE], I32)
        trash_i = sb("e_trash_i", [P, 2, TC], I32)
        trash = sb("e_trash", [P, 2, TC])
        small = sb("e_small", [P, 6, TC])
        kept = sb("e_kept", [P, 2, TC])
        place = sb("e_place", [P, 2, TC])
        place_out = sb("e_place_out", [P, 2, TC])
        idx_put = sb("e_idx_put", [P, 2, TC], I32)
        prob = sb("e_prob", [P, TC, NE])
        rest, chosen, ping, pong = (sb(f"e_work{i}", [P, TC, NE]) for i in range(4))
        picks = [sb(f"e_pick{k}", [P, TC, NE]) for k in range(2)]
        total = sb("e_total", [P, NE])
        earlier = sb("e_earlier", [P, NE])
        banks = [ctx.enter_context(nc.psum_tensor(f"pe{i}", [P, 512], F32)) for i in range(2)]

        loaded = sem("e_router_loaded")
        iota_ready = sem("e_iota_ready")
        before_ready = sem("e_before_ready")
        logits_ready = sem("e_logits")
        shifted = sem("e_logits_shifted")
        exp_ready = sem("e_exp_ready")
        total_ready = sem("e_totals_ready")
        earlier_ready = sem("e_earlier_ready")
        places_ready = sem("e_places_ready")
        scattered = sem("e_rows_scattered")
        dve_chain = sem("e_dve_chain")
        pool_chain = sem("e_pool_chain")

        block = ctx.enter_context(nc.Block())

        @block.tensor
        def _(pe):
            pe.wait_ge(loaded, 16)
            for c in range(TC):
                mm = pe.matmul(banks[0][:, c * NE:(c + 1) * NE], hT_all[:, c, :], wr[:], start=True, stop=True)
            mm.then_inc(logits_ready, 1)
            pe.wait_ge(total_ready, 1)
            pe.wait_ge(before_ready, 1)
            pe.matmul(banks[1][:, 0:NE], before[:], total[:], start=True, stop=True).then_inc(earlier_ready, 1)

        @block.scalar
        def _(act):
            act.wait_ge(shifted, 1)
            act.activation(prob[:], prob[:], ACT.Exp).then_inc(exp_ready, 1)

        @block.vector
        def _(dve):
            chain = Chain(dve, dve_chain)

            def wide(a):
                return a.unsqueeze(2).broadcast_to([P, TC, NE])

            dve.wait_ge(logits_ready, 1)
            l = banks[0][:, 0:TC * NE].rearrange("p (c e) -> p c e", e=NE)
            chain(dve.tensor_reduce(small[:, 0, :], l, AX.X, ALU.max))
            dve.tensor_tensor(prob[:], l, wide(small[:, 0, :]), ALU.subtract).then_inc(shifted, 1)
            dve.wait_ge(iota_ready, 1)
            dve.tensor_copy(rev[:], rev_i[:])
            dve.tensor_copy(trash[:], trash_i[:])
            dve.wait_ge(exp_ready, 1)
            chain(dve.tensor_reduce(small[:, 1, :], prob[:], AX.X, ALU.add))
            chain(dve.reciprocal(small[:, 2, :], small[:, 1, :]))
            chain(dve.tensor_tensor(prob[:], prob[:], wide(small[:, 2, :]), ALU.mult))
            src = prob
            for k, pick in enumerate(picks):
                chain(dve.tensor_reduce(small[:, 3 + k, :], src[:], AX.X, ALU.max))
                chain(dve.tensor_tensor(pick[:], src[:], wide(small[:, 3 + k, :]), ALU.is_equal))
                chain(dve.tensor_tensor(pick[:], pick[:], rev[:], ALU.mult))
                chain(dve.tensor_reduce(small[:, 5, :], pick[:], AX.X, ALU.max))
                chain(dve.tensor_tensor(pick[:], pick[:], wide(small[:, 5, :]), ALU.is_equal))
                if k == 0:
                    chain(dve.scalar_tensor_tensor(rest[:], pick[:], -2.0, prob[:], ALU.mult, ALU.add))
                    src = rest
            chain(dve.tensor_tensor(chosen[:], picks[0][:], picks[1][:], ALU.add))
            dve.tensor_reduce(total[:], chosen[:].rearrange("p c e -> p e c"), AX.X, ALU.add).then_inc(total_ready, 1)
            a, b = ping, pong
            chain(dve.tensor_copy(a[:], chosen[:]))
            n = 1
            while n < TC:
                chain(dve.tensor_copy(b[:, 0:n], a[:, 0:n]))
                chain(dve.tensor_tensor(b[:, n:TC], a[:, n:TC], a[:, 0:TC - n], ALU.add))
                a, b = b, a
                n *= 2
            chain(dve.tensor_tensor(b[:], a[:], chosen[:], ALU.subtract))
            dve.wait_ge(earlier_ready, 1)
            chain(dve.tensor_copy(earlier[:], banks[1][:, 0:NE]))
            chain(dve.tensor_tensor(b[:], b[:], earlier[:].unsqueeze(1).broadcast_to([P, TC, NE]), ALU.add))
            chain(dve.tensor_scalar(a[:], b[:], CAP - 0.5, None, ALU.is_le))
            chain(dve.scalar_tensor_tensor(b[:], rev[:], -float(CAP), b[:], ALU.mult, ALU.add))
            chain(dve.tensor_scalar(b[:], b[:], float(SLOTS), None, ALU.add))
            chain(dve.tensor_tensor(b[:], b[:], a[:], ALU.mult))
            for k, pick in enumerate(picks):
                chain(dve.tensor_tensor(rest[:], pick[:], b[:], ALU.mult))
                chain(dve.tensor_reduce(place[:, k, :], rest[:], AX.X, ALU.add))
                chain(dve.tensor_tensor(rest[:], pick[:], a[:], ALU.mult))
                chain(dve.tensor_reduce(kept[:, k, :], rest[:], AX.X, ALU.add))
            chain(dve.tensor_tensor(place_out[:], kept[:], trash[:], ALU.mult))
            chain(dve.tensor_tensor(place_out[:], place_out[:], trash[:], ALU.subtract))
            chain(dve.tensor_tensor(place_out[:], place[:], place_out[:], ALU.subtract))
            dve.tensor_copy(idx_put[:], place_out[:]).then_inc(places_ready, 1)
            dve.tensor_copy(idx_get[:], place[:])
            chain(dve.tensor_tensor(small[:, 0, :], small[:, 3, :], small[:, 4, :], ALU.add))
            chain(dve.reciprocal(small[:, 1, :], small[:, 0, :]))
            for k in range(2):
                chain(dve.tensor_tensor(kept[:, k, :], kept[:, k, :], small[:, 3 + k, :], ALU.mult))
                chain(dve.tensor_tensor(gate_w[:, k, :], kept[:, k, :], small[:, 1, :], ALU.mult))

        @block.gpsimd
        def _(pool):
            pool.iota(trash_i[:], pattern=[[TC * P, 2], [P, TC]], base=SLOTS, channel_multiplier=1)
            pool.iota(rev_i[:], pattern=[[0, TC], [-1, NE]], base=NE, channel_multiplier=0).then_inc(iota_ready, 1)
            chain = Chain(pool, pool_chain)
            chain(pool.memset(before[:], 1.0))
            pool.affine_select(out=before[:], in_=before[:], compare_op=ALU.is_ge, fill=0.0, base=-1,
                               pattern=[[1, P]], channel_multiplier=-1).then_inc(before_ready, 1)
            pool.wait_ge(places_ready, 1)
            for c in range(TC):
                for k in range(2):
                    pool.indirect_dma_start(out=xs, out_offset=bass.IndirectOffsetOnAxis(ap=idx_put[:, k, c:c + 1], axis=0),
                                            in_=hn_all[:, c, :], in_offset=None).then_inc(scattered, 16)
            pool.wait_ge(scattered, 16 * 2 * TC)

        @block.sync
        def _(sy):
            sy.dma_start(wr[:], A["L1_ffn_router_weight"]).then_inc(loaded, 16)


def experts(nc, A, K, xs, ys):
    U = 4
    GT = 2
    W = GT * P
    PER = CAP // W
    ITEMS = U * PER
    with ExitStack() as ctx:
        def sb(name, shape, dt=F32):
            return ctx.enter_context(nc.sbuf_tensor(name, shape, dt))

        sems = []

        def sem(name):
            s = ctx.enter_context(nc.semaphore(name, num=FIRST_SEM + ROUTE_SEMS + len(sems)))
            sems.append(s)
            return s

        def sets(n, name, shape):
            return Sets([sb(f"{name}{i}", shape) for i in range(n)])

        XS, YS = 4, 4
        ident = K["ident"]
        w1 = sb("m_w1", [P, U, F])
        w2 = sb("m_w2", [P, U, FC, D])
        ln2 = sb("m_ln2", [P, 2])
        x = sets(XS, "m_x", [P, GT, D])
        hT = sets(2, "m_hT", [P, W])
        hid = sets(2, "m_hid", [P, FC, W])
        y = sets(YS, "m_y", [P, GT, D])
        banks = [ctx.enter_context(nc.psum_tensor(f"pm{i}", [P, 512], F32)) for i in range(8)]

        ln_loaded = sem("m_ln_loaded")
        meet = Meeting(sem, ["sync", "scalar", "tensor", "vector"])
        n_setup = len(sems)
        ring = Ring(banks, sem)
        w_loaded = [sem(f"m_w{e}_loaded") for e in range(U)]
        x_loaded = [sem(f"m_x{i}_loaded") for i in range(XS)]
        y_ready = Counted(sem("m_y_ready"))
        stored = [sem(f"m_y{i}_stored") for i in range(YS)]
        first, last = sems[n_setup].num, sems[-1].num
        block = ctx.enter_context(nc.Block())

        @block.tensor
        def _(pe):
            def transposes(n):
                pe.wait_ge(x_loaded[n % XS], 16 * (n // XS + 1))
                ps = ring.open(pe, "hT", n)
                for t in range(GT):
                    mm = pe.transpose(ps[:, t * P:(t + 1) * P], x[n][:, t, :], ident[:])
                mm.then_inc(ring.filled("hT", n), 1)

            def up(n):
                if n % PER == 0:
                    pe.wait_ge(w_loaded[n // PER], 32)
                ring.wait_read(pe, "hT", n)
                for half in range(2):
                    ps = ring.open(pe, "up", n, half)
                    for i in range(2):
                        c = 2 * half + i
                        mm = pe.matmul(ps[:, i * W:(i + 1) * W], w1[:, n // PER, c * P:(c + 1) * P], hT[n][:],
                                       start=True, stop=True)
                    mm.then_inc(ring.filled("up", n, half), 1)

            def down(n):
                for half in range(2):
                    ring.wait_read(pe, "up", n, half)
                ps = ring.open(pe, "down", n)
                for t in range(GT):
                    for c in range(FC):
                        mm = pe.matmul(ps[:, t * P:(t + 1) * P], hid[n][:, c, t * P:(t + 1) * P], w2[:, n // PER, c, :],
                                       start=(c == 0), stop=(c == FC - 1))
                mm.then_inc(ring.filled("down", n), 1)

            with pe.Fori(0, NE // U) as it:
                transposes(0)
                for n in range(ITEMS + 1):
                    if n + 1 < ITEMS:
                        transposes(n + 1)
                    if n < ITEMS:
                        up(n)
                    if n >= 1:
                        down(n - 1)
                meet.join(pe, "tensor")

        @block.scalar
        def _(act):
            act.dma_start(ln2[:, 0:1], col(A["L1_ffn_ln2_weight"]), allow_slow_non_contiguous=True).then_inc(ln_loaded, 16)
            act.dma_start(ln2[:, 1:2], col(A["L1_ffn_ln2_bias"]), allow_slow_non_contiguous=True).then_inc(ln_loaded, 16)
            act.wait_ge(ln_loaded, 32)

            def rows(n):
                ps = ring.wait(act, "hT", n)
                act.activation(hT[n][:], ps[:, 0:W], ACT.Identity, scale=ln2[:, 0:1], bias=ln2[:, 1:2])\
                    .then_inc(ring.read("hT", n), 1)

            with act.Fori(0, NE // U) as it:
                rows(0)
                for n in range(ITEMS):
                    if n + 1 < ITEMS:
                        rows(n + 1)
                    if n >= 2:
                        ring.wait(act, "down", n - 2)
                    for half in range(2):
                        ps = ring.wait(act, "up", n, half)
                        act.activation(hid[n][:, 2 * half:2 * half + 2, :].rearrange("p c n -> p (c n)"), ps[:],
                                       ACT.Gelu).then_inc(ring.read("up", n, half), 1)
                meet.join(act, "scalar")

        @block.vector
        def _(dve):
            with dve.Fori(0, NE // U) as it:
                for n in range(ITEMS):
                    if n >= YS:
                        dve.wait_ge(stored[n % YS], 16 * (n // YS))
                    ps = ring.wait(dve, "down", n)
                    dve.tensor_copy(y[n][:].rearrange("p t d -> p (t d)"), ps[:, 0:GT * D]).then_inc(y_ready.sem, 1)
                    dve.wait_ge(*y_ready.at(n + 1))
                    dve.sem_inc(ring.read("down", n), 1)
                meet.join(dve, "vector")

        @block.gpsimd
        def _(pool):
            with pool.Fori(0, NE // U) as it:
                meet.lead(pool, first, last)

        @block.sync
        def _(sy):
            yo = ys.rearrange("(i n t p) d -> i n p t d", i=NE // U, t=GT, p=P)
            xi = xs[0:SLOTS].rearrange("(i n t p) d -> i n p t d", i=NE // U, t=GT, p=P)
            w1i = A["L1_ffn_moe_w1"].rearrange("(i e) k f -> i e k f", e=U)
            w2i = A["L1_ffn_moe_w2"].rearrange("(i e) (c p) n -> i e p c n", e=U, p=P)
            with sy.Fori(0, NE // U) as it:
                def load_weights(e):
                    sy.dma_start(w1[:, e, :], w1i[it, e]).then_inc(w_loaded[e], 16)
                    sy.dma_start(w2[:, e], w2i[it, e]).then_inc(w_loaded[e], 16)

                def store(n):
                    sy.wait_ge(*y_ready.at(n + 1))
                    sy.dma_start(yo[it, n], y[n][:]).then_inc(stored[n % YS], 16)

                for n in range(ITEMS):
                    if n >= XS:
                        ring.wait(sy, "hT", n - XS)
                    sy.dma_start(x[n][:], xi[it, n]).then_inc(x_loaded[n % XS], 16)
                    if n < U:
                        load_weights(n)
                    if n >= XS:
                        store(n - XS)
                for n in range(ITEMS - XS, ITEMS):
                    store(n)
                for i in range(YS):
                    sy.wait_ge(stored[i], 16 * ((ITEMS - 1 - i) // YS + 1))
                meet.join(sy, "sync")


def combine(nc, K, acc_all, idx_get, gate_w, ys, out):
    with ExitStack() as ctx:
        def sb(name, shape, dt=F32):
            return ctx.enter_context(nc.sbuf_tensor(name, shape, dt))

        sems = []

        def sem(name):
            s = ctx.enter_context(nc.semaphore(name, num=FIRST_SEM + ROUTE_SEMS + EXPERT_SEMS + len(sems)))
            sems.append(s)
            return s

        g = Sets([sb(f"f_rows{i}", [P, 2, TG, D]) for i in range(2)])
        y = Sets([sb(f"f_y{i}", [P, TG, D]) for i in range(2)])
        stats = sb("f_stats", [P, TG, 6])
        mv = Sets([sb(f"f_mv{i}", [P, TG, 2]) for i in range(2)])
        rstd = Sets([sb(f"f_rstd{i}", [P, 2 * TG]) for i in range(2)])
        fetched = [sem(f"f_rows{i}_fetched") for i in range(2)]
        summed = sem("f_summed")
        mv_ready = sem("f_moments_ready")
        rstd_ready = sem("f_roots_ready")
        y_ready = sem("f_y_ready")
        stored = [sem(f"f_y{i}_stored") for i in range(2)]
        dve_chain = sem("f_dve_chain")
        pool_chain = sem("f_pool_chain")
        block = ctx.enter_context(nc.Block())

        @block.gpsimd
        def _(pool):
            chain = Chain(pool, pool_chain)

            def root(n):
                pool.wait_ge(mv_ready, TG * (n + 1))
                chain(pool.tensor_scalar(rstd[n][:, 0:TG], mv[n][:, :, 1], LN_EPS, None, ALU.add))
                pool.tensor_tensor(rstd[n][:, TG:2 * TG], rstd[n][:, 0:TG], K["eps_half"][:, 0:TG], ALU.pow)\
                    .then_inc(rstd_ready, 1)

            for n in range(NG):
                if n >= 2:
                    pool.wait_ge(summed, n - 1)
                for t in range(TG):
                    for k in range(2):
                        c = n * TG + t
                        pool.indirect_dma_start(out=g[n][:, k, t, :], out_offset=None, in_=ys,
                                                in_offset=bass.IndirectOffsetOnAxis(ap=idx_get[:, k, c:c + 1], axis=0))\
                            .then_inc(fetched[n % 2], 16)
                if n >= 1:
                    root(n - 1)
            root(NG - 1)

        @block.vector
        def _(dve):
            chain = Chain(dve, dve_chain)

            def finish(n):
                dve.wait_ge(rstd_ready, n + 1)
                if n >= 2:
                    dve.wait_ge(stored[n % 2], 16 * (n // 2))
                for t in range(TG):
                    dve.tensor_scalar(y[n][:, t, :], acc_all[:, n * TG + t, :], mv[n][:, t, 0:1],
                                      rstd[n][:, TG + t:TG + t + 1], ALU.subtract, ALU.mult).then_inc(y_ready, 1)

            for n in range(NG):
                dve.wait_ge(fetched[n % 2], 16 * 2 * TG * (n // 2 + 1))
                for k in range(2):
                    for t in range(TG):
                        c = n * TG + t
                        ins = dve.scalar_tensor_tensor(acc_all[:, c, :], g[n][:, k, t, :], gate_w[:, k, c:c + 1],
                                                       acc_all[:, c, :], ALU.mult, ALU.add)
                    chain(ins)
                dve.sem_inc(summed, 1)
                for t in range(TG):
                    chain(dve.bn_stats(stats[:, t, :], acc_all[:, n * TG + t, :]))
                for t in range(TG):
                    dve.bn_aggr(mv[n][:, t, :], stats[:, t, :]).then_inc(mv_ready, 1)
                if n >= 1:
                    finish(n - 1)
            finish(NG - 1)

        @block.sync
        def _(sy):
            xo = out.rearrange("b n d -> (b n) d").rearrange("(p g t) d -> g p t d", p=P, t=TG)
            for n in range(NG):
                sy.wait_ge(y_ready, TG * (n + 1))
                sy.dma_start(xo[n], y[n][:]).then_inc(stored[n % 2], 16)
            for i in range(2):
                sy.wait_ge(stored[i], 16 * (NG // 2))


def kernel(**inputs):
    import concourse.bacc as bacc
    from concourse.bass_utils import run_bass_kernel_spmd

    nc = bacc.Bacc("TRN2", target_bir_lowering=False, num_devices=1)
    arrays, A = {}, {}
    for name, a in inputs.items():
        a = np.ascontiguousarray(a)
        arrays[f"in_{name}_dram"] = a
        A[name] = nc.dram_tensor(f"in_{name}_dram", a.shape, mybir.dt.from_np(a.dtype), kind="ExternalInput").ap()
    out = nc.dram_tensor("out_0_dram", (B, N, D), F32, kind="ExternalOutput").ap()
    build(nc, A, out)
    r = run_bass_kernel_spmd(nc, [arrays], core_ids=[0])
    return r.results[0]["out_0_dram"]
```
